# Optimizing a Trainium2 kernel written in Bass

```python
import numpy as np
import jax
import jax.numpy as jnp

def _softmax(x, axis=-1):
    return jax.nn.softmax(x, axis=axis)

def _gelu(x):
    return jax.nn.gelu(x, approximate=True)

def _silu(x):
    return jax.nn.silu(x)

def _sigmoid(x):
    return jax.nn.sigmoid(x)

def _layernorm(x, axis=-1, eps=1e-05):
    m = jnp.mean(x, axis=axis, keepdims=True)
    v = jnp.var(x, axis=axis, keepdims=True)
    return (x - m) / jnp.sqrt(v + eps)

def _scatter_add(tgt, idx, src, axis=0):
    return tgt.at[idx].add(src)

def _segment_sum(src, seg, n):
    return jax.ops.segment_sum(src, seg, n)
kernel_name = 'mk_decoder_preln_d4_seqx_r4_24ebf9'

def setup_inputs(seed: int=0):
    np.random.seed(seed)
    _w = jnp.asarray

    def _rec_inputs():
        import jax
        import jax.numpy as jnp
        _rk = jax.random.key(seed)
        x = -0.0005207 + 1.001 * jax.random.normal(jax.random.fold_in(_rk, 1), (2, 1024, 256), jnp.float32)
        _lenS = 1024 - jax.random.randint(jax.random.fold_in(_rk, 7), (2,), 0, max(1, 1024 // 4) + 1, jnp.int32)
        _lenS2 = 77 - jax.random.randint(jax.random.fold_in(_rk, 8), (2,), 0, max(1, 77 // 4) + 1, jnp.int32)
        _ctx_1024P = jax.random.normal(jax.random.fold_in(_rk, 12), (2, 16, 256), jnp.float32)
        _ctx_1024c = jax.random.dirichlet(jax.random.fold_in(_rk, 512), 0.3 * jnp.ones((16,), jnp.float32), (2, 77))
        _ctx_1024t = jnp.einsum('bsk,bkd->bsd', _ctx_1024c, _ctx_1024P)
        _ctx_1024t = _ctx_1024t * jax.lax.rsqrt(jnp.mean(jnp.square(_ctx_1024t)) + 1e-12) * 0.953939
        ctx_1024 = 0.00191187 + 0.999416 * (_ctx_1024t + 0.3 * jax.random.normal(jax.random.fold_in(_rk, 612), (2, 77, 256), jnp.float32))
        _validS = jnp.arange(1024)[None, :] < _lenS[:, None]
        _validS2 = jnp.arange(77)[None, :] < _lenS2[:, None]
        _causal = jnp.tril(jnp.ones((1024, 1024), dtype=bool))
        mask_BxS_ff1 = jnp.where(jnp.ones((2, 1024), dtype=bool), 1.0, 0.0).astype(jnp.float32)
        mask_BxS2_ik0 = jnp.where(jnp.broadcast_to(_validS2[:, :], (2, 77)), 0, 1).astype(jnp.int32)
        return (x, ctx_1024, mask_BxS_ff1, mask_BxS2_ik0)
    x, ctx_1024, mask_BxS_ff1, mask_BxS2_ik0 = _rec_inputs()

    def _L0_attn_setup():
        import jax, jax.numpy as jnp
        import numpy as np
        import math
        N_HEAD = 16
        ROPE_BASE = 10000.0

        def _rope_cos_sin(seq_len, head_dim, dtype):
            half = head_dim // 2
            inv_freq = ROPE_BASE ** (-(jnp.arange(half, dtype=jnp.float32) * 2.0 / head_dim))
            t = jnp.arange(seq_len, dtype=jnp.float32)
            ang = t[:, None] * inv_freq[None, :]
            return (jnp.cos(ang).astype(dtype), jnp.sin(ang).astype(dtype))

        def _apply_rope(x, cos, sin):
            x1 = x[..., 0::2]
            x2 = x[..., 1::2]
            c = cos[None, :, None, :]
            s = sin[None, :, None, :]
            out = jnp.stack([x1 * c - x2 * s, x1 * s + x2 * c], axis=-1)
            return out.reshape(x.shape)
        key = jax.random.key(seed)
        kx, kq, kk, kv, ko = jax.random.split(key, 5)
        B, S, H = (2, 512, 256)
        x = jax.random.normal(kx, (B, S, H), dtype=jnp.float32)
        scale = 0.02
        w_q = jax.random.normal(kq, (H, H), dtype=jnp.float32) * scale
        w_k = jax.random.normal(kk, (H, H), dtype=jnp.float32) * scale
        w_v = jax.random.normal(kv, (H, H), dtype=jnp.float32) * scale
        w_o = jax.random.normal(ko, (H, H), dtype=jnp.float32) * scale
        return {'x': x, 'w_q': w_q, 'w_k': w_k, 'w_v': w_v, 'w_o': w_o}
    _L0_attn_all = _L0_attn_setup()
    _L0_attn_in = {k: v for k, v in _L0_attn_all.items() if k in ('w_q', 'w_k', 'w_v', 'w_o')}
    del _L0_attn_all

    def _L0_xattn_setup():
        import jax, jax.numpy as jnp
        import numpy as np
        B, F, T, D = (8, 64, 32, 256)
        NEG = -1e+30
        key = jax.random.key(seed)
        ks = jax.random.split(key, 10)
        s = 1.0 / np.sqrt(D)
        return {'features': jax.random.normal(ks[0], (B, F, D), jnp.float32), 'masks': jnp.ones((B, F), jnp.float32), 'textual_features': jax.random.normal(ks[1], (B, T, D), jnp.float32), 'q_masks': jax.random.randint(ks[2], (B, T), 0, 2, jnp.int32), 'Ws': jax.random.normal(ks[3], (D, D), jnp.float32) * s, 'W': jax.random.normal(ks[4], (D, D), jnp.float32) * s, 'w': jax.random.normal(ks[5], (D, 1), jnp.float32) * s, 'b': jax.random.normal(ks[6], (1, D), jnp.float32) * s, 'Wcw': jax.random.normal(ks[7], (1, D), jnp.float32) * s, 'bcw': jnp.zeros((1,), jnp.float32), 'Wcb': jax.random.normal(ks[8], (1, D), jnp.float32) * s, 'bcb': jnp.zeros((1,), jnp.float32)}
    _L0_xattn_all = _L0_xattn_setup()
    _L0_xattn_in = {k: v for k, v in _L0_xattn_all.items() if k in ('Ws', 'W', 'w', 'b', 'Wcw', 'bcw', 'Wcb', 'bcb')}
    del _L0_xattn_all

    def _L0_ffn_setup():
        import jax, jax.numpy as jnp
        import numpy as np
        B, S, D, H, E = (4, 512, 256, 512, 8)
        key = jax.random.key(seed)
        ks = jax.random.split(key, 8)
        scale = 0.02
        return {'x': jax.random.normal(ks[0], (B, S, D), dtype=jnp.float32), 'Wr': jax.random.normal(ks[1], (D, E), dtype=jnp.float32) * scale, 'br': jnp.zeros((E,), dtype=jnp.float32), 'W1': jax.random.normal(ks[2], (E, D, H), dtype=jnp.float32) * scale, 'b1': jnp.zeros((E, H), dtype=jnp.float32), 'W2': jax.random.normal(ks[3], (E, H, D), dtype=jnp.float32) * scale, 'b2': jnp.zeros((E, D), dtype=jnp.float32)}
    _L0_ffn_all = _L0_ffn_setup()
    _L0_ffn_in = {k: v for k, v in _L0_ffn_all.items() if k in ('Wr', 'br', 'W1', 'b1', 'W2', 'b2')}
    del _L0_ffn_all

    def _L1_attn_setup():
        import jax, jax.numpy as jnp
        import numpy as np
        B, T, C = (8, 512, 256)

        def _rotate(z, cos_a, sin_a):
            b, t, c = z.shape
            z = z.reshape(b, t, c // 2, 2)
            z0, z1 = (z[..., 0], z[..., 1])
            r0 = cos_a * z0 + sin_a * z1
            r1 = -sin_a * z0 + cos_a * z1
            return jnp.stack([r0, r1], axis=-1).reshape(b, t, c)
        key = jax.random.key(seed)
        ks = jax.random.split(key, 9)
        s = 1.0 / np.sqrt(C)
        return {'x': jax.random.normal(ks[0], (B, T, C), dtype=jnp.float32), 'Wk': jax.random.uniform(ks[1], (C, C), jnp.float32, -s, s), 'bk': jax.random.uniform(ks[2], (C,), jnp.float32, -s, s), 'Wq': jax.random.uniform(ks[3], (C, C), jnp.float32, -s, s), 'bq': jax.random.uniform(ks[4], (C,), jnp.float32, -s, s), 'Wv': jax.random.uniform(ks[5], (C, C), jnp.float32, -s, s), 'bv': jax.random.uniform(ks[6], (C,), jnp.float32, -s, s), 'Wp': jax.random.uniform(ks[7], (C, C), jnp.float32, -s, s), 'bp': jax.random.uniform(ks[8], (C,), jnp.float32, -s, s)}
    _L1_attn_all = _L1_attn_setup()
    _L1_attn_in = {k: v for k, v in _L1_attn_all.items() if k in ('Wk', 'bk', 'Wq', 'bq', 'Wv', 'bv', 'Wp', 'bp')}
    del _L1_attn_all

    def _L1_xattn_setup():
        import jax, jax.numpy as jnp
        import numpy as np
        B, S, E = (8, 512, 256)
        EPS = 0.001

        def _layer_norm(x, gamma, beta):
            mu = jnp.mean(x, axis=-1, keepdims=True)
            var = jnp.mean(jnp.square(x - mu), axis=-1, keepdims=True)
            return gamma * (x - mu) * jax.lax.rsqrt(var + EPS) + beta

        def _attention(q_in, k_in, v_in, WQ, WK, WV, causal):
            Q = jnp.einsum('bse,ed->bsd', q_in, WQ)
            K = jnp.einsum('bse,ed->bsd', k_in, WK)
            V = jnp.einsum('bse,ed->bsd', v_in, WV)
            d = K.shape[-1]
            scores = jnp.einsum('bqd,bkd->bqk', Q, K) / jnp.sqrt(jnp.float32(d))
            if causal:
                qlen, klen = (scores.shape[-2], scores.shape[-1])
                mask = jnp.triu(jnp.ones((qlen, klen), bool), k=1)
                scores = jnp.where(mask[None], -jnp.inf, scores)
            p = jax.nn.softmax(scores, axis=-1)
            return jnp.einsum('bqk,bkd->bqd', p, V)
        key = jax.random.key(seed)
        ks = jax.random.split(key, 10)
        sc = 1.0 / np.sqrt(E)
        return {'inputs': jax.random.normal(ks[0], (B, S, E), jnp.float32), 'context': jax.random.normal(ks[1], (B, S, E), jnp.float32), 'Wq': jax.random.normal(ks[2], (E, E), jnp.float32) * sc, 'Wk': jax.random.normal(ks[3], (E, E), jnp.float32) * sc, 'Wv': jax.random.normal(ks[4], (E, E), jnp.float32) * sc, 'Wcq': jax.random.normal(ks[5], (E, E), jnp.float32) * sc, 'Wck': jax.random.normal(ks[6], (E, E), jnp.float32) * sc, 'Wcv': jax.random.normal(ks[7], (E, E), jnp.float32) * sc, 'gamma': jnp.ones((E,), jnp.float32), 'beta': jnp.zeros((E,), jnp.float32), 'W1': jax.random.normal(ks[8], (E, E), jnp.float32) * sc, 'b1': jnp.zeros((E,), jnp.float32)}
    _L1_xattn_all = _L1_xattn_setup()
    _L1_xattn_in = {k: v for k, v in _L1_xattn_all.items() if k in ('Wq', 'Wk', 'Wv', 'Wcq', 'Wck', 'Wcv', 'gamma', 'beta', 'W1', 'b1')}
    del _L1_xattn_all

    def _L1_ffn_setup():
        import jax, jax.numpy as jnp
        import numpy as np
        EPS = 1e-05

        def rmsnorm(x):
            return x * jax.lax.rsqrt(jnp.mean(x * x, axis=-1, keepdims=True) + EPS)

        def act_quant(x):
            scale = 127.0 / jnp.clip(jnp.max(jnp.abs(x), axis=-1, keepdims=True), 1e-05)
            q = jnp.clip(jnp.round(x * scale), -128.0, 127.0) / scale
            return x + jax.lax.stop_gradient(q - x)

        def weight_quant(w):
            scale = 1.0 / jnp.clip(jnp.mean(jnp.abs(w)), 1e-05)
            q = jnp.clip(jnp.round(w * scale), -1.0, 1.0) / scale
            return w + jax.lax.stop_gradient(q - w)

        def bitlinear(x, w, b):
            xq = act_quant(rmsnorm(x))
            wq = weight_quant(w)
            return jnp.einsum('bsd,fd->bsf', xq, wq) + b
        key = jax.random.key(seed)
        k0, k1, k2 = jax.random.split(key, 3)
        B, S, D, F = (2, 2048, 256, 1024)
        x = jax.random.normal(k0, (B, S, D), dtype=jnp.float32)
        w1 = jax.random.normal(k1, (F, D), dtype=jnp.float32) * (1.0 / np.sqrt(D))
        b1 = jnp.zeros((F,), dtype=jnp.float32)
        w2 = jax.random.normal(k2, (D, F), dtype=jnp.float32) * (1.0 / np.sqrt(F))
        b2 = jnp.zeros((D,), dtype=jnp.float32)
        return {'x': x, 'w1': w1, 'b1': b1, 'w2': w2, 'b2': b2}
    _L1_ffn_all = _L1_ffn_setup()
    _L1_ffn_in = {k: v for k, v in _L1_ffn_all.items() if k in ('w1', 'b1', 'w2', 'b2')}
    del _L1_ffn_all

    def _L2_attn_setup():
        import jax, jax.numpy as jnp
        import numpy as np
        B, T, HS, H, R = (4, 512, 256, 16, 16)
        D = HS // H
        LOGIT_01 = float(np.log(0.1 / 0.9))
        LOGIT_098 = float(np.log(0.98 / 0.02))

        def _rope_cos_sin(seq_len, dim, base=10000.0):
            half = dim // 2
            inv_freq = 1.0 / base ** (jnp.arange(half, dtype=jnp.float32) / half)
            freqs = jnp.arange(seq_len, dtype=jnp.float32)[:, None] * inv_freq[None, :]
            return (jnp.cos(freqs), jnp.sin(freqs))

        def _apply_rope(x, cos, sin):
            c = cos[None, :, None, :]
            s = sin[None, :, None, :]
            x1 = x[..., 0::2]
            x2 = x[..., 1::2]
            r1 = x1 * c - x2 * s
            r2 = x1 * s + x2 * c
            return jnp.stack((r1, r2), axis=-1).reshape(x.shape)
        key = jax.random.key(seed)
        ks = jax.random.split(key, 10)

        def rn(k, shape, s=0.02):
            return jax.random.normal(k, shape, dtype=jnp.float32) * s
        return {'x': jax.random.normal(ks[0], (B, T, HS), dtype=jnp.float32), 'q_w': rn(ks[1], (HS, HS)), 'k_w': rn(ks[2], (HS, HS)), 'v_w': rn(ks[3], (HS, HS)), 'Wq': rn(ks[4], (H, R, D), 0.05), 'Wk': rn(ks[5], (H, R, D), 0.05), 'g_w': rn(ks[6], (H * R, HS)), 'g_b': jnp.full((H * R,), LOGIT_01, dtype=jnp.float32), 'base_decay_logits': jnp.full((H, R), LOGIT_098, dtype=jnp.float32), 'out_w': rn(ks[7], (HS, HS)), 'out_b': jnp.zeros((HS,), dtype=jnp.float32), 'ln_g': jnp.ones((HS,), dtype=jnp.float32), 'ln_b': jnp.zeros((HS,), dtype=jnp.float32)}
    _L2_attn_all = _L2_attn_setup()
    _L2_attn_in = {k: v for k, v in _L2_attn_all.items() if k in ('q_w', 'k_w', 'v_w', 'Wq', 'Wk', 'g_w', 'g_b', 'base_decay_logits', 'out_w', 'out_b', 'ln_g', 'ln_b')}
    del _L2_attn_all

    def _L2_xattn_setup():
        import jax, jax.numpy as jnp
        import numpy as np
        D = 256
        H = 16
        HD = D // H
        B, S = (2, 512)
        key = jax.random.key(seed)
        ks = jax.random.split(key, 11)
        s = 0.02
        return {'q': jax.random.normal(ks[0], (B, S, D), jnp.float32), 'k': jax.random.normal(ks[1], (B, S, D), jnp.float32), 'v': jax.random.normal(ks[2], (B, S, D), jnp.float32), 'Wq': jax.random.normal(ks[3], (D, D), jnp.float32) * s, 'bq': jnp.zeros((D,), jnp.float32), 'Wk': jax.random.normal(ks[4], (D, HD), jnp.float32) * s, 'bk': jnp.zeros((HD,), jnp.float32), 'Wv': jax.random.normal(ks[5], (D, HD), jnp.float32) * s, 'bv': jnp.zeros((HD,), jnp.float32), 'Wo': jax.random.normal(ks[6], (D, D), jnp.float32) * s, 'bo': jnp.zeros((D,), jnp.float32)}
    _L2_xattn_all = _L2_xattn_setup()
    _L2_xattn_in = {k: v for k, v in _L2_xattn_all.items() if k in ('Wq', 'bq', 'Wk', 'bk', 'Wv', 'bv', 'Wo', 'bo')}
    del _L2_xattn_all

    def _L2_ffn_setup():
        import jax, jax.numpy as jnp
        import numpy as np
        DIM = 256
        DEPTH = 7
        PAR = 8
        N_NODES = 2 ** (DEPTH + 1) - 1
        WIDTH = PAR * N_NODES
        key = jax.random.key(seed)
        k1, k2, k3, k4 = jax.random.split(key, 4)
        init_k = float(np.sqrt(1.0 / DIM))
        init_k2 = float(np.sqrt(1.0 / ((DEPTH + 1) * PAR)))
        oldx = jax.random.normal(k1, (4, 512, DIM), dtype=jnp.float32)
        W_in = jax.random.uniform(k2, (WIDTH, DIM), jnp.float32, -init_k, init_k)
        b_in = jax.random.uniform(k3, (WIDTH,), jnp.float32, -init_k, init_k)
        W_out = jax.random.uniform(k4, (DIM, WIDTH), jnp.float32, -init_k2, init_k2)
        return {'oldx': oldx, 'W_in': W_in, 'b_in': b_in, 'W_out': W_out}
    _L2_ffn_all = _L2_ffn_setup()
    _L2_ffn_in = {k: v for k, v in _L2_ffn_all.items() if k in ('W_in', 'b_in', 'W_out')}
    del _L2_ffn_all

    def _L3_attn_setup():
        import jax, jax.numpy as jnp
        import numpy as np
        from functools import partial
        B, S, D, H, DK, DV, DFF = (4, 512, 256, 8, 128, 128, 1024)
        EPS = 1e-06

        def rms_norm(x):
            return x * jax.lax.rsqrt(jnp.mean(x * x, axis=-1, keepdims=True) + EPS)

        def l2norm(x):
            return x * jax.lax.rsqrt(jnp.sum(x * x, axis=-1, keepdims=True) + EPS)

        def gated_delta_net(h, Wq, Wk, Wv, Wb, Wa, A_log, dt_bias, Wg, o_norm_w, Wo):
            b, s, _ = h.shape
            q = l2norm(jax.nn.silu(h @ Wq).reshape(b, s, H, DK))
            k = l2norm(jax.nn.silu(h @ Wk).reshape(b, s, H, DK))
            v = jax.nn.silu(h @ Wv).reshape(b, s, H, DV)
            beta = jax.nn.sigmoid(h @ Wb)
            g = -jnp.exp(A_log) * jax.nn.softplus(h @ Wa + dt_bias)
            alpha = jnp.exp(g)
            scale = DK ** (-0.5)
            tm = lambda a: jnp.moveaxis(a, 1, 0)
            qs, ks_, vs, als, bts = (tm(q), tm(k), tm(v), tm(alpha), tm(beta))

            def step(Sst, inp):
                q_t, k_t, v_t, a_t, b_t = inp
                Sst = Sst * a_t[..., None, None]
                kv = jnp.einsum('bhd,bhde->bhe', k_t, Sst)
                delta = (v_t - kv) * b_t[..., None]
                Sst = Sst + jnp.einsum('bhd,bhe->bhde', k_t, delta)
                o_t = jnp.einsum('bhd,bhde->bhe', q_t, Sst) * scale
                return (Sst, o_t)
            S0 = jnp.zeros((b, H, DK, DV), dtype=h.dtype)
            _, o = jax.lax.scan(step, S0, (qs, ks_, vs, als, bts))
            o = jnp.moveaxis(o, 0, 1)
            gate = (h @ Wg).reshape(b, s, H, DV)
            o = rms_norm(o) * o_norm_w * jax.nn.silu(gate)
            return o.reshape(b, s, H * DV) @ Wo
        key = jax.random.key(seed)
        ks = jax.random.split(key, 16)
        w = lambda k, shp: jax.random.normal(k, shp, dtype=jnp.float32) * 0.02
        return {'x': jax.random.normal(ks[0], (B, S, D), dtype=jnp.float32), 'Wq': w(ks[1], (D, H * DK)), 'Wk': w(ks[2], (D, H * DK)), 'Wv': w(ks[3], (D, H * DV)), 'Wb': w(ks[4], (D, H)), 'Wa': w(ks[5], (D, H)), 'A_log': jnp.log(jnp.linspace(1.0, 8.0, H).astype(jnp.float32)), 'dt_bias': jax.random.normal(ks[6], (H,), dtype=jnp.float32) * 0.1, 'Wg': w(ks[7], (D, H * DV)), 'o_norm_w': jnp.ones((DV,), dtype=jnp.float32), 'Wo': w(ks[8], (H * DV, D)), 'W_fc': w(ks[9], (D, DFF)), 'W_proj': w(ks[10], (DFF, D))}
    _L3_attn_all = _L3_attn_setup()
    _L3_attn_in = {k: v for k, v in _L3_attn_all.items() if k in ('Wq', 'Wk', 'Wv', 'Wb', 'Wa', 'A_log', 'dt_bias', 'Wg', 'o_norm_w', 'Wo', 'W_fc', 'W_proj')}
    del _L3_attn_all

    def _L3_xattn_setup():
        import jax, jax.numpy as jnp
        import numpy as np
        D, H = (256, 16)
        DH = D // H

        def _split_heads(z):
            b, t, _ = z.shape
            return z.reshape(b, t, H, DH).transpose(0, 2, 1, 3)
        key = jax.random.key(seed)
        ks = jax.random.split(key, 11)
        b, t, ta = (2, 512, 375)
        s = 1.0 / np.sqrt(D)
        return {'x': jax.random.normal(ks[0], (b, t, D), dtype=jnp.float32), 'xa': jax.random.normal(ks[1], (b, ta, D), dtype=jnp.float32), 'Wqkv': jax.random.normal(ks[2], (D, 3 * D), dtype=jnp.float32) * s, 'bqkv': jax.random.normal(ks[3], (3 * D,), dtype=jnp.float32) * 0.01, 'Wqkv_aux': jax.random.normal(ks[4], (D, 3 * D), dtype=jnp.float32) * s, 'bqkv_aux': jax.random.normal(ks[5], (3 * D,), dtype=jnp.float32) * 0.01, 'Wo': jax.random.normal(ks[6], (D, D), dtype=jnp.float32) * s, 'bo': jax.random.normal(ks[7], (D,), dtype=jnp.float32) * 0.01, 'g': jnp.zeros((H,), dtype=jnp.float32)}
    _L3_xattn_all = _L3_xattn_setup()
    _L3_xattn_in = {k: v for k, v in _L3_xattn_all.items() if k in ('Wqkv', 'bqkv', 'Wqkv_aux', 'bqkv_aux', 'Wo', 'bo', 'g')}
    del _L3_xattn_all

    def _L3_ffn_setup():
        import jax, jax.numpy as jnp
        import numpy as np
        B, S, H = (4, 512, 256)
        E, K = (8, 2)
        I_R, I_S = (4 * H, 8 * H)
        CAP_FACTOR = 1.25
        SCALE = 1.0
        key = jax.random.key(seed)
        ks = jax.random.split(key, 9)
        std = 0.02
        return {'x': jax.random.normal(ks[0], (B, S, H), jnp.float32), 'router_w': std * jax.random.normal(ks[1], (E, H), jnp.float32), 'rg': std * jax.random.normal(ks[2], (E, H, I_R), jnp.float32), 'ru': std * jax.random.normal(ks[3], (E, H, I_R), jnp.float32), 'rd': std * jax.random.normal(ks[4], (E, I_R, H), jnp.float32), 'sg': std * jax.random.normal(ks[5], (H, I_S), jnp.float32), 'su': std * jax.random.normal(ks[6], (H, I_S), jnp.float32), 'sd': std * jax.random.normal(ks[7], (I_S, H), jnp.float32)}
    _L3_ffn_all = _L3_ffn_setup()
    _L3_ffn_in = {k: v for k, v in _L3_ffn_all.items() if k in ('router_w', 'rg', 'ru', 'rd', 'sg', 'su', 'sd')}
    del _L3_ffn_all
    return {'x': x, 'ctx_1024': ctx_1024, 'mask_BxS_ff1': mask_BxS_ff1, 'mask_BxS2_ik0': mask_BxS2_ik0, 'L0_attn_w_q': _L0_attn_in['w_q'], 'L0_attn_w_k': _L0_attn_in['w_k'], 'L0_attn_w_v': _L0_attn_in['w_v'], 'L0_attn_w_o': _L0_attn_in['w_o'], 'L0_xattn_Ws': _L0_xattn_in['Ws'], 'L0_xattn_W': _L0_xattn_in['W'], 'L0_xattn_w': _L0_xattn_in['w'], 'L0_xattn_b': _L0_xattn_in['b'], 'L0_xattn_Wcw': _L0_xattn_in['Wcw'], 'L0_xattn_bcw': _L0_xattn_in['bcw'], 'L0_xattn_Wcb': _L0_xattn_in['Wcb'], 'L0_xattn_bcb': _L0_xattn_in['bcb'], 'L0_ffn_Wr': _L0_ffn_in['Wr'], 'L0_ffn_br': _L0_ffn_in['br'], 'L0_ffn_W1': _L0_ffn_in['W1'], 'L0_ffn_b1': _L0_ffn_in['b1'], 'L0_ffn_W2': _L0_ffn_in['W2'], 'L0_ffn_b2': _L0_ffn_in['b2'], 'L1_attn_Wk': _L1_attn_in['Wk'], 'L1_attn_bk': _L1_attn_in['bk'], 'L1_attn_Wq': _L1_attn_in['Wq'], 'L1_attn_bq': _L1_attn_in['bq'], 'L1_attn_Wv': _L1_attn_in['Wv'], 'L1_attn_bv': _L1_attn_in['bv'], 'L1_attn_Wp': _L1_attn_in['Wp'], 'L1_attn_bp': _L1_attn_in['bp'], 'L1_xattn_Wq': _L1_xattn_in['Wq'], 'L1_xattn_Wk': _L1_xattn_in['Wk'], 'L1_xattn_Wv': _L1_xattn_in['Wv'], 'L1_xattn_Wcq': _L1_xattn_in['Wcq'], 'L1_xattn_Wck': _L1_xattn_in['Wck'], 'L1_xattn_Wcv': _L1_xattn_in['Wcv'], 'L1_xattn_gamma': _L1_xattn_in['gamma'], 'L1_xattn_beta': _L1_xattn_in['beta'], 'L1_xattn_W1': _L1_xattn_in['W1'], 'L1_xattn_b1': _L1_xattn_in['b1'], 'L1_ffn_w1': _L1_ffn_in['w1'], 'L1_ffn_b1': _L1_ffn_in['b1'], 'L1_ffn_w2': _L1_ffn_in['w2'], 'L1_ffn_b2': _L1_ffn_in['b2'], 'L2_attn_q_w': _L2_attn_in['q_w'], 'L2_attn_k_w': _L2_attn_in['k_w'], 'L2_attn_v_w': _L2_attn_in['v_w'], 'L2_attn_Wq': _L2_attn_in['Wq'], 'L2_attn_Wk': _L2_attn_in['Wk'], 'L2_attn_g_w': _L2_attn_in['g_w'], 'L2_attn_g_b': _L2_attn_in['g_b'], 'L2_attn_base_decay_logits': _L2_attn_in['base_decay_logits'], 'L2_attn_out_w': _L2_attn_in['out_w'], 'L2_attn_out_b': _L2_attn_in['out_b'], 'L2_attn_ln_g': _L2_attn_in['ln_g'], 'L2_attn_ln_b': _L2_attn_in['ln_b'], 'L2_xattn_Wq': _L2_xattn_in['Wq'], 'L2_xattn_bq': _L2_xattn_in['bq'], 'L2_xattn_Wk': _L2_xattn_in['Wk'], 'L2_xattn_bk': _L2_xattn_in['bk'], 'L2_xattn_Wv': _L2_xattn_in['Wv'], 'L2_xattn_bv': _L2_xattn_in['bv'], 'L2_xattn_Wo': _L2_xattn_in['Wo'], 'L2_xattn_bo': _L2_xattn_in['bo'], 'L2_ffn_W_in': _L2_ffn_in['W_in'], 'L2_ffn_b_in': _L2_ffn_in['b_in'], 'L2_ffn_W_out': _L2_ffn_in['W_out'], 'L3_attn_Wq': _L3_attn_in['Wq'], 'L3_attn_Wk': _L3_attn_in['Wk'], 'L3_attn_Wv': _L3_attn_in['Wv'], 'L3_attn_Wb': _L3_attn_in['Wb'], 'L3_attn_Wa': _L3_attn_in['Wa'], 'L3_attn_A_log': _L3_attn_in['A_log'], 'L3_attn_dt_bias': _L3_attn_in['dt_bias'], 'L3_attn_Wg': _L3_attn_in['Wg'], 'L3_attn_o_norm_w': _L3_attn_in['o_norm_w'], 'L3_attn_Wo': _L3_attn_in['Wo'], 'L3_attn_W_fc': _L3_attn_in['W_fc'], 'L3_attn_W_proj': _L3_attn_in['W_proj'], 'L3_xattn_Wqkv': _L3_xattn_in['Wqkv'], 'L3_xattn_bqkv': _L3_xattn_in['bqkv'], 'L3_xattn_Wqkv_aux': _L3_xattn_in['Wqkv_aux'], 'L3_xattn_bqkv_aux': _L3_xattn_in['bqkv_aux'], 'L3_xattn_Wo': _L3_xattn_in['Wo'], 'L3_xattn_bo': _L3_xattn_in['bo'], 'L3_xattn_g': _L3_xattn_in['g'], 'L3_ffn_router_w': _L3_ffn_in['router_w'], 'L3_ffn_rg': _L3_ffn_in['rg'], 'L3_ffn_ru': _L3_ffn_in['ru'], 'L3_ffn_rd': _L3_ffn_in['rd'], 'L3_ffn_sg': _L3_ffn_in['sg'], 'L3_ffn_su': _L3_ffn_in['su'], 'L3_ffn_sd': _L3_ffn_in['sd']}

def reference(x, ctx_1024, mask_BxS_ff1, mask_BxS2_ik0, L0_attn_w_q, L0_attn_w_k, L0_attn_w_v, L0_attn_w_o, L0_xattn_Ws, L0_xattn_W, L0_xattn_w, L0_xattn_b, L0_xattn_Wcw, L0_xattn_bcw, L0_xattn_Wcb, L0_xattn_bcb, L0_ffn_Wr, L0_ffn_br, L0_ffn_W1, L0_ffn_b1, L0_ffn_W2, L0_ffn_b2, L1_attn_Wk, L1_attn_bk, L1_attn_Wq, L1_attn_bq, L1_attn_Wv, L1_attn_bv, L1_attn_Wp, L1_attn_bp, L1_xattn_Wq, L1_xattn_Wk, L1_xattn_Wv, L1_xattn_Wcq, L1_xattn_Wck, L1_xattn_Wcv, L1_xattn_gamma, L1_xattn_beta, L1_xattn_W1, L1_xattn_b1, L1_ffn_w1, L1_ffn_b1, L1_ffn_w2, L1_ffn_b2, L2_attn_q_w, L2_attn_k_w, L2_attn_v_w, L2_attn_Wq, L2_attn_Wk, L2_attn_g_w, L2_attn_g_b, L2_attn_base_decay_logits, L2_attn_out_w, L2_attn_out_b, L2_attn_ln_g, L2_attn_ln_b, L2_xattn_Wq, L2_xattn_bq, L2_xattn_Wk, L2_xattn_bk, L2_xattn_Wv, L2_xattn_bv, L2_xattn_Wo, L2_xattn_bo, L2_ffn_W_in, L2_ffn_b_in, L2_ffn_W_out, L3_attn_Wq, L3_attn_Wk, L3_attn_Wv, L3_attn_Wb, L3_attn_Wa, L3_attn_A_log, L3_attn_dt_bias, L3_attn_Wg, L3_attn_o_norm_w, L3_attn_Wo, L3_attn_W_fc, L3_attn_W_proj, L3_xattn_Wqkv, L3_xattn_bqkv, L3_xattn_Wqkv_aux, L3_xattn_bqkv_aux, L3_xattn_Wo, L3_xattn_bo, L3_xattn_g, L3_ffn_router_w, L3_ffn_rg, L3_ffn_ru, L3_ffn_rd, L3_ffn_sg, L3_ffn_su, L3_ffn_sd):
    import jax
    import jax.numpy as jnp

    def _L0_attn_ref(x, w_q, w_k, w_v, w_o):
        import jax, jax.numpy as jnp
        import numpy as np
        import math
        N_HEAD = 16
        ROPE_BASE = 10000.0

        def _rope_cos_sin(seq_len, head_dim, dtype):
            half = head_dim // 2
            inv_freq = ROPE_BASE ** (-(jnp.arange(half, dtype=jnp.float32) * 2.0 / head_dim))
            t = jnp.arange(seq_len, dtype=jnp.float32)
            ang = t[:, None] * inv_freq[None, :]
            return (jnp.cos(ang).astype(dtype), jnp.sin(ang).astype(dtype))

        def _apply_rope(x, cos, sin):
            x1 = x[..., 0::2]
            x2 = x[..., 1::2]
            c = cos[None, :, None, :]
            s = sin[None, :, None, :]
            out = jnp.stack([x1 * c - x2 * s, x1 * s + x2 * c], axis=-1)
            return out.reshape(x.shape)
        B, S, H = x.shape
        d = H // N_HEAD
        q = (x @ w_q.T).reshape(B, S, N_HEAD, d)
        k = (x @ w_k.T).reshape(B, S, N_HEAD, d)
        v = (x @ w_v.T).reshape(B, S, N_HEAD, d)
        cos, sin = _rope_cos_sin(S, d, x.dtype)
        q = _apply_rope(q, cos, sin)
        k = _apply_rope(k, cos, sin)
        scores = jnp.einsum('bqhd,bkhd->bhqk', q, k) / math.sqrt(d)
        coefs = jax.nn.softmax(scores, axis=-1)
        causal = jnp.tril(jnp.ones((S, S), dtype=bool))
        coefs = jnp.where(causal[None, None], coefs, 0.0)
        out = jnp.einsum('bhqk,bkhd->bqhd', coefs, v).reshape(B, S, H)
        return out @ w_o.T

    def _L0_xattn_ref(features, masks, textual_features, q_masks, Ws, W, w, b, Wcw, bcw, Wcb, bcb):
        import jax, jax.numpy as jnp
        import numpy as np
        B, F, T, D = (8, 64, 32, 256)
        NEG = -1e+30
        txt_proj = jnp.einsum('btd,de->bte', textual_features, Ws)
        feat_proj = jnp.einsum('bfd,de->bfe', features, W)
        h = jnp.tanh(txt_proj[:, None, :, :] + feat_proj[:, :, None, :] + b[None, None, :, :][..., 0, :])
        rho = jnp.einsum('bftd,d->bft', h, w[:, 0])
        qm = q_masks.astype(jnp.float32)
        rho = rho + (1.0 - qm)[:, None, :] * NEG
        att = jax.nn.softmax(rho, axis=-1)
        txt_h = jnp.einsum('bft,btd->bfd', att, textual_features)
        w_s = jnp.tanh(jnp.einsum('bfd,od->bfo', txt_h, Wcw) + bcw)
        b_s = jnp.tanh(jnp.einsum('bfd,od->bfo', txt_h, Wcb) + bcb)
        return w_s * features + b_s

    def _L0_ffn_ref(x, Wr, br, W1, b1, W2, b2):
        import jax, jax.numpy as jnp
        import numpy as np
        B, S, D, H, E = (4, 512, 256, 512, 8)
        d = x.shape[-1]
        tokens = x.reshape(-1, d)
        logits = tokens @ Wr + br
        probs = jax.nn.softmax(logits, axis=-1)
        expert = jnp.argmax(probs, axis=-1)
        max_prob = jnp.take_along_axis(probs, expert[:, None], axis=-1)
        h = jax.nn.relu(jnp.einsum('td,edh->teh', tokens, W1) + b1[None])
        y = jnp.einsum('teh,ehd->ted', h, W2) + b2[None]
        out = jnp.take_along_axis(y, expert[:, None, None], axis=1)[:, 0, :]
        return (out * max_prob).reshape(x.shape)

    def _L1_attn_ref(x, Wk, bk, Wq, bq, Wv, bv, Wp, bp):
        import jax, jax.numpy as jnp
        import numpy as np
        B, T, C = (8, 512, 256)

        def _rotate(z, cos_a, sin_a):
            b, t, c = z.shape
            z = z.reshape(b, t, c // 2, 2)
            z0, z1 = (z[..., 0], z[..., 1])
            r0 = cos_a * z0 + sin_a * z1
            r1 = -sin_a * z0 + cos_a * z1
            return jnp.stack([r0, r1], axis=-1).reshape(b, t, c)
        b, t, c = x.shape
        half = c // 2
        k = x @ Wk + bk
        q = x @ Wq + bq
        v = x @ Wv + bv
        angle = jnp.outer(jnp.arange(t, dtype=jnp.float32), jnp.arange(half, dtype=jnp.float32))[::-1]
        cos_a = jnp.cos(angle)
        sin_a = jnp.sin(angle)
        k = _rotate(k, cos_a, sin_a)
        q = _rotate(q, cos_a, sin_a)
        wei = jnp.einsum('bic,bjc->bij', k, q) * c ** (-0.5)
        mask = jnp.tril(jnp.ones((t, t), dtype=bool))
        wei = jnp.where(mask, wei, -jnp.inf)
        wei = jax.nn.softplus(wei)
        out = wei @ v
        out = out @ Wp + bp
        return out

    def _L1_xattn_ref(inputs, context, Wq, Wk, Wv, Wcq, Wck, Wcv, gamma, beta, W1, b1):
        import jax, jax.numpy as jnp
        import numpy as np
        B, S, E = (8, 512, 256)
        EPS = 0.001

        def _layer_norm(x, gamma, beta):
            mu = jnp.mean(x, axis=-1, keepdims=True)
            var = jnp.mean(jnp.square(x - mu), axis=-1, keepdims=True)
            return gamma * (x - mu) * jax.lax.rsqrt(var + EPS) + beta

        def _attention(q_in, k_in, v_in, WQ, WK, WV, causal):
            Q = jnp.einsum('bse,ed->bsd', q_in, WQ)
            K = jnp.einsum('bse,ed->bsd', k_in, WK)
            V = jnp.einsum('bse,ed->bsd', v_in, WV)
            d = K.shape[-1]
            scores = jnp.einsum('bqd,bkd->bqk', Q, K) / jnp.sqrt(jnp.float32(d))
            if causal:
                qlen, klen = (scores.shape[-2], scores.shape[-1])
                mask = jnp.triu(jnp.ones((qlen, klen), bool), k=1)
                scores = jnp.where(mask[None], -jnp.inf, scores)
            p = jax.nn.softmax(scores, axis=-1)
            return jnp.einsum('bqk,bkd->bqd', p, V)
        a = _attention(inputs, inputs, inputs, Wq, Wk, Wv, causal=True) + inputs
        h = _layer_norm(a, gamma, beta)
        c = _attention(h, context, context, Wcq, Wck, Wcv, causal=False) + h
        h = _layer_norm(c, gamma, beta)
        f = jax.nn.relu(jnp.einsum('bse,ed->bsd', h, W1) + b1)
        out = _layer_norm(f + h, gamma, beta)
        return jax.nn.relu(out)

    def _L1_ffn_ref(x, w1, b1, w2, b2):
        import jax, jax.numpy as jnp
        import numpy as np
        EPS = 1e-05

        def rmsnorm(x):
            return x * jax.lax.rsqrt(jnp.mean(x * x, axis=-1, keepdims=True) + EPS)

        def act_quant(x):
            scale = 127.0 / jnp.clip(jnp.max(jnp.abs(x), axis=-1, keepdims=True), 1e-05)
            q = jnp.clip(jnp.round(x * scale), -128.0, 127.0) / scale
            return x + jax.lax.stop_gradient(q - x)

        def weight_quant(w):
            scale = 1.0 / jnp.clip(jnp.mean(jnp.abs(w)), 1e-05)
            q = jnp.clip(jnp.round(w * scale), -1.0, 1.0) / scale
            return w + jax.lax.stop_gradient(q - w)

        def bitlinear(x, w, b):
            xq = act_quant(rmsnorm(x))
            wq = weight_quant(w)
            return jnp.einsum('bsd,fd->bsf', xq, wq) + b
        h = bitlinear(x, w1, b1)
        h = jax.nn.gelu(h, approximate=False)
        return bitlinear(h, w2, b2)

    def _L2_attn_ref(x, q_w, k_w, v_w, Wq, Wk, g_w, g_b, base_decay_logits, out_w, out_b, ln_g, ln_b):
        import jax, jax.numpy as jnp
        import numpy as np
        B, T, HS, H, R = (4, 512, 256, 16, 16)
        D = HS // H
        LOGIT_01 = float(np.log(0.1 / 0.9))
        LOGIT_098 = float(np.log(0.98 / 0.02))

        def _rope_cos_sin(seq_len, dim, base=10000.0):
            half = dim // 2
            inv_freq = 1.0 / base ** (jnp.arange(half, dtype=jnp.float32) / half)
            freqs = jnp.arange(seq_len, dtype=jnp.float32)[:, None] * inv_freq[None, :]
            return (jnp.cos(freqs), jnp.sin(freqs))

        def _apply_rope(x, cos, sin):
            c = cos[None, :, None, :]
            s = sin[None, :, None, :]
            x1 = x[..., 0::2]
            x2 = x[..., 1::2]
            r1 = x1 * c - x2 * s
            r2 = x1 * s + x2 * c
            return jnp.stack((r1, r2), axis=-1).reshape(x.shape)
        b, t, hs = x.shape
        h, r, d = Wq.shape
        q = (x @ q_w.T).reshape(b, t, h, d)
        k = (x @ k_w.T).reshape(b, t, h, d)
        v = (x @ v_w.T).reshape(b, t, h, d)
        cos, sin = _rope_cos_sin(t, d)
        q = _apply_rope(q, cos, sin)
        k = _apply_rope(k, cos, sin)
        q_r = jnp.einsum('bthd,hrd->bthr', q, Wq)
        k_r = jnp.einsum('bthd,hrd->bthr', k, Wk)
        g = jax.nn.sigmoid((x @ g_w.T + g_b).reshape(b, t, h, r))
        decay = jax.nn.sigmoid(base_decay_logits)[None, :, :, None]
        scale = 1.0 / jnp.sqrt(jnp.asarray(d, dtype=x.dtype))

        def step(M, inp):
            q_t, k_t, v_t, g_t = inp
            M = M * decay + jnp.einsum('bhr,bhd->bhrd', g_t * k_t * scale, v_t)
            y = jnp.einsum('bhr,bhrd->bhd', q_t, M)
            return (M, y)
        xs = (q_r.transpose(1, 0, 2, 3), k_r.transpose(1, 0, 2, 3), v.transpose(1, 0, 2, 3), g.transpose(1, 0, 2, 3))
        M0 = jnp.zeros((b, h, r, d), dtype=x.dtype)
        _, Y = jax.lax.scan(step, M0, xs)
        Y = Y.transpose(1, 0, 2, 3).reshape(b, t, hs)
        out = Y @ out_w.T + out_b
        hres = x + out
        mu = jnp.mean(hres, axis=-1, keepdims=True)
        var = jnp.mean((hres - mu) ** 2, axis=-1, keepdims=True)
        return (hres - mu) / jnp.sqrt(var + 1e-05) * ln_g + ln_b

    def _L2_xattn_ref(q, k, v, Wq, bq, Wk, bk, Wv, bv, Wo, bo):
        import jax, jax.numpy as jnp
        import numpy as np
        D = 256
        H = 16
        HD = D // H
        B, S = (2, 512)
        Bsz, Sq, Dm = q.shape
        qh = (q @ Wq + bq).reshape(Bsz, Sq, H, HD).transpose(0, 2, 1, 3)
        kh = k @ Wk + bk
        vh = v @ Wv + bv
        scores = jnp.einsum('bhqd,bkd->bhqk', qh, kh) / jnp.sqrt(jnp.float32(HD))
        scores = jnp.clip(scores, -1000000.0, 1000000.0)
        attn = jax.nn.softmax(scores, axis=-1)
        out = jnp.einsum('bhqk,bkd->bhqd', attn, vh)
        out = out.transpose(0, 2, 1, 3).reshape(Bsz, Sq, Dm)
        return out @ Wo + bo

    def _L2_ffn_ref(oldx, W_in, b_in, W_out):
        import jax, jax.numpy as jnp
        import numpy as np
        DIM = 256
        DEPTH = 7
        PAR = 8
        N_NODES = 2 ** (DEPTH + 1) - 1
        WIDTH = PAR * N_NODES
        x = oldx.reshape(-1, DIM)
        B = x.shape[0]
        logits = x @ W_in.T + b_in
        decisions = (logits > 0).astype(jnp.int32).reshape(B, PAR, N_NODES)
        acts = jax.nn.silu(logits).reshape(B, PAR, N_NODES)
        current = jnp.zeros((B, PAR), dtype=jnp.int32)
        dmap = jax.nn.one_hot(current, N_NODES, dtype=acts.dtype)
        for d in range(DEPTH):
            cur_platform = 2 ** d - 1
            next_platform = 2 ** (d + 1) - 1
            moves = jnp.take_along_axis(decisions, current[..., None], axis=2)[..., 0]
            current = (current - cur_platform) * 2 + moves + next_platform
            dmap = dmap + jax.nn.one_hot(current, N_NODES, dtype=acts.dtype)
        masked = acts * jax.lax.stop_gradient(dmap)
        out = masked.reshape(B, WIDTH) @ W_out.T
        return out.reshape(oldx.shape)

    def _L3_attn_ref(x, Wq, Wk, Wv, Wb, Wa, A_log, dt_bias, Wg, o_norm_w, Wo, W_fc, W_proj):
        import jax, jax.numpy as jnp
        import numpy as np
        from functools import partial
        B, S, D, H, DK, DV, DFF = (4, 512, 256, 8, 128, 128, 1024)
        EPS = 1e-06

        def rms_norm(x):
            return x * jax.lax.rsqrt(jnp.mean(x * x, axis=-1, keepdims=True) + EPS)

        def l2norm(x):
            return x * jax.lax.rsqrt(jnp.sum(x * x, axis=-1, keepdims=True) + EPS)

        def gated_delta_net(h, Wq, Wk, Wv, Wb, Wa, A_log, dt_bias, Wg, o_norm_w, Wo):
            b, s, _ = h.shape
            q = l2norm(jax.nn.silu(h @ Wq).reshape(b, s, H, DK))
            k = l2norm(jax.nn.silu(h @ Wk).reshape(b, s, H, DK))
            v = jax.nn.silu(h @ Wv).reshape(b, s, H, DV)
            beta = jax.nn.sigmoid(h @ Wb)
            g = -jnp.exp(A_log) * jax.nn.softplus(h @ Wa + dt_bias)
            alpha = jnp.exp(g)
            scale = DK ** (-0.5)
            tm = lambda a: jnp.moveaxis(a, 1, 0)
            qs, ks_, vs, als, bts = (tm(q), tm(k), tm(v), tm(alpha), tm(beta))

            def step(Sst, inp):
                q_t, k_t, v_t, a_t, b_t = inp
                Sst = Sst * a_t[..., None, None]
                kv = jnp.einsum('bhd,bhde->bhe', k_t, Sst)
                delta = (v_t - kv) * b_t[..., None]
                Sst = Sst + jnp.einsum('bhd,bhe->bhde', k_t, delta)
                o_t = jnp.einsum('bhd,bhde->bhe', q_t, Sst) * scale
                return (Sst, o_t)
            S0 = jnp.zeros((b, H, DK, DV), dtype=h.dtype)
            _, o = jax.lax.scan(step, S0, (qs, ks_, vs, als, bts))
            o = jnp.moveaxis(o, 0, 1)
            gate = (h @ Wg).reshape(b, s, H, DV)
            o = rms_norm(o) * o_norm_w * jax.nn.silu(gate)
            return o.reshape(b, s, H * DV) @ Wo
        ln_scale = 1.0
        h = gated_delta_net(ln_scale * rms_norm(x), Wq, Wk, Wv, Wb, Wa, A_log, dt_bias, Wg, o_norm_w, Wo)
        x = x + h
        m = ln_scale * rms_norm(x)
        y = jnp.square(jax.nn.relu(m @ W_fc)) @ W_proj
        return x + y

    def _L3_xattn_ref(x, xa, Wqkv, bqkv, Wqkv_aux, bqkv_aux, Wo, bo, g):
        import jax, jax.numpy as jnp
        import numpy as np
        D, H = (256, 16)
        DH = D // H

        def _split_heads(z):
            b, t, _ = z.shape
            return z.reshape(b, t, H, DH).transpose(0, 2, 1, 3)
        qkv = x @ Wqkv + bqkv
        qkv_a = xa @ Wqkv_aux + bqkv_aux
        q, k, v = (_split_heads(c) for c in jnp.split(qkv, 3, axis=-1))
        qa, ka, va = (_split_heads(c) for c in jnp.split(qkv_a, 3, axis=-1))
        scale = 1.0 / jnp.sqrt(jnp.float32(DH))
        dots = jnp.einsum('bhqd,bhkd->bhqk', q, k) * scale
        dots_aux = jnp.einsum('bhqd,bhkd->bhqk', q, ka) * scale
        p = jax.nn.softmax(dots, axis=-1)
        pa = jax.nn.softmax(dots_aux, axis=-1)
        h_main = jnp.einsum('bhqk,bhkd->bhqd', p, v)
        h_aux = jnp.einsum('bhqk,bhkd->bhqd', pa, va)
        gate = jax.nn.sigmoid(g).reshape(1, H, 1, 1)
        out = h_main * (1.0 - gate) + h_aux * gate
        b, _, t, _ = out.shape
        out = out.transpose(0, 2, 1, 3).reshape(b, t, H * DH)
        return out @ Wo + bo

    def _L3_ffn_ref(x, router_w, rg, ru, rd, sg, su, sd):
        import jax, jax.numpy as jnp
        import numpy as np
        B, S, H = (4, 512, 256)
        E, K = (8, 2)
        I_R, I_S = (4 * H, 8 * H)
        CAP_FACTOR = 1.25
        SCALE = 1.0
        b, s, h = x.shape
        T = b * s
        capacity = max(int(CAP_FACTOR * T / E), 1)
        xf = x.reshape(T, h)
        eps = jnp.finfo(x.dtype).eps
        xn = xf * jax.lax.rsqrt(jnp.mean(xf * xf, axis=-1, keepdims=True) + eps)
        logits = xn @ router_w.T
        probs = jax.nn.softmax(logits, axis=-1)
        topk_p, topk_i = jax.lax.top_k(probs, K)
        rw = topk_p / jnp.sum(topk_p, axis=-1, keepdims=True)
        one_hot = jax.nn.one_hot(topk_i, E, dtype=x.dtype)
        mask = one_hot.sum(1)
        wdense = (one_hot * rw[..., None]).sum(1)
        sel = mask.T.astype(bool)
        order = jnp.argsort(~sel, axis=1, stable=True)
        dispatch = order[:, :capacity]
        count = sel.sum(axis=1)
        valid = (jnp.arange(capacity)[None, :] < count[:, None]).astype(x.dtype)
        xg = xf[dispatch]
        gate = jax.nn.silu(jnp.einsum('ech,ehi->eci', xg, rg))
        up = jnp.einsum('ech,ehi->eci', xg, ru)
        eout = jnp.einsum('eci,eih->ech', gate * up, rd)
        w = jnp.take_along_axis(wdense.T, dispatch, axis=1)
        contrib = eout * (w * valid)[..., None]
        routed = jnp.zeros_like(xf).at[dispatch.reshape(-1)].add(contrib.reshape(-1, h))
        shared = jax.nn.silu(x @ sg) * (x @ su) @ sd
        return shared + SCALE * routed.reshape(b, s, h)
    x = x + _L0_attn_ref(_layernorm(x, axis=-1), L0_attn_w_q, L0_attn_w_k, L0_attn_w_v, L0_attn_w_o)
    x = x + _L0_xattn_ref(_layernorm(x, axis=-1), mask_BxS_ff1, ctx_1024, mask_BxS2_ik0, L0_xattn_Ws, L0_xattn_W, L0_xattn_w, L0_xattn_b, L0_xattn_Wcw, L0_xattn_bcw, L0_xattn_Wcb, L0_xattn_bcb)
    x = x + _L0_ffn_ref(_layernorm(x, axis=-1), L0_ffn_Wr, L0_ffn_br, L0_ffn_W1, L0_ffn_b1, L0_ffn_W2, L0_ffn_b2)
    x = x + _L1_attn_ref(_layernorm(x, axis=-1), L1_attn_Wk, L1_attn_bk, L1_attn_Wq, L1_attn_bq, L1_attn_Wv, L1_attn_bv, L1_attn_Wp, L1_attn_bp)
    x = x + _L1_xattn_ref(_layernorm(x, axis=-1), ctx_1024, L1_xattn_Wq, L1_xattn_Wk, L1_xattn_Wv, L1_xattn_Wcq, L1_xattn_Wck, L1_xattn_Wcv, L1_xattn_gamma, L1_xattn_beta, L1_xattn_W1, L1_xattn_b1)
    x = x + _L1_ffn_ref(_layernorm(x, axis=-1), L1_ffn_w1, L1_ffn_b1, L1_ffn_w2, L1_ffn_b2)
    x = x + _L2_attn_ref(_layernorm(x, axis=-1), L2_attn_q_w, L2_attn_k_w, L2_attn_v_w, L2_attn_Wq, L2_attn_Wk, L2_attn_g_w, L2_attn_g_b, L2_attn_base_decay_logits, L2_attn_out_w, L2_attn_out_b, L2_attn_ln_g, L2_attn_ln_b)
    x = x + _L2_xattn_ref(_layernorm(x, axis=-1), ctx_1024, ctx_1024, L2_xattn_Wq, L2_xattn_bq, L2_xattn_Wk, L2_xattn_bk, L2_xattn_Wv, L2_xattn_bv, L2_xattn_Wo, L2_xattn_bo)
    x = x + _L2_ffn_ref(_layernorm(x, axis=-1), L2_ffn_W_in, L2_ffn_b_in, L2_ffn_W_out)
    x = x + _L3_attn_ref(_layernorm(x, axis=-1), L3_attn_Wq, L3_attn_Wk, L3_attn_Wv, L3_attn_Wb, L3_attn_Wa, L3_attn_A_log, L3_attn_dt_bias, L3_attn_Wg, L3_attn_o_norm_w, L3_attn_Wo, L3_attn_W_fc, L3_attn_W_proj)
    x = x + _L3_xattn_ref(_layernorm(x, axis=-1), ctx_1024, L3_xattn_Wqkv, L3_xattn_bqkv, L3_xattn_Wqkv_aux, L3_xattn_bqkv_aux, L3_xattn_Wo, L3_xattn_bo, L3_xattn_g)
    x = x + _L3_ffn_ref(_layernorm(x, axis=-1), L3_ffn_router_w, L3_ffn_rg, L3_ffn_ru, L3_ffn_rd, L3_ffn_sg, L3_ffn_su, L3_ffn_sd)
    return x

_drawn_inputs = setup_inputs


def setup_inputs(seed=0):
    import zlib

    import numpy as np

    out = dict(_drawn_inputs(seed))
    spreads = {'L0_ffn_br': (0.0, 0.1),
     'L0_ffn_b1': (0.0, 0.1),
     'L0_ffn_b2': (0.0, 0.1),
     'L1_xattn_gamma': (1.0, 0.2),
     'L1_xattn_beta': (0.0, 0.367),
     'L1_xattn_b1': (0.0, 0.8),
     'L1_ffn_b1': (0.0, 0.775),
     'L1_ffn_b2': (0.0, 0.708),
     'L2_attn_g_b': (-2.1972246170043945, 0.6),
     'L2_attn_base_decay_logits': (3.891820192337036, 0.6),
     'L2_attn_out_b': (0.0, 2.0),
     'L2_attn_ln_g': (1.0, 0.6),
     'L2_attn_ln_b': (0.0, 0.8),
     'L2_xattn_bq': (0.0, 0.8),
     'L2_xattn_bk': (0.0, 2.0),
     'L2_xattn_bv': (0.0, 0.8),
     'L2_xattn_bo': (0.0, 0.8),
     'L3_attn_o_norm_w': (1.0, 0.6),
     'L3_xattn_g': (0.0, 2.0)}
    factors = {'L0_attn_w_q': 8.0,
     'L0_attn_w_k': 8.0,
     'L0_attn_w_v': 2.766,
     'L0_attn_w_o': 3.16,
     'L0_xattn_W': 5.221,
     'L0_xattn_b': 8.0,
     'L0_ffn_Wr': 3.059,
     'L0_ffn_W1': 3.625,
     'L1_attn_bk': 6.747,
     'L1_attn_bq': 7.154,
     'L1_attn_bp': 8.0,
     'L1_xattn_Wq': 7.04,
     'L1_xattn_Wk': 6.138,
     'L1_xattn_Wcq': 4.323,
     'L1_xattn_Wck': 4.045,
     'L2_attn_q_w': 8.0,
     'L2_attn_k_w': 8.0,
     'L2_attn_v_w': 8.0,
     'L2_attn_Wq': 8.0,
     'L2_attn_Wk': 8.0,
     'L2_attn_g_w': 8.0,
     'L2_attn_out_w': 8.0,
     'L2_xattn_Wq': 8.0,
     'L2_xattn_Wk': 8.0,
     'L2_xattn_Wv': 8.0,
     'L2_xattn_Wo': 8.0,
     'L2_ffn_W_in': 3.63,
     'L2_ffn_b_in': 8.0,
     'L2_ffn_W_out': 3.358,
     'L3_attn_Wq': 8.0,
     'L3_attn_Wk': 8.0,
     'L3_attn_Wv': 8.0,
     'L3_attn_Wb': 8.0,
     'L3_attn_Wa': 8.0,
     'L3_attn_A_log': 8.0,
     'L3_attn_dt_bias': 21.44,
     'L3_attn_Wg': 8.0,
     'L3_attn_Wo': 8.0,
     'L3_attn_W_fc': 8.0,
     'L3_attn_W_proj': 8.0,
     'L3_xattn_bqkv': 54.588,
     'L3_xattn_Wqkv_aux': 2.853,
     'L3_xattn_bqkv_aux': 199.822,
     'L3_xattn_bo': 64.0,
     'L3_ffn_router_w': 8.0,
     'L3_ffn_rg': 8.0,
     'L3_ffn_ru': 8.0,
     'L3_ffn_rd': 8.0,
     'L3_ffn_sg': 8.0,
     'L3_ffn_su': 8.0,
     'L3_ffn_sd': 8.0,
     'L0_xattn_Wcb': 13.704}
    for name, (base, spread) in spreads.items():
        noise = np.random.default_rng([zlib.crc32(name.encode()), seed]).standard_normal(out[name].shape)
        drawn = base * np.exp(spread * noise) if base else spread * noise
        out[name] = jnp.asarray(drawn.astype(out[name].dtype))
    for name, factor in factors.items():
        out[name] = (out[name] * factor).astype(out[name].dtype)
    return out
```

```python
from contextlib import ExitStack

import numpy as np
import concourse.bass as bass
from concourse import mybir

P = 128
B = 2
S = 1024
N = B * S
NT = N // P
ST = S // P
D = 256
KC = D // P
S2 = 77
H = 16
DH = D // H

F32 = mybir.dt.float32
BF16 = mybir.dt.bfloat16
I32 = mybir.dt.int32
ALU = mybir.AluOpType
ACT = mybir.ActivationFunctionType
AX = mybir.AxisListType


class Stage(ExitStack):

    def __init__(self, nc, name):
        super().__init__()
        self.nc, self.name, self.sems = nc, name, []

    def sb(self, name, shape, dt=F32):
        return self.enter_context(self.nc.sbuf_tensor(f"{self.name}_{name}", shape, dt))

    def ps(self, name, shape, dt=F32):
        return self.enter_context(self.nc.psum_tensor(f"{self.name}_{name}", shape, dt))

    def sem(self, name):
        s = self.enter_context(self.nc.semaphore(f"{self.name}_{name}"))
        self.sems.append(s)
        return s

    def __exit__(self, *exc):
        if exc[0] is None:
            for s in self.sems:
                self.nc.gpsimd.sem_clear(s)
            self.nc.all_engine_barrier()
        return super().__exit__(*exc)


class Core:

    def __init__(self, nc, ctx, dram):
        def sb(name, shape, dt=F32):
            return ctx.enter_context(nc.sbuf_tensor(name, shape, dt))

        self.nc, self.dram = nc, dram
        self.x = sb("x_res", [P, NT, D])
        self.xT = sb("xT", [P, KC, N])
        self.ident = sb("ident", [P, P])
        self.lower = sb("lower", [P, P])
        self.ones = sb("ones", [P, P])
        self.ctxT = sb("ctxT", [P, KC, B * S2])


def setup(c):
    nc = c.nc
    with Stage(nc, "setup") as st:
        x_in, zeroed, done = st.sem("x_in"), st.sem("zeroed"), st.sem("done")
        with nc.Block() as block:
            @block.sync
            def _(sp):
                sp.dma_start(c.x[:], c.dram["x"].rearrange("b (t p) d -> p (b t) d", p=P)).then_inc(x_in, 16)
                sp.dma_start(c.ctxT[:], c.dram["ctxT"].rearrange("(k p) n -> p k n", p=P)).then_inc(x_in, 16)
                sp.wait_ge(x_in, 32)

            @block.gpsimd
            def _(pool):
                pool.memset(c.ident[:], 0.0).then_inc(zeroed, 1)
                pool.memset(c.ones[:], 1.0).then_inc(zeroed, 1)
                pool.wait_ge(zeroed, 2)
                pool.affine_select(out=c.ident[:], in_=c.ident[:], compare_op=ALU.not_equal, fill=1.0,
                                   base=0, pattern=[[-1, P]], channel_multiplier=1).then_inc(done, 1)
                pool.affine_select(out=c.lower[:], in_=c.ones[:], compare_op=ALU.is_ge, fill=0.0,
                                   base=0, pattern=[[1, P]], channel_multiplier=-1).then_inc(done, 1)
                pool.wait_ge(done, 2)


def norm_transpose(c, name, src, dst_tok=None, dst_T=None, eps=1e-5, gamma=None, beta=None, post=None, rms=False):
    nc = c.nc
    with Stage(nc, name) as st:
        stats = st.sb("stats", [P, NT, 6])
        mv = st.sb("mv", [P, NT, 2])
        std = st.sb("std", [P, NT])
        rstd = st.sb("rstd", [P, NT])
        shift = st.sb("shift", [P, NT])
        row = st.sb("row", [P, 2, D])
        gb = st.sb("gb", [P, 2, D])
        tp = st.ps("tp", [P, 2, 512])
        affine_in = st.sem("affine_in")
        var_ready, std_ready = st.sem("var_ready"), st.sem("std_ready")
        rows_ready, tok_ready, turned, free_row = st.sem("rows"), st.sem("tok"), st.sem("turned"), st.sem("free_row")
        free_tp = st.sem("free_tp")
        affine = gamma is not None
        with nc.Block() as block:
            @block.sync
            def _(sp):
                if affine:
                    for i, v in enumerate((gamma, beta)):
                        sp.dma_start(gb[:, i, :], v.rearrange("(a n) -> a n", a=1).broadcast_to([P, D])).then_inc(affine_in, 16)
                    sp.wait_ge(affine_in, 32)

            @block.vector
            def _(dve):
                dve.sem_inc(free_row, 2)
                with dve.Fori(0, NT) as t:
                    dve.bn_stats(stats[:, bass.ds(t, 1), :], src[:, bass.ds(t, 1), :])
                dve.drain()
                for t in range(NT):
                    dve.bn_aggr(mv[:, t, :], stats[:, t, :])
                dve.drain()
                if rms:
                    dve.tensor_tensor(shift[:], mv[:, :, 0], mv[:, :, 0], ALU.mult)
                    dve.drain()
                    dve.tensor_tensor(mv[:, :, 1], mv[:, :, 1], shift[:], ALU.add)
                    dve.drain()
                dve.tensor_scalar(std[:], mv[:, :, 1], eps, None, ALU.add).then_inc(var_ready, 1)
                dve.wait_ge(std_ready, 1)
                dve.reciprocal(rstd[:], std[:])
                dve.drain()
                dve.scalar_tensor_tensor(out=shift[:], in0=mv[:, :, 0], scalar=0.0 if rms else -1.0, in1=rstd[:],
                                         op0=ALU.mult, op1=ALU.mult)
                dve.drain()
                with dve.Fori(0, NT // 2) as i:
                    for j in range(2):
                        t = i * 2 + j
                        dve.wait_ge(free_row, t + 1)
                        dve.tensor_scalar(row[:, j:j + 1, :], src[:, bass.ds(t, 1), :], rstd[:, bass.ds(t, 1)],
                                          shift[:, bass.ds(t, 1)], ALU.mult, ALU.add).then_inc(rows_ready, 1)

            @block.gpsimd
            def _(pool):
                if affine:
                    pool.wait_ge(affine_in, 32)
                if affine or dst_tok is not None:
                    with pool.Fori(0, NT // 2) as i:
                        for j in range(2):
                            t = i * 2 + j
                            pool.wait_ge(rows_ready, t + 1)
                            if affine:
                                pool.tensor_tensor(row[:, j, :], row[:, j, :], gb[:, 0, :], ALU.mult)
                                pool.drain()
                                last = pool.tensor_tensor(row[:, j, :], row[:, j, :], gb[:, 1, :], ALU.add)
                                pool.drain()
                            if dst_tok is not None:
                                last = pool.tensor_copy(dst_tok[:, bass.ds(t, 1), :], row[:, j:j + 1, :])
                            last.then_inc(tok_ready if dst_T is not None else free_row, 1)

            if dst_T is not None:
                shaped = tok_ready if (affine or dst_tok is not None) else rows_ready

                @block.tensor
                def _(pe):
                    with pe.Fori(0, NT // 2) as i:
                        for j in range(2):
                            pe.wait_ge(shaped, i * 2 + (j + 1))
                            pe.wait_ge(free_tp, i * 2 + (j + 1))
                            for k in range(KC):
                                last = pe.transpose(tp[:, j, k * P:(k + 1) * P], row[:, j, k * P:(k + 1) * P], c.ident[:])
                            last.then_inc(turned, 1)

            @block.scalar
            def _(act):
                act.sem_inc(free_tp, 2)
                act.wait_ge(var_ready, 1)
                act.activation(std[:], std[:], ACT.Sqrt).then_inc(std_ready, 1)
                if dst_T is not None:
                    with act.Fori(0, NT // 2) as i:
                        for j in range(2):
                            t = i * 2 + j
                            act.wait_ge(turned, t + 1)
                            act.activation(dst_T[:, :, bass.ts(t, P)],
                                           tp[:, j, 0:D].rearrange("p (k n) -> p k n", k=KC), ACT.Copy).then_inc(free_tp, 1)
                            act.sem_inc(free_row, 1)


def project_add(c, name, src, w, bias=None, scale_src=None):
    nc = c.nc
    with Stage(nc, name) as st:
        row = st.sb("row", [P, 2, D])
        rowT = st.sb("rowT", [P, 2, D])
        w_sb = st.sb("w", [P, KC, D])
        b_sb = st.sb("b", [P, D])
        tp = st.ps("tp", [P, 2, 512])
        out = st.ps("out", [P, 2, 512])
        w_in = st.sem("w_in")
        row_ready, turned, rowT_ready, multiplied, added = (st.sem(n) for n in ("row", "turned", "rowT", "mult", "added"))
        with nc.Block() as block:
            @block.sync
            def _(sp):
                sp.dma_start(w_sb[:], w.rearrange("(k p) n -> p k n", p=P)).then_inc(w_in, 16)
                if bias is not None:
                    sp.dma_start(b_sb[:], bias.rearrange("(a n) -> a n", a=1).broadcast_to([P, D])).then_inc(w_in, 16)
                sp.wait_ge(w_in, 32 if bias is not None else 16)

            @block.gpsimd
            def _(pool):
                with pool.Fori(0, NT // 2) as i:
                    for j in range(2):
                        pool.wait_ge(turned, i * 2 + j)
                        pool.tensor_copy(row[:, j:j + 1, :], src[:, bass.ds(i * 2 + j, 1), :]).then_inc(row_ready, 1)

            @block.tensor
            def _(pe):
                pe.wait_ge(w_in, 32 if bias is not None else 16)
                with pe.Fori(0, NT // 2) as i:
                    for j in range(2):
                        pe.wait_ge(row_ready, i * 2 + (j + 1))
                        pe.wait_ge(rowT_ready, i * 2)
                        for k in range(KC):
                            last = pe.transpose(tp[:, j, k * P:(k + 1) * P], row[:, j, k * P:(k + 1) * P], c.ident[:])
                        last.then_inc(turned, 1)
                    for j in range(2):
                        pe.wait_ge(rowT_ready, i * 2 + (j + 1))
                        pe.wait_ge(added, i * 2)
                        for k in range(KC):
                            last = pe.matmul(out[:, j, 0:D], rowT[:, j, k * P:(k + 1) * P], w_sb[:, k, :],
                                             start=(k == 0), stop=(k == KC - 1))
                        last.then_inc(multiplied, 1)

            @block.scalar
            def _(act):
                with act.Fori(0, NT // 2) as i:
                    for j in range(2):
                        act.wait_ge(turned, i * 2 + (j + 1))
                        act.wait_ge(multiplied, i * 2)
                        act.activation(rowT[:, j, :], tp[:, j, 0:D], ACT.Copy).then_inc(rowT_ready, 1)

            @block.vector
            def _(dve):
                if bias is not None:
                    dve.wait_ge(w_in, 32)
                with dve.Fori(0, NT // 2) as i:
                    for j in range(2):
                        t = i * 2 + j
                        dve.wait_ge(multiplied, t + 1)
                        x_t = c.x[:, bass.ds(t, 1), :]
                        dve.tensor_tensor(x_t, x_t, out[:, j:j + 1, 0:D], ALU.add).then_inc(added, 1)
                        if bias is not None:
                            dve.drain()
                            dve.tensor_tensor(x_t, x_t, b_sb[:].rearrange("p (a d) -> p a d", a=1), ALU.add)


HC = 4
SLOT = 32
NC4 = H // HC


def self_attention(c, name, wqk, wv, ao, causal_after, rope, bias, bv=None):
    nc = c.nc
    kinds = wqk.shape[2]
    LH = S // 512
    nU = 2 * LH
    ROW = DH
    CD = HC * DH
    with Stage(nc, name) as st:
        xb = st.sb("xb", [P, KC, S])
        w = st.sb("w", [P, kinds, KC, P])
        w_v = st.sb("w_v", [P, KC, CD])
        b = st.sb("b", [P, 2])
        bv_sb = st.sb("bv", [P, CD])
        cs = st.sb("cs", [P, 2, S]) if rope is not None else None
        t1 = st.sb("t1", [P, 2, 512])
        t2 = st.sb("t2", [P, 2, 512])
        qk = st.sb("qk", [P, 2, S])
        qk16 = st.sb("qk16", [P, 2, S], BF16)
        v = st.sb("v", [P, ST, HC, SLOT])
        ones_v = st.sb("ones_v", [P, SLOT])
        upper = st.sb("upper", [P, P])
        negmax = st.sb("negmax", [P, ST, HC, SLOT])
        pt = st.sb("pt", [P, 4, 2, 512])
        diag = st.sb("diag", [P, 2, 2, 2, P])
        oT = st.sb("oT", [P, 512])
        recip = st.sb("recip", [P, 4, HC])
        ps = st.ps("ps", [P, 8, 512])
        names = ("w_in", "w_free", "c_in", "x_ready", "x_free", "init", "proj", "rot", "sum", "qk_ready", "v_mm", "v_ready",
                 "mx_mm", "mx_done", "mx_T", "aug", "sc", "ex", "dg", "pv", "oT_ready", "o_T", "o_done", "pv_used")
        s = {n: st.sem(n) for n in names}
        WI = 64 if bv is not None else 48
        NU2 = ST * 2 * LH

        with nc.Block() as block:
            @block.sync
            def _(sp):
                if rope is not None:
                    sp.dma_start(cs[:], rope.rearrange("a p n -> p a n")).then_inc(s["c_in"], 16)
                for it in range(B * NC4):
                    ci = it % NC4
                    sp.wait_ge(s["v_mm"], it)
                    sp.wait_ge(s["v_ready"], it)
                    sp.dma_start(w[:], wqk[ci]).then_inc(s["w_in"], 16)
                    sp.dma_start(w_v[:], wv[ci]).then_inc(s["w_in"], 16)
                    sp.dma_start(b[:], bias[ci]).then_inc(s["w_in"], 16)
                    if bv is not None:
                        sp.dma_start(bv_sb[:], bv[ci]).then_inc(s["w_in"], 16)
                sp.wait_ge(s["w_in"], B * NC4 * WI)

            @block.gpsimd
            def _(pool):
                pool.memset(v[:], 0.0)
                pool.memset(ones_v[:], 0.0)
                pool.memset(negmax[:], 0.0)
                pool.memset(upper[:], 1.0)
                pool.drain()
                pool.memset(v[:, :, :, ROW:ROW + 1], 1.0)
                pool.memset(ones_v[:, ROW:ROW + 1], 1.0)
                pool.tensor_tensor(upper[:], upper[:], c.lower[:], ALU.subtract)
                pool.drain()
                pool.sem_inc(s["init"], 1)
                if rope is not None:
                    pool.wait_ge(s["c_in"], 16)
                with pool.Fori(0, B) as bi:
                    pool.wait_ge(s["v_mm"], bi * NC4)
                    pool.tensor_copy(xb[:], c.xT[:, :, bass.ds(bi * S, S)]).then_inc(s["x_ready"], 1)
                    with pool.Fori(0, NC4) as ci:
                        it = bi * NC4 + ci
                        for u in range(nU):
                            which, h = u % 2, u // 2
                            out = qk[:, which, h * 512:(h + 1) * 512]
                            if rope is not None:
                                pool.wait_ge(s["rot"], it * nU + (u + 1))
                                pool.tensor_tensor(out, t1[:, u % 2, :], t2[:, u % 2, :], ALU.add).then_inc(s["sum"], 1)

            @block.tensor
            def _(pe):
                pe.wait_ge(s["init"], 1)
                with pe.Fori(0, B) as bi:
                    with pe.Fori(0, NC4) as ci:
                        it = bi * NC4 + ci
                        pe.wait_ge(s["x_ready"], bi + 1)
                        pe.wait_ge(s["w_in"], it * WI + WI)
                        pe.wait_ge(s["o_done"], it * LH)
                        for u in range(nU):
                            which, h = u % 2, u // 2
                            if u >= 2:
                                pe.wait_ge(s["rot"], it * nU + (u - 1))
                            for g in range(kinds // 2):
                                for k in range(KC):
                                    last = pe.matmul(ps[:, 2 * (u % 2) + g, :], w[:, which + 2 * g, k, :],
                                                     xb[:, k, h * 512:(h + 1) * 512], start=(k == 0), stop=(k == KC - 1))
                            last.then_inc(s["proj"], 1)
                        for t in range(ST):
                            for k in range(KC):
                                last = pe.matmul(ps[:, 4, t * CD:(t + 1) * CD], xb[:, k, t * P:(t + 1) * P],
                                                 w_v[:, k, :], start=(k == 0), stop=(k == KC - 1))
                        last.then_inc(s["v_mm"], 1)
                        pe.wait_ge(s["qk_ready"], it * nU + nU)
                        for m in range(HC * ST):
                            hd, t = m % HC, m // HC
                            r = m % 2
                            if m >= 2:
                                pe.wait_ge(s["mx_done"], it * HC * ST + (m - 1))
                            for h in range(LH):
                                last = pe.matmul(ps[:, 2 * r + h, :], qk16[SLOT * hd:SLOT * hd + SLOT, 0, t * P:(t + 1) * P],
                                                 qk16[SLOT * hd:SLOT * hd + SLOT, 1, h * 512:(h + 1) * 512],
                                                 start=True, stop=True)
                            last.then_inc(s["mx_mm"], 1)
                        pe.wait_ge(s["mx_done"], it * HC * ST + HC * ST)
                        for t in range(ST):
                            last = pe.transpose(ps[:, 6 + t // 4, (t % 4) * P:(t % 4 + 1) * P],
                                                negmax[:, t, :, :].rearrange("p h s -> p (h s)"), c.ident[:])
                        last.then_inc(s["mx_T"], 1)
                        pe.wait_ge(s["aug"], it + 1)
                        pe.wait_ge(s["v_ready"], it + 1)

                        def scores(n):
                            qh, kt, pr = n // (2 * ST), (n // 2) % ST, n % 2
                            if n >= 2:
                                pe.wait_ge(s["ex"], it * NU2 + (n - 1))
                            for e in range(2):
                                sl = SLOT * (2 * pr + e)
                                last = pe.matmul(ps[:, 2 * pr + e, :], qk[sl:sl + SLOT, 1, kt * P:(kt + 1) * P],
                                                 qk[sl:sl + SLOT, 0, qh * 512:(qh + 1) * 512], start=True, stop=True)
                            last.then_inc(s["sc"], 1)

                        def weigh(n):
                            qh, kt, pr = n // (2 * ST), (n // 2) % ST, n % 2
                            pe.wait_ge(s["ex"], it * NU2 + (n + 1))
                            j = kt - 4 * qh
                            on_diag = causal_after and 0 <= j < 4
                            if on_diag:
                                pe.wait_ge(s["dg"], it * 2 * ST + 2 * kt + (pr + 1))
                            for e in range(2):
                                hd = 2 * pr + e
                                out = ps[SLOT * hd:SLOT * hd + SLOT, 4 + qh, :]
                                src = pt[:, n % 4, e, :]
                                vv = v[:, kt, hd, :]
                                parts = []
                                if not causal_after or j < 0:
                                    parts = [(vv, src, 0, 512)]
                                elif j >= 4:
                                    parts = [(ones_v[:], src, 0, 512)]
                                else:
                                    if j > 0:
                                        parts.append((ones_v[:], src[:, 0:j * P], 0, j * P))
                                    parts.append((vv, diag[:, n % 2, 0, e, :], j * P, (j + 1) * P))
                                    parts.append((ones_v[:], diag[:, n % 2, 1, e, :], j * P, (j + 1) * P))
                                    if j < 3:
                                        parts.append((vv, src[:, (j + 1) * P:512], (j + 1) * P, 512))
                                for q, (lhs, rhs, a, z) in enumerate(parts):
                                    last = pe.matmul(out[:, a:z], lhs, rhs, start=(kt == 0 and q == 0),
                                                     stop=(kt == ST - 1), skip_group_check=True)
                            last.then_inc(s["pv"], 1)

                        def turn(qh):
                            pe.wait_ge(s["oT_ready"], it * LH + (qh + 1))
                            for t in range(4):
                                last = pe.transpose(ps[:, 6, t * P:(t + 1) * P], oT[:, t * P:(t + 1) * P], c.ident[:])
                            last.then_inc(s["o_T"], 1)

                        for n in range(NU2 + 2):
                            if n < NU2:
                                scores(n)
                            if n >= 2:
                                weigh(n - 2)
                            if n - 2 == NU2 // LH + 1:
                                turn(0)
                        turn(1)

            @block.scalar
            def _(act):
                with act.Fori(0, B * NC4) as it:
                    for u in range(nU):
                        which, h = u % 2, u // 2
                        act.wait_ge(s["sum"] if rope is not None else s["rot"], it * nU + (u + 1))
                        act.activation(qk16[:, which, h * 512:(h + 1) * 512], qk[:, which, h * 512:(h + 1) * 512],
                                       ACT.Copy).then_inc(s["qk_ready"], 1)
                    for n in range(NU2):
                        act.wait_ge(s["sc"], it * NU2 + (n + 1))
                        if n >= 4:
                            act.wait_ge(s["pv"], it * NU2 + (n - 3))
                        act.activation(pt[:, n % 4, :, :], ps[:, 2 * (n % 2):2 * (n % 2) + 2, :], ACT.Exp,
                                       scale=DH ** -0.5).then_inc(s["ex"], 1)

            @block.vector
            def _(dve):
                dve.wait_ge(s["init"], 1)
                if rope is not None:
                    dve.wait_ge(s["c_in"], 16)
                with dve.Fori(0, B) as bi:
                    with dve.Fori(0, NC4) as ci:
                        it = bi * NC4 + ci
                        dve.wait_ge(s["w_in"], it * WI + WI)
                        for u in range(nU):
                            which, h = u % 2, u // 2
                            dve.wait_ge(s["proj"], it * nU + (u + 1))
                            src0, src1 = ps[:, 2 * (u % 2), :], ps[:, 2 * (u % 2) + 1, :]
                            if rope is not None:
                                if u >= 2:
                                    dve.wait_ge(s["sum"], it * nU + (u - 1))
                                if which == 1:
                                    dve.scalar_tensor_tensor(out=t1[:, u % 2, :], in0=src0, scalar=b[:, 1:2],
                                                             in1=cs[:, 0, h * 512:(h + 1) * 512], op0=ALU.add, op1=ALU.mult)
                                else:
                                    dve.tensor_tensor(t1[:, u % 2, :], src0, cs[:, 0, h * 512:(h + 1) * 512], ALU.mult)
                                dve.tensor_tensor(t2[:, u % 2, :], src1, cs[:, 1, h * 512:(h + 1) * 512], ALU.mult).then_inc(s["rot"], 1)
                            else:
                                dve.tensor_scalar(qk[:, which, h * 512:(h + 1) * 512], src0, b[:, which:which + 1], None,
                                                  ALU.add).then_inc(s["rot"], 1)
                        dve.wait_ge(s["v_mm"], it + 1)
                        vsrc = ps[:, 4, :].rearrange("p (t h d) -> p t h d", t=ST, h=HC)
                        if bv is not None:
                            vb = bv_sb[:].rearrange("p (a h d) -> p a h d", a=1, h=HC).broadcast_to([P, ST, HC, DH])
                            dve.tensor_tensor(v[:, :, :, 0:DH], vsrc, vb, ALU.add).then_inc(s["v_ready"], 1)
                        else:
                            dve.tensor_copy(v[:, :, :, 0:DH], vsrc).then_inc(s["v_ready"], 1)
                        for m in range(HC * ST):
                            hd, t = m % HC, m // HC
                            dve.wait_ge(s["mx_mm"], it * HC * ST + (m + 1))
                            dve.tensor_reduce(negmax[:, t, hd, ROW:ROW + 1], ps[:, 2 * (m % 2):2 * (m % 2) + 2, :],
                                              AX.XY, ALU.max, negate=True).then_inc(s["mx_done"], 1)
                        dve.wait_ge(s["mx_T"], it + 1)
                        last = dve.tensor_tensor(qk[:, 0, :].rearrange("p (a n) -> p a n", a=LH),
                                                 qk[:, 0, :].rearrange("p (a n) -> p a n", a=LH), ps[:, 6:8, :], ALU.add)
                        last.then_inc(s["aug"], 1)

                        def finish(qh):
                            dve.wait_ge(s["pv"], it * NU2 + NU2 // LH * (qh + 1))
                            dve.tensor_copy(oT[:], ps[:, 4 + qh, :]).then_inc(s["oT_ready"], 1)
                            dve.wait_ge(s["o_T"], it * LH + (qh + 1))
                            o = ps[:, 6, :].rearrange("p (t h s) -> p t h s", t=4, h=HC)
                            dve.reciprocal(recip[:], o[:, :, :, ROW])
                            dve.drain()
                            r4 = recip[:].rearrange("p t (h a) -> p t h a", a=1).broadcast_to([P, 4, HC, DH])
                            dst = ao[:, bass.ds(bi * ST + 4 * qh, 4), bass.ds(ci * CD, CD)].rearrange("p t (h d) -> p t h d", h=HC)
                            dve.tensor_tensor(dst, o[:, :, :, 0:DH], r4, ALU.mult).then_inc(s["o_done"], 1)

                        for n in range(NU2):
                            qh, kt, pr = n // (2 * ST), (n // 2) % ST, n % 2
                            j = kt - 4 * qh
                            if causal_after and 0 <= j < 4:
                                dve.wait_ge(s["ex"], it * NU2 + (n + 1))
                                if kt >= 1:
                                    before = n - 2 if j > 0 else 2 * (kt - 1) + pr
                                    dve.wait_ge(s["pv"], it * NU2 + (before + 1))
                                for z, mask in enumerate((c.lower, upper)):
                                    mk = mask[:].rearrange("p (a n) -> p a n", a=1).broadcast_to([P, 2, P])
                                    last = dve.tensor_tensor(diag[:, n % 2, z, :, :], pt[:, n % 4, :, j * P:(j + 1) * P],
                                                             mk, ALU.mult)
                                last.then_inc(s["dg"], 1)
                            if n == NU2 // LH + 1:
                                finish(0)
                        finish(1)



def load_weights(sp, pairs, sem):
    for dst, src in pairs:
        sp.dma_start(dst, src).then_inc(sem, 16)
    return 16 * len(pairs)


def row_bcast(v, n, parts=P):
    return v.rearrange("(a n) -> a n", a=1).broadcast_to([parts, n])


def linear_T(c, name, srcT, jobs, width=N):
    nc = c.nc
    step = min(512, width)
    nb = width // step
    with Stage(nc, name) as st:
        ps = st.ps("ps", [P, 8, 512])
        w_in, proj_a, proj_v, free_a, free_v = (st.sem(n) for n in ("w_in", "proj_a", "proj_v", "free_a", "free_v"))
        loads, chunks = [], []
        for q, (w, dst, bias, func) in enumerate(jobs):
            M = w.shape[1]
            w_sb = st.sb(f"w{q}", [P, KC, M])
            loads.append((w_sb[:], w.rearrange("(k p) m -> p k m", p=P)))
            b_sb = None
            if bias is not None:
                b_sb = st.sb(f"b{q}", [P, M // P])
                loads.append((b_sb[:], bias))
            for m in range(M // P):
                lane = "a" if func is not None or len(chunks) % 2 == 0 else "v"
                at = sum(x[0] == lane for x in chunks)
                chunks.append((lane, at, w_sb, b_sb, dst, m, func))
        per = {lane: sum(x[0] == lane for x in chunks) for lane in "av"}
        assert all(n <= 4 or n % 4 == 0 for n in per.values())
        total = 16 * len(loads)
        proj, free = {"a": proj_a, "v": proj_v}, {"a": free_a, "v": free_v}
        bank = {"a": 0, "v": 4}
        with nc.Block() as block:
            @block.sync
            def _(sp):
                load_weights(sp, loads, w_in)
                sp.wait_ge(w_in, total)

            @block.tensor
            def _(pe):
                pe.wait_ge(w_in, total)
                with pe.Fori(0, nb) as n:
                    for lane, at, w_sb, b_sb, dst, m, func in chunks:
                        pe.wait_ge(free[lane], n * per[lane] + (at + 1))
                        for k in range(KC):
                            last = pe.matmul(ps[:, bank[lane] + at % 4, 0:step], w_sb[:, k, m * P:(m + 1) * P],
                                             srcT[:, k, bass.ts(n, step)], start=(k == 0), stop=(k == KC - 1))
                        last.then_inc(proj[lane], 1)

            @block.scalar
            def _(act):
                act.sem_inc(free_a, min(4, per["a"]))
                act.wait_ge(w_in, total)
                with act.Fori(0, nb) as n:
                    for lane, at, w_sb, b_sb, dst, m, func in chunks:
                        if lane == "a":
                            act.wait_ge(proj_a, n * per["a"] + (at + 1))
                            act.activation(dst[:, m, bass.ts(n, step)], ps[:, at % 4, 0:step], func or ACT.Identity,
                                           bias=0.0 if b_sb is None else b_sb[:, m:m + 1]).then_inc(free_a, 1)

            @block.vector
            def _(dve):
                if per["v"]:
                    dve.sem_inc(free_v, min(4, per["v"]))
                    dve.wait_ge(w_in, total)
                    with dve.Fori(0, nb) as n:
                        for lane, at, w_sb, b_sb, dst, m, func in chunks:
                            if lane == "v":
                                dve.wait_ge(proj_v, n * per["v"] + (at + 1))
                                dve.tensor_scalar(dst[:, m, bass.ts(n, step)], ps[:, 4 + at % 4, 0:step],
                                                  0.0 if b_sb is None else b_sb[:, m:m + 1], None, ALU.add).then_inc(free_v, 1)


def rope_T(c, name, srcT, jobs, table, per_chunk):
    nc = c.nc
    with Stage(nc, name) as st:
        ps = st.ps("ps", [P, 8, 512])
        t12 = st.sb("t12", [P, 4, 2, 512])
        tk = KC if per_chunk else 1
        cs = st.sb("cs", [P, 2, tk, S])
        w_in, proj, rot, summed = (st.sem(n) for n in ("w_in", "proj", "rot", "summed"))
        loads = [(cs[:, i, :, :], table[i].rearrange("k p s -> p k s") if per_chunk else table[i].rearrange("p (a s) -> p a s", a=1))
                 for i in range(2)]
        sbs = []
        for q, (w, ws, dst, b, bs) in enumerate(jobs):
            w_sb, b_sb = st.sb(f"w{q}", [P, 2, KC, D]), None
            loads += [(w_sb[:, 0], w.rearrange("(k p) m -> p k m", p=P)), (w_sb[:, 1], ws.rearrange("(k p) m -> p k m", p=P))]
            if b is not None:
                b_sb = st.sb(f"b{q}", [P, 2, KC])
                loads += [(b_sb[:, 0], b), (b_sb[:, 1], bs)]
            sbs.append((w_sb, b_sb, dst))
        total = 16 * len(loads)
        units = [(h, q, m) for h in range(S // 512) for q in range(len(jobs)) for m in range(KC)]
        U = len(units)
        assert U % 4 == 0
        with nc.Block() as block:
            @block.sync
            def _(sp):
                load_weights(sp, loads, w_in)
                sp.wait_ge(w_in, total)

            @block.tensor
            def _(pe):
                pe.wait_ge(w_in, total)
                with pe.Fori(0, B) as bi:
                    for i, (h, q, m) in enumerate(units):
                        pe.wait_ge(rot, bi * U + (i - 3) if i >= 4 else bi * U)
                        for g in range(2):
                            for k in range(KC):
                                last = pe.matmul(ps[:, 2 * (i % 4) + g, :], sbs[q][0][:, g, k, m * P:(m + 1) * P],
                                                 srcT[:, k, bass.ds(bi * S + h * 512, 512)], start=(k == 0), stop=(k == KC - 1))
                        last.then_inc(proj, 1)

            @block.vector
            def _(dve):
                dve.wait_ge(w_in, total)
                with dve.Fori(0, B) as bi:
                    for i, (h, q, m) in enumerate(units):
                        dve.wait_ge(proj, bi * U + (i + 1))
                        dve.wait_ge(summed, bi * U + (i - 3) if i >= 4 else bi * U)
                        for g in range(2):
                            out, src = t12[:, i % 4, g, :], ps[:, 2 * (i % 4) + g, :]
                            tab = cs[:, g, m if per_chunk else 0, h * 512:(h + 1) * 512]
                            if sbs[q][1] is None:
                                last = dve.tensor_tensor(out, src, tab, ALU.mult)
                            else:
                                last = dve.scalar_tensor_tensor(out=out, in0=src, scalar=sbs[q][1][:, g, m:m + 1], in1=tab,
                                                                op0=ALU.add, op1=ALU.mult)
                        last.then_inc(rot, 1)

            @block.gpsimd
            def _(pool):
                with pool.Fori(0, B) as bi:
                    for i, (h, q, m) in enumerate(units):
                        pool.wait_ge(rot, bi * U + (i + 1))
                        pool.tensor_tensor(sbs[q][2][:, m, bass.ds(bi * S + h * 512, 512)], t12[:, i % 4, 0, :],
                                           t12[:, i % 4, 1, :], ALU.add).then_inc(summed, 1)


def linear_tok(c, name, srcT, w, dst=None, bias=None, resid=None, relu=False, tiles=NT, rows=P):
    nc = c.nc
    M = w.shape[1]
    with Stage(nc, name) as st:
        ps = st.ps("ps", [P, 4, 512])
        w_sb = st.sb("w", [P, KC, M])
        b_sb = st.sb("b", [P, M])
        w_in, mult, out = st.sem("w_in"), st.sem("mult"), st.sem("out")
        loads = [(w_sb[:], w.rearrange("(k p) m -> p k m", p=P))]
        if bias is not None:
            loads.append((b_sb[:], row_bcast(bias, M)))
        total = 16 * len(loads)
        with nc.Block() as block:
            @block.sync
            def _(sp):
                load_weights(sp, loads, w_in)
                sp.wait_ge(w_in, total)

            @block.tensor
            def _(pe):
                pe.wait_ge(w_in, total)
                for t in range(tiles):
                    if t >= 4:
                        pe.wait_ge(out, t - 3)
                    for k in range(KC):
                        last = pe.matmul(ps[0:rows, t % 4, 0:M], srcT[:, k, t * rows:(t + 1) * rows], w_sb[:, k, :],
                                         start=(k == 0), stop=(k == KC - 1))
                    last.then_inc(mult, 1)

            @block.vector
            def _(dve):
                dve.wait_ge(w_in, total)
                for t in range(tiles):
                    dve.wait_ge(mult, t + 1)
                    d, p_ = dst[0:rows, t, :], ps[0:rows, t % 4, 0:M]
                    if bias is None and not relu and resid is None:
                        dve.tensor_copy(d, p_).then_inc(out, 1)
                        continue
                    if bias is not None:
                        last = dve.tensor_tensor(d, p_, b_sb[0:rows, :], ALU.add)
                        src = d
                    else:
                        src = p_
                    if relu:
                        if bias is not None:
                            dve.drain()
                        last = dve.scalar_tensor_tensor(out=d, in0=src, scalar=0.0, in1=resid[0:rows, t, :],
                                                        op0=ALU.max, op1=ALU.add)
                    elif resid is not None:
                        if bias is not None:
                            dve.drain()
                        last = dve.tensor_tensor(d, src, resid[0:rows, t, :], ALU.add)
                    last.then_inc(out, 1)


def additive_attention(c, name, feat, feT, txb, sw, sb_rows):
    nc, d = c.nc, c.dram
    HALVES = S // 512
    G = ST // 2
    with Stage(nc, name) as st:
        h = st.sb("h", [P, 2, KC, S])
        z0 = st.sb("z0", [P, 2, S])
        z = st.sb("z", [P, 2, S])
        w_col = st.sb("w_col", [P, KC])
        sel = st.sb("sel", [P, 2 * S2 - 1])
        m_i = st.sb("m_i", [S2, B], I32)
        m_f = st.sb("m_f", [S2, B])
        bc = st.sb("bc", [P, 2])
        rT = st.sb("rT", [S2, S])
        nmax = st.sb("nmax", [P, ST])
        e = st.sb("e", [P, ST, S2])
        es = st.sb("es", [P, 2, ST, S2])
        sums = st.sb("sums", [P, 3, ST])
        gate = st.sb("gate", [P, 2, ST])
        tmp = st.sb("tmp", [P, 2, D])
        rho = st.ps("rho", [P, 2, 512])
        rT_ps = st.ps("rT_ps", [P, 2, 512])
        names = ("w_in", "init", "tanh", "z0d", "z", "row", "rho_read", "turned", "nmax", "exp", "sums", "gate", "added")
        s = {n: st.sem(n) for n in names}
        loads = [(w_col[:], d["l0x_w"]), (m_i[:], d["mask2T"]),
                 (bc[:, 0:1], row_bcast(d["l0x_bcw"], 1)), (bc[:, 1:2], row_bcast(d["l0x_bcb"], 1))]
        total = 16 * len(loads)
        with nc.Block() as block:
            @block.sync
            def _(sp):
                load_weights(sp, loads, s["w_in"])
                sp.wait_ge(s["w_in"], total)

            @block.gpsimd
            def _(pool):
                pool.memset(sel[:], 0.0)
                pool.drain()
                pool.memset(sel[:, S2 - 1:S2], 1.0)
                pool.drain()
                pool.sem_inc(s["init"], 1)

            @block.scalar
            def _(act):
                act.wait_ge(s["w_in"], total)
                with act.Fori(0, B) as bi:
                    for t in range(S2):
                        if t >= 2:
                            act.wait_ge(s["z"], bi * S2 + (t - 1))
                        else:
                            act.wait_ge(s["z"], bi * S2)
                        for k in range(KC):
                            last = act.activation(h[:, t % 2, k, :], feT[:, k, bass.ds(bi * S, S)], ACT.Tanh,
                                                  bias=txb[:, k, bass.ds(bi * S2 + t, 1)])
                        last.then_inc(s["tanh"], 1)
                    act.wait_ge(s["nmax"], bi + 1)
                    for t in range(ST):
                        last = act.activation(e[:, t, :], rT_ps[:, t // G, (t % G) * S2:(t % G + 1) * S2], ACT.Exp,
                                              bias=nmax[:, t:t + 1])
                    last.then_inc(s["exp"], 1)
                    act.wait_ge(s["sums"], bi + 1)
                    for g in range(2):
                        last = act.activation(gate[:, g, :], gate[:, g, :], ACT.Tanh, bias=bc[:, g:g + 1])
                    last.then_inc(s["gate"], 1)

            @block.vector
            def _(dve):
                dve.wait_ge(s["w_in"], total)
                dve.tensor_copy(m_f[:], m_i[:])
                dve.drain()
                dve.tensor_scalar(m_f[:], m_f[:], -1.0, 1.0, ALU.mult, ALU.add)
                dve.drain()
                dve.tensor_scalar(m_f[:], m_f[:], -1e30, None, ALU.mult)
                with dve.Fori(0, B) as bi:
                    for t in range(S2):
                        dve.wait_ge(s["tanh"], bi * S2 + (t + 1))
                        dve.wait_ge(s["row"], bi * S2 + (t - 1) if t >= 2 else bi * S2)
                        dve.tensor_scalar(z0[:, t % 2, :], h[:, t % 2, 1, :], w_col[:, 1:2], None, ALU.mult)
                        dve.drain()
                        dve.scalar_tensor_tensor(out=z[:, t % 2, :], in0=h[:, t % 2, 0, :], scalar=w_col[:, 0:1],
                                                 in1=z0[:, t % 2, :], op0=ALU.mult, op1=ALU.add).then_inc(s["z"], 1)
                    dve.wait_ge(s["row"], bi * S2 + S2)
                    dve.tensor_scalar(rT[:].rearrange("p (a n) -> p a n", a=HALVES), rho[0:S2, :, :],
                                      m_f[:, bass.ds(bi, 1)], None, ALU.add).then_inc(s["rho_read"], 1)
                    dve.wait_ge(s["turned"], bi + 1)
                    for q in range(2):
                        last = dve.tensor_reduce(nmax[:, q * G:(q + 1) * G], rT_ps[:, q, 0:G * S2].rearrange("p (t n) -> p t n", t=G),
                                                 AX.X, ALU.max, negate=True)
                    last.then_inc(s["nmax"], 1)
                    dve.wait_ge(s["exp"], bi + 1)
                    dve.tensor_reduce(sums[:, 0, :], e[:], AX.X, ALU.add)
                    for g, rowv in enumerate((sw, sb_rows)):
                        r = rowv[:, bass.ds(bi, 1), :].broadcast_to([P, ST, S2])
                        dve.tensor_tensor(es[:, g], e[:], r, ALU.mult)
                    dve.drain()
                    dve.tensor_reduce(sums[:, 1:3, :], es[:], AX.X, ALU.add)
                    dve.reciprocal(sums[:, 0, :], sums[:, 0, :])
                    dve.drain()
                    dve.tensor_tensor(gate[:], sums[:, 1:3, :], sums[:, 0:1, :].broadcast_to([P, 2, ST]), ALU.mult).then_inc(s["sums"], 1)
                    dve.wait_ge(s["gate"], bi + 1)
                    for t in range(ST):
                        dve.tensor_scalar(tmp[:, t % 2:t % 2 + 1, :], feat[:, bass.ds(bi * ST + t, 1), :], gate[:, 0, t:t + 1],
                                          gate[:, 1, t:t + 1], ALU.mult, ALU.add)
                        dve.drain()
                        x_t = c.x[:, bass.ds(bi * ST + t, 1), :]
                        dve.tensor_tensor(x_t, x_t, tmp[:, t % 2:t % 2 + 1, :], ALU.add)

            @block.tensor
            def _(pe):
                pe.wait_ge(s["init"], 1)
                with pe.Fori(0, B) as bi:
                    pe.wait_ge(s["rho_read"], bi)
                    for t in range(S2):
                        pe.wait_ge(s["z"], bi * S2 + (t + 1))
                        for hf in range(HALVES):
                            last = pe.matmul(rho[0:S2, hf, :], sel[:, S2 - 1 - t:2 * S2 - 1 - t], z[:, t % 2, hf * 512:(hf + 1) * 512],
                                             start=(t == 0), stop=(t == S2 - 1))
                        last.then_inc(s["row"], 1)
                    pe.wait_ge(s["rho_read"], bi + 1)
                    pe.wait_ge(s["exp"], bi)
                    for t in range(ST):
                        last = pe.transpose(rT_ps[:, t // G, (t % G) * S2:(t % G + 1) * S2], rT[:, t * P:(t + 1) * P],
                                            c.ident[0:S2, 0:S2])
                    last.then_inc(s["turned"], 1)


def ctx_rows(c, name, cols, dst):
    nc = c.nc
    with Stage(nc, name) as st:
        w = st.sb("w", [P, len(cols), KC, P])
        ps = st.ps("ps", [P, 2, 512])
        w_in, mult, out = st.sem("w_in"), st.sem("mult"), st.sem("out")
        with nc.Block() as block:
            @block.sync
            def _(sp):
                load_weights(sp, [(w[:, i], v.rearrange("(k p) m -> p k m", p=P)) for i, v in enumerate(cols)], w_in)
                sp.wait_ge(w_in, 16 * len(cols))

            @block.tensor
            def _(pe):
                pe.wait_ge(w_in, 16 * len(cols))
                for i in range(len(cols)):
                    for k in range(KC):
                        last = pe.matmul(ps[:, i, 0:B * S2], w[:, i, k, :], c.ctxT[:, k, :], start=(k == 0), stop=(k == KC - 1))
                last.then_inc(mult, 1)

            @block.vector
            def _(dve):
                dve.wait_ge(mult, 1)
                for i in range(len(cols)):
                    dve.tensor_copy(dst[i][:].rearrange("p b t -> p (b t)"), ps[:, i, 0:B * S2])


E = 8
CAPACITY = N * 5 // 4 // E


def route(c, name, srcT, w, wgt, bias=None, top=1):
    nc = c.nc
    with Stage(nc, name) as st:
        w_sb = st.sb("w", [P, KC, E])
        b_sb = st.sb("b", [E, 1])
        lT = st.sb("lT", [E, N])
        L = st.sb("L", [P, NT, E])
        rank = st.sb("rank", [P, E])
        m = st.sb("m", [P, 2, NT, 1])
        p_ = st.sb("p", [P, NT, E])
        rk = st.sb("rk", [P, NT, 1])
        sel = st.sb("sel", [P, 2, NT, E])
        tmp = st.sb("tmp", [P, NT, E])
        tot = st.sb("tot", [P, 2, NT, 1])
        strict = st.sb("strict", [P, P])
        cum = st.sb("cum", [P, NT, E])
        before = st.sb("before", [P, NT, E])
        lps = st.ps("lps", [P, 4, 512])
        tps = st.ps("tps", [P, 512])
        cps = st.ps("cps", [P, 2, 512])
        names = ("w_in", "mult", "lT_ready", "turned", "shifted", "exp", "chosen", "counted", "rank_ready")
        s = {n: st.sem(n) for n in names}
        loads = [(w_sb[:], w.rearrange("(k p) e -> p k e", p=P))]
        if bias is not None:
            loads.append((b_sb[:], bias))
        total = 16 * len(loads)
        flat = [P, NT, E]
        with nc.Block() as block:
            @block.sync
            def _(sp):
                load_weights(sp, loads, s["w_in"])
                sp.wait_ge(s["w_in"], total)

            @block.gpsimd
            def _(pool):
                for e in range(E):
                    last = pool.memset(rank[:, e:e + 1], float(E - e))
                pool.tensor_tensor(strict[:], c.lower[:], c.ident[:], ALU.subtract)
                pool.drain()
                pool.sem_inc(s["rank_ready"], 1)

            @block.tensor
            def _(pe):
                pe.wait_ge(s["w_in"], total)
                for n in range(4):
                    for k in range(KC):
                        last = pe.matmul(lps[0:E, n, :], w_sb[:, k, :], srcT[:, k, n * 512:(n + 1) * 512],
                                         start=(k == 0), stop=(k == KC - 1))
                last.then_inc(s["mult"], 1)
                pe.wait_ge(s["lT_ready"], 1)
                for t in range(NT):
                    last = pe.transpose(tps[:, t * E:(t + 1) * E], lT[:, t * P:(t + 1) * P], c.ident[0:E, 0:E])
                last.then_inc(s["turned"], 1)
                if top == 2:
                    pe.wait_ge(s["chosen"], 1)
                    pe.wait_ge(s["rank_ready"], 1)
                    mask = cum[:].rearrange("p t e -> p (t e)")
                    pe.matmul(cps[:, 0, 0:NT * E], strict[:], mask, start=True, stop=True)
                    pe.matmul(cps[:, 1, 0:NT * E], c.ones[:], mask, start=True, stop=True).then_inc(s["counted"], 1)

            @block.scalar
            def _(act):
                act.wait_ge(s["shifted"], 1)
                act.activation(p_[:], p_[:], ACT.Exp).then_inc(s["exp"], 1)

            @block.vector
            def _(dve):
                dve.wait_ge(s["w_in"], total)
                dve.wait_ge(s["mult"], 1)
                lv = lT[:].rearrange("e (n q) -> e n q", n=4)
                if bias is not None:
                    dve.tensor_scalar(lv, lps[0:E, :, :], b_sb[:, 0:1], None, ALU.add).then_inc(s["lT_ready"], 1)
                else:
                    dve.tensor_copy(lv, lps[0:E, :, :]).then_inc(s["lT_ready"], 1)
                dve.wait_ge(s["turned"], 1)
                dve.tensor_copy(L[:].rearrange("p t e -> p (t e)"), tps[:, 0:NT * E])
                dve.drain()
                dve.wait_ge(s["rank_ready"], 1)
                rb = rank[:].rearrange("p (a e) -> p a e", a=1).broadcast_to(flat)

                def choose(i):
                    dve.tensor_reduce(m[:, i, :, 0], L[:], AX.X, ALU.max)
                    dve.drain()
                    if i == 0:
                        dve.tensor_tensor(p_[:], L[:], m[:, 0].broadcast_to(flat), ALU.subtract)
                        dve.drain()
                        dve.sem_inc(s["shifted"], 1)
                    dve.tensor_tensor(sel[:, i], L[:], m[:, i].broadcast_to(flat), ALU.is_equal)
                    dve.drain()
                    dve.tensor_tensor(sel[:, i], sel[:, i], rb, ALU.mult)
                    dve.drain()
                    dve.tensor_reduce(rk[:, :, 0], sel[:, i], AX.X, ALU.max)
                    dve.drain()
                    dve.tensor_tensor(sel[:, i], sel[:, i], rk[:].broadcast_to(flat), ALU.is_equal)
                    dve.drain()

                choose(0)
                if top == 1:
                    dve.wait_ge(s["exp"], 1)
                    dve.tensor_reduce(tot[:, 0, :, 0], p_[:], AX.X, ALU.add)
                    dve.drain()
                    dve.reciprocal(tot[:, 0], tot[:, 0])
                    dve.drain()
                    dve.tensor_tensor(wgt[:, :, 0:E], sel[:, 0], tot[:, 0].broadcast_to(flat), ALU.mult)
                    return
                dve.scalar_tensor_tensor(out=L[:], in0=sel[:, 0], scalar=-3e38, in1=L[:], op0=ALU.mult, op1=ALU.add)
                dve.drain()
                choose(1)
                dve.wait_ge(s["exp"], 1)
                dve.tensor_tensor(cum[:], sel[:, 0], sel[:, 1], ALU.add)
                dve.drain()
                dve.sem_inc(s["chosen"], 1)
                dve.tensor_tensor(tmp[:], p_[:], cum[:], ALU.mult)
                dve.drain()
                dve.tensor_reduce(tot[:, 0, :, 0], tmp[:], AX.X, ALU.add)
                dve.drain()
                dve.reciprocal(tot[:, 0], tot[:, 0])
                dve.drain()
                dve.tensor_tensor(tmp[:], tmp[:], tot[:, 0].broadcast_to(flat), ALU.mult)
                dve.wait_ge(s["counted"], 1)
                dve.memset(before[:, 0, :], 0.0)
                dve.drain()
                for t in range(1, NT):
                    dve.tensor_tensor(before[:, t, :], before[:, t - 1, :], cps[:, 1, (t - 1) * E:t * E], ALU.add)
                    dve.drain()
                dve.tensor_tensor(before[:].rearrange("p t e -> p (t e)"), before[:].rearrange("p t e -> p (t e)"),
                                  cps[:, 0, 0:NT * E], ALU.add)
                dve.drain()
                dve.tensor_scalar(before[:], before[:], float(CAPACITY), None, ALU.is_lt)
                dve.drain()
                dve.tensor_tensor(wgt[:, :, 0:E], tmp[:], before[:], ALU.mult)


def experts(c, name, srcT, wgt, n_experts, inner, w1, w2, gate=None, b1=None, square=False):
    nc = c.nc
    MI = inner // P
    NB = N // 512
    G = 1 if gate is None else 2
    with Stage(nc, name) as st:
        w1_sb = st.sb("w1", [P, 2, G, KC, inner])
        w2_sb = st.sb("w2", [P, 2, MI, D])
        b_sb = st.sb("b", [P, 2, MI])
        hT = st.sb("hT", [P, 2, MI, 512])
        gated = st.sb("gated", [P, 2, 512])
        ps = st.ps("ps", [P, 8, 512])
        names = ("w_in0", "w_in1", "w_free0", "w_free1", "up", "sil", "h", "down", "added")
        s = {n: st.sem(n) for n in names}
        UI = 2 * NB
        loads = G + 1 + (b1 is not None)
        with nc.Block() as block:
            @block.sync
            def _(sp):
                for e in range(n_experts):
                    j = e % 2
                    sp.wait_ge(s[f"w_free{j}"], e // 2)
                    for g, ww in enumerate([w1] if gate is None else [gate, w1]):
                        sp.dma_start(w1_sb[:, j, g], ww[e].rearrange("(k p) m -> p k m", p=P)).then_inc(s[f"w_in{j}"], 16)
                    sp.dma_start(w2_sb[:, j], w2[e].rearrange("(k p) m -> p k m", p=P)).then_inc(s[f"w_in{j}"], 16)
                    if b1 is not None:
                        sp.dma_start(b_sb[:, j], b1[e]).then_inc(s[f"w_in{j}"], 16)
                for j in range(2):
                    sp.wait_ge(s[f"w_in{j}"], n_experts // 2 * 16 * loads)

            @block.tensor
            def _(pe):
                with pe.Fori(0, n_experts // 2) as i:
                    def up(u):
                        j, n = u // NB, u % NB
                        if n == 0:
                            pe.wait_ge(s[f"w_in{j}"], (i + 1) * (16 * loads))
                        for m in range(MI):
                            q = u * MI + m
                            pe.wait_ge(s["h"], i * (UI * MI) + (q - 1) if q >= 2 else i * (UI * MI))
                            for g in range(G):
                                for k in range(KC):
                                    last = pe.matmul(ps[:, 2 * (m % 2) + g, :], w1_sb[:, j, g, k, m * P:(m + 1) * P],
                                                     srcT[:, k, n * 512:(n + 1) * 512], start=(k == 0), stop=(k == KC - 1))
                            last.then_inc(s["up"], 1)

                    def down(u):
                        j = u // NB
                        pe.wait_ge(s["h"], i * (UI * MI) + (u + 1) * MI)
                        for t in range(4):
                            q = u * 4 + t
                            pe.wait_ge(s["added"], i * (UI * 4) + (q - 3) if q >= 4 else i * (UI * 4))
                            for m in range(MI):
                                last = pe.matmul(ps[:, 4 + t, 0:D], hT[:, u % 2, m, t * P:(t + 1) * P], w2_sb[:, j, m, :],
                                                 start=(m == 0), stop=(m == MI - 1))
                            last.then_inc(s["down"], 1)

                    for u in range(UI + 1):
                        if u < UI:
                            up(u)
                        if u >= 1:
                            down(u - 1)

            @block.scalar
            def _(act):
                with act.Fori(0, n_experts // 2) as i:
                    for u in range(UI):
                        j = u // NB
                        for m in range(MI):
                            q = u * MI + m
                            act.wait_ge(s["up"], i * (UI * MI) + (q + 1))
                            if m == 0:
                                act.wait_ge(s["down"], i * (UI * 4) + (u - 1) * 4 if u >= 2 else i * (UI * 4))
                            if square:
                                act.wait_ge(s["h"], i * (UI * MI) + (q - 1) if q >= 2 else i * (UI * MI))
                                act.activation(gated[:, m % 2, :], ps[:, 2 * (m % 2), :], ACT.Relu).then_inc(s["sil"], 1)
                            elif gate is None:
                                act.activation(hT[:, u % 2, m, :], ps[:, 2 * (m % 2), :], ACT.Relu,
                                               bias=b_sb[:, j, m:m + 1]).then_inc(s["h"], 1)
                            else:
                                act.wait_ge(s["h"], i * (UI * MI) + (q - 1) if q >= 2 else i * (UI * MI))
                                act.activation(gated[:, m % 2, :], ps[:, 2 * (m % 2), :], ACT.Silu).then_inc(s["sil"], 1)

            @block.vector
            def _(dve):
                with dve.Fori(0, n_experts // 2) as i:
                    def add_out(u):
                        j, n = u // NB, u % NB
                        if n == 0:
                            dve.drain()
                        for t in range(4):
                            dve.wait_ge(s["down"], i * (UI * 4) + (u * 4 + t + 1))
                            x_t = c.x[:, 4 * n + t, :]
                            dve.scalar_tensor_tensor(out=x_t, in0=ps[:, 4 + t, 0:D], scalar=wgt[:, 4 * n + t, bass.ds(i * 2 + j, 1)],
                                                     in1=x_t, op0=ALU.mult, op1=ALU.add).then_inc(s["added"], 1)
                        if n == NB - 1:
                            dve.sem_inc(s[f"w_free{j}"], 1)

                    for u in range(UI + 1):
                        if u < UI and (gate is not None or square):
                            for m in range(MI):
                                q = u * MI + m
                                dve.wait_ge(s["sil"], i * (UI * MI) + (q + 1))
                                if m == 0:
                                    dve.wait_ge(s["down"], i * (UI * 4) + (u - 1) * 4 if u >= 2 else i * (UI * 4))
                                other = gated[:, m % 2, :] if square else ps[:, 2 * (m % 2) + 1, :]
                                dve.tensor_tensor(hT[:, u % 2, m, :], gated[:, m % 2, :], other, ALU.mult).then_inc(s["h"], 1)
                        if u >= 1:
                            add_out(u - 1)


def add_expert_bias(c, name, wgt, b2):
    nc = c.nc
    with Stage(nc, name) as st:
        wT = st.sb("wT", [E, N])
        b_sb = st.sb("b", [E, D])
        tps = st.ps("tps", [P, 4, 512])
        ps = st.ps("ps", [P, 4, 512])
        w_in, turned, copied, mult, added = (st.sem(n) for n in ("w_in", "turned", "copied", "mult", "added"))
        with nc.Block() as block:
            @block.sync
            def _(sp):
                sp.dma_start(b_sb[:], b2).then_inc(w_in, 16)
                sp.wait_ge(w_in, 16)

            @block.tensor
            def _(pe):
                for t in range(NT):
                    last = pe.transpose(tps[0:E, t // 4, (t % 4) * P:(t % 4 + 1) * P], wgt[:, t, 0:E], c.ident[:])
                last.then_inc(turned, 1)
                pe.wait_ge(w_in, 16)
                pe.wait_ge(copied, 1)
                for t in range(NT):
                    if t >= 4:
                        pe.wait_ge(added, t - 3)
                    pe.matmul(ps[:, t % 4, 0:D], wT[:, t * P:(t + 1) * P], b_sb[:], start=True, stop=True).then_inc(mult, 1)

            @block.scalar
            def _(act):
                act.wait_ge(turned, 1)
                act.activation(wT[:].rearrange("e (n q) -> e n q", n=4), tps[0:E, :, :], ACT.Copy).then_inc(copied, 1)

            @block.vector
            def _(dve):
                for t in range(NT):
                    dve.wait_ge(mult, t + 1)
                    dve.tensor_tensor(c.x[:, t, :], c.x[:, t, :], ps[:, t % 4, 0:D], ALU.add).then_inc(added, 1)


def softplus_attention(c, name, qT, kT, v, out):
    nc = c.nc
    units = [(b, qb, j) for b in range(B) for qb in range(S // 512) for j in range(4 * (qb + 1))]
    R = 3
    with Stage(nc, name) as st:
        la = st.sb("la", [P, R, 512])
        wt = st.sb("wt", [P, R, 512])
        ps = st.ps("ps", [P, R, 512])
        po = st.ps("po", [P, 2, 2, 512])
        s = {n: st.sem(n) for n in ("score", "abs", "log", "w", "pv", "read")}
        blocks = {}
        for u, (b, qb, j) in enumerate(units):
            blocks.setdefault((b, qb), []).append(u)
        order = list(blocks)
        with nc.Block() as block:
            @block.tensor
            def _(pe):
                def scores(u):
                    b, qb, j = units[u]
                    if u >= R:
                        pe.wait_ge(s["w"], u - R + 1)
                    for k in range(KC):
                        last = pe.matmul(ps[:, u % R, :], qT[:, k, b * S + j * P:b * S + (j + 1) * P],
                                         kT[:, k, b * S + qb * 512:b * S + (qb + 1) * 512], start=(k == 0), stop=(k == KC - 1))
                    last.then_inc(s["score"], 1)

                def weigh(u):
                    b, qb, j = units[u]
                    o = order.index((b, qb))
                    if j == 0 and o >= 2:
                        pe.wait_ge(s["read"], o - 1)
                    pe.wait_ge(s["w"], u + 1)
                    for t in range(max(0, j - 4 * qb), 4):
                        last = pe.matmul(po[:, o % 2, t // 2, (t % 2) * D:(t % 2 + 1) * D], wt[:, u % R, t * P:(t + 1) * P],
                                         v[:, b * ST + j, :], start=(j == 0 and t % 2 == 0), stop=(j == 4 * qb + t),
                                         skip_group_check=True)
                    last.then_inc(s["pv"], 1)

                for u in range(len(units) + 2):
                    if u < len(units):
                        scores(u)
                    if u >= 2:
                        weigh(u - 2)

            @block.scalar
            def _(act):
                for u in range(len(units)):
                    act.wait_ge(s["score"], u + 1)
                    if u >= R:
                        act.wait_ge(s["w"], u - R + 1)
                    a = la[:, u % R, :]
                    act.activation(a, ps[:, u % R, :], ACT.Abs, scale=D ** -0.5).then_inc(s["abs"], 1)
                    act.drain()
                    act.activation(a, a, ACT.Exp, scale=-1.0)
                    act.drain()
                    act.activation(a, a, ACT.Ln, bias=1.0).then_inc(s["log"], 1)

            @block.vector
            def _(dve):
                def copy_out(o):
                    b, qb = order[o]
                    dve.wait_ge(s["pv"], blocks[(b, qb)][-1] + 1)
                    dve.tensor_copy(out[:, b * ST + 4 * qb:b * ST + 4 * qb + 4, :].rearrange("p (g t) d -> p g (t d)", g=2),
                                    po[:, o % 2, :, :]).then_inc(s["read"], 1)

                for u, (b, qb, j) in enumerate(units):
                    dve.wait_ge(s["abs"], u + 1)
                    if u >= R:
                        dve.wait_ge(s["pv"], u - R + 1)
                    wu = wt[:, u % R, :]
                    dve.tensor_scalar(wu, ps[:, u % R, :], D ** -0.5, 0.0, ALU.mult, ALU.max)
                    dve.drain()
                    dve.wait_ge(s["log"], u + 1)
                    last = dve.tensor_tensor(wu, wu, la[:, u % R, :], ALU.add)
                    jj = j - 4 * qb
                    if jj >= 0:
                        dve.drain()
                        dg = wt[:, u % R, jj * P:(jj + 1) * P]
                        last = dve.tensor_tensor(dg, dg, c.lower[:], ALU.mult)
                    last.then_inc(s["w"], 1)
                    o = order.index((b, qb))
                    if j == 1 and o >= 1:
                        copy_out(o - 1)
                copy_out(len(order) - 1)


def softmax_attention(c, name, qT, kT, v, out, resid, causal):
    nc = c.nc
    with Stage(nc, name) as st:
        upper = st.sb("upper", [P, P])
        nm = st.sb("nm", [P, 2, 2])
        total = st.sb("total", [P, 2, 2])
        p_ = st.sb("p", [P, 2, S])
        pT = st.sb("pT", [P, 2, S])
        ps = st.ps("ps", [P, 2, 2, 512])
        pTp = st.ps("pTp", [P, 2, 512])
        po = st.ps("po", [P, 2, 512])
        s = {n: st.sem(n) for n in ("mask", "score", "nmax", "exp", "turned", "copied", "pv", "out")}

        def keys(t):
            b, q = t // ST, t % ST
            return (b * S, (q + 1) * P) if causal else (b * S2, S2)

        with nc.Block() as block:
            @block.gpsimd
            def _(pool):
                pool.memset(upper[:], 0.0)
                pool.drain()
                pool.affine_select(out=upper[:], in_=upper[:], compare_op=ALU.is_ge, fill=-1e30, base=0,
                                   pattern=[[-1, P]], channel_multiplier=1).then_inc(s["mask"], 1)

            @block.tensor
            def _(pe):
                def scores(t):
                    k0, nk = keys(t)
                    if t >= 2:
                        pe.wait_ge(s["exp"], t - 1)
                    for a in range(0, nk, 512):
                        w = min(512, nk - a)
                        for k in range(KC):
                            last = pe.matmul(ps[:, t % 2, a // 512, 0:w], qT[:, k, t * P:(t + 1) * P],
                                             kT[:, k, k0 + a:k0 + a + w], start=(k == 0), stop=(k == KC - 1))
                    last.then_inc(s["score"], 1)

                def weigh(t):
                    k0, nk = keys(t)
                    pe.wait_ge(s["exp"], t + 1)
                    if t >= 1:
                        pe.wait_ge(s["copied"], t)
                    nj = (nk + P - 1) // P
                    for j in range(nj):
                        w = min(P, nk - j * P)
                        last = pe.transpose(pTp[0:w, j // 4, (j % 4) * P:(j % 4 + 1) * P], p_[:, t % 2, j * P:j * P + w], c.ident[:])
                    last.then_inc(s["turned"], 1)
                    pe.wait_ge(s["copied"], t + 1)
                    if t >= 2:
                        pe.wait_ge(s["out"], t - 1)
                    for j in range(nj):
                        w = min(P, nk - j * P)
                        vt = v[0:w, t // ST * ST + j, :] if causal else v[0:w, t // ST, :]
                        last = pe.matmul(po[:, t % 2, 0:D], pT[0:w, t % 2, j * P:(j + 1) * P], vt, start=(j == 0), stop=(j == nj - 1))
                    last.then_inc(s["pv"], 1)

                for t in range(NT + 1):
                    if t < NT:
                        scores(t)
                    if t >= 1:
                        weigh(t - 1)

            @block.scalar
            def _(act):
                for t in range(NT):
                    k0, nk = keys(t)
                    act.wait_ge(s["nmax"], t + 1)
                    if t >= 2:
                        act.wait_ge(s["turned"], t - 1)
                    g, w = (nk // 512, 512) if nk > 512 and nk % 512 == 0 else (1, nk)
                    act.activation(p_[:, t % 2, 0:nk], ps[:, t % 2].rearrange("p g n -> p (g n)")[:, 0:nk], ACT.Exp, scale=D ** -0.5,
                                   bias=nm[:, t % 2, 1:2], accum_out=total[:, t % 2, 0:1]).then_inc(s["exp"], 1)
                    act.wait_ge(s["turned"], t + 1)
                    if t >= 2:
                        act.wait_ge(s["pv"], t - 1)
                    rows = min(nk, P)
                    cols = (nk + P - 1) // P * P
                    act.activation(pT[0:rows, t % 2, 0:cols], pTp[:].rearrange("p g n -> p (g n)")[0:rows, 0:cols],
                                   ACT.Copy).then_inc(s["copied"], 1)

            @block.vector
            def _(dve):
                dve.wait_ge(s["mask"], 1)

                def top(t):
                    k0, nk = keys(t)
                    dve.wait_ge(s["score"], t + 1)
                    flat = ps[:, t % 2].rearrange("p g n -> p (g n)")
                    if causal:
                        dg = flat[:, nk - P:nk]
                        dve.tensor_tensor(dg, dg, upper[:], ALU.add)
                        dve.drain()
                    dve.tensor_reduce(nm[:, t % 2, 0:1], flat[:, 0:nk], AX.X, ALU.max, negate=True)
                    dve.drain()
                    dve.tensor_scalar(nm[:, t % 2, 1:2], nm[:, t % 2, 0:1], D ** -0.5, None, ALU.mult).then_inc(s["nmax"], 1)

                def finish(t):
                    dve.wait_ge(s["exp"], t + 1)
                    dve.reciprocal(total[:, t % 2, 1:2], total[:, t % 2, 0:1])
                    dve.drain()
                    dve.wait_ge(s["pv"], t + 1)
                    dve.scalar_tensor_tensor(out=out[:, t, :], in0=po[:, t % 2, 0:D], scalar=total[:, t % 2, 1:2],
                                             in1=resid[:, t, :], op0=ALU.mult, op1=ALU.add).then_inc(s["out"], 1)

                for t in range(NT + 1):
                    if t < NT:
                        top(t)
                    if t >= 1:
                        finish(t - 1)


def load(c, name, dst, src):
    with Stage(c.nc, name) as st:
        came = st.sem("in")
        with c.nc.Block() as block:
            @block.sync
            def _(sp):
                sp.dma_start(dst[:], src).then_inc(came, 16)
                sp.wait_ge(came, 16)


def add_to_x(c, name, src, relu=False):
    with Stage(c.nc, name) as st:
        with c.nc.Block() as block:
            @block.vector
            def _(dve):
                if relu:
                    dve.scalar_tensor_tensor(out=c.x[:], in0=src[:], scalar=0.0, in1=c.x[:], op0=ALU.max, op1=ALU.add)
                else:
                    dve.tensor_tensor(c.x[:], src[:], c.x[:], ALU.add)


MAGIC = 12582912.0


def quantize_weights(c, name, w, dst, size):
    nc = c.nc
    K, M = w.shape
    k_ = K // P
    with Stage(nc, name) as st:
        w_sb = st.sb("w", [P, k_, M])
        part = st.sb("part", [P, 2])
        ps = st.ps("ps", [P, 8])
        w_in, summed, total = st.sem("w_in"), st.sem("summed"), st.sem("total")
        with nc.Block() as block:
            @block.sync
            def _(sp):
                sp.dma_start(w_sb[:], w.rearrange("(k p) m -> p k m", p=P)).then_inc(w_in, 16)
                sp.wait_ge(w_in, 16)

            @block.tensor
            def _(pe):
                pe.wait_ge(summed, 1)
                pe.matmul(ps[:, 0:1], c.ones[:], part[:, 0:1], start=True, stop=True).then_inc(total, 1)

            @block.vector
            def _(dve):
                dve.wait_ge(w_in, 16)
                dve.tensor_reduce(part[:, 0:1], w_sb[:], AX.XY, ALU.add, apply_absolute_value=True).then_inc(summed, 1)
                dve.wait_ge(total, 1)
                dve.tensor_scalar(size[:], ps[:, 0:1], 1.0 / (K * M), 1e-5, ALU.mult, ALU.max)
                dve.drain()
                dve.reciprocal(part[:, 1:2], size[:])
                dve.drain()
                dve.tensor_scalar(w_sb[:], w_sb[:], part[:, 1:2], -1.0, ALU.mult, ALU.max)
                dve.drain()
                dve.tensor_scalar(w_sb[:], w_sb[:], 1.0, MAGIC, ALU.min, ALU.add)
                dve.drain()
                dve.tensor_scalar(dst[:], w_sb[:], MAGIC, None, ALU.subtract)


def quantized_ffn(c, name, r, w1q, s1, w2q, s2, b1, b2):
    nc = c.nc
    F = w1q.shape[2]
    FC = F // P
    with Stage(nc, name) as st:
        b1_sb = st.sb("b1", [P, F])
        b2_sb = st.sb("b2", [P, D])
        idb = st.sb("idb", [P, P], BF16)
        am = st.sb("am", [P, 6, NT])
        am2 = st.sb("am2", [P, 8, NT])
        t_f = st.sb("t_f", [P, 2, F])
        q = st.sb("q", [P, 2, F], BF16)
        qT = st.sb("qT", [P, 2, F], BF16)
        g = st.sb("g", [P, NT, F])
        h = st.sb("h", [P, 2, F])
        sq = st.sb("sq", [P, F])
        tp = st.ps("tp", [P, 2, 1024], BF16)
        ps = st.ps("ps", [P, 2, 2, 512])
        names = ("w_in", "q", "turned", "qT", "mult", "h", "gelu", "stats", "var", "sd", "q2", "turned2", "qT2", "mult2", "added")
        s = {n: st.sem(n) for n in names}
        HALF = NT // 2

        def quantize(dve, dst, src, tmp, scale):
            dve.tensor_scalar(tmp, src, scale, -128.0, ALU.mult, ALU.max)
            dve.drain()
            dve.tensor_scalar(tmp, tmp, 127.0, MAGIC, ALU.min, ALU.add)
            dve.drain()
            return dve.tensor_scalar(dst, tmp, MAGIC, None, ALU.subtract)

        with nc.Block() as block:
            @block.sync
            def _(sp):
                load_weights(sp, [(b1_sb[:], row_bcast(b1, F)), (b2_sb[:], row_bcast(b2, D))], s["w_in"])
                sp.wait_ge(s["w_in"], 32)

            @block.vector
            def _(dve):
                dve.tensor_copy(idb[:], c.ident[:])
                dve.tensor_reduce(am[:, 0, :], r[:], AX.X, ALU.max, apply_absolute_value=True)
                dve.drain()
                dve.tensor_scalar(am[:, 0, :], am[:, 0, :], 1e-5, 1.0 / 127.0, ALU.max, ALU.mult)
                dve.drain()
                dve.reciprocal(am[:, 1, :], am[:, 0, :])
                dve.tensor_scalar(am[:, 2, :], am[:, 0, :], s1[:, 0:1], None, ALU.mult)
                dve.drain()
                dve.wait_ge(s["w_in"], 32)
                with dve.Fori(0, HALF) as i:
                    for j in range(2):
                        t = bass.ds(i * 2 + j, 1)
                        dve.wait_ge(s["turned"], i * 2)
                        quantize(dve, q[:, j:j + 1, 0:D], r[:, t, :], t_f[:, j:j + 1, 0:D], am[:, 1, t]).then_inc(s["q"], 1)
                    for j in range(2):
                        t = bass.ds(i * 2 + j, 1)
                        dve.wait_ge(s["mult"], i * 2 + (j + 1))
                        dve.wait_ge(s["gelu"], i * 2)
                        dve.scalar_tensor_tensor(out=h[:, j, :].rearrange("p (a n) -> p a n", a=2), in0=ps[:, j], scalar=am[:, 2, t],
                                                 in1=b1_sb[:].rearrange("p (a n) -> p a n", a=2), op0=ALU.mult,
                                                 op1=ALU.add).then_inc(s["h"], 1)
                dve.wait_ge(s["gelu"], NT)
                dve.tensor_reduce(am2[:, 0, :], g[:], AX.X, ALU.max, apply_absolute_value=True)
                dve.tensor_scalar(am2[:, 1, :], am2[:, 7, :], 1.0 / F, 1e-5, ALU.mult, ALU.add).then_inc(s["var"], 1)
                dve.drain()
                dve.wait_ge(s["sd"], 1)
                dve.reciprocal(am2[:, 2, :], am2[:, 1, :])
                dve.drain()
                dve.tensor_tensor(am2[:, 3, :], am2[:, 0, :], am2[:, 2, :], ALU.mult)
                dve.drain()
                dve.tensor_scalar(am2[:, 3, :], am2[:, 3, :], 1e-5, 1.0 / 127.0, ALU.max, ALU.mult)
                dve.drain()
                dve.reciprocal(am2[:, 4, :], am2[:, 3, :])
                dve.drain()
                dve.tensor_tensor(am2[:, 5, :], am2[:, 4, :], am2[:, 2, :], ALU.mult)
                dve.tensor_scalar(am2[:, 6, :], am2[:, 3, :], s2[:, 0:1], None, ALU.mult)
                dve.drain()
                with dve.Fori(0, HALF) as i:
                    for j in range(2):
                        t = bass.ds(i * 2 + j, 1)
                        dve.wait_ge(s["turned2"], i * 2)
                        quantize(dve, q[:, j:j + 1, :], g[:, t, :], t_f[:, j:j + 1, :], am2[:, 5, t]).then_inc(s["q2"], 1)
                    for j in range(2):
                        t = bass.ds(i * 2 + j, 1)
                        dve.wait_ge(s["mult2"], i * 2 + (j + 1))
                        dve.scalar_tensor_tensor(out=h[:, j:j + 1, 0:D], in0=ps[:, j, 0:1, 0:D], scalar=am2[:, 6, t],
                                                 in1=c.x[:, t, :], op0=ALU.mult, op1=ALU.add).then_inc(s["added"], 1)
                        dve.drain()
                        dve.tensor_tensor(c.x[:, t, :], h[:, j:j + 1, 0:D], b2_sb[:].rearrange("p (a d) -> p a d", a=1), ALU.add)

            @block.tensor
            def _(pe):
                for q_s, t_s, qT_s, m_s, h_s, nk, wide in ((s["q"], s["turned"], s["qT"], s["mult"], s["h"], KC, True),
                                                           (s["q2"], s["turned2"], s["qT2"], s["mult2"], s["added"], FC, False)):
                    with pe.Fori(0, HALF) as i:
                        for j in range(2):
                            pe.wait_ge(q_s, i * 2 + (j + 1))
                            pe.wait_ge(qT_s, i * 2)
                            for k in range(nk):
                                last = pe.transpose(tp[:, j, k * P:(k + 1) * P], q[:, j, k * P:(k + 1) * P], idb[:])
                            last.then_inc(t_s, 1)
                        for j in range(2):
                            pe.wait_ge(qT_s, i * 2 + (j + 1))
                            pe.wait_ge(h_s, i * 2)
                            for n in range(F // 512 if wide else 1):
                                for k in range(nk):
                                    rhs = w1q[:, k, n * 512:(n + 1) * 512] if wide else w2q[:, k, :]
                                    last = pe.matmul(ps[:, j, n, 0:512 if wide else D], qT[:, j, k * P:(k + 1) * P], rhs,
                                                     start=(k == 0), stop=(k == nk - 1))
                            last.then_inc(m_s, 1)

            @block.scalar
            def _(act):
                with act.Fori(0, HALF) as i:
                    for j in range(2):
                        act.wait_ge(s["turned"], i * 2 + (j + 1))
                        act.wait_ge(s["mult"], i * 2)
                        act.activation(qT[:, j, 0:D], tp[:, j, 0:D], ACT.Copy).then_inc(s["qT"], 1)
                    for j in range(2):
                        act.wait_ge(s["h"], i * 2 + (j + 1))
                        g_t = g[:, bass.ds(i * 2 + j, 1), :]
                        act.activation(g_t, h[:, j:j + 1, :], ACT.Gelu)
                        act.drain()
                        act.activation(sq[:].rearrange("p (a n) -> p a n", a=1), g_t, ACT.Square,
                                       accum_out=am2[:, 7, bass.ds(i * 2 + j, 1)]).then_inc(s["gelu"], 1)
                        act.drain()
                act.wait_ge(s["var"], 1)
                act.activation(am2[:, 1, :], am2[:, 1, :], ACT.Sqrt).then_inc(s["sd"], 1)
                with act.Fori(0, HALF) as i:
                    for j in range(2):
                        act.wait_ge(s["turned2"], i * 2 + (j + 1))
                        act.wait_ge(s["mult2"], i * 2)
                        act.activation(qT[:, j, :], tp[:, j, :], ACT.Copy).then_inc(s["qT2"], 1)


def per_head_T(c, name, qT, kT, gT, wq, wk, scale):
    nc = c.nc
    with Stage(nc, name) as st:
        w = st.sb("w", [P, 2, KC, P])
        ps = st.ps("ps", [P, 2, 4, 512])
        w_in, mult_q, mult_k, out_q, out_k = (st.sem(n) for n in ("w_in", "mult_q", "mult_k", "out_q", "out_k"))
        units = [(k, n) for k in range(KC) for n in range(N // 512)]
        with nc.Block() as block:
            @block.sync
            def _(sp):
                load_weights(sp, [(w[:, i], v.rearrange("k p m -> p k m")) for i, v in enumerate((wq, wk))], w_in)
                sp.wait_ge(w_in, 32)

            @block.tensor
            def _(pe):
                pe.wait_ge(w_in, 32)
                for u, (k, n) in enumerate(units):
                    for i, (t, mult, out) in enumerate(((qT, mult_q, out_q), (kT, mult_k, out_k))):
                        if u >= 4:
                            pe.wait_ge(out, u - 3)
                        pe.matmul(ps[:, i, u % 4, :], w[:, i, k, :], t[:, k, n * 512:(n + 1) * 512],
                                  start=True, stop=True).then_inc(mult, 1)

            @block.scalar
            def _(act):
                for u, (k, n) in enumerate(units):
                    act.wait_ge(mult_q, u + 1)
                    act.activation(qT[:, k, n * 512:(n + 1) * 512], ps[:, 0, u % 4, :], ACT.Copy).then_inc(out_q, 1)

            @block.vector
            def _(dve):
                for u, (k, n) in enumerate(units):
                    cols = slice(n * 512, (n + 1) * 512)
                    dve.wait_ge(mult_k, u + 1)
                    dve.scalar_tensor_tensor(out=kT[:, k, cols], in0=ps[:, 1, u % 4, :], scalar=scale, in1=gT[:, k, cols],
                                             op0=ALU.mult, op1=ALU.mult).then_inc(out_k, 1)


def recurrence(c, name, qT, kT, vT, decay_logits, spread, gather):
    nc = c.nc
    with Stage(nc, name) as st:
        dl = st.sb("dl", [P, KC])
        sg = st.sb("sg", [P, 2, DH, P])
        kv = st.sb("kv", [P, 2, S])
        M = st.sb("M", [P, 2, S])
        qM = st.sb("qM", [P, 2, S])
        qb = st.sb("qb", [P, KC, S])
        vb = st.ps("vb", [P, 2, 2, 512])
        y = st.ps("y", [P, KC, 2, 512])
        names = ("w_in", "decay", "spread", "kv", "M", "q", "qM", "gathered", "y_out")
        s = {n: st.sem(n) for n in names}
        U = KC * DH
        with nc.Block() as block:
            @block.sync
            def _(sp):
                load_weights(sp, [(dl[:], decay_logits), (sg[:, 0], spread), (sg[:, 1], gather)], s["w_in"])
                sp.wait_ge(s["w_in"], 48)

            @block.tensor
            def _(pe):
                pe.wait_ge(s["w_in"], 48)
                with pe.Fori(0, B) as bi:
                    def copies(u):
                        k, d = u // DH, u % DH
                        pe.wait_ge(s["kv"], bi * U + (u - 1) if u >= 2 else bi * U)
                        for h in range(2):
                            last = pe.matmul(vb[:, u % 2, h, :], sg[:, 0, d, :], vT[:, k, bass.ds(bi * S + h * 512, 512)],
                                             start=True, stop=True)
                        last.then_inc(s["spread"], 1)

                    def sums(u):
                        k, d = u // DH, u % DH
                        if d == 0:
                            pe.wait_ge(s["y_out"], bi * KC)
                        pe.wait_ge(s["qM"], bi * U + (u + 1))
                        for h in range(2):
                            last = pe.matmul(y[:, k, h, :], sg[:, 1, d, :], qM[:, u % 2, h * 512:(h + 1) * 512],
                                             start=(d == 0), stop=(d == DH - 1))
                        last.then_inc(s["gathered"], 1)

                    for u in range(U + 2):
                        if u < U:
                            copies(u)
                        if u >= 2:
                            sums(u - 2)

            @block.vector
            def _(dve):
                dve.wait_ge(s["decay"], 1)
                with dve.Fori(0, B) as bi:
                    for u in range(U):
                        k, d = u // DH, u % DH
                        dve.wait_ge(s["spread"], bi * U + (u + 1))
                        dve.tensor_tensor(kv[:, u % 2, :].rearrange("p (h n) -> p h n", h=2),
                                          kT[:, k, bass.ds(bi * S, S)].rearrange("p (h n) -> p h n", h=2), vb[:, u % 2], ALU.mult).then_inc(s["kv"], 1)
                        dve.drain()
                        dve.wait_ge(s["qM"], bi * U + (u - 1) if u >= 2 else bi * U)
                        dve.tensor_tensor_scan(M[:, u % 2, :], dl[:, k:k + 1].broadcast_to([P, S]), kv[:, u % 2, :], 0.0,
                                               ALU.mult, ALU.add).then_inc(s["M"], 1)

            @block.gpsimd
            def _(pool):
                with pool.Fori(0, B) as bi:
                    for u in range(U):
                        k = u // DH
                        pool.wait_ge(s["q"], bi + 1)
                        pool.wait_ge(s["M"], bi * U + (u + 1))
                        pool.wait_ge(s["gathered"], bi * U + (u - 1) if u >= 2 else bi * U)
                        pool.tensor_tensor(qM[:, u % 2, :], M[:, u % 2, :], qb[:, k, :], ALU.mult).then_inc(s["qM"], 1)

            @block.scalar
            def _(act):
                act.wait_ge(s["w_in"], 48)
                act.activation(dl[:], dl[:], ACT.Sigmoid).then_inc(s["decay"], 1)
                with act.Fori(0, B) as bi:
                    act.activation(qb[:], qT[:, :, bass.ds(bi * S, S)], ACT.Copy).then_inc(s["q"], 1)
                    for k in range(KC):
                        act.wait_ge(s["gathered"], bi * U + (k + 1) * DH)
                        act.activation(vT[:, k, bass.ds(bi * S, S)].rearrange("p (h n) -> p h n", h=2), y[:, k], ACT.Copy).then_inc(s["y_out"], 1)


def cross_heads(c, name, qT, kT, v, out, clip=None):
    nc = c.nc
    HK = P // DH
    W = HK * S2
    HW = W // 2
    with Stage(nc, name) as st:
        hm = st.sb("hm", [P, HK])
        kb = st.sb("kb", [P, KC, B, HK, S2])
        sc = st.sb("sc", [P, 2, HK, S2])
        ex = st.sb("ex", [P, 2, HK, S2])
        mx = st.sb("mx", [P, 2, HK])
        sm = st.sb("sm", [P, 2, HK])
        eT = st.sb("eT", [S2, 2, HK, P])
        ps = st.ps("ps", [P, 2, 2, 512])
        tp = st.ps("tp", [P, 2, 512])
        po = st.ps("po", [P, 2, 512])
        names = ("w_in", "kb", "score", "read", "shift", "exp", "turned", "copied", "pv", "out")
        s = {n: st.sem(n) for n in names}
        units = [(t, k) for t in range(NT) for k in range(KC)]
        with nc.Block() as block:
            @block.sync
            def _(sp):
                sp.dma_start(hm[:], c.dram["head_mask"]).then_inc(s["w_in"], 16)
                sp.wait_ge(s["w_in"], 16)

            @block.tensor
            def _(pe):
                pe.wait_ge(s["kb"], 1)

                def scores(u):
                    t, k = units[u]
                    if u >= 2:
                        pe.wait_ge(s["read"], u - 1)
                    rhs = kb[:, k, t // ST].rearrange("p h n -> p (h n)")
                    for a in range(2):
                        last = pe.matmul(ps[:, u % 2, a, 0:HW], qT[:, k, t * P:(t + 1) * P], rhs[:, a * HW:(a + 1) * HW],
                                         start=True, stop=True)
                    last.then_inc(s["score"], 1)

                def weigh(u):
                    t, k = units[u]
                    pe.wait_ge(s["exp"], u + 1)
                    if u >= 1:
                        pe.wait_ge(s["copied"], u)
                    for h in range(HK):
                        last = pe.transpose(tp[0:S2, h // 4, (h % 4) * P:(h % 4 + 1) * P], ex[:, u % 2, h, :], c.ident[:])
                    last.then_inc(s["turned"], 1)
                    pe.wait_ge(s["copied"], u + 1)
                    if u >= 2:
                        pe.wait_ge(s["out"], u - 1)
                    for h in range(HK):
                        col = k * P + h * DH
                        last = pe.matmul(po[:, u % 2, h * DH:(h + 1) * DH], eT[:, u % 2, h, :], v[0:S2, t // ST, col:col + DH],
                                         start=True, stop=True)
                    last.then_inc(s["pv"], 1)

                for u in range(len(units) + 1):
                    if u < len(units):
                        scores(u)
                    if u >= 1:
                        weigh(u - 1)

            @block.scalar
            def _(act):
                for u in range(len(units)):
                    act.wait_ge(s["shift"], u + 1)
                    if u >= 2:
                        act.wait_ge(s["turned"], u - 1)
                    act.activation(ex[:, u % 2], sc[:, u % 2], ACT.Exp, scale=DH ** -0.5).then_inc(s["exp"], 1)
                    act.wait_ge(s["turned"], u + 1)
                    if u >= 2:
                        act.wait_ge(s["pv"], u - 1)
                    act.activation(eT[:, u % 2].rearrange("p (a h) n -> p a (h n)", a=2), tp[0:S2, :, :], ACT.Copy).then_inc(s["copied"], 1)

            @block.vector
            def _(dve):
                dve.wait_ge(s["w_in"], 16)
                shape = [P, HK, S2]
                for k in range(KC):
                    for b in range(B):
                        keys = kT[:, k:k + 1, b * S2:(b + 1) * S2].broadcast_to(shape)
                        mask = hm[:].rearrange("p (h a) -> p h a", a=1).broadcast_to(shape)
                        dve.tensor_tensor(kb[:, k, b], keys, mask, ALU.mult)
                dve.drain()
                dve.sem_inc(s["kb"], 1)

                def top(u):
                    dve.wait_ge(s["score"], u + 1)
                    if u >= 2:
                        dve.wait_ge(s["exp"], u - 1)
                    o, src = sc[:, u % 2].rearrange("p (a h) n -> p a (h n)", a=2), ps[:, u % 2, :, 0:HW]
                    if clip is None:
                        dve.tensor_copy(o, src).then_inc(s["read"], 1)
                    else:
                        dve.tensor_scalar(o, src, clip, -clip, ALU.min, ALU.max).then_inc(s["read"], 1)
                    dve.drain()
                    dve.tensor_reduce(mx[:, u % 2, :], sc[:, u % 2], AX.X, ALU.max)
                    dve.drain()
                    m = mx[:, u % 2, :].rearrange("p (h a) -> p h a", a=1).broadcast_to(shape)
                    dve.tensor_tensor(sc[:, u % 2], sc[:, u % 2], m, ALU.subtract).then_inc(s["shift"], 1)

                def finish(u):
                    t, k = units[u]
                    dve.wait_ge(s["exp"], u + 1)
                    dve.tensor_reduce(sm[:, u % 2, :], ex[:, u % 2], AX.X, ALU.add)
                    dve.drain()
                    dve.reciprocal(sm[:, u % 2, :], sm[:, u % 2, :])
                    dve.drain()
                    dve.wait_ge(s["pv"], u + 1)
                    r = sm[:, u % 2, :].rearrange("p (h a) -> p h a", a=1).broadcast_to([P, HK, DH])
                    dve.tensor_tensor(out[:, t, k * P:(k + 1) * P].rearrange("p (h d) -> p h d", h=HK),
                                      po[:, u % 2, 0:P].rearrange("p (h d) -> p h d", h=HK), r, ALU.mult).then_inc(s["out"], 1)

                for u in range(len(units) + 1):
                    if u < len(units):
                        top(u)
                    if u >= 1:
                        finish(u - 1)


def tree_ffn(c, name, srcT, w_in_T, b_in, w_out_T):
    nc = c.nc
    DEPTH, PAR = 7, 8
    NODES = 2 ** (DEPTH + 1) - 1
    W = PAR * NODES
    Q = W // 4
    WC = w_out_T.shape[0] // P
    with Stage(nc, name) as st:
        wi = st.sb("wi", [P, KC, W])
        bi_sb = st.sb("bi", [P, W])
        wo = st.sb("wo", [P, WC, D])
        l = st.sb("l", [P, 2, W])
        go = st.sb("go", [P, 2, W])
        on = st.sb("on", [P, 2, W])
        act_ = st.sb("act", [P, 2, WC * P])
        aT = st.sb("aT", [P, 2, 4, P])
        xt = st.sb("xt", [P, 2, KC, P])
        ps = st.ps("ps", [P, 4, 512])
        tp = st.ps("tp", [P, 2, 512])
        po = st.ps("po", [P, 2, 512])
        names = ("w_in", "x", "init", "logit", "l", "silu", "path", "masked", "turned", "aT", "out", "added")
        s = {n: st.sem(n) for n in names}
        GT = WC // 4
        with nc.Block() as block:
            @block.sync
            def _(sp):
                load_weights(sp, [(wi[:], w_in_T.rearrange("(k p) m -> p k m", p=P)), (bi_sb[:], row_bcast(b_in, W)),
                                  (wo[:], w_out_T.rearrange("(k p) m -> p k m", p=P))], s["w_in"])
                sp.wait_ge(s["w_in"], 48)

            @block.tensor
            def _(pe):
                pe.wait_ge(s["w_in"], 48)
                with pe.Fori(0, NT // 2) as i:
                    def logits(j):
                        pe.wait_ge(s["x"], i * 2 + (j + 1))
                        pe.wait_ge(s["l"], i * 2 + j)
                        for g in range(4):
                            for k in range(KC):
                                last = pe.matmul(ps[:, g, 0:Q], xt[:, j, k, :], wi[:, k, g * Q:(g + 1) * Q],
                                                 start=(k == 0), stop=(k == KC - 1))
                        last.then_inc(s["logit"], 1)

                    def turn(j, g):
                        q = j * GT + g
                        if g == 0:
                            pe.wait_ge(s["masked"], i * 2 + (j + 1))
                        pe.wait_ge(s["aT"], i * (2 * GT) + (q - 1) if q >= 2 else i * (2 * GT))
                        for m in range(4):
                            last = pe.transpose(tp[:, q % 2, m * P:(m + 1) * P], act_[:, j, (4 * g + m) * P:(4 * g + m + 1) * P], c.ident[:])
                        last.then_inc(s["turned"], 1)

                    def project(j, g):
                        q = j * GT + g
                        if g == 0:
                            pe.wait_ge(s["added"], i * 2)
                        pe.wait_ge(s["aT"], i * (2 * GT) + (q + 1))
                        for m in range(4):
                            last = pe.matmul(po[:, j, 0:D], aT[:, q % 2, m, :], wo[:, 4 * g + m, :],
                                             start=(g == 0 and m == 0), stop=(g == GT - 1 and m == 3))
                        last.then_inc(s["out"], 1)

                    logits(0)
                    logits(1)
                    for q in range(2 * GT + 1):
                        if q < 2 * GT:
                            turn(q // GT, q % GT)
                        if q >= 1:
                            project((q - 1) // GT, (q - 1) % GT)

            @block.gpsimd
            def _(pool):
                pool.memset(act_[:, :, W:WC * P], 0.0)
                on4 = on[:].rearrange("p r (a n) -> p r a n", a=PAR)
                pool.memset(on4[:, :, :, 0:1], 1.0)
                pool.drain()
                pool.sem_inc(s["init"], 1)
                with pool.Fori(0, NT // 2) as i:
                    for j in range(2):
                        pool.wait_ge(s["logit"], i * 2)
                        pool.tensor_copy(xt[:, j], srcT[:, :, bass.ds((i * 2 + j) * P, P)]).then_inc(s["x"], 1)
                    for j in range(2):
                        pool.wait_ge(s["silu"], i * 2 + (j + 1))
                        pool.wait_ge(s["path"], i * 2 + (j + 1))
                        pool.tensor_tensor(act_[:, j, 0:W], act_[:, j, 0:W], on[:, j, :], ALU.mult).then_inc(s["masked"], 1)

            @block.scalar
            def _(act):
                with act.Fori(0, NT // 2) as i:
                    for j in range(2):
                        act.wait_ge(s["l"], i * 2 + (j + 1))
                        act.wait_ge(s["turned"], i * (2 * GT))
                        act.activation(act_[:, j, 0:W], l[:, j, :], ACT.Silu).then_inc(s["silu"], 1)
                    for q in range(2 * GT):
                        act.wait_ge(s["turned"], i * (2 * GT) + (q + 1))
                        act.wait_ge(s["out"], i * (2 * GT) + (q - 1) if q >= 2 else i * (2 * GT))
                        act.activation(aT[:, q % 2].rearrange("p m n -> p (m n)"), tp[:, q % 2, :], ACT.Copy).then_inc(s["aT"], 1)

            @block.vector
            def _(dve):
                dve.wait_ge(s["w_in"], 48)
                dve.wait_ge(s["init"], 1)
                with dve.Fori(0, NT // 2) as i:
                    for j in range(2):
                        dve.wait_ge(s["logit"], i * 2 + (j + 1))
                        dve.wait_ge(s["silu"], i * 2)
                        dve.tensor_tensor(l[:, j, :].rearrange("p (g n) -> p g n", g=4), ps[:, :, 0:Q],
                                          bi_sb[:].rearrange("p (g n) -> p g n", g=4), ALU.add).then_inc(s["l"], 1)
                        dve.drain()
                        dve.tensor_scalar(go[:, j, :], l[:, j, :], 0.0, None, ALU.is_gt)
                        dve.drain()
                        dve.wait_ge(s["masked"], i * 2)
                        on3 = on[:, j, :].rearrange("p (a n) -> p a n", a=PAR)
                        go3 = go[:, j, :].rearrange("p (a n) -> p a n", a=PAR)
                        for lev in range(DEPTH):
                            here, n = 2 ** lev - 1, 2 ** lev
                            below = 2 * here + 1
                            right = on3[:, :, below + 1:below + 2 * n:2]
                            dve.tensor_tensor(right, on3[:, :, here:here + n], go3[:, :, here:here + n], ALU.mult)
                            dve.drain()
                            last = dve.tensor_tensor(on3[:, :, below:below + 2 * n:2], on3[:, :, here:here + n], right, ALU.subtract)
                            if lev < DEPTH - 1:
                                dve.drain()
                        last.then_inc(s["path"], 1)
                    for j in range(2):
                        x_t = c.x[:, bass.ds(i * 2 + j, 1), :]
                        dve.wait_ge(s["out"], i * (2 * GT) + (j + 1) * GT)
                        dve.tensor_tensor(x_t, x_t, po[:, j:j + 1, 0:D], ALU.add).then_inc(s["added"], 1)


H3 = 8
DK = 128
M_INCL, M_STRICT, M_BLOCK, M_J16, M_J32, M_J64 = range(6)


def delta_gates(c, name, ba, dt_bias, a_log, coef):
    nc = c.nc
    with Stage(nc, name) as st:
        rows = st.sb("rows", [P, 2, H3])
        masks = st.sb("masks", [P, P])
        z = st.sb("z", [P, H3, NT])
        l = st.sb("l", [P, H3, NT])
        ps = st.ps("ps", [P, 4, 512])
        s = {n: st.sem(n) for n in ("in", "z", "log", "g", "sum")}
        with nc.Block() as block:
            @block.sync
            def _(sp):
                load_weights(sp, [(rows[:, 0], row_bcast(dt_bias, H3)), (rows[:, 1], row_bcast(a_log, H3)),
                                  (masks[:], c.dram["masks"][:, M_STRICT, :])], s["in"])
                sp.wait_ge(s["in"], 48)

            @block.vector
            def _(dve):
                dve.wait_ge(s["in"], 48)
                dt = rows[:, 0].rearrange("p (h a) -> p h a", a=1).broadcast_to([P, H3, NT])
                dve.tensor_tensor(z[:], ba[:, :, H3:2 * H3].rearrange("p t h -> p h t"), dt, ALU.add)
                dve.tensor_copy(coef[:, 0], ba[:, :, 0:H3].rearrange("p t h -> p h t"))
                dve.drain()
                dve.sem_inc(s["z"], 1)
                dve.wait_ge(s["log"], 1)
                dve.scalar_tensor_tensor(out=z[:], in0=z[:], scalar=0.0, in1=l[:], op0=ALU.max, op1=ALU.add)
                dve.drain()
                ea = rows[:, 1].rearrange("p (h a) -> p h a", a=1).broadcast_to([P, H3, NT])
                dve.scalar_tensor_tensor(out=coef[:, 1], in0=z[:], scalar=-1.0, in1=ea, op0=ALU.mult, op1=ALU.mult).then_inc(s["g"], 1)

            @block.tensor
            def _(pe):
                pe.wait_ge(s["in"], 48)
                pe.wait_ge(s["g"], 1)
                g = coef[:, 1].rearrange("p h t -> p (h t)")
                for i, m in enumerate((c.lower, masks, c.ones)):
                    last = pe.matmul(ps[:, i, 0:H3 * NT], m[:], g, start=True, stop=True)
                last.then_inc(s["sum"], 1)

            @block.scalar
            def _(act):
                act.wait_ge(s["z"], 1)
                act.activation(coef[:, 0], coef[:, 0], ACT.Sigmoid)
                act.activation(l[:], z[:], ACT.Abs)
                act.drain()
                act.activation(l[:], l[:], ACT.Exp, scale=-1.0)
                act.activation(rows[:, 1], rows[:, 1], ACT.Exp)
                act.drain()
                act.activation(l[:], l[:], ACT.Ln, bias=1.0).then_inc(s["log"], 1)
                act.wait_ge(s["sum"], 1)
                for i in range(3):
                    act.activation(coef[:, 2 + i].rearrange("p h t -> p (h t)"), ps[:, i, 0:H3 * NT], ACT.Exp)


def delta_project(c, name, head, w, coef, hc, qkvg, bgk, kT, qT, qgT):
    nc = c.nc
    with Stage(nc, name) as st:
        w_sb = st.sb("w", [P, KC, 4 * DK])
        sq = st.sb("sq", [P, 2, 4, 2 * DK])
        ss = st.sb("ss", [P, NT, 2])
        bg = st.sb("bg", [P, NT])
        ps = st.ps("ps", [P, 4, 512])
        tp = st.ps("tp", [P, 4, 512])
        s = {n: st.sem(n) for n in ("w_in", "proj", "silu", "ss", "sd", "k", "q", "hc", "turned", "copied", "qg")}
        with nc.Block() as block:
            @block.sync
            def _(sp):
                sp.dma_start(w_sb[:], w[bass.ds(head, 1)].rearrange("a (k p) m -> p (a k) m", p=P)).then_inc(s["w_in"], 16)
                sp.wait_ge(s["w_in"], 16)

            @block.gpsimd
            def _(pool):
                pool.wait_ge(s["silu"], NT)
                pool.wait_ge(s["hc"], 1)
                v = qkvg[:, :, 2 * DK:3 * DK]
                pool.tensor_tensor(v, v, hc[:, 0, :].rearrange("p (t a) -> p t a", a=1).broadcast_to([P, NT, DK]), ALU.mult)

            @block.tensor
            def _(pe):
                pe.wait_ge(s["w_in"], 16)
                for t in range(NT):
                    if t >= 4:
                        pe.wait_ge(s["silu"], t - 3)
                    for k in range(KC):
                        last = pe.matmul(ps[:, t % 4, :], c.xT[:, k, t * P:(t + 1) * P], w_sb[:, k, :], start=(k == 0), stop=(k == KC - 1))
                    last.then_inc(s["proj"], 1)
                for g in range(12):
                    kind = g // 4
                    if g % 4 == 0:
                        pe.wait_ge((s["k"], s["q"], s["qg"])[kind], 1)
                    if g >= 4:
                        pe.wait_ge(s["copied"], g - 3)
                    a = (DK, 0, 0)[kind]
                    for m in range(4):
                        last = pe.transpose(tp[:, g % 4, m * P:(m + 1) * P], qkvg[:, 4 * (g % 4) + m, a:a + DK], c.ident[:])
                    last.then_inc(s["turned"], 1)

            @block.scalar
            def _(act):
                for t in range(NT):
                    act.wait_ge(s["proj"], t + 1)
                    act.activation(qkvg[:, t, :], ps[:, t % 4, :], ACT.Silu).then_inc(s["silu"], 1)
                act.wait_ge(s["ss"], 1)
                act.activation(ss[:], ss[:], ACT.Sqrt).then_inc(s["sd"], 1)
                for g in range(12):
                    act.wait_ge(s["turned"], g + 1)
                    dst = (kT, qT, qgT)[g // 4]
                    act.activation(dst[:, 4 * (g % 4):4 * (g % 4) + 4, :].rearrange("p t d -> p (t d)"), tp[:, g % 4, :],
                                   ACT.Copy).then_inc(s["copied"], 1)

            @block.vector
            def _(dve):
                dve.tensor_copy(hc[:], coef[:, :, bass.ds(head, 1), :].rearrange("p c a t -> p c (a t)"))
                dve.drain()
                dve.sem_inc(s["hc"], 1)
                dve.tensor_tensor(bg[:], hc[:, 0, :], hc[:, 2, :], ALU.mult)
                for g in range(4):
                    dve.wait_ge(s["silu"], 4 * (g + 1))
                    qk = qkvg[:, 4 * g:4 * g + 4, 0:2 * DK]
                    dve.tensor_tensor(sq[:, g % 2], qk, qk, ALU.mult)
                    dve.drain()
                    dve.tensor_reduce(ss[:, 4 * g:4 * g + 4, :], sq[:, g % 2].rearrange("p t (w d) -> p t w d", w=2), AX.X, ALU.add)
                dve.drain()
                dve.tensor_scalar(ss[:], ss[:], 1e-6, None, ALU.add).then_inc(s["ss"], 1)
                dve.wait_ge(s["sd"], 1)
                dve.reciprocal(ss[:], ss[:])
                dve.drain()
                dve.tensor_scalar(ss[:, :, 0:1], ss[:, :, 0:1], DK ** -0.5, None, ALU.mult)
                q, k = qkvg[:, :, 0:DK], qkvg[:, :, DK:2 * DK]
                full = [P, NT, DK]

                def col(v):
                    return v.rearrange("p (t a) -> p t a", a=1).broadcast_to(full)
                dve.tensor_tensor(k, k, ss[:, :, 1:2].broadcast_to(full), ALU.mult).then_inc(s["k"], 1)
                dve.drain()
                dve.tensor_tensor(q, q, ss[:, :, 0:1].broadcast_to(full), ALU.mult).then_inc(s["q"], 1)
                dve.tensor_tensor(bgk[:], k, col(bg[:]), ALU.mult)
                dve.drain()
                dve.wait_ge(s["turned"], 4)
                dve.tensor_tensor(k, k, col(hc[:, 3, :]), ALU.mult)
                dve.wait_ge(s["turned"], 8)
                dve.tensor_tensor(q, q, col(hc[:, 2, :]), ALU.mult).then_inc(s["qg"], 1)


def delta_invert(c, name, masks, hc, qkvg, bgk, kT, qT, U, WT, PT):
    nc = c.nc
    STEPS = 13
    with Stage(nc, name) as st:
        def four(n):
            return st.sb(n, [P, 2, 4, P])
        gs, bs, Dm, DT, L, LT, n1, n1T, n2, n2T, T, TT, X, Lm = (four(n) for n in (
            "gs", "bs", "D", "DT", "L", "LT", "n1", "n1T", "n2", "n2T", "T", "TT", "X", "Lm"))
        ps = st.ps("ps", [P, 2, 3, 512])
        s = {n: st.sem(n) for n in ("gs", "mm", "act", "dve", "lm")}

        def wide(m, g):
            return m[:, g].rearrange("p t d -> p (t d)")

        def mask(m):
            return masks[:, m:m + 1, :].broadcast_to([P, 4, P])

        A = [1, 2, 1, 1, 1, 0, 1, 0, 0, 0, 0, 0, 1]

        def done(r, n, g, per=None):
            if per is None:
                return 2 * STEPS * r + 2 * n + g + 1
            return 2 * sum(per) * r + 2 * sum(per[:n]) + per[n] * (g + 1)

        with nc.Block() as block:
            @block.tensor
            def _(pe):
                for r in range(2):
                    for n in range(STEPS):
                        for g in range(2):
                            t0 = (2 * r + g) * 4
                            if n == 0:
                                pe.wait_ge(s["gs"], 2 * r + g + 1)
                                if r == 1:
                                    pe.wait_ge(s["dve"], done(0, STEPS - 1, g))
                                    pe.wait_ge(s["act"], done(0, STEPS - 1, g, A))
                            else:
                                pe.wait_ge(s["dve"], done(r, n - 1, g))
                                pe.wait_ge(s["act"], done(r, n - 1, g, A))

                            def mm(bank, lhs, rhs):
                                for m in range(4):
                                    q = pe.matmul(ps[:, g, bank, m * P:(m + 1) * P], lhs(m), rhs(m), start=True, stop=True)
                                return q

                            def turn(bank, src):
                                for m in range(4):
                                    q = pe.transpose(ps[:, g, bank, m * P:(m + 1) * P], src[:, g, m, :], c.ident[:])
                                return q

                            def of(b):
                                return lambda m: b[:, g, m, :]

                            def tok(b):
                                return lambda m: b[:, t0 + m, :]
                            if n == 0:
                                pe.matmul(ps[:, g, 0, :], c.lower[:], wide(gs, g), start=True, stop=True)
                                last = mm(1, tok(kT), tok(kT))
                            elif n == 1:
                                turn(0, L)
                                last = turn(1, Dm)
                            elif n == 2:
                                mm(0, of(n1T), of(n1))
                                mm(1, of(n1), of(n1T))
                                last = mm(2, tok(kT), tok(qT))
                            elif n == 3:
                                mm(0, of(n2T), of(n2))
                                mm(1, of(n2), of(n2T))
                                last = mm(2, of(n2T), of(T))
                            elif n == 4:
                                mm(0, of(n1), of(n1T))
                                last = mm(2, of(n1T), of(T))
                            elif n == 5:
                                last = mm(2, of(n2T), of(T))
                            elif n in (6, 8, 10):
                                if n == 6:
                                    turn(0, T)
                                pe.wait_ge(s["lm"], 6 * r + (n - 6) + g + 1)
                                last = mm(1, of(Lm), of(T))
                            elif n in (7, 9):
                                mm(0, of(TT), of(X))
                                last = mm(1, of(X), of(TT))
                            elif n == 11:
                                last = mm(1, of(X), of(TT))
                            else:
                                mm(0, of(TT), lambda m: qkvg[:, t0 + m, 2 * DK:3 * DK])
                                last = mm(1, tok(bgk), of(TT))
                            last.then_inc(s["mm"], 1)

            @block.scalar
            def _(act):
                for r in range(2):
                    for n in range(STEPS):
                        for g in range(2):
                            t0 = (2 * r + g) * 4
                            copies = {1: [(LT, 0), (DT, 1)], 2: [(n2, 0)], 3: [(n1, 0)], 4: [(n2T, 0)], 6: [(TT, 0)]}
                            if not A[n]:
                                continue
                            act.wait_ge(s["mm"], done(r, n, g))
                            if n == 0:
                                act.activation(wide(Dm, g), ps[:, g, 0, :], ACT.Exp).then_inc(s["act"], 1)
                            elif n == STEPS - 1:
                                act.activation(U[:, t0:t0 + 4, :].rearrange("p t d -> p (t d)"), ps[:, g, 0, :],
                                               ACT.Copy).then_inc(s["act"], 1)
                            else:
                                for dst, bank in copies[n]:
                                    act.activation(wide(dst, g), ps[:, g, bank, :], ACT.Copy).then_inc(s["act"], 1)

            @block.gpsimd
            def _(pool):
                for r in range(2):
                    for n in (6, 8, 10):
                        for g in range(2):
                            if n == 6:
                                pool.wait_ge(s["act"], done(r, 1, g, A))
                                if r == 1:
                                    pool.wait_ge(s["mm"], done(0, 10, g))
                            else:
                                pool.wait_ge(s["mm"], done(r, n - 2, g))
                            pool.tensor_tensor(Lm[:, g], LT[:, g], mask((M_J16, M_J32, M_J64)[(n - 6) // 2]), ALU.mult).then_inc(s["lm"], 1)

            @block.vector
            def _(dve):
                def col(v):
                    return v.rearrange("p (t a) -> p t a", a=1).broadcast_to([P, 4, P])

                for r in range(2):
                    for g in range(2):
                        t0 = (2 * r + g) * 4
                        dve.tensor_tensor(gs[:, g], mask(M_STRICT), col(hc[:, 1, t0:t0 + 4]), ALU.mult).then_inc(s["gs"], 1)
                        dve.tensor_tensor(bs[:, g], mask(M_STRICT), col(hc[:, 0, t0:t0 + 4]), ALU.mult)
                    dve.drain()
                    for n in range(STEPS):
                        for g in range(2):
                            t0 = (2 * r + g) * 4

                            def bank(i):
                                return ps[:, g, i, :].rearrange("p (t d) -> p t d", t=4)
                            dve.wait_ge(s["mm"], done(r, n, g))
                            if n == 0:
                                dve.wait_ge(s["act"], done(r, 0, g, A))
                                dve.tensor_tensor(Dm[:, g], Dm[:, g], mask(M_INCL), ALU.mult)
                                dve.tensor_tensor(L[:, g], bank(1), bs[:, g], ALU.mult)
                                dve.drain()
                                last = dve.tensor_tensor(L[:, g], L[:, g], Dm[:, g], ALU.mult)
                            elif n == 1:
                                dve.wait_ge(s["act"], done(r, 1, g, A))
                                dve.scalar_tensor_tensor(out=n1[:, g], in0=L[:, g], scalar=-1.0, in1=mask(M_BLOCK), op0=ALU.mult, op1=ALU.mult)
                                dve.scalar_tensor_tensor(out=n1T[:, g], in0=LT[:, g], scalar=-1.0, in1=mask(M_BLOCK), op0=ALU.mult, op1=ALU.mult)
                                dve.drain()
                                idb = c.ident[:].rearrange("p (a n) -> p a n", a=1).broadcast_to([P, 4, P])
                                last = dve.tensor_tensor(T[:, g], n1[:, g], idb, ALU.add)
                            elif n == 2:
                                dve.tensor_tensor(PT[:, t0:t0 + 4, :], bank(2), DT[:, g], ALU.mult)
                                last = dve.tensor_copy(n2T[:, g], bank(1))
                            elif n == 3:
                                dve.tensor_copy(n1T[:, g], bank(1))
                                last = dve.tensor_tensor(T[:, g], T[:, g], bank(2), ALU.add)
                            elif n in (4, 5):
                                last = dve.tensor_tensor(T[:, g], T[:, g], bank(2), ALU.add)
                            elif n in (6, 8, 10):
                                last = dve.tensor_copy(X[:, g], bank(1))
                            elif n in (7, 9):
                                dve.tensor_tensor(T[:, g], T[:, g], bank(0), ALU.subtract)
                                last = dve.tensor_tensor(TT[:, g], TT[:, g], bank(1), ALU.subtract)
                            elif n == 11:
                                last = dve.tensor_tensor(TT[:, g], TT[:, g], bank(1), ALU.subtract)
                            else:
                                last = dve.tensor_copy(WT[:, t0:t0 + 4, :], bank(1))
                            dve.drain()
                            dve.sem_inc(s["dve"], 1)


def delta_scan(c, name, hc, qkvg, qgT, U, WT, PT, o):
    nc = c.nc
    with Stage(nc, name) as st:
        Sst = st.sb("S", [P, B, DK])
        dl = st.sb("dl", [P, 2, B, DK])
        ws = st.ps("ws", [P, 512])
        op = st.ps("op", [P, 2, 512])
        sp_ = st.ps("sp", [P, 512])
        s = {n: st.sem(n) for n in ("S", "ws", "dl", "o", "o_out")}
        U4, o4 = (m[:].rearrange("p (b t) d -> p b t d", b=B) for m in (U, o))
        with nc.Block() as block:
            @block.tensor
            def _(pe):
                for n in range(ST):
                    pe.wait_ge(s["S"], n + 1)
                    for b in range(B):
                        last = pe.matmul(ws[:, b * DK:(b + 1) * DK], WT[:, b * ST + n, :], Sst[:, b, :], start=True, stop=True)
                    last.then_inc(s["ws"], 1)
                    pe.wait_ge(s["dl"], n + 1)
                    if n >= 2:
                        pe.wait_ge(s["o_out"], n - 1)
                    for b in range(B):
                        t = b * ST + n
                        dst = op[:, n % 2, b * DK:(b + 1) * DK]
                        pe.matmul(dst, qgT[:, t, :], Sst[:, b, :], start=True, stop=False)
                        pe.matmul(dst, PT[:, t, :], dl[:, n % 2, b, :], start=False, stop=True)
                        last = pe.matmul(sp_[:, b * DK:(b + 1) * DK], qkvg[:, t, DK:2 * DK], dl[:, n % 2, b, :], start=True, stop=True)
                    last.then_inc(s["o"], 1)

            @block.scalar
            def _(act):
                for n in range(ST):
                    act.wait_ge(s["o"], n + 1)
                    act.activation(o4[:, :, n, :], op[:, n % 2, 0:B * DK].rearrange("p (b d) -> p b d", b=B), ACT.Copy).then_inc(s["o_out"], 1)

            @block.vector
            def _(dve):
                dve.memset(Sst[:], 0.0).then_inc(s["S"], 1)
                for n in range(ST):
                    dve.wait_ge(s["ws"], n + 1)
                    dve.tensor_tensor(dl[:, n % 2], U4[:, :, n, :], ws[:, 0:B * DK].rearrange("p (b d) -> p b d", b=B), ALU.subtract).then_inc(s["dl"], 1)
                    dve.wait_ge(s["o"], n + 1)
                    for b in range(B):
                        t = b * ST + n
                        dve.scalar_tensor_tensor(out=Sst[:, b, :], in0=Sst[:, b, :], scalar=hc[:, 4, t:t + 1], in1=sp_[:, b * DK:(b + 1) * DK],
                                                 op0=ALU.mult, op1=ALU.add)
                    dve.drain()
                    dve.sem_inc(s["S"], 1)


def delta_output(c, name, head, w_o, norm_w, qkvg, o, xi):
    nc = c.nc
    with Stage(nc, name) as st:
        w_sb = st.sb("w", [P, D])
        nw = st.sb("nw", [P, DK])
        sq = st.sb("sq", [P, NT, DK])
        ss = st.sb("ss", [P, NT])
        tp = st.ps("tp", [P, 4, 512])
        ps = st.ps("ps", [P, 4, 512])
        s = {n: st.sem(n) for n in ("w_in", "ss", "sd", "gate", "o", "turned", "oT", "mult", "added")}
        full = [P, NT, DK]
        with nc.Block() as block:
            @block.sync
            def _(sp):
                sp.dma_start(w_sb[:], w_o[bass.ds(head, 1)].rearrange("a p m -> p (a m)")).then_inc(s["w_in"], 16)
                sp.dma_start(nw[:], row_bcast(norm_w, DK)).then_inc(s["w_in"], 16)
                sp.wait_ge(s["w_in"], 32)

            @block.gpsimd
            def _(pool):
                pool.wait_ge(s["w_in"], 32)
                gate = qkvg[:, :, 3 * DK:4 * DK]
                pool.tensor_tensor(gate, gate, nw[:].rearrange("p (a d) -> p a d", a=1).broadcast_to(full), ALU.mult).then_inc(s["gate"], 1)

            @block.vector
            def _(dve):
                dve.tensor_tensor(sq[:], o[:], o[:], ALU.mult)
                dve.drain()
                dve.tensor_reduce(ss[:], sq[:], AX.X, ALU.add)
                dve.drain()
                dve.tensor_scalar(ss[:], ss[:], 1.0 / DK, 1e-6, ALU.mult, ALU.add).then_inc(s["ss"], 1)
                dve.wait_ge(s["sd"], 1)
                dve.reciprocal(ss[:], ss[:])
                dve.drain()
                dve.tensor_tensor(o[:], o[:], ss[:].rearrange("p (t a) -> p t a", a=1).broadcast_to(full), ALU.mult)
                dve.drain()
                dve.wait_ge(s["gate"], 1)
                dve.tensor_tensor(o[:], o[:], qkvg[:, :, 3 * DK:4 * DK], ALU.mult).then_inc(s["o"], 1)
                for g in range(NT // 2):
                    dve.wait_ge(s["mult"], g + 1)
                    x2 = xi[:, 2 * g:2 * g + 2, :]
                    dve.tensor_tensor(x2, x2, ps[:, g % 4, :].rearrange("p (t d) -> p t d", t=2), ALU.add).then_inc(s["added"], 1)

            @block.scalar
            def _(act):
                act.wait_ge(s["ss"], 1)
                act.activation(ss[:], ss[:], ACT.Sqrt).then_inc(s["sd"], 1)
                for g in range(4):
                    act.wait_ge(s["turned"], g + 1)
                    act.activation(sq[:, 4 * g:4 * g + 4, :].rearrange("p t d -> p (t d)"), tp[:, g, :], ACT.Copy).then_inc(s["oT"], 1)

            @block.tensor
            def _(pe):
                pe.wait_ge(s["o"], 1)
                for g in range(4):
                    for m in range(4):
                        last = pe.transpose(tp[:, g, m * P:(m + 1) * P], o[:, 4 * g + m, :], c.ident[:])
                    last.then_inc(s["turned"], 1)
                pe.wait_ge(s["w_in"], 32)
                for g in range(NT // 2):
                    pe.wait_ge(s["oT"], g // 2 + 1)
                    if g >= 4:
                        pe.wait_ge(s["added"], g - 3)
                    for m in range(2):
                        last = pe.matmul(ps[:, g % 4, m * D:(m + 1) * D], sq[:, 2 * g + m, :], w_sb[:], start=True, stop=True)
                    last.then_inc(s["mult"], 1)


def mix_heads(c, name, main, aux, gate_row):
    nc = c.nc
    with Stage(nc, name) as st:
        g = st.sb("g", [P, 2, D])
        g_in, g_ready = st.sem("g_in"), st.sem("g_ready")
        with nc.Block() as block:
            @block.sync
            def _(sp):
                sp.dma_start(g[:, 0], row_bcast(gate_row, D)).then_inc(g_in, 16)
                sp.wait_ge(g_in, 16)

            @block.scalar
            def _(act):
                act.wait_ge(g_in, 16)
                act.activation(g[:, 0], g[:, 0], ACT.Sigmoid).then_inc(g_ready, 1)

            @block.vector
            def _(dve):
                dve.wait_ge(g_ready, 1)
                dve.tensor_scalar(g[:, 1], g[:, 0], -1.0, 1.0, ALU.mult, ALU.add)
                dve.drain()
                dve.tensor_tensor(aux[:], aux[:], g[:, 0:1].broadcast_to([P, NT, D]), ALU.mult)
                dve.tensor_tensor(main[:], main[:], g[:, 1:2].broadcast_to([P, NT, D]), ALU.mult)
                dve.drain()
                dve.tensor_tensor(main[:], main[:], aux[:], ALU.add)


def fill(c, name, dst, value):
    with Stage(c.nc, name) as st:
        with c.nc.Block() as block:
            @block.vector
            def _(dve):
                dve.memset(dst, value)


def rope_table(lanes):
    inv = (np.float32(10000.0) ** (-(np.arange(DH // 2, dtype=np.float32) * np.float32(2.0) / np.float32(DH)))).astype(np.float32)
    ang = np.arange(S, dtype=np.float32)[:, None] * inv[None, :]
    co, si = np.cos(ang), np.sin(ang)
    out = np.zeros((2, P, S), np.float32)
    out[0] = 1.0
    for p, j in enumerate(lanes):
        if j >= 0:
            out[0, p] = co[:, j // 2]
            out[1, p] = si[:, j // 2] * (1.0 if j % 2 else -1.0)
    return out


def head_blocks(w):
    out = np.zeros((KC, P, P), np.float32)
    n = P // DH
    for h in range(H):
        a = (h % n) * DH
        out[h // n, a:a + DH, a:a + DH] = w[h].T
    return out


def spread_gather():
    spread = np.zeros((DH, P, P), np.float32)
    for d in range(DH):
        for m in range(P):
            spread[d, m // DH * DH + d, m] = 1.0
    return spread.transpose(1, 0, 2), spread.transpose(2, 0, 1)


def chunk_masks():
    i, j = np.arange(P)[:, None], np.arange(P)[None, :]
    m = [j <= i, j < i, i // 16 == j // 16]
    for w in (16, 32, 64):
        m.append((i // w % 2 == 0) & (j // w == i // w + 1))
    return np.stack(m, 1).astype(np.float32)


def rotation_table():
    ang = np.outer(np.arange(S, dtype=np.float32), np.arange(D // 2, dtype=np.float32))[::-1]
    co, si = np.repeat(np.cos(ang), 2, 1).T, np.repeat(np.sin(ang), 2, 1).T.copy()
    si[1::2] *= -1.0
    return np.stack([co, si]).reshape(2, KC, P, S).astype(np.float32)


SLOT_LANES = [p % SLOT if p % SLOT < DH else -1 for p in range(P)]


def slotted(w):
    out = np.zeros((NC4, P, KC, P), np.float32)
    a = np.asarray(w).reshape(KC, P, NC4, HC, DH).transpose(2, 1, 0, 3, 4)
    out.reshape(NC4, P, KC, HC, SLOT)[..., 0:DH] = a
    return out


def slotted_bias(b, extra):
    out = np.zeros((NC4, HC, SLOT), np.float32)
    if b is not None:
        out[:, :, 0:DH] = np.asarray(b).reshape(NC4, HC, DH)
    out[:, :, DH] = extra
    return out.reshape(NC4, P)


def chunked_v(w):
    return np.ascontiguousarray(np.asarray(w).reshape(KC, P, NC4, HC * DH).transpose(2, 1, 0, 3))


def swap_pairs(w):
    w = np.asarray(w)
    return w.reshape(*w.shape[:-1], -1, 2)[..., ::-1].reshape(w.shape)


def as_cols(b):
    return np.asarray(b).reshape(-1, P).T


def lay_out(i):
    a = {"x": i["x"], "ctxT": i["ctx_1024"].reshape(B * S2, D).T, "mask2T": i["mask_BxS2_ik0"].T}
    qT, kT = i["L0_attn_w_q"].T, i["L0_attn_w_k"].T
    a["l0a_wqk"] = np.stack([slotted(qT), slotted(kT), slotted(swap_pairs(qT)), slotted(swap_pairs(kT))], 2)
    a["l0a_b"] = np.stack([slotted_bias(None, 0.0), slotted_bias(None, 1.0)], 2)
    a["l0a_wv"] = chunked_v(i["L0_attn_w_v"].T)
    a["l0a_wo"] = i["L0_attn_w_o"].T
    a["rope_slots"] = rope_table(SLOT_LANES)
    for n in ("Ws", "W", "bcw", "bcb"):
        a["l0x_" + n] = i["L0_xattn_" + n]
    a["l0x_w"] = as_cols(i["L0_xattn_w"])
    a["l0x_b"] = as_cols(i["L0_xattn_b"])
    a["l0x_wcw"] = np.broadcast_to(i["L0_xattn_Wcw"].T, (D, P))
    a["l0x_wcb"] = np.broadcast_to(i["L0_xattn_Wcb"].T, (D, P))
    for n in ("Wr", "W1", "W2", "b2"):
        a["l0f_" + n] = i["L0_ffn_" + n]
    a["l0f_br"] = i["L0_ffn_br"].reshape(E, 1)
    a["l0f_b1"] = i["L0_ffn_b1"].reshape(E, -1, P).transpose(0, 2, 1)
    for n in "kqvp":
        a["l1a_W" + n] = i["L1_attn_W" + n]
    for n in "kq":
        a["l1a_W" + n + "s"] = swap_pairs(i["L1_attn_W" + n])
        a["l1a_b" + n] = as_cols(i["L1_attn_b" + n])
        a["l1a_b" + n + "s"] = as_cols(swap_pairs(i["L1_attn_b" + n]))
    a["l1a_bv"], a["l1a_bp"] = i["L1_attn_bv"], i["L1_attn_bp"]
    a["l1a_cs"] = rotation_table()
    for n in ("Wq", "Wk", "Wv", "Wcq", "Wck", "Wcv", "gamma", "beta", "W1", "b1"):
        a["l1x_" + n] = i["L1_xattn_" + n]
    a["l1f_w1"], a["l1f_w2"] = i["L1_ffn_w1"].T, i["L1_ffn_w2"].T
    a["l1f_b1"], a["l1f_b2"] = i["L1_ffn_b1"], i["L1_ffn_b2"]
    for n in "qkvg":
        a["l2a_w" + n] = i["L2_attn_" + n + "_w"].T
    a["l2a_wqs"], a["l2a_wks"] = swap_pairs(a["l2a_wq"]), swap_pairs(a["l2a_wk"])
    a["l2a_bg"] = as_cols(i["L2_attn_g_b"])
    a["rope_heads"] = rope_table([p % DH for p in range(P)])
    a["l2a_Wq"], a["l2a_Wk"] = head_blocks(i["L2_attn_Wq"]), head_blocks(i["L2_attn_Wk"])
    a["l2a_decay"] = as_cols(i["L2_attn_base_decay_logits"])
    a["spread"], a["gather"] = spread_gather()
    a["l2a_wo"] = i["L2_attn_out_w"].T
    for n in ("out_b", "ln_g", "ln_b"):
        a["l2a_" + n] = i["L2_attn_" + n]
    a["head_mask"] = (np.arange(P)[:, None] // DH == np.arange(P // DH)[None, :]).astype(np.float32)
    a["l2x_wq"], a["l2x_bq"], a["l2x_wo"], a["l2x_bo"] = i["L2_xattn_Wq"], as_cols(i["L2_xattn_bq"]), i["L2_xattn_Wo"], i["L2_xattn_bo"]
    a["l2x_wk"], a["l2x_bk"] = np.tile(i["L2_xattn_Wk"], (1, H)), as_cols(np.tile(i["L2_xattn_bk"], H))
    a["l2x_wv"], a["l2x_bv"] = np.tile(i["L2_xattn_Wv"], (1, H)), np.tile(i["L2_xattn_bv"], H)
    a["l2f_wi"], a["l2f_bi"] = i["L2_ffn_W_in"].T, i["L2_ffn_b_in"]
    width = i["L2_ffn_W_out"].shape[1]
    a["l2f_wo"] = np.pad(i["L2_ffn_W_out"].T, ((0, -width % P), (0, 0)))
    per_head = [i["L3_attn_W" + n].reshape(D, H3, DK) for n in "qkvg"]
    a["l3a_w"] = np.concatenate(per_head, 2).transpose(1, 0, 2)
    a["l3a_wba"] = np.concatenate([i["L3_attn_Wb"], i["L3_attn_Wa"]], 1)
    a["l3a_alog"], a["l3a_dt"] = i["L3_attn_A_log"], i["L3_attn_dt_bias"]
    a["l3a_nw"] = i["L3_attn_o_norm_w"]
    a["l3a_wo"] = i["L3_attn_Wo"].reshape(H3, DK, D)
    a["l3a_fc"] = i["L3_attn_W_fc"].reshape(D, 2, -1).transpose(1, 0, 2)
    a["l3a_pr"] = i["L3_attn_W_proj"].reshape(2, -1, D)
    a["masks"] = chunk_masks()
    wq, wk, wv = np.split(i["L3_xattn_Wqkv"], 3, 1)
    bq, bk, bv = np.split(i["L3_xattn_bqkv"], 3)
    a["l3x_wqk"] = np.stack([slotted(wq), slotted(wk)], 2)
    a["l3x_b"] = np.stack([slotted_bias(bq, 0.0), slotted_bias(bk, 1.0)], 2)
    a["l3x_wv"] = chunked_v(wv)
    a["l3x_bv"] = np.broadcast_to(bv.reshape(NC4, 1, HC * DH), (NC4, P, HC * DH))
    a["l3x_q"], a["l3x_bq"] = wq, as_cols(bq)
    _, a["l3x_ka"], a["l3x_va"] = np.split(i["L3_xattn_Wqkv_aux"], 3, 1)
    _, bka, a["l3x_bva"] = np.split(i["L3_xattn_bqkv_aux"], 3)
    a["l3x_bka"] = as_cols(bka)
    a["l3x_g"] = np.repeat(i["L3_xattn_g"], DH)
    a["l3x_wo"], a["l3x_bo"] = i["L3_xattn_Wo"], i["L3_xattn_bo"]
    a["l3f_r"] = i["L3_ffn_router_w"].T
    a["l3f_g"] = np.concatenate([i["L3_ffn_rg"], i["L3_ffn_sg"].reshape(D, 2, -1).transpose(1, 0, 2)])
    a["l3f_u"] = np.concatenate([i["L3_ffn_ru"], i["L3_ffn_su"].reshape(D, 2, -1).transpose(1, 0, 2)])
    a["l3f_d"] = np.concatenate([i["L3_ffn_rd"], i["L3_ffn_sd"].reshape(2, -1, D)])
    return a


def l0_attn(c):
    nc, d = c.nc, c.dram
    norm_transpose(c, "l0a_ln", c.x, dst_T=c.xT)
    with nc.sbuf_tensor("l0a_ao", [P, NT, D], F32) as ao:
        self_attention(c, "l0a", d["l0a_wqk"], d["l0a_wv"], ao, True, d["rope_slots"], d["l0a_b"])
        project_add(c, "l0a_o", ao, d["l0a_wo"])


def l0_xattn(c):
    nc, d = c.nc, c.dram
    with nc.sbuf_tensor("l0x_feat", [P, NT, D], F32) as feat, nc.sbuf_tensor("l0x_feT", [P, KC, N], F32) as feT, \
            nc.sbuf_tensor("l0x_txb", [P, KC, B * S2], F32) as txb, nc.sbuf_tensor("l0x_sw", [P, B, S2], F32) as sw, \
            nc.sbuf_tensor("l0x_sb", [P, B, S2], F32) as sbr:
        norm_transpose(c, "l0x_ln", c.x, dst_tok=feat, dst_T=c.xT)
        linear_T(c, "l0x_f", c.xT, [(d["l0x_W"], feT, None, None)])
        linear_T(c, "l0x_t", c.ctxT, [(d["l0x_Ws"], txb, d["l0x_b"], None)], width=B * S2)
        ctx_rows(c, "l0x_s", [d["l0x_wcw"], d["l0x_wcb"]], [sw, sbr])
        additive_attention(c, "l0x", feat, feT, txb, sw, sbr)


def l0_ffn(c):
    nc, d = c.nc, c.dram
    norm_transpose(c, "l0f_ln", c.x, dst_T=c.xT)
    with nc.sbuf_tensor("l0f_wgt", [P, NT, E], F32) as wgt:
        route(c, "l0f_r", c.xT, d["l0f_Wr"], wgt, bias=d["l0f_br"])
        experts(c, "l0f_e", c.xT, wgt, E, 512, d["l0f_W1"], d["l0f_W2"], b1=d["l0f_b1"])
        add_expert_bias(c, "l0f_b", wgt, d["l0f_b2"])


def tile_ctx(c, names):
    ctx = ExitStack()
    return ctx, [ctx.enter_context(c.nc.sbuf_tensor(n, shape, dt)) for n, shape, dt in names]


def l1_attn(c):
    d = c.dram
    norm_transpose(c, "l1a_ln", c.x, dst_T=c.xT)
    ctx, (qT, kT, v) = tile_ctx(c, [("l1a_qT", [P, KC, N], F32), ("l1a_kT", [P, KC, N], F32), ("l1a_v", [P, NT, D], F32)])
    with ctx:
        rope_T(c, "l1a_qk", c.xT, [(d["l1a_Wq"], d["l1a_Wqs"], qT, d["l1a_bq"], d["l1a_bqs"]),
                                   (d["l1a_Wk"], d["l1a_Wks"], kT, d["l1a_bk"], d["l1a_bks"])], d["l1a_cs"], True)
        linear_tok(c, "l1a_vp", c.xT, d["l1a_Wv"], v, bias=d["l1a_bv"])
        with c.nc.sbuf_tensor("l1a_ao", [P, NT, D], F32) as ao:
            softplus_attention(c, "l1a", qT, kT, v, ao)
            project_add(c, "l1a_o", ao, d["l1a_Wp"], bias=d["l1a_bp"])


def l1_xattn(c):
    d = c.dram
    big = [P, NT, D]
    ctx, (hn, qT, kT, v, a) = tile_ctx(c, [("l1x_hn", big, F32), ("l1x_qT", [P, KC, N], F32), ("l1x_kT", [P, KC, N], F32),
                                           ("l1x_v", big, F32), ("l1x_a", big, F32)])
    gb = dict(eps=1e-3, gamma=d["l1x_gamma"], beta=d["l1x_beta"])
    with ctx:
        norm_transpose(c, "l1x_ln", c.x, dst_tok=hn, dst_T=c.xT)
        linear_T(c, "l1x_qk", c.xT, [(d["l1x_Wq"], qT, None, None), (d["l1x_Wk"], kT, None, None)])
        linear_tok(c, "l1x_vp", c.xT, d["l1x_Wv"], v)
        softmax_attention(c, "l1x_self", qT, kT, v, a, hn, True)
        norm_transpose(c, "l1x_ln1", a, dst_tok=hn, dst_T=c.xT, **gb)
        linear_T(c, "l1x_cq", c.xT, [(d["l1x_Wcq"], qT, None, None)])
        linear_T(c, "l1x_ck", c.ctxT, [(d["l1x_Wck"], kT, None, None)], width=B * S2)
        linear_tok(c, "l1x_cv", c.ctxT, d["l1x_Wcv"], v, tiles=B, rows=S2)
        softmax_attention(c, "l1x_cross", qT, kT, v, a, hn, False)
        norm_transpose(c, "l1x_ln2", a, dst_tok=hn, dst_T=c.xT, **gb)
        linear_tok(c, "l1x_f", c.xT, d["l1x_W1"], a, bias=d["l1x_b1"], resid=hn, relu=True)
        norm_transpose(c, "l1x_ln3", a, dst_tok=hn, **gb)
        add_to_x(c, "l1x_add", hn, relu=True)


def l1_ffn(c):
    d = c.dram
    F = d["l1f_b1"].shape[0]
    ctx, (r, w1q, w2q, s1, s2) = tile_ctx(c, [("l1f_r", [P, NT, D], F32), ("l1f_w1q", [P, KC, F], BF16),
                                              ("l1f_w2q", [P, F // P, D], BF16), ("l1f_s1", [P, 1], F32), ("l1f_s2", [P, 1], F32)])
    with ctx:
        norm_transpose(c, "l1f_ln", c.x, dst_tok=r)
        norm_transpose(c, "l1f_rms", r, dst_tok=r, rms=True)
        quantize_weights(c, "l1f_q1", d["l1f_w1"], w1q, s1)
        quantize_weights(c, "l1f_q2", d["l1f_w2"], w2q, s2)
        quantized_ffn(c, "l1f", r, w1q, s1, w2q, s2, d["l1f_b1"], d["l1f_b2"])


def l2_attn(c):
    d = c.dram
    big = [P, NT, D]
    bigT = [P, KC, N]
    ctx, (xn, qT, kT, vT, gT) = tile_ctx(c, [("l2a_xn", big, F32), ("l2a_qT", bigT, F32), ("l2a_kT", bigT, F32),
                                             ("l2a_vT", bigT, F32), ("l2a_gT", bigT, F32)])
    with ctx:
        norm_transpose(c, "l2a_ln", c.x, dst_tok=xn, dst_T=c.xT)
        rope_T(c, "l2a_qk", c.xT, [(d["l2a_wq"], d["l2a_wqs"], qT, None, None), (d["l2a_wk"], d["l2a_wks"], kT, None, None)],
               d["rope_heads"], False)
        linear_T(c, "l2a_vg", c.xT, [(d["l2a_wv"], vT, None, None), (d["l2a_wg"], gT, d["l2a_bg"], ACT.Sigmoid)])
        per_head_T(c, "l2a_h", qT, kT, gT, d["l2a_Wq"], d["l2a_Wk"], DH ** -0.5)
        recurrence(c, "l2a_r", qT, kT, vT, d["l2a_decay"], d["spread"], d["gather"])
        with c.nc.sbuf_tensor("l2a_a", big, F32) as a:
            linear_tok(c, "l2a_o", vT, d["l2a_wo"], a, bias=d["l2a_out_b"], resid=xn)
            norm_transpose(c, "l2a_ln1", a, dst_tok=xn, gamma=d["l2a_ln_g"], beta=d["l2a_ln_b"])
        add_to_x(c, "l2a_add", xn)


def l2_xattn(c):
    d = c.dram
    ctx, (qT, kT, v, ao) = tile_ctx(c, [("l2x_qT", [P, KC, N], F32), ("l2x_kT", [P, KC, B * S2], F32),
                                        ("l2x_v", [P, B, D], F32), ("l2x_ao", [P, NT, D], F32)])
    with ctx:
        norm_transpose(c, "l2x_ln", c.x, dst_T=c.xT)
        linear_T(c, "l2x_q", c.xT, [(d["l2x_wq"], qT, d["l2x_bq"], None)])
        linear_T(c, "l2x_k", c.ctxT, [(d["l2x_wk"], kT, d["l2x_bk"], None)], width=B * S2)
        linear_tok(c, "l2x_vp", c.ctxT, d["l2x_wv"], v, bias=d["l2x_bv"], tiles=B, rows=S2)
        cross_heads(c, "l2x", qT, kT, v, ao, clip=1e6 * DH ** 0.5)
        project_add(c, "l2x_o", ao, d["l2x_wo"], bias=d["l2x_bo"])


def l2_ffn(c):
    d = c.dram
    norm_transpose(c, "l2f_ln", c.x, dst_T=c.xT)
    tree_ffn(c, "l2f", c.xT, d["l2f_wi"], d["l2f_bi"], d["l2f_wo"])


def l3_attn(c):
    nc, d = c.nc, c.dram
    with nc.sbuf_tensor("l3a_xi", [P, NT, D], F32) as xi:
        norm_transpose(c, "l3a_ln", c.x, dst_tok=xi)
        norm_transpose(c, "l3a_rms", xi, dst_T=c.xT, eps=1e-6, rms=True)
        tiles = [P, NT, DK]
        ctx, (masks, coef, hc, qkvg, bgk, kT, qT, qgT, U, WT, PT) = tile_ctx(c, [
            ("l3a_masks", [P, 6, P], F32), ("l3a_coef", [P, 5, H3, NT], F32), ("l3a_hc", [P, 5, NT], F32),
            ("l3a_qkvg", [P, NT, 4 * DK], F32)] + [("l3a_" + n, tiles, F32) for n in ("bgk", "kT", "qT", "qgT", "U", "WT", "PT")])
        with ctx:
            with nc.sbuf_tensor("l3a_ba", [P, NT, 2 * H3], F32) as ba:
                linear_tok(c, "l3a_bap", c.xT, d["l3a_wba"], ba)
                delta_gates(c, "l3a_g", ba, d["l3a_dt"], d["l3a_alog"], coef)
            load(c, "l3a_m", masks, d["masks"])
            with nc.Fori(0, H3) as head:
                delta_project(c, "l3a_p", head, d["l3a_w"], coef, hc, qkvg, bgk, kT, qT, qgT)
                delta_invert(c, "l3a_i", masks, hc, qkvg, bgk, kT, qT, U, WT, PT)
                delta_scan(c, "l3a_s", hc, qkvg, qgT, U, WT, PT, qT)
                delta_output(c, "l3a_o", head, d["l3a_wo"], d["l3a_nw"], qkvg, qT, xi)
        norm_transpose(c, "l3a_ln2", xi, dst_T=c.xT, eps=1e-6, rms=True)
        add_to_x(c, "l3a_add", xi)
    with nc.sbuf_tensor("l3a_one", [P, NT, 2], F32) as one:
        fill(c, "l3a_f1", one[:], 1.0)
        experts(c, "l3a_mlp", c.xT, one, 2, d["l3a_fc"].shape[2], d["l3a_fc"], d["l3a_pr"], square=True)


def l3_xattn(c):
    nc, d = c.nc, c.dram
    norm_transpose(c, "l3x_ln", c.x, dst_T=c.xT)
    with nc.sbuf_tensor("l3x_ao", [P, NT, D], F32) as ao:
        self_attention(c, "l3x_s", d["l3x_wqk"], d["l3x_wv"], ao, False, None, d["l3x_b"], d["l3x_bv"])
        ctx, (qT, kT, v, aux) = tile_ctx(c, [("l3x_qT", [P, KC, N], F32), ("l3x_kT", [P, KC, B * S2], F32),
                                             ("l3x_v", [P, B, D], F32), ("l3x_aux", [P, NT, D], F32)])
        with ctx:
            linear_T(c, "l3x_qp", c.xT, [(d["l3x_q"], qT, d["l3x_bq"], None)])
            linear_T(c, "l3x_kp", c.ctxT, [(d["l3x_ka"], kT, d["l3x_bka"], None)], width=B * S2)
            linear_tok(c, "l3x_vp", c.ctxT, d["l3x_va"], v, bias=d["l3x_bva"], tiles=B, rows=S2)
            cross_heads(c, "l3x_c", qT, kT, v, aux)
            mix_heads(c, "l3x_m", ao, aux, d["l3x_g"])
        project_add(c, "l3x_o", ao, d["l3x_wo"], bias=d["l3x_bo"])


def l3_ffn(c):
    nc, d = c.nc, c.dram
    with nc.sbuf_tensor("l3f_wgt", [P, NT, E + 2], F32) as wgt:
        fill(c, "l3f_one", wgt[:, :, E:E + 2], 1.0)
        ctx, (feat, rT) = tile_ctx(c, [("l3f_feat", [P, NT, D], F32), ("l3f_rT", [P, KC, N], F32)])
        with ctx:
            norm_transpose(c, "l3f_ln", c.x, dst_tok=feat, dst_T=c.xT)
            norm_transpose(c, "l3f_rms", feat, dst_T=rT, eps=float(np.finfo(np.float32).eps), rms=True)
            route(c, "l3f_route", rT, d["l3f_r"], wgt, top=2)
        experts(c, "l3f_e", c.xT, wgt, E + 2, d["l3f_g"].shape[2], d["l3f_u"], d["l3f_d"], gate=d["l3f_g"])


SUBLAYERS = [l0_attn, l0_xattn, l0_ffn, l1_attn, l1_xattn, l1_ffn, l2_attn, l2_xattn, l2_ffn, l3_attn, l3_xattn, l3_ffn]


def store(c, out):
    with Stage(c.nc, "store") as st:
        stored = st.sem("stored")
        with c.nc.Block() as block:
            @block.sync
            def _(sp):
                sp.dma_start(out.rearrange("b (t p) d -> p (b t) d", p=P), c.x[:]).then_inc(stored, 16)
                sp.wait_ge(stored, 16)


def decoder_kernel(nc, dram, out, sublayers):
    with ExitStack() as ctx:
        c = Core(nc, ctx, dram)
        setup(c)
        for f in sublayers:
            f(c)
        store(c, out)


def build(nc, inputs, sublayers):
    arrays, dram = {}, {}
    for name, a in lay_out({k: np.asarray(v) for k, v in inputs.items()}).items():
        a = np.ascontiguousarray(a)
        arrays[f"in_{name}"] = a
        dram[name] = nc.dram_tensor(f"in_{name}", a.shape, mybir.dt.from_np(a.dtype), kind="ExternalInput").ap()
    out = nc.dram_tensor("out_x", (B, S, D), F32, kind="ExternalOutput").ap()
    decoder_kernel(nc, dram, out, sublayers)
    return arrays


def kernel(**inputs):
    import concourse.bacc as bacc
    from concourse.bass_utils import run_bass_kernel_spmd
    nc = bacc.Bacc("TRN2", target_bir_lowering=False, num_devices=1)
    arrays = build(nc, inputs, SUBLAYERS)
    r = run_bass_kernel_spmd(nc, [arrays], core_ids=[0])
    return r.results[0]["out_x"]
```

```python
from contextlib import ExitStack

import numpy as np
import concourse.bass as bass
from concourse import mybir

P = 128
B = 2
S = 1024
N = B * S
NT = N // P
ST = S // P
D = 256
KC = D // P
S2 = 77
H = 16
DH = D // H

F32 = mybir.dt.float32
BF16 = mybir.dt.bfloat16
I32 = mybir.dt.int32
ALU = mybir.AluOpType
ACT = mybir.ActivationFunctionType
AX = mybir.AxisListType


class Stage(ExitStack):

    def __init__(self, nc, name):
        super().__init__()
        self.nc, self.name, self.sems = nc, name, []

    def sb(self, name, shape, dt=F32):
        return self.enter_context(self.nc.sbuf_tensor(f"{self.name}_{name}", shape, dt))

    def ps(self, name, shape, dt=F32):
        return self.enter_context(self.nc.psum_tensor(f"{self.name}_{name}", shape, dt))

    def sem(self, name, primed=False):
        s = self.enter_context(self.nc.semaphore(f"{self.name}_{name}"))
        self.sems.append(s)
        if primed:
            self.nc.gpsimd.sem_inc(s, 1)
        return s

    def __exit__(self, *exc):
        if exc[0] is None:
            for s in self.sems:
                self.nc.gpsimd.sem_clear(s)
            self.nc.all_engine_barrier()
        return super().__exit__(*exc)


class Core:

    def __init__(self, nc, ctx, dram):
        def sb(name, shape, dt=F32):
            return ctx.enter_context(nc.sbuf_tensor(name, shape, dt))

        self.nc, self.dram = nc, dram
        self.x = sb("x_res", [P, NT, D])
        self.xT = sb("xT", [P, KC, N])
        self.ident = sb("ident", [P, P])
        self.lower = sb("lower", [P, P])
        self.ones = sb("ones", [P, P])
        self.ctxT = sb("ctxT", [P, KC, B * S2])


def setup(c):
    nc = c.nc
    with Stage(nc, "setup") as st:
        x_in, zeroed, done = st.sem("x_in"), st.sem("zeroed"), st.sem("done")
        with nc.Block() as block:
            @block.sync
            def _(sp):
                sp.dma_start(c.x[:], c.dram["x"].rearrange("b (t p) d -> p (b t) d", p=P)).then_inc(x_in, 16)
                sp.dma_start(c.ctxT[:], c.dram["ctxT"].rearrange("(k p) n -> p k n", p=P)).then_inc(x_in, 16)
                sp.wait_ge(x_in, 32)

            @block.gpsimd
            def _(pool):
                pool.memset(c.ident[:], 0.0).then_inc(zeroed, 1)
                pool.memset(c.ones[:], 1.0).then_inc(zeroed, 1)
                pool.wait_ge(zeroed, 2)
                pool.affine_select(out=c.ident[:], in_=c.ident[:], compare_op=ALU.not_equal, fill=1.0,
                                   base=0, pattern=[[-1, P]], channel_multiplier=1).then_inc(done, 1)
                pool.affine_select(out=c.lower[:], in_=c.ones[:], compare_op=ALU.is_ge, fill=0.0,
                                   base=0, pattern=[[1, P]], channel_multiplier=-1).then_inc(done, 1)
                pool.wait_ge(done, 2)


def norm_transpose(c, name, src, dst_tok=None, dst_T=None, eps=1e-5, gamma=None, beta=None, post=None, rms=False):
    nc = c.nc
    with Stage(nc, name) as st:
        stats = st.sb("stats", [P, NT, 6])
        mv = st.sb("mv", [P, NT, 2])
        std = st.sb("std", [P, NT])
        rstd = st.sb("rstd", [P, NT])
        shift = st.sb("shift", [P, NT])
        row = st.sb("row", [P, 2, D])
        gb = st.sb("gb", [P, 2, D])
        tp = st.ps("tp", [P, 2, 512])
        affine_in = st.sem("affine_in")
        var_ready, std_ready = st.sem("var_ready"), st.sem("std_ready")
        rows_ready, tok_ready, turned, free_row = st.sem("rows"), st.sem("tok"), st.sem("turned"), st.sem("free_row")
        free_tp = st.sem("free_tp")
        affine = gamma is not None
        with nc.Block() as block:
            @block.sync
            def _(sp):
                if affine:
                    for i, v in enumerate((gamma, beta)):
                        sp.dma_start(gb[:, i, :], v.rearrange("(a n) -> a n", a=1).broadcast_to([P, D])).then_inc(affine_in, 16)
                    sp.wait_ge(affine_in, 32)

            @block.vector
            def _(dve):
                dve.sem_inc(free_row, 2)
                with dve.Fori(0, NT) as t:
                    dve.bn_stats(stats[:, bass.ds(t, 1), :], src[:, bass.ds(t, 1), :])
                dve.drain()
                for t in range(NT):
                    dve.bn_aggr(mv[:, t, :], stats[:, t, :])
                dve.drain()
                if rms:
                    dve.tensor_tensor(shift[:], mv[:, :, 0], mv[:, :, 0], ALU.mult)
                    dve.drain()
                    dve.tensor_tensor(mv[:, :, 1], mv[:, :, 1], shift[:], ALU.add)
                    dve.drain()
                dve.tensor_scalar(std[:], mv[:, :, 1], eps, None, ALU.add).then_inc(var_ready, 1)
                dve.wait_ge(std_ready, 1)
                dve.reciprocal(rstd[:], std[:])
                dve.drain()
                dve.scalar_tensor_tensor(out=shift[:], in0=mv[:, :, 0], scalar=0.0 if rms else -1.0, in1=rstd[:],
                                         op0=ALU.mult, op1=ALU.mult)
                dve.drain()
                with dve.Fori(0, NT // 2) as i:
                    for j in range(2):
                        t = i * 2 + j
                        dve.wait_ge(free_row, t + 1)
                        dve.tensor_scalar(row[:, j:j + 1, :], src[:, bass.ds(t, 1), :], rstd[:, bass.ds(t, 1)],
                                          shift[:, bass.ds(t, 1)], ALU.mult, ALU.add).then_inc(rows_ready, 1)

            @block.gpsimd
            def _(pool):
                if affine:
                    pool.wait_ge(affine_in, 32)
                if affine or dst_tok is not None:
                    with pool.Fori(0, NT // 2) as i:
                        for j in range(2):
                            t = i * 2 + j
                            pool.wait_ge(rows_ready, t + 1)
                            if affine:
                                pool.tensor_tensor(row[:, j, :], row[:, j, :], gb[:, 0, :], ALU.mult)
                                pool.drain()
                                last = pool.tensor_tensor(row[:, j, :], row[:, j, :], gb[:, 1, :], ALU.add)
                                pool.drain()
                            if dst_tok is not None:
                                last = pool.tensor_copy(dst_tok[:, bass.ds(t, 1), :], row[:, j:j + 1, :])
                            last.then_inc(tok_ready if dst_T is not None else free_row, 1)

            if dst_T is not None:
                shaped = tok_ready if (affine or dst_tok is not None) else rows_ready

                @block.tensor
                def _(pe):
                    with pe.Fori(0, NT // 2) as i:
                        for j in range(2):
                            pe.wait_ge(shaped, i * 2 + (j + 1))
                            pe.wait_ge(free_tp, i * 2 + (j + 1))
                            for k in range(KC):
                                last = pe.transpose(tp[:, j, k * P:(k + 1) * P], row[:, j, k * P:(k + 1) * P], c.ident[:])
                            last.then_inc(turned, 1)

            @block.scalar
            def _(act):
                act.sem_inc(free_tp, 2)
                act.wait_ge(var_ready, 1)
                act.activation(std[:], std[:], ACT.Sqrt).then_inc(std_ready, 1)
                if dst_T is not None:
                    with act.Fori(0, NT // 2) as i:
                        for j in range(2):
                            t = i * 2 + j
                            act.wait_ge(turned, t + 1)
                            act.activation(dst_T[:, :, bass.ts(t, P)],
                                           tp[:, j, 0:D].rearrange("p (k n) -> p k n", k=KC), ACT.Copy).then_inc(free_tp, 1)
                            act.sem_inc(free_row, 1)


def project_add(c, name, src, w, bias=None, scale_src=None):
    nc = c.nc
    with Stage(nc, name) as st:
        row = st.sb("row", [P, 2, D])
        rowT = st.sb("rowT", [P, 2, D])
        w_sb = st.sb("w", [P, KC, D])
        b_sb = st.sb("b", [P, D])
        tp = st.ps("tp", [P, 2, 512])
        out = st.ps("out", [P, 2, 512])
        w_in = st.sem("w_in")
        row_ready, turned, rowT_ready, multiplied, added = (
            st.sem(n, primed=n != "row") for n in ("row", "turned", "rowT", "mult", "added"))
        with nc.Block() as block:
            @block.sync
            def _(sp):
                sp.dma_start(w_sb[:], w.rearrange("(k p) n -> p k n", p=P)).then_inc(w_in, 16)
                if bias is not None:
                    sp.dma_start(b_sb[:], bias.rearrange("(a n) -> a n", a=1).broadcast_to([P, D])).then_inc(w_in, 16)
                sp.wait_ge(w_in, 32 if bias is not None else 16)

            @block.gpsimd
            def _(pool):
                with pool.Fori(0, NT // 2) as i:
                    for j in range(2):
                        pool.wait_ge(turned, i * 2 + (j + 1))
                        pool.tensor_copy(row[:, j:j + 1, :], src[:, bass.ds(i * 2 + j, 1), :]).then_inc(row_ready, 1)

            @block.tensor
            def _(pe):
                pe.wait_ge(w_in, 32 if bias is not None else 16)
                with pe.Fori(0, NT // 2) as i:
                    for j in range(2):
                        pe.wait_ge(row_ready, i * 2 + (j + 1))
                        pe.wait_ge(rowT_ready, i * 2 + 1)
                        for k in range(KC):
                            last = pe.transpose(tp[:, j, k * P:(k + 1) * P], row[:, j, k * P:(k + 1) * P], c.ident[:])
                        last.then_inc(turned, 1)
                    for j in range(2):
                        pe.wait_ge(rowT_ready, i * 2 + (j + 2))
                        pe.wait_ge(added, i * 2 + 1)
                        for k in range(KC):
                            last = pe.matmul(out[:, j, 0:D], rowT[:, j, k * P:(k + 1) * P], w_sb[:, k, :],
                                             start=(k == 0), stop=(k == KC - 1))
                        last.then_inc(multiplied, 1)

            @block.scalar
            def _(act):
                with act.Fori(0, NT // 2) as i:
                    for j in range(2):
                        act.wait_ge(turned, i * 2 + (j + 2))
                        act.wait_ge(multiplied, i * 2 + 1)
                        act.activation(rowT[:, j, :], tp[:, j, 0:D], ACT.Copy).then_inc(rowT_ready, 1)

            @block.vector
            def _(dve):
                if bias is not None:
                    dve.wait_ge(w_in, 32)
                with dve.Fori(0, NT // 2) as i:
                    for j in range(2):
                        t = i * 2 + j
                        dve.wait_ge(multiplied, t + 2)
                        x_t = c.x[:, bass.ds(t, 1), :]
                        dve.tensor_tensor(x_t, x_t, out[:, j:j + 1, 0:D], ALU.add).then_inc(added, 1)
                        if bias is not None:
                            dve.drain()
                            dve.tensor_tensor(x_t, x_t, b_sb[:].rearrange("p (a d) -> p a d", a=1), ALU.add)


PART_PRODUCTS = ((0, 0), (1, 0), (2, 0), (0, 1), (1, 1), (0, 2), (1, 2))
SR = len(PART_PRODUCTS) * DH + 3
HC = 4
SLOT = 32
NC4 = H // HC


def self_attention(c, name, wqk, wv, ao, causal_after, rope, bias, bv=None):
    nc = c.nc
    kinds = wqk.shape[2]
    LH = S // 512
    nU = 2 * LH
    ROW = DH
    CD = HC * DH
    with Stage(nc, name) as st:
        xb = st.sb("xb", [P, KC, S])
        w = st.sb("w", [P, kinds, KC, P])
        w_v = st.sb("w_v", [P, KC, CD])
        b = st.sb("b", [P, 2])
        bv_sb = st.sb("bv", [P, CD])
        cs = st.sb("cs", [P, 2, S]) if rope is not None else None
        t1 = st.sb("t1", [P, 2, 512])
        t2 = st.sb("t2", [P, 2, 512])
        qk = st.sb("qk", [P, 2, S])
        part = st.sb("part", [P, 3, 2, S], BF16)
        stacked = st.sb("stacked", [P, 2, HC, S], BF16)
        place = st.sb("place", [P, 2, 3, SR])
        place16 = st.sb("place16", [P, 2, 3, SR], BF16)
        ident16 = st.sb("ident16", [P, P], BF16)
        v = st.sb("v", [P, ST, HC, SLOT])
        ones_v = st.sb("ones_v", [P, SLOT])
        upper = st.sb("upper", [P, P])
        negmax = st.sb("negmax", [P, ST, HC, 1])
        nm_row = st.sb("nm_row", [P, ST, HC, SR], BF16)
        pt = st.sb("pt", [P, 4, 2, 512])
        diag = st.sb("diag", [P, 2, 2, 2, P])
        oT = st.sb("oT", [P, 512])
        recip = st.sb("recip", [P, 4, HC])
        ps = st.ps("ps", [P, 8, 512])
        names = ("w_in", "w_free", "c_in", "x_ready", "x_free", "init", "proj", "rot", "sum", "v_mm", "v_ready",
                 "mx_mm", "mx_done", "nm", "p1", "rest", "p2", "p3", "stack", "stacked", "sc", "ex", "dg", "pv", "oT_ready", "o_T", "o_done", "pv_used")
        s = {n: st.sem(n, primed=n in ("v_mm", "o_done",)) for n in names}
        C_IN = 32 if rope is not None else 16
        WI = 64 if bv is not None else 48
        NU2 = ST * 2 * LH
        MH = HC * ST // 2
        NR = 4 * HC

        def unit(a, u):
            return a[:, u % 2, u // 2 * 512:(u // 2 + 1) * 512]

        with nc.Block() as block:
            @block.sync
            def _(sp):
                sp.dma_start(place[:], c.dram["part_place"]).then_inc(s["c_in"], 16)
                if rope is not None:
                    sp.dma_start(cs[:], rope.rearrange("a p n -> p a n")).then_inc(s["c_in"], 16)
                for it in range(B * NC4):
                    ci = it % NC4
                    sp.wait_ge(s["v_mm"], it + 1)
                    sp.wait_ge(s["v_ready"], it)
                    sp.dma_start(w[:], wqk[ci]).then_inc(s["w_in"], 16)
                    sp.dma_start(w_v[:], wv[ci]).then_inc(s["w_in"], 16)
                    sp.dma_start(b[:], bias[ci]).then_inc(s["w_in"], 16)
                    if bv is not None:
                        sp.dma_start(bv_sb[:], bv[ci]).then_inc(s["w_in"], 16)
                sp.wait_ge(s["c_in"], C_IN)
                sp.wait_ge(s["w_in"], B * NC4 * WI)

            @block.gpsimd
            def _(pool):
                pool.memset(v[:], 0.0)
                pool.memset(ones_v[:], 0.0)
                pool.memset(nm_row[:], 0.0)
                pool.tensor_copy(ident16[:], c.ident[:])
                pool.memset(upper[:], 1.0)
                pool.drain()
                pool.memset(v[:, :, :, ROW:ROW + 1], 1.0)
                pool.memset(ones_v[:, ROW:ROW + 1], 1.0)
                pool.tensor_tensor(upper[:], upper[:], c.lower[:], ALU.subtract)
                pool.drain()
                pool.wait_ge(s["c_in"], C_IN)
                pool.tensor_copy(place16[:], place[:])
                pool.drain()
                pool.sem_inc(s["init"], 1)
                with pool.Fori(0, B) as bi:
                    pool.wait_ge(s["v_mm"], bi * NC4 + 1)
                    pool.tensor_copy(xb[:], c.xT[:, :, bass.ds(bi * S, S)]).then_inc(s["x_ready"], 1)
                    with pool.Fori(0, NC4) as ci:
                        it = bi * NC4 + ci
                        for u in range(nU + 2):
                            if rope is not None and u < nU:
                                pool.wait_ge(s["rot"], it * nU + (u + 1))
                                pool.tensor_tensor(unit(qk[:], u), t1[:, u % 2, :], t2[:, u % 2, :], ALU.add).then_inc(s["sum"], 1)
                            if 1 <= u <= nU:
                                pool.wait_ge(s["p1"], it * nU + u)
                                pool.tensor_tensor(unit(qk[:], u - 1), unit(qk[:], u - 1), unit(part[:, 0], u - 1),
                                                   ALU.subtract).then_inc(s["rest"], 1)
                            if u >= 2:
                                pool.wait_ge(s["p2"], it * nU + (u - 1))
                                pool.tensor_tensor(unit(part[:, 2], u - 2), unit(qk[:], u - 2), unit(part[:, 1], u - 2),
                                                   ALU.subtract).then_inc(s["p3"], 1)

            @block.tensor
            def _(pe):
                pe.wait_ge(s["init"], 1)
                with pe.Fori(0, B) as bi:
                    with pe.Fori(0, NC4) as ci:
                        it = bi * NC4 + ci
                        pe.wait_ge(s["x_ready"], bi + 1)
                        pe.wait_ge(s["w_in"], it * WI + WI)
                        pe.wait_ge(s["o_done"], it * LH + 1)
                        for u in range(nU):
                            which, h = u % 2, u // 2
                            if u >= 2:
                                pe.wait_ge(s["rot"], it * nU + (u - 1))
                            for g in range(kinds // 2):
                                for k in range(KC):
                                    last = pe.matmul(ps[:, 2 * (u % 2) + g, :], w[:, which + 2 * g, k, :],
                                                     xb[:, k, h * 512:(h + 1) * 512], start=(k == 0), stop=(k == KC - 1))
                            last.then_inc(s["proj"], 1)
                        for t in range(ST):
                            for k in range(KC):
                                last = pe.matmul(ps[:, 4, t * CD:(t + 1) * CD], xb[:, k, t * P:(t + 1) * P],
                                                 w_v[:, k, :], start=(k == 0), stop=(k == KC - 1))
                        last.then_inc(s["v_mm"], 1)
                        def maxima(m, bank):
                            hd, t = m % HC, m // HC
                            for h in range(LH):
                                last = pe.matmul(ps[:, bank + h, :], part[SLOT * hd:SLOT * hd + SLOT, 0, 0, t * P:(t + 1) * P],
                                                 part[SLOT * hd:SLOT * hd + SLOT, 0, 1, h * 512:(h + 1) * 512],
                                                 start=True, stop=True)
                            last.then_inc(s["mx_mm"], 1)

                        def stack(r):
                            which = 1 if r < 2 * HC else 0
                            hd, h = (r // 2, r % 2) if which else (r % HC, (r - 2 * HC) // HC)
                            if r >= 2:
                                pe.wait_ge(s["stacked"], it * NR + (r - 1))
                            out = ps[0:SR, 6 + r % 2, :]
                            slot = slice(SLOT * hd, SLOT * hd + SLOT)
                            for a in range(3):
                                last = pe.matmul(out, place16[slot, which, a, :], part[slot, a, which, h * 512:(h + 1) * 512],
                                                 start=(a == 0), stop=(a == 2), skip_group_check=True)
                            if which == 0:
                                for t in range(4):
                                    last = pe.matmul(out[:, t * P:(t + 1) * P], nm_row[:, 4 * h + t, hd, :], ident16[:],
                                                     start=False, stop=True, skip_group_check=True)
                            last.then_inc(s["stack"], 1)

                        pe.wait_ge(s["p1"], it * nU + nU)
                        for m in range(MH):
                            if m >= 2:
                                pe.wait_ge(s["mx_done"], it * (2 * MH) + (m - 1))
                            maxima(m, 2 * (m % 2))
                            if m % 2:
                                if m == 1:
                                    pe.wait_ge(s["p3"], it * nU + nU)
                                stack(m // 2)
                        pe.wait_ge(s["nm"], it * 2 + 1)
                        for q in range(HC):
                            stack(2 * HC + q)
                        pe.wait_ge(s["v_ready"], it + 1)

                        def scores(n):
                            qh, kt, pr = n // (2 * ST), (n // 2) % ST, n % 2
                            if n >= 2:
                                pe.wait_ge(s["ex"], it * NU2 + (n - 1))
                            if kt == 0:
                                pe.wait_ge(s["stacked"], it * NR + ((2 + qh) * HC + 2 * pr + 2))
                            for e in range(2):
                                last = pe.matmul(ps[:, 2 * pr + e, :], stacked[0:SR, 1, 2 * pr + e, kt * P:(kt + 1) * P],
                                                 stacked[0:SR, 0, 2 * pr + e, qh * 512:(qh + 1) * 512], start=True, stop=True)
                            last.then_inc(s["sc"], 1)

                        def weigh(n):
                            qh, kt, pr = n // (2 * ST), (n // 2) % ST, n % 2
                            pe.wait_ge(s["ex"], it * NU2 + (n + 1))
                            j = kt - 4 * qh
                            on_diag = causal_after and 0 <= j < 4
                            if on_diag:
                                pe.wait_ge(s["dg"], it * 2 * ST + 2 * kt + (pr + 1))
                            for e in range(2):
                                hd = 2 * pr + e
                                out = ps[SLOT * hd:SLOT * hd + SLOT, 4 + qh, :]
                                src = pt[:, n % 4, e, :]
                                vv = v[:, kt, hd, :]
                                parts = []
                                if not causal_after or j < 0:
                                    parts = [(vv, src, 0, 512)]
                                elif j >= 4:
                                    parts = [(ones_v[:], src, 0, 512)]
                                else:
                                    if j > 0:
                                        parts.append((ones_v[:], src[:, 0:j * P], 0, j * P))
                                    parts.append((vv, diag[:, n % 2, 0, e, :], j * P, (j + 1) * P))
                                    parts.append((ones_v[:], diag[:, n % 2, 1, e, :], j * P, (j + 1) * P))
                                    if j < 3:
                                        parts.append((vv, src[:, (j + 1) * P:512], (j + 1) * P, 512))
                                for q, (lhs, rhs, a, z) in enumerate(parts):
                                    last = pe.matmul(out[:, a:z], lhs, rhs, start=(kt == 0 and q == 0),
                                                     stop=(kt == ST - 1), skip_group_check=True)
                            last.then_inc(s["pv"], 1)

                        def turn(qh):
                            pe.wait_ge(s["oT_ready"], it * LH + (qh + 1))
                            for t in range(4):
                                last = pe.transpose(ps[:, 6, t * P:(t + 1) * P], oT[:, t * P:(t + 1) * P], c.ident[:])
                            last.then_inc(s["o_T"], 1)

                        for n in range(NU2 + 2):
                            if n < NU2:
                                scores(n)
                            if n < MH:
                                pe.wait_ge(s["mx_done"], it * (2 * MH) + (MH + n))
                                if n == 0:
                                    pe.wait_ge(s["stacked"], it * NR + 3 * HC)
                                maxima(MH + n, 6)
                            if n >= 2:
                                weigh(n - 2)
                            if n == MH - 1:
                                pe.wait_ge(s["nm"], it * 2 + 2)
                                for q in range(HC):
                                    stack(3 * HC + q)
                            if n - 2 == NU2 // LH + 1:
                                turn(0)
                        turn(1)

            @block.scalar
            def _(act):
                with act.Fori(0, B * NC4) as it:
                    for u in range(nU + 1):
                        if u < nU:
                            act.wait_ge(s["sum"] if rope is not None else s["rot"], it * nU + (u + 1))
                            act.activation(unit(part[:, 0], u), unit(qk[:], u), ACT.Copy).then_inc(s["p1"], 1)
                        if u >= 1:
                            act.wait_ge(s["rest"], it * nU + u)
                            act.activation(unit(part[:, 1], u - 1), unit(qk[:], u - 1), ACT.Copy).then_inc(s["p2"], 1)

                    def take(r):
                        which = 1 if r < 2 * HC else 0
                        hd, h = (r // 2, r % 2) if which else (r % HC, (r - 2 * HC) // HC)
                        act.wait_ge(s["stack"], it * NR + (r + 1))
                        act.activation(stacked[0:SR, which, hd, h * 512:(h + 1) * 512], ps[0:SR, 6 + r % 2, :],
                                       ACT.Copy).then_inc(s["stacked"], 1)

                    for q in range(3 * HC):
                        take(q)
                    for n in range(NU2):
                        if n == MH:
                            for q in range(HC):
                                take(3 * HC + q)
                        act.wait_ge(s["sc"], it * NU2 + (n + 1))
                        if n >= 4:
                            act.wait_ge(s["pv"], it * NU2 + (n - 3))
                        act.activation(pt[:, n % 4, :, :], ps[:, 2 * (n % 2):2 * (n % 2) + 2, :], ACT.Exp,
                                       scale=DH ** -0.5).then_inc(s["ex"], 1)

            @block.vector
            def _(dve):
                dve.wait_ge(s["init"], 1)
                if rope is not None:
                    dve.wait_ge(s["c_in"], C_IN)
                with dve.Fori(0, B) as bi:
                    with dve.Fori(0, NC4) as ci:
                        it = bi * NC4 + ci
                        dve.wait_ge(s["w_in"], it * WI + WI)
                        for u in range(nU):
                            which, h = u % 2, u // 2
                            dve.wait_ge(s["proj"], it * nU + (u + 1))
                            src0, src1 = ps[:, 2 * (u % 2), :], ps[:, 2 * (u % 2) + 1, :]
                            if rope is not None:
                                if u >= 2:
                                    dve.wait_ge(s["sum"], it * nU + (u - 1))
                                if which == 1:
                                    dve.scalar_tensor_tensor(out=t1[:, u % 2, :], in0=src0, scalar=b[:, 1:2],
                                                             in1=cs[:, 0, h * 512:(h + 1) * 512], op0=ALU.add, op1=ALU.mult)
                                else:
                                    dve.tensor_tensor(t1[:, u % 2, :], src0, cs[:, 0, h * 512:(h + 1) * 512], ALU.mult)
                                dve.tensor_tensor(t2[:, u % 2, :], src1, cs[:, 1, h * 512:(h + 1) * 512], ALU.mult).then_inc(s["rot"], 1)
                            else:
                                dve.tensor_scalar(qk[:, which, h * 512:(h + 1) * 512], src0, b[:, which:which + 1], None,
                                                  ALU.add).then_inc(s["rot"], 1)
                        dve.wait_ge(s["v_mm"], it + 2)
                        vsrc = ps[:, 4, :].rearrange("p (t h d) -> p t h d", t=ST, h=HC)
                        if bv is not None:
                            vb = bv_sb[:].rearrange("p (a h d) -> p a h d", a=1, h=HC).broadcast_to([P, ST, HC, DH])
                            dve.tensor_tensor(v[:, :, :, 0:DH], vsrc, vb, ALU.add).then_inc(s["v_ready"], 1)
                        else:
                            dve.tensor_copy(v[:, :, :, 0:DH], vsrc).then_inc(s["v_ready"], 1)
                        def maximum(m, bank):
                            dve.wait_ge(s["mx_mm"], it * (2 * MH) + (m + 1))
                            dve.tensor_reduce(negmax[:, m // HC, m % HC, :], ps[:, bank:bank + 2, :],
                                              AX.XY, ALU.max, negate=True).then_inc(s["mx_done"], 1)

                        def place_maxima(h):
                            nm, row = negmax[:, 4 * h:4 * h + 4], nm_row[:, 4 * h:4 * h + 4]
                            dve.drain()
                            for a in range(3):
                                last = dve.tensor_copy(row[:, :, :, SR - 3 + a:SR - 2 + a], nm)
                                if a < 2:
                                    dve.drain()
                                    dve.tensor_tensor(nm, nm, row[:, :, :, SR - 3 + a:SR - 2 + a], ALU.subtract)
                                    dve.drain()
                            last.then_inc(s["nm"], 1)

                        for m in range(MH):
                            maximum(m, 2 * (m % 2))
                        place_maxima(0)

                        def finish(qh):
                            dve.wait_ge(s["pv"], it * NU2 + NU2 // LH * (qh + 1))
                            dve.tensor_copy(oT[:], ps[:, 4 + qh, :]).then_inc(s["oT_ready"], 1)
                            dve.wait_ge(s["o_T"], it * LH + (qh + 1))
                            o = ps[:, 6, :].rearrange("p (t h s) -> p t h s", t=4, h=HC)
                            dve.reciprocal(recip[:], o[:, :, :, ROW])
                            dve.drain()
                            r4 = recip[:].rearrange("p t (h a) -> p t h a", a=1).broadcast_to([P, 4, HC, DH])
                            dst = ao[:, bass.ds(bi * ST + 4 * qh, 4), bass.ds(ci * CD, CD)].rearrange("p t (h d) -> p t h d", h=HC)
                            dve.tensor_tensor(dst, o[:, :, :, 0:DH], r4, ALU.mult).then_inc(s["o_done"], 1)

                        for n in range(NU2):
                            qh, kt, pr = n // (2 * ST), (n // 2) % ST, n % 2
                            j = kt - 4 * qh
                            if n < MH:
                                maximum(MH + n, 6)
                            if n == MH - 1:
                                place_maxima(1)
                            if causal_after and 0 <= j < 4:
                                dve.wait_ge(s["ex"], it * NU2 + (n + 1))
                                if kt >= 1:
                                    before = n - 2 if j > 0 else 2 * (kt - 1) + pr
                                    dve.wait_ge(s["pv"], it * NU2 + (before + 1))
                                for z, mask in enumerate((c.lower, upper)):
                                    mk = mask[:].rearrange("p (a n) -> p a n", a=1).broadcast_to([P, 2, P])
                                    last = dve.tensor_tensor(diag[:, n % 2, z, :, :], pt[:, n % 4, :, j * P:(j + 1) * P],
                                                             mk, ALU.mult)
                                last.then_inc(s["dg"], 1)
                            if n == NU2 // LH + 1:
                                finish(0)
                        finish(1)



def load_weights(sp, pairs, sem):
    for dst, src in pairs:
        sp.dma_start(dst, src).then_inc(sem, 16)
    return 16 * len(pairs)


def row_bcast(v, n, parts=P):
    return v.rearrange("(a n) -> a n", a=1).broadcast_to([parts, n])


def linear_T(c, name, srcT, jobs, width=N):
    nc = c.nc
    step = min(512, width)
    nb = width // step
    with Stage(nc, name) as st:
        ps = st.ps("ps", [P, 8, 512])
        w_in, proj_a, proj_v, free_a, free_v = (st.sem(n) for n in ("w_in", "proj_a", "proj_v", "free_a", "free_v"))
        loads, chunks = [], []
        for q, (w, dst, bias, func) in enumerate(jobs):
            M = w.shape[1]
            w_sb = st.sb(f"w{q}", [P, KC, M])
            loads.append((w_sb[:], w.rearrange("(k p) m -> p k m", p=P)))
            b_sb = None
            if bias is not None:
                b_sb = st.sb(f"b{q}", [P, M // P])
                loads.append((b_sb[:], bias))
            for m in range(M // P):
                lane = "a" if func is not None or len(chunks) % 2 == 0 else "v"
                at = sum(x[0] == lane for x in chunks)
                chunks.append((lane, at, w_sb, b_sb, dst, m, func))
        per = {lane: sum(x[0] == lane for x in chunks) for lane in "av"}
        assert all(n <= 4 or n % 4 == 0 for n in per.values())
        total = 16 * len(loads)
        proj, free = {"a": proj_a, "v": proj_v}, {"a": free_a, "v": free_v}
        bank = {"a": 0, "v": 4}
        with nc.Block() as block:
            @block.sync
            def _(sp):
                load_weights(sp, loads, w_in)
                sp.wait_ge(w_in, total)

            @block.tensor
            def _(pe):
                pe.wait_ge(w_in, total)
                with pe.Fori(0, nb) as n:
                    for lane, at, w_sb, b_sb, dst, m, func in chunks:
                        pe.wait_ge(free[lane], n * per[lane] + (at + 1))
                        for k in range(KC):
                            last = pe.matmul(ps[:, bank[lane] + at % 4, 0:step], w_sb[:, k, m * P:(m + 1) * P],
                                             srcT[:, k, bass.ts(n, step)], start=(k == 0), stop=(k == KC - 1))
                        last.then_inc(proj[lane], 1)

            @block.scalar
            def _(act):
                act.sem_inc(free_a, min(4, per["a"]))
                act.wait_ge(w_in, total)
                with act.Fori(0, nb) as n:
                    for lane, at, w_sb, b_sb, dst, m, func in chunks:
                        if lane == "a":
                            act.wait_ge(proj_a, n * per["a"] + (at + 1))
                            act.activation(dst[:, m, bass.ts(n, step)], ps[:, at % 4, 0:step], func or ACT.Identity,
                                           bias=0.0 if b_sb is None else b_sb[:, m:m + 1]).then_inc(free_a, 1)

            @block.vector
            def _(dve):
                if per["v"]:
                    dve.sem_inc(free_v, min(4, per["v"]))
                    dve.wait_ge(w_in, total)
                    with dve.Fori(0, nb) as n:
                        for lane, at, w_sb, b_sb, dst, m, func in chunks:
                            if lane == "v":
                                dve.wait_ge(proj_v, n * per["v"] + (at + 1))
                                dve.tensor_scalar(dst[:, m, bass.ts(n, step)], ps[:, 4 + at % 4, 0:step],
                                                  0.0 if b_sb is None else b_sb[:, m:m + 1], None, ALU.add).then_inc(free_v, 1)


def rope_T(c, name, srcT, jobs, table, per_chunk):
    nc = c.nc
    with Stage(nc, name) as st:
        ps = st.ps("ps", [P, 8, 512])
        t12 = st.sb("t12", [P, 4, 2, 512])
        tk = KC if per_chunk else 1
        cs = st.sb("cs", [P, 2, tk, S])
        w_in, proj, rot, summed = (st.sem(n, primed=n in ("rot", "summed")) for n in ("w_in", "proj", "rot", "summed"))
        loads = [(cs[:, i, :, :], table[i].rearrange("k p s -> p k s") if per_chunk else table[i].rearrange("p (a s) -> p a s", a=1))
                 for i in range(2)]
        sbs = []
        for q, (w, ws, dst, b, bs) in enumerate(jobs):
            w_sb, b_sb = st.sb(f"w{q}", [P, 2, KC, D]), None
            loads += [(w_sb[:, 0], w.rearrange("(k p) m -> p k m", p=P)), (w_sb[:, 1], ws.rearrange("(k p) m -> p k m", p=P))]
            if b is not None:
                b_sb = st.sb(f"b{q}", [P, 2, KC])
                loads += [(b_sb[:, 0], b), (b_sb[:, 1], bs)]
            sbs.append((w_sb, b_sb, dst))
        total = 16 * len(loads)
        units = [(h, q, m) for h in range(S // 512) for q in range(len(jobs)) for m in range(KC)]
        U = len(units)
        assert U % 4 == 0
        with nc.Block() as block:
            @block.sync
            def _(sp):
                load_weights(sp, loads, w_in)
                sp.wait_ge(w_in, total)

            @block.tensor
            def _(pe):
                pe.wait_ge(w_in, total)
                with pe.Fori(0, B) as bi:
                    for i, (h, q, m) in enumerate(units):
                        pe.wait_ge(rot, bi * U + (i - 2) if i >= 4 else bi * U + 1)
                        for g in range(2):
                            for k in range(KC):
                                last = pe.matmul(ps[:, 2 * (i % 4) + g, :], sbs[q][0][:, g, k, m * P:(m + 1) * P],
                                                 srcT[:, k, bass.ds(bi * S + h * 512, 512)], start=(k == 0), stop=(k == KC - 1))
                        last.then_inc(proj, 1)

            @block.vector
            def _(dve):
                dve.wait_ge(w_in, total)
                with dve.Fori(0, B) as bi:
                    for i, (h, q, m) in enumerate(units):
                        dve.wait_ge(proj, bi * U + (i + 1))
                        dve.wait_ge(summed, bi * U + (i - 2) if i >= 4 else bi * U + 1)
                        for g in range(2):
                            out, src = t12[:, i % 4, g, :], ps[:, 2 * (i % 4) + g, :]
                            tab = cs[:, g, m if per_chunk else 0, h * 512:(h + 1) * 512]
                            if sbs[q][1] is None:
                                last = dve.tensor_tensor(out, src, tab, ALU.mult)
                            else:
                                last = dve.scalar_tensor_tensor(out=out, in0=src, scalar=sbs[q][1][:, g, m:m + 1], in1=tab,
                                                                op0=ALU.add, op1=ALU.mult)
                        last.then_inc(rot, 1)

            @block.gpsimd
            def _(pool):
                with pool.Fori(0, B) as bi:
                    for i, (h, q, m) in enumerate(units):
                        pool.wait_ge(rot, bi * U + (i + 2))
                        pool.tensor_tensor(sbs[q][2][:, m, bass.ds(bi * S + h * 512, 512)], t12[:, i % 4, 0, :],
                                           t12[:, i % 4, 1, :], ALU.add).then_inc(summed, 1)


def linear_tok(c, name, srcT, w, dst=None, bias=None, resid=None, relu=False, tiles=NT, rows=P):
    nc = c.nc
    M = w.shape[1]
    with Stage(nc, name) as st:
        ps = st.ps("ps", [P, 4, 512])
        w_sb = st.sb("w", [P, KC, M])
        b_sb = st.sb("b", [P, M])
        w_in, mult, out = st.sem("w_in"), st.sem("mult"), st.sem("out")
        loads = [(w_sb[:], w.rearrange("(k p) m -> p k m", p=P))]
        if bias is not None:
            loads.append((b_sb[:], row_bcast(bias, M)))
        total = 16 * len(loads)
        with nc.Block() as block:
            @block.sync
            def _(sp):
                load_weights(sp, loads, w_in)
                sp.wait_ge(w_in, total)

            @block.tensor
            def _(pe):
                pe.wait_ge(w_in, total)
                for t in range(tiles):
                    if t >= 4:
                        pe.wait_ge(out, t - 3)
                    for k in range(KC):
                        last = pe.matmul(ps[0:rows, t % 4, 0:M], srcT[:, k, t * rows:(t + 1) * rows], w_sb[:, k, :],
                                         start=(k == 0), stop=(k == KC - 1))
                    last.then_inc(mult, 1)

            @block.vector
            def _(dve):
                dve.wait_ge(w_in, total)
                for t in range(tiles):
                    dve.wait_ge(mult, t + 1)
                    d, p_ = dst[0:rows, t, :], ps[0:rows, t % 4, 0:M]
                    if bias is None and not relu and resid is None:
                        dve.tensor_copy(d, p_).then_inc(out, 1)
                        continue
                    if bias is not None:
                        last = dve.tensor_tensor(d, p_, b_sb[0:rows, :], ALU.add)
                        src = d
                    else:
                        src = p_
                    if relu:
                        if bias is not None:
                            dve.drain()
                        last = dve.scalar_tensor_tensor(out=d, in0=src, scalar=0.0, in1=resid[0:rows, t, :],
                                                        op0=ALU.max, op1=ALU.add)
                    elif resid is not None:
                        if bias is not None:
                            dve.drain()
                        last = dve.tensor_tensor(d, src, resid[0:rows, t, :], ALU.add)
                    last.then_inc(out, 1)


def additive_attention(c, name, feat, feT, txb, sw, sb_rows):
    nc, d = c.nc, c.dram
    HALVES = S // 512
    G = ST // 2
    with Stage(nc, name) as st:
        h = st.sb("h", [P, 2, KC, S])
        z0 = st.sb("z0", [P, 2, S])
        z = st.sb("z", [P, 2, S])
        w_col = st.sb("w_col", [P, KC])
        sel = st.sb("sel", [P, 2 * S2 - 1])
        m_i = st.sb("m_i", [S2, B], I32)
        m_f = st.sb("m_f", [S2, B])
        bc = st.sb("bc", [P, 2])
        rT = st.sb("rT", [S2, S])
        nmax = st.sb("nmax", [P, ST])
        e = st.sb("e", [P, ST, S2])
        es = st.sb("es", [P, 2, ST, S2])
        sums = st.sb("sums", [P, 3, ST])
        gate = st.sb("gate", [P, 2, ST])
        tmp = st.sb("tmp", [P, 2, D])
        rho = st.ps("rho", [P, 2, 512])
        rT_ps = st.ps("rT_ps", [P, 2, 512])
        names = ("w_in", "init", "tanh", "z0d", "z", "row", "rho_read", "turned", "nmax", "exp", "sums", "gate", "added")
        s = {n: st.sem(n, primed=n in ("z", "row", "rho_read", "exp",)) for n in names}
        loads = [(w_col[:], d["l0x_w"]), (m_i[:], d["mask2T"]),
                 (bc[:, 0:1], row_bcast(d["l0x_bcw"], 1)), (bc[:, 1:2], row_bcast(d["l0x_bcb"], 1))]
        total = 16 * len(loads)
        with nc.Block() as block:
            @block.sync
            def _(sp):
                load_weights(sp, loads, s["w_in"])
                sp.wait_ge(s["w_in"], total)

            @block.gpsimd
            def _(pool):
                pool.memset(sel[:], 0.0)
                pool.drain()
                pool.memset(sel[:, S2 - 1:S2], 1.0)
                pool.drain()
                pool.sem_inc(s["init"], 1)

            @block.scalar
            def _(act):
                act.wait_ge(s["w_in"], total)
                with act.Fori(0, B) as bi:
                    for t in range(S2):
                        if t >= 2:
                            act.wait_ge(s["z"], bi * S2 + t)
                        else:
                            act.wait_ge(s["z"], bi * S2 + 1)
                        for k in range(KC):
                            last = act.activation(h[:, t % 2, k, :], feT[:, k, bass.ds(bi * S, S)], ACT.Tanh,
                                                  bias=txb[:, k, bass.ds(bi * S2 + t, 1)])
                        last.then_inc(s["tanh"], 1)
                    act.wait_ge(s["nmax"], bi + 1)
                    for t in range(ST):
                        last = act.activation(e[:, t, :], rT_ps[:, t // G, (t % G) * S2:(t % G + 1) * S2], ACT.Exp,
                                              bias=nmax[:, t:t + 1])
                    last.then_inc(s["exp"], 1)
                    act.wait_ge(s["sums"], bi + 1)
                    for g in range(2):
                        last = act.activation(gate[:, g, :], gate[:, g, :], ACT.Tanh, bias=bc[:, g:g + 1])
                    last.then_inc(s["gate"], 1)

            @block.vector
            def _(dve):
                dve.wait_ge(s["w_in"], total)
                dve.tensor_copy(m_f[:], m_i[:])
                dve.drain()
                dve.tensor_scalar(m_f[:], m_f[:], -1.0, 1.0, ALU.mult, ALU.add)
                dve.drain()
                dve.tensor_scalar(m_f[:], m_f[:], -1e30, None, ALU.mult)
                with dve.Fori(0, B) as bi:
                    for t in range(S2):
                        dve.wait_ge(s["tanh"], bi * S2 + (t + 1))
                        dve.wait_ge(s["row"], bi * S2 + t if t >= 2 else bi * S2 + 1)
                        dve.tensor_scalar(z0[:, t % 2, :], h[:, t % 2, 1, :], w_col[:, 1:2], None, ALU.mult)
                        dve.drain()
                        dve.scalar_tensor_tensor(out=z[:, t % 2, :], in0=h[:, t % 2, 0, :], scalar=w_col[:, 0:1],
                                                 in1=z0[:, t % 2, :], op0=ALU.mult, op1=ALU.add).then_inc(s["z"], 1)
                    dve.wait_ge(s["row"], bi * S2 + (S2 + 1))
                    dve.tensor_scalar(rT[:].rearrange("p (a n) -> p a n", a=HALVES), rho[0:S2, :, :],
                                      m_f[:, bass.ds(bi, 1)], None, ALU.add).then_inc(s["rho_read"], 1)
                    dve.wait_ge(s["turned"], bi + 1)
                    for q in range(2):
                        last = dve.tensor_reduce(nmax[:, q * G:(q + 1) * G], rT_ps[:, q, 0:G * S2].rearrange("p (t n) -> p t n", t=G),
                                                 AX.X, ALU.max, negate=True)
                    last.then_inc(s["nmax"], 1)
                    dve.wait_ge(s["exp"], bi + 2)
                    dve.tensor_reduce(sums[:, 0, :], e[:], AX.X, ALU.add)
                    for g, rowv in enumerate((sw, sb_rows)):
                        r = rowv[:, bass.ds(bi, 1), :].broadcast_to([P, ST, S2])
                        dve.tensor_tensor(es[:, g], e[:], r, ALU.mult)
                    dve.drain()
                    dve.tensor_reduce(sums[:, 1:3, :], es[:], AX.X, ALU.add)
                    dve.reciprocal(sums[:, 0, :], sums[:, 0, :])
                    dve.drain()
                    dve.tensor_tensor(gate[:], sums[:, 1:3, :], sums[:, 0:1, :].broadcast_to([P, 2, ST]), ALU.mult).then_inc(s["sums"], 1)
                    dve.wait_ge(s["gate"], bi + 1)
                    for t in range(ST):
                        dve.tensor_scalar(tmp[:, t % 2:t % 2 + 1, :], feat[:, bass.ds(bi * ST + t, 1), :], gate[:, 0, t:t + 1],
                                          gate[:, 1, t:t + 1], ALU.mult, ALU.add)
                        dve.drain()
                        x_t = c.x[:, bass.ds(bi * ST + t, 1), :]
                        dve.tensor_tensor(x_t, x_t, tmp[:, t % 2:t % 2 + 1, :], ALU.add)

            @block.tensor
            def _(pe):
                pe.wait_ge(s["init"], 1)
                with pe.Fori(0, B) as bi:
                    pe.wait_ge(s["rho_read"], bi + 1)
                    for t in range(S2):
                        pe.wait_ge(s["z"], bi * S2 + (t + 2))
                        for hf in range(HALVES):
                            last = pe.matmul(rho[0:S2, hf, :], sel[:, S2 - 1 - t:2 * S2 - 1 - t], z[:, t % 2, hf * 512:(hf + 1) * 512],
                                             start=(t == 0), stop=(t == S2 - 1))
                        last.then_inc(s["row"], 1)
                    pe.wait_ge(s["rho_read"], bi + 2)
                    pe.wait_ge(s["exp"], bi + 1)
                    for t in range(ST):
                        last = pe.transpose(rT_ps[:, t // G, (t % G) * S2:(t % G + 1) * S2], rT[:, t * P:(t + 1) * P],
                                            c.ident[0:S2, 0:S2])
                    last.then_inc(s["turned"], 1)


def ctx_rows(c, name, cols, dst):
    nc = c.nc
    with Stage(nc, name) as st:
        w = st.sb("w", [P, len(cols), KC, P])
        ps = st.ps("ps", [P, 2, 512])
        w_in, mult, out = st.sem("w_in"), st.sem("mult"), st.sem("out")
        with nc.Block() as block:
            @block.sync
            def _(sp):
                load_weights(sp, [(w[:, i], v.rearrange("(k p) m -> p k m", p=P)) for i, v in enumerate(cols)], w_in)
                sp.wait_ge(w_in, 16 * len(cols))

            @block.tensor
            def _(pe):
                pe.wait_ge(w_in, 16 * len(cols))
                for i in range(len(cols)):
                    for k in range(KC):
                        last = pe.matmul(ps[:, i, 0:B * S2], w[:, i, k, :], c.ctxT[:, k, :], start=(k == 0), stop=(k == KC - 1))
                last.then_inc(mult, 1)

            @block.vector
            def _(dve):
                dve.wait_ge(mult, 1)
                for i in range(len(cols)):
                    dve.tensor_copy(dst[i][:].rearrange("p b t -> p (b t)"), ps[:, i, 0:B * S2])


E = 8
CAPACITY = N * 5 // 4 // E
NO_SLOT = 1024.0


def route(c, name, srcT, w, wgt, bias=None, top=1, slot=None):
    nc = c.nc
    with Stage(nc, name) as st:
        w_sb = st.sb("w", [P, KC, E])
        b_sb = st.sb("b", [E, 1])
        lT = st.sb("lT", [E, N])
        L = st.sb("L", [P, NT, E])
        rank = st.sb("rank", [P, E])
        m = st.sb("m", [P, 2, NT, 1])
        p_ = st.sb("p", [P, NT, E])
        rk = st.sb("rk", [P, NT, 1])
        sel = st.sb("sel", [P, 2, NT, E])
        tmp = st.sb("tmp", [P, NT, E])
        tot = st.sb("tot", [P, 2, NT, 1])
        strict = st.sb("strict", [P, P])
        cum = st.sb("cum", [P, NT, E])
        before = st.sb("before", [P, NT, E])
        lps = st.ps("lps", [P, 4, 512])
        tps = st.ps("tps", [P, 512])
        cps = st.ps("cps", [P, 2, 512])
        names = ("w_in", "mult", "lT_ready", "turned", "shifted", "exp", "chosen", "counted", "rank_ready")
        s = {n: st.sem(n) for n in names}
        loads = [(w_sb[:], w.rearrange("(k p) e -> p k e", p=P))]
        if bias is not None:
            loads.append((b_sb[:], bias))
        total = 16 * len(loads)
        flat = [P, NT, E]
        with nc.Block() as block:
            @block.sync
            def _(sp):
                load_weights(sp, loads, s["w_in"])
                sp.wait_ge(s["w_in"], total)

            @block.gpsimd
            def _(pool):
                for e in range(E):
                    last = pool.memset(rank[:, e:e + 1], float(E - e))
                pool.tensor_tensor(strict[:], c.lower[:], c.ident[:], ALU.subtract)
                pool.drain()
                pool.sem_inc(s["rank_ready"], 1)

            @block.tensor
            def _(pe):
                pe.wait_ge(s["w_in"], total)
                for n in range(4):
                    for k in range(KC):
                        last = pe.matmul(lps[0:E, n, :], w_sb[:, k, :], srcT[:, k, n * 512:(n + 1) * 512],
                                         start=(k == 0), stop=(k == KC - 1))
                last.then_inc(s["mult"], 1)
                pe.wait_ge(s["lT_ready"], 1)
                for t in range(NT):
                    last = pe.transpose(tps[:, t * E:(t + 1) * E], lT[:, t * P:(t + 1) * P], c.ident[0:E, 0:E])
                last.then_inc(s["turned"], 1)
                if top == 2:
                    pe.wait_ge(s["chosen"], 1)
                    pe.wait_ge(s["rank_ready"], 1)
                    mask = cum[:].rearrange("p t e -> p (t e)")
                    pe.matmul(cps[:, 0, 0:NT * E], strict[:], mask, start=True, stop=True)
                    pe.matmul(cps[:, 1, 0:NT * E], c.ones[:], mask, start=True, stop=True).then_inc(s["counted"], 1)

            @block.scalar
            def _(act):
                act.wait_ge(s["shifted"], 1)
                act.activation(p_[:], p_[:], ACT.Exp).then_inc(s["exp"], 1)

            @block.vector
            def _(dve):
                dve.wait_ge(s["w_in"], total)
                dve.wait_ge(s["mult"], 1)
                lv = lT[:].rearrange("e (n q) -> e n q", n=4)
                if bias is not None:
                    dve.tensor_scalar(lv, lps[0:E, :, :], b_sb[:, 0:1], None, ALU.add).then_inc(s["lT_ready"], 1)
                else:
                    dve.tensor_copy(lv, lps[0:E, :, :]).then_inc(s["lT_ready"], 1)
                dve.wait_ge(s["turned"], 1)
                dve.tensor_copy(L[:].rearrange("p t e -> p (t e)"), tps[:, 0:NT * E])
                dve.drain()
                dve.wait_ge(s["rank_ready"], 1)
                rb = rank[:].rearrange("p (a e) -> p a e", a=1).broadcast_to(flat)

                def choose(i):
                    dve.tensor_reduce(m[:, i, :, 0], L[:], AX.X, ALU.max)
                    dve.drain()
                    if i == 0:
                        dve.tensor_tensor(p_[:], L[:], m[:, 0].broadcast_to(flat), ALU.subtract)
                        dve.drain()
                        dve.sem_inc(s["shifted"], 1)
                    dve.tensor_tensor(sel[:, i], L[:], m[:, i].broadcast_to(flat), ALU.is_equal)
                    dve.drain()
                    dve.tensor_tensor(sel[:, i], sel[:, i], rb, ALU.mult)
                    dve.drain()
                    dve.tensor_reduce(rk[:, :, 0], sel[:, i], AX.X, ALU.max)
                    dve.drain()
                    dve.tensor_tensor(sel[:, i], sel[:, i], rk[:].broadcast_to(flat), ALU.is_equal)
                    dve.drain()

                choose(0)
                if top == 1:
                    dve.wait_ge(s["exp"], 1)
                    dve.tensor_reduce(tot[:, 0, :, 0], p_[:], AX.X, ALU.add)
                    dve.drain()
                    dve.reciprocal(tot[:, 0], tot[:, 0])
                    dve.drain()
                    dve.tensor_tensor(wgt[:, :, 0:E], sel[:, 0], tot[:, 0].broadcast_to(flat), ALU.mult)
                    return
                dve.scalar_tensor_tensor(out=L[:], in0=sel[:, 0], scalar=-3e38, in1=L[:], op0=ALU.mult, op1=ALU.add)
                dve.drain()
                choose(1)
                dve.wait_ge(s["exp"], 1)
                dve.tensor_tensor(cum[:], sel[:, 0], sel[:, 1], ALU.add)
                dve.drain()
                dve.sem_inc(s["chosen"], 1)
                dve.tensor_tensor(tmp[:], p_[:], cum[:], ALU.mult)
                dve.drain()
                dve.tensor_reduce(tot[:, 0, :, 0], tmp[:], AX.X, ALU.add)
                dve.drain()
                dve.reciprocal(tot[:, 0], tot[:, 0])
                dve.drain()
                dve.tensor_tensor(tmp[:], tmp[:], tot[:, 0].broadcast_to(flat), ALU.mult)
                dve.wait_ge(s["counted"], 1)
                dve.memset(before[:, 0, :], 0.0)
                dve.drain()
                for t in range(1, NT):
                    dve.tensor_tensor(before[:, t, :], before[:, t - 1, :], cps[:, 1, (t - 1) * E:t * E], ALU.add)
                    dve.drain()
                dve.tensor_tensor(before[:].rearrange("p t e -> p (t e)"), before[:].rearrange("p t e -> p (t e)"),
                                  cps[:, 0, 0:NT * E], ALU.add)
                dve.drain()
                dve.tensor_scalar(slot[:, :, 0:E], before[:], -NO_SLOT, None, ALU.add)
                dve.tensor_scalar(before[:], before[:], float(CAPACITY), None, ALU.is_lt)
                dve.memset(slot[:, :, E:E + 2], NO_SLOT)
                dve.drain()
                dve.tensor_tensor(wgt[:, :, 0:E], tmp[:], before[:], ALU.mult)
                dve.tensor_tensor(before[:], before[:], cum[:], ALU.mult)
                dve.drain()
                dve.tensor_tensor(slot[:, :, 0:E], slot[:, :, 0:E], before[:], ALU.mult)
                dve.drain()
                dve.tensor_scalar(slot[:, :, 0:E], slot[:, :, 0:E], NO_SLOT, None, ALU.add)


def experts(c, name, srcT, wgt, n_experts, inner, w1, w2, gate=None, b1=None, square=False):
    nc = c.nc
    MI = inner // P
    NB = N // 512
    G = 1 if gate is None else 2
    with Stage(nc, name) as st:
        w1_sb = st.sb("w1", [P, 2, G, KC, inner])
        w2_sb = st.sb("w2", [P, 2, MI, D])
        b_sb = st.sb("b", [P, 2, MI])
        hT = st.sb("hT", [P, 2, MI, 512])
        gated = st.sb("gated", [P, 2, 512])
        ps = st.ps("ps", [P, 8, 512])
        names = ("w_in0", "w_in1", "w_free0", "w_free1", "up", "sil", "h", "down", "added")
        s = {n: st.sem(n, primed=n in ("h", "added", "down",)) for n in names}
        UI = 2 * NB
        loads = G + 1 + (b1 is not None)
        with nc.Block() as block:
            @block.sync
            def _(sp):
                for e in range(n_experts):
                    j = e % 2
                    sp.wait_ge(s[f"w_free{j}"], e // 2)
                    for g, ww in enumerate([w1] if gate is None else [gate, w1]):
                        sp.dma_start(w1_sb[:, j, g], ww[e].rearrange("(k p) m -> p k m", p=P)).then_inc(s[f"w_in{j}"], 16)
                    sp.dma_start(w2_sb[:, j], w2[e].rearrange("(k p) m -> p k m", p=P)).then_inc(s[f"w_in{j}"], 16)
                    if b1 is not None:
                        sp.dma_start(b_sb[:, j], b1[e]).then_inc(s[f"w_in{j}"], 16)
                for j in range(2):
                    sp.wait_ge(s[f"w_in{j}"], n_experts // 2 * 16 * loads)

            @block.tensor
            def _(pe):
                with pe.Fori(0, n_experts // 2) as i:
                    def up(u):
                        j, n = u // NB, u % NB
                        if n == 0:
                            pe.wait_ge(s[f"w_in{j}"], (i + 1) * (16 * loads))
                        for m in range(MI):
                            q = u * MI + m
                            pe.wait_ge(s["h"], i * (UI * MI) + q if q >= 2 else i * (UI * MI) + 1)
                            for g in range(G):
                                for k in range(KC):
                                    last = pe.matmul(ps[:, 2 * (m % 2) + g, :], w1_sb[:, j, g, k, m * P:(m + 1) * P],
                                                     srcT[:, k, n * 512:(n + 1) * 512], start=(k == 0), stop=(k == KC - 1))
                            last.then_inc(s["up"], 1)

                    def down(u):
                        j = u // NB
                        pe.wait_ge(s["h"], i * (UI * MI) + ((u + 1) * MI + 1))
                        for t in range(4):
                            q = u * 4 + t
                            pe.wait_ge(s["added"], i * (UI * 4) + (q - 2) if q >= 4 else i * (UI * 4) + 1)
                            for m in range(MI):
                                last = pe.matmul(ps[:, 4 + t, 0:D], hT[:, u % 2, m, t * P:(t + 1) * P], w2_sb[:, j, m, :],
                                                 start=(m == 0), stop=(m == MI - 1))
                            last.then_inc(s["down"], 1)

                    for u in range(UI + 1):
                        if u < UI:
                            up(u)
                        if u >= 1:
                            down(u - 1)

            @block.scalar
            def _(act):
                with act.Fori(0, n_experts // 2) as i:
                    for u in range(UI):
                        j = u // NB
                        for m in range(MI):
                            q = u * MI + m
                            act.wait_ge(s["up"], i * (UI * MI) + (q + 1))
                            if m == 0:
                                act.wait_ge(s["down"], i * (UI * 4) + ((u - 1) * 4 + 1) if u >= 2 else i * (UI * 4) + 1)
                            if square:
                                act.wait_ge(s["h"], i * (UI * MI) + q if q >= 2 else i * (UI * MI) + 1)
                                act.activation(gated[:, m % 2, :], ps[:, 2 * (m % 2), :], ACT.Relu).then_inc(s["sil"], 1)
                            elif gate is None:
                                act.activation(hT[:, u % 2, m, :], ps[:, 2 * (m % 2), :], ACT.Relu,
                                               bias=b_sb[:, j, m:m + 1]).then_inc(s["h"], 1)
                            else:
                                act.wait_ge(s["h"], i * (UI * MI) + q if q >= 2 else i * (UI * MI) + 1)
                                act.activation(gated[:, m % 2, :], ps[:, 2 * (m % 2), :], ACT.Silu).then_inc(s["sil"], 1)

            @block.vector
            def _(dve):
                with dve.Fori(0, n_experts // 2) as i:
                    def add_out(u):
                        j, n = u // NB, u % NB
                        if n == 0:
                            dve.drain()
                        for t in range(4):
                            dve.wait_ge(s["down"], i * (UI * 4) + (u * 4 + t + 2))
                            x_t = c.x[:, 4 * n + t, :]
                            dve.scalar_tensor_tensor(out=x_t, in0=ps[:, 4 + t, 0:D], scalar=wgt[:, 4 * n + t, bass.ds(i * 2 + j, 1)],
                                                     in1=x_t, op0=ALU.mult, op1=ALU.add).then_inc(s["added"], 1)
                        if n == NB - 1:
                            dve.sem_inc(s[f"w_free{j}"], 1)

                    for u in range(UI + 1):
                        if u < UI and (gate is not None or square):
                            for m in range(MI):
                                q = u * MI + m
                                dve.wait_ge(s["sil"], i * (UI * MI) + (q + 1))
                                if m == 0:
                                    dve.wait_ge(s["down"], i * (UI * 4) + ((u - 1) * 4 + 1) if u >= 2 else i * (UI * 4) + 1)
                                other = gated[:, m % 2, :] if square else ps[:, 2 * (m % 2) + 1, :]
                                dve.tensor_tensor(hT[:, u % 2, m, :], gated[:, m % 2, :], other, ALU.mult).then_inc(s["h"], 1)
                        if u >= 1:
                            add_out(u - 1)


def routed_experts(c, name, feat, wgt, slot, inner, w_gate, w_up, w_down, row_slots, part_slots, head_rows):
    nc = c.nc
    C = CAPACITY
    MI = inner // P
    SC = -(-C // P)
    CW = [min(P, C - P * k) for k in range(SC)]
    BT = 512 // P
    NB = NT // BT
    PAIRS = NT // 2
    with Stage(nc, name) as st:
        parts = st.sb("parts", [P, 3, NT, D], BF16)
        sel = st.sb("sel", [P, 2, NT, C], BF16)
        xg = st.sb("xg", [P, KC, C])
        hT = st.sb("hT", [P, MI, C])
        gated = st.sb("gated", [P, 2, C])
        w1 = st.sb("w1", [P, 2, 2, KC, inner])
        w2 = st.sb("w2", [P, 2, MI, D])
        ep = st.sb("ep", [P, 3, SC, D], BF16)
        er = st.sb("er", [P, SC, D])
        selT = st.sb("selT", [P, 2, SC, 512], BF16)
        slotT = st.sb("slotT", [E, N])
        rsel = st.sb("rsel", [E, 1, P])
        heads = st.sb("heads", [E, E, P])
        row = st.sb("row", [P, C])
        col = st.sb("col", [P, SC])
        ps = st.ps("ps", [P, 8, 512])
        names = ("w_in0", "w_in1", "c_in", "parts0", "parts1", "slots", "slotT", "sel", "gath", "xg", "rsel", "up", "sil", "h",
                 "down", "bc", "selT", "ep", "sc", "added")
        s = {n: st.sem(n, primed=n in ("h", "added")) for n in names}
        with nc.Block() as block:
            @block.sync
            def _(sp):
                load_weights(sp, [(row[:], row_bcast(row_slots, C)), (col[:], part_slots), (heads[:], head_rows)], s["c_in"])
                for e in range(E):
                    j = e % 2
                    if e >= 2:
                        sp.wait_ge(s["down"], e - 1)
                    load_weights(sp, [(w1[:, j, 0], w_gate[e].rearrange("(k p) m -> p k m", p=P)),
                                      (w1[:, j, 1], w_up[e].rearrange("(k p) m -> p k m", p=P)),
                                      (w2[:, j], w_down[e].rearrange("(k p) m -> p k m", p=P))], s[f"w_in{j}"])
                sp.wait_ge(s["c_in"], 48)
                for j in range(2):
                    sp.wait_ge(s[f"w_in{j}"], E // 2 * 48)

            @block.gpsimd
            def _(pool):
                f = feat[:, NT // 2:NT, :]
                pool.tensor_copy(parts[:, 0, NT // 2:NT, :], f)
                pool.drain()
                pool.tensor_tensor(f, f, parts[:, 0, NT // 2:NT, :], ALU.subtract)
                pool.drain()
                pool.tensor_copy(parts[:, 1, NT // 2:NT, :], f)
                pool.drain()
                pool.tensor_tensor(parts[:, 2, NT // 2:NT, :], f, parts[:, 1, NT // 2:NT, :], ALU.subtract).then_inc(s["parts1"], 1)

            @block.tensor
            def _(pe):
                for t in range(NT):
                    last = pe.transpose(ps[0:E, 2 + t // BT, (t % BT) * P:(t % BT + 1) * P], slot[:, t, 0:E], c.ident[:])
                last.then_inc(s["slots"], 1)
                pe.wait_ge(s["c_in"], 48)
                pe.wait_ge(s["slotT"], 1)
                pe.wait_ge(s["parts0"], 1)
                with pe.Fori(0, E // 2) as i:
                    def gather(j):
                        for t in range(NT):
                            if j == 0 and t == NT // 2:
                                pe.wait_ge(s["parts1"], 1)
                            pe.wait_ge(s["sel"], i * (2 * NT) + (j * NT + t + 1))
                            for k in range(KC):
                                for a in range(3):
                                    last = pe.matmul(ps[:, k, 0:C], parts[:, a, t, k * P:(k + 1) * P], sel[:, j, t, :],
                                                     start=(t == 0 and a == 0), stop=(t == NT - 1 and a == 2))
                        last.then_inc(s["gath"], 1)

                    def spread(n):
                        pe.matmul(ps[:, 2 + n % 2, :], rsel[:, 0, :], slotT[:, n * 512:(n + 1) * 512],
                                  start=True, stop=True).then_inc(s["bc"], 1)

                    def feed_forward(j):
                        pe.wait_ge(s[f"w_in{j}"], (i + 1) * 48)
                        pe.wait_ge(s["xg"], i * 2 + (j + 1))
                        for m in range(MI):
                            pe.wait_ge(s["h"], i * (2 * MI) + max(j * MI + m, 1))
                            if m == 1:
                                pe.wait_ge(s["added"], i * (2 * PAIRS) + (j * PAIRS + 1))
                            for g in range(2):
                                for k in range(KC):
                                    last = pe.matmul(ps[:, 2 + 2 * (m % 2) + g, 0:C], w1[:, j, g, k, m * P:(m + 1) * P], xg[:, k, :],
                                                     start=(k == 0), stop=(k == KC - 1))
                            last.then_inc(s["up"], 1)
                        pe.wait_ge(s["rsel"], i * 2 + (j + 1))
                        pe.wait_ge(s["h"], i * (2 * MI) + (j * MI + MI))
                        spread(0)
                        spread(1)
                        pe.wait_ge(s["h"], i * (2 * MI) + (j * MI + MI + 1))
                        for k in range(SC):
                            for m in range(MI):
                                last = pe.matmul(ps[0:CW[k], 6 + k // 2, (k % 2) * D:(k % 2 + 1) * D], hT[:, m, k * P:k * P + CW[k]],
                                                 w2[:, j, m, :], start=(m == 0), stop=(m == MI - 1))
                        last.then_inc(s["down"], 1)

                    def scatter(j):
                        pe.wait_ge(s["ep"], i * 2 + (j + 1))
                        for pr in range(PAIRS):
                            n = pr // 2
                            if pr % 2 == 0:
                                pe.wait_ge(s["selT"], i * (2 * NB) + (j * NB + n + 1))
                            if pr >= 2:
                                pe.wait_ge(s["added"], i * (2 * PAIRS) + (j * PAIRS + pr))
                            for q in range(2):
                                t = 2 * (pr % 2) + q
                                for k in range(SC):
                                    for a in range(3):
                                        last = pe.matmul(ps[:, 4 + pr % 2, q * D:(q + 1) * D], selT[0:CW[k], n % 2, k, t * P:(t + 1) * P],
                                                         ep[0:CW[k], a, k, :], start=(k == 0 and a == 0), stop=(k == SC - 1 and a == 2))
                            last.then_inc(s["sc"], 1)
                            if pr % 2 == 1 and n + 2 < NB:
                                spread(n + 2)

                    gather(0)
                    feed_forward(0)
                    gather(1)
                    scatter(0)
                    feed_forward(1)
                    scatter(1)

            @block.scalar
            def _(act):
                with act.Fori(0, E // 2) as i:
                    for j in range(2):
                        act.wait_ge(s["gath"], i * 2 + (j + 1))
                        act.activation(xg[:], ps[:, 0:KC, 0:C], ACT.Copy).then_inc(s["xg"], 1)
                        for m in range(MI):
                            act.wait_ge(s["up"], i * (2 * MI) + (j * MI + m + 1))
                            act.wait_ge(s["h"], i * (2 * MI) + max(j * MI + m, 1))
                            act.activation(gated[:, m % 2, :], ps[:, 2 + 2 * (m % 2), 0:C], ACT.Silu).then_inc(s["sil"], 1)

            @block.vector
            def _(dve):
                f = feat[:, 0:NT // 2, :]
                dve.tensor_copy(parts[:, 0, 0:NT // 2, :], f)
                dve.drain()
                dve.tensor_tensor(f, f, parts[:, 0, 0:NT // 2, :], ALU.subtract)
                dve.wait_ge(s["slots"], 1)
                dve.tensor_copy(slotT[:].rearrange("e (n q) -> e n q", n=NB), ps[0:E, 2:2 + NB, :]).then_inc(s["slotT"], 1)
                dve.drain()
                dve.tensor_copy(parts[:, 1, 0:NT // 2, :], f)
                dve.drain()
                dve.tensor_tensor(parts[:, 2, 0:NT // 2, :], f, parts[:, 1, 0:NT // 2, :], ALU.subtract).then_inc(s["parts0"], 1)
                dve.wait_ge(s["c_in"], 48)

                def choose(t, j, e):
                    dve.tensor_scalar(sel[:, j, t, :], row[:], slot[:, t, e], None, ALU.is_equal).then_inc(s["sel"], 1)

                for t in range(NT):
                    choose(t, 0, slice(0, 1))
                with dve.Fori(0, E // 2) as i:
                    for j in range(2):
                        dve.tensor_copy(rsel[:], heads[:, bass.ds(i * 2 + j, 1), :]).then_inc(s["rsel"], 1)
                        dve.wait_ge(s["gath"], i * 2 + (j + 1))
                        for m in range(MI):
                            for t in range(m * NT // MI, (m + 1) * NT // MI):
                                choose(t, 1 - j, bass.ds(i * 2 + (j + 1), 1))
                            dve.wait_ge(s["sil"], i * (2 * MI) + (j * MI + m + 1))
                            dve.tensor_tensor(hT[:, m, :], gated[:, m % 2, :], ps[:, 3 + 2 * (m % 2), 0:C], ALU.mult).then_inc(s["h"], 1)

                        def compare(n):
                            dve.wait_ge(s["bc"], i * (2 * NB) + (j * NB + n + 1))
                            if n >= 2:
                                dve.wait_ge(s["sc"], i * (2 * PAIRS) + (j * PAIRS + 2 * (n - 1)))
                            for k in range(SC):
                                last = dve.tensor_scalar(selT[:, n % 2, k, :], ps[:, 2 + n % 2, :], col[:, k:k + 1], None, ALU.is_equal)
                            last.then_inc(s["selT"], 1)

                        compare(0)
                        compare(1)
                        dve.wait_ge(s["down"], i * 2 + (j + 1))
                        full, rest = SC // 2 * 2, SC % 2
                        out = [(er[:, 0:full, :], [ep[:, a, 0:full, :] for a in range(3)],
                                ps[:, 6, :].rearrange("p (k d) -> p k d", d=D))]
                        if rest:
                            out.append((er[0:CW[-1], full:SC, :], [ep[0:CW[-1], a, full:SC, :] for a in range(3)],
                                        ps[0:CW[-1], 7:8, 0:D]))
                        for r_, e_, o_ in out:
                            dve.tensor_copy(e_[0], o_)
                        dve.drain()
                        for r_, e_, o_ in out:
                            dve.tensor_tensor(r_, o_, e_[0], ALU.subtract)
                        dve.drain()
                        for r_, e_, o_ in out:
                            dve.tensor_copy(e_[1], r_)
                        dve.drain()
                        for r_, e_, o_ in out:
                            last = dve.tensor_tensor(e_[2], r_, e_[1], ALU.subtract)
                        last.then_inc(s["ep"], 1)
                        for pr in range(PAIRS):
                            dve.wait_ge(s["sc"], i * (2 * PAIRS) + (j * PAIRS + pr + 1))
                            for q in range(2):
                                x_t = c.x[:, 2 * pr + q, :]
                                last = dve.scalar_tensor_tensor(out=x_t, in0=ps[:, 4 + pr % 2, q * D:(q + 1) * D],
                                                                scalar=wgt[:, 2 * pr + q, bass.ds(i * 2 + j, 1)], in1=x_t,
                                                                op0=ALU.mult, op1=ALU.add)
                            last.then_inc(s["added"], 1)
                            if pr % 2 == 1 and pr // 2 + 2 < NB:
                                compare(pr // 2 + 2)


def add_expert_bias(c, name, wgt, b2):
    nc = c.nc
    with Stage(nc, name) as st:
        wT = st.sb("wT", [E, N])
        b_sb = st.sb("b", [E, D])
        tps = st.ps("tps", [P, 4, 512])
        ps = st.ps("ps", [P, 4, 512])
        w_in, turned, copied, mult, added = (st.sem(n) for n in ("w_in", "turned", "copied", "mult", "added"))
        with nc.Block() as block:
            @block.sync
            def _(sp):
                sp.dma_start(b_sb[:], b2).then_inc(w_in, 16)
                sp.wait_ge(w_in, 16)

            @block.tensor
            def _(pe):
                for t in range(NT):
                    last = pe.transpose(tps[0:E, t // 4, (t % 4) * P:(t % 4 + 1) * P], wgt[:, t, 0:E], c.ident[:])
                last.then_inc(turned, 1)
                pe.wait_ge(w_in, 16)
                pe.wait_ge(copied, 1)
                for t in range(NT):
                    if t >= 4:
                        pe.wait_ge(added, t - 3)
                    pe.matmul(ps[:, t % 4, 0:D], wT[:, t * P:(t + 1) * P], b_sb[:], start=True, stop=True).then_inc(mult, 1)

            @block.scalar
            def _(act):
                act.wait_ge(turned, 1)
                act.activation(wT[:].rearrange("e (n q) -> e n q", n=4), tps[0:E, :, :], ACT.Copy).then_inc(copied, 1)

            @block.vector
            def _(dve):
                for t in range(NT):
                    dve.wait_ge(mult, t + 1)
                    dve.tensor_tensor(c.x[:, t, :], c.x[:, t, :], ps[:, t % 4, 0:D], ALU.add).then_inc(added, 1)


def softplus_attention(c, name, qT, kT, v, out):
    nc = c.nc
    units = [(b, qb, j) for b in range(B) for qb in range(S // 512) for j in range(4 * (qb + 1))]
    R = 3
    with Stage(nc, name) as st:
        la = st.sb("la", [P, R, 512])
        wt = st.sb("wt", [P, R, 512])
        ps = st.ps("ps", [P, R, 512])
        po = st.ps("po", [P, 2, 2, 512])
        s = {n: st.sem(n) for n in ("score", "abs", "log", "w", "pv", "read")}
        blocks = {}
        for u, (b, qb, j) in enumerate(units):
            blocks.setdefault((b, qb), []).append(u)
        order = list(blocks)
        with nc.Block() as block:
            @block.tensor
            def _(pe):
                def scores(u):
                    b, qb, j = units[u]
                    if u >= R:
                        pe.wait_ge(s["w"], u - R + 1)
                    for k in range(KC):
                        last = pe.matmul(ps[:, u % R, :], qT[:, k, b * S + j * P:b * S + (j + 1) * P],
                                         kT[:, k, b * S + qb * 512:b * S + (qb + 1) * 512], start=(k == 0), stop=(k == KC - 1))
                    last.then_inc(s["score"], 1)

                def weigh(u):
                    b, qb, j = units[u]
                    o = order.index((b, qb))
                    if j == 0 and o >= 2:
                        pe.wait_ge(s["read"], o - 1)
                    pe.wait_ge(s["w"], u + 1)
                    for t in range(max(0, j - 4 * qb), 4):
                        last = pe.matmul(po[:, o % 2, t // 2, (t % 2) * D:(t % 2 + 1) * D], wt[:, u % R, t * P:(t + 1) * P],
                                         v[:, b * ST + j, :], start=(j == 0 and t % 2 == 0), stop=(j == 4 * qb + t),
                                         skip_group_check=True)
                    last.then_inc(s["pv"], 1)

                for u in range(len(units) + 2):
                    if u < len(units):
                        scores(u)
                    if u >= 2:
                        weigh(u - 2)

            @block.scalar
            def _(act):
                for u in range(len(units)):
                    act.wait_ge(s["score"], u + 1)
                    if u >= R:
                        act.wait_ge(s["w"], u - R + 1)
                    a = la[:, u % R, :]
                    act.activation(a, ps[:, u % R, :], ACT.Abs, scale=D ** -0.5).then_inc(s["abs"], 1)
                    act.drain()
                    act.activation(a, a, ACT.Exp, scale=-1.0)
                    act.drain()
                    act.activation(a, a, ACT.Ln, bias=1.0).then_inc(s["log"], 1)

            @block.vector
            def _(dve):
                def copy_out(o):
                    b, qb = order[o]
                    dve.wait_ge(s["pv"], blocks[(b, qb)][-1] + 1)
                    dve.tensor_copy(out[:, b * ST + 4 * qb:b * ST + 4 * qb + 4, :].rearrange("p (g t) d -> p g (t d)", g=2),
                                    po[:, o % 2, :, :]).then_inc(s["read"], 1)

                for u, (b, qb, j) in enumerate(units):
                    dve.wait_ge(s["abs"], u + 1)
                    if u >= R:
                        dve.wait_ge(s["pv"], u - R + 1)
                    wu = wt[:, u % R, :]
                    dve.tensor_scalar(wu, ps[:, u % R, :], D ** -0.5, 0.0, ALU.mult, ALU.max)
                    dve.drain()
                    dve.wait_ge(s["log"], u + 1)
                    last = dve.tensor_tensor(wu, wu, la[:, u % R, :], ALU.add)
                    jj = j - 4 * qb
                    if jj >= 0:
                        dve.drain()
                        dg = wt[:, u % R, jj * P:(jj + 1) * P]
                        last = dve.tensor_tensor(dg, dg, c.lower[:], ALU.mult)
                    last.then_inc(s["w"], 1)
                    o = order.index((b, qb))
                    if j == 1 and o >= 1:
                        copy_out(o - 1)
                copy_out(len(order) - 1)


def softmax_attention(c, name, qT, kT, v, out, resid, causal):
    nc = c.nc
    with Stage(nc, name) as st:
        upper = st.sb("upper", [P, P])
        nm = st.sb("nm", [P, 2, 2])
        total = st.sb("total", [P, 2, 2])
        p_ = st.sb("p", [P, 2, S])
        pT = st.sb("pT", [P, 2, S])
        ps = st.ps("ps", [P, 2, 2, 512])
        pTp = st.ps("pTp", [P, 2, 512])
        po = st.ps("po", [P, 2, 512])
        s = {n: st.sem(n) for n in ("mask", "score", "nmax", "exp", "turned", "copied", "pv", "out")}

        def keys(t):
            b, q = t // ST, t % ST
            return (b * S, (q + 1) * P) if causal else (b * S2, S2)

        with nc.Block() as block:
            @block.gpsimd
            def _(pool):
                pool.memset(upper[:], 0.0)
                pool.drain()
                pool.affine_select(out=upper[:], in_=upper[:], compare_op=ALU.is_ge, fill=-1e30, base=0,
                                   pattern=[[-1, P]], channel_multiplier=1).then_inc(s["mask"], 1)

            @block.tensor
            def _(pe):
                def scores(t):
                    k0, nk = keys(t)
                    if t >= 2:
                        pe.wait_ge(s["exp"], t - 1)
                    for a in range(0, nk, 512):
                        w = min(512, nk - a)
                        for k in range(KC):
                            last = pe.matmul(ps[:, t % 2, a // 512, 0:w], qT[:, k, t * P:(t + 1) * P],
                                             kT[:, k, k0 + a:k0 + a + w], start=(k == 0), stop=(k == KC - 1))
                    last.then_inc(s["score"], 1)

                def weigh(t):
                    k0, nk = keys(t)
                    pe.wait_ge(s["exp"], t + 1)
                    if t >= 1:
                        pe.wait_ge(s["copied"], t)
                    nj = (nk + P - 1) // P
                    for j in range(nj):
                        w = min(P, nk - j * P)
                        last = pe.transpose(pTp[0:w, j // 4, (j % 4) * P:(j % 4 + 1) * P], p_[:, t % 2, j * P:j * P + w], c.ident[:])
                    last.then_inc(s["turned"], 1)
                    pe.wait_ge(s["copied"], t + 1)
                    if t >= 2:
                        pe.wait_ge(s["out"], t - 1)
                    for j in range(nj):
                        w = min(P, nk - j * P)
                        vt = v[0:w, t // ST * ST + j, :] if causal else v[0:w, t // ST, :]
                        last = pe.matmul(po[:, t % 2, 0:D], pT[0:w, t % 2, j * P:(j + 1) * P], vt, start=(j == 0), stop=(j == nj - 1))
                    last.then_inc(s["pv"], 1)

                for t in range(NT + 1):
                    if t < NT:
                        scores(t)
                    if t >= 1:
                        weigh(t - 1)

            @block.scalar
            def _(act):
                for t in range(NT):
                    k0, nk = keys(t)
                    act.wait_ge(s["nmax"], t + 1)
                    if t >= 2:
                        act.wait_ge(s["turned"], t - 1)
                    g, w = (nk // 512, 512) if nk > 512 and nk % 512 == 0 else (1, nk)
                    act.activation(p_[:, t % 2, 0:nk], ps[:, t % 2].rearrange("p g n -> p (g n)")[:, 0:nk], ACT.Exp, scale=D ** -0.5,
                                   bias=nm[:, t % 2, 1:2], accum_out=total[:, t % 2, 0:1]).then_inc(s["exp"], 1)
                    act.wait_ge(s["turned"], t + 1)
                    if t >= 2:
                        act.wait_ge(s["pv"], t - 1)
                    rows = min(nk, P)
                    cols = (nk + P - 1) // P * P
                    act.activation(pT[0:rows, t % 2, 0:cols], pTp[:].rearrange("p g n -> p (g n)")[0:rows, 0:cols],
                                   ACT.Copy).then_inc(s["copied"], 1)

            @block.vector
            def _(dve):
                dve.wait_ge(s["mask"], 1)

                def top(t):
                    k0, nk = keys(t)
                    dve.wait_ge(s["score"], t + 1)
                    flat = ps[:, t % 2].rearrange("p g n -> p (g n)")
                    if causal:
                        dg = flat[:, nk - P:nk]
                        dve.tensor_tensor(dg, dg, upper[:], ALU.add)
                        dve.drain()
                    dve.tensor_reduce(nm[:, t % 2, 0:1], flat[:, 0:nk], AX.X, ALU.max, negate=True)
                    dve.drain()
                    dve.tensor_scalar(nm[:, t % 2, 1:2], nm[:, t % 2, 0:1], D ** -0.5, None, ALU.mult).then_inc(s["nmax"], 1)

                def finish(t):
                    dve.wait_ge(s["exp"], t + 1)
                    dve.reciprocal(total[:, t % 2, 1:2], total[:, t % 2, 0:1])
                    dve.drain()
                    dve.wait_ge(s["pv"], t + 1)
                    dve.scalar_tensor_tensor(out=out[:, t, :], in0=po[:, t % 2, 0:D], scalar=total[:, t % 2, 1:2],
                                             in1=resid[:, t, :], op0=ALU.mult, op1=ALU.add).then_inc(s["out"], 1)

                for t in range(NT + 1):
                    if t < NT:
                        top(t)
                    if t >= 1:
                        finish(t - 1)


def load(c, name, dst, src):
    with Stage(c.nc, name) as st:
        came = st.sem("in")
        with c.nc.Block() as block:
            @block.sync
            def _(sp):
                sp.dma_start(dst[:], src).then_inc(came, 16)
                sp.wait_ge(came, 16)


def add_to_x(c, name, src, relu=False):
    with Stage(c.nc, name) as st:
        with c.nc.Block() as block:
            @block.vector
            def _(dve):
                if relu:
                    dve.scalar_tensor_tensor(out=c.x[:], in0=src[:], scalar=0.0, in1=c.x[:], op0=ALU.max, op1=ALU.add)
                else:
                    dve.tensor_tensor(c.x[:], src[:], c.x[:], ALU.add)


MAGIC = 12582912.0


def quantize_weights(c, name, w, dst, size):
    nc = c.nc
    K, M = w.shape
    k_ = K // P
    with Stage(nc, name) as st:
        w_sb = st.sb("w", [P, k_, M])
        part = st.sb("part", [P, 2])
        ps = st.ps("ps", [P, 8])
        w_in, summed, total = st.sem("w_in"), st.sem("summed"), st.sem("total")
        with nc.Block() as block:
            @block.sync
            def _(sp):
                sp.dma_start(w_sb[:], w.rearrange("(k p) m -> p k m", p=P)).then_inc(w_in, 16)
                sp.wait_ge(w_in, 16)

            @block.tensor
            def _(pe):
                pe.wait_ge(summed, 1)
                pe.matmul(ps[:, 0:1], c.ones[:], part[:, 0:1], start=True, stop=True).then_inc(total, 1)

            @block.vector
            def _(dve):
                dve.wait_ge(w_in, 16)
                dve.tensor_reduce(part[:, 0:1], w_sb[:], AX.XY, ALU.add, apply_absolute_value=True).then_inc(summed, 1)
                dve.wait_ge(total, 1)
                dve.tensor_scalar(size[:], ps[:, 0:1], 1.0 / (K * M), 1e-5, ALU.mult, ALU.max)
                dve.drain()
                dve.reciprocal(part[:, 1:2], size[:])
                dve.drain()
                dve.tensor_scalar(w_sb[:], w_sb[:], part[:, 1:2], -1.0, ALU.mult, ALU.max)
                dve.drain()
                dve.tensor_scalar(w_sb[:], w_sb[:], 1.0, MAGIC, ALU.min, ALU.add)
                dve.drain()
                dve.tensor_scalar(dst[:], w_sb[:], MAGIC, None, ALU.subtract)


def quantized_ffn(c, name, r, w1q, s1, w2q, s2, b1, b2):
    nc = c.nc
    F = w1q.shape[2]
    FC = F // P
    with Stage(nc, name) as st:
        b1_sb = st.sb("b1", [P, F])
        b2_sb = st.sb("b2", [P, D])
        idb = st.sb("idb", [P, P], BF16)
        am = st.sb("am", [P, 6, NT])
        am2 = st.sb("am2", [P, 8, NT])
        t_f = st.sb("t_f", [P, 2, F])
        q = st.sb("q", [P, 2, F], BF16)
        qT = st.sb("qT", [P, 2, F], BF16)
        g = st.sb("g", [P, NT, F])
        h = st.sb("h", [P, 2, F])
        sq = st.sb("sq", [P, F])
        tp = st.ps("tp", [P, 2, 1024], BF16)
        ps = st.ps("ps", [P, 2, 2, 512])
        names = ("w_in", "q", "turned", "qT", "mult", "h", "gelu", "stats", "var", "sd", "q2", "turned2", "qT2", "mult2", "added")
        s = {n: st.sem(n, primed=n in ("turned", "mult", "gelu", "turned2", "mult2", "qT", "qT2", "h", "added",)) for n in names}
        HALF = NT // 2

        def quantize(dve, dst, src, tmp, scale):
            dve.tensor_scalar(tmp, src, scale, -128.0, ALU.mult, ALU.max)
            dve.drain()
            dve.tensor_scalar(tmp, tmp, 127.0, MAGIC, ALU.min, ALU.add)
            dve.drain()
            return dve.tensor_scalar(dst, tmp, MAGIC, None, ALU.subtract)

        with nc.Block() as block:
            @block.sync
            def _(sp):
                load_weights(sp, [(b1_sb[:], row_bcast(b1, F)), (b2_sb[:], row_bcast(b2, D))], s["w_in"])
                sp.wait_ge(s["w_in"], 32)

            @block.vector
            def _(dve):
                dve.tensor_copy(idb[:], c.ident[:])
                dve.tensor_reduce(am[:, 0, :], r[:], AX.X, ALU.max, apply_absolute_value=True)
                dve.drain()
                dve.tensor_scalar(am[:, 0, :], am[:, 0, :], 1e-5, 1.0 / 127.0, ALU.max, ALU.mult)
                dve.drain()
                dve.reciprocal(am[:, 1, :], am[:, 0, :])
                dve.tensor_scalar(am[:, 2, :], am[:, 0, :], s1[:, 0:1], None, ALU.mult)
                dve.drain()
                dve.wait_ge(s["w_in"], 32)
                with dve.Fori(0, HALF) as i:
                    for j in range(2):
                        t = bass.ds(i * 2 + j, 1)
                        dve.wait_ge(s["turned"], i * 2 + 1)
                        quantize(dve, q[:, j:j + 1, 0:D], r[:, t, :], t_f[:, j:j + 1, 0:D], am[:, 1, t]).then_inc(s["q"], 1)
                    for j in range(2):
                        t = bass.ds(i * 2 + j, 1)
                        dve.wait_ge(s["mult"], i * 2 + (j + 2))
                        dve.wait_ge(s["gelu"], i * 2 + 1)
                        dve.scalar_tensor_tensor(out=h[:, j, :].rearrange("p (a n) -> p a n", a=2), in0=ps[:, j], scalar=am[:, 2, t],
                                                 in1=b1_sb[:].rearrange("p (a n) -> p a n", a=2), op0=ALU.mult,
                                                 op1=ALU.add).then_inc(s["h"], 1)
                dve.wait_ge(s["gelu"], NT + 1)
                dve.tensor_reduce(am2[:, 0, :], g[:], AX.X, ALU.max, apply_absolute_value=True)
                dve.tensor_scalar(am2[:, 1, :], am2[:, 7, :], 1.0 / F, 1e-5, ALU.mult, ALU.add).then_inc(s["var"], 1)
                dve.drain()
                dve.wait_ge(s["sd"], 1)
                dve.reciprocal(am2[:, 2, :], am2[:, 1, :])
                dve.drain()
                dve.tensor_tensor(am2[:, 3, :], am2[:, 0, :], am2[:, 2, :], ALU.mult)
                dve.drain()
                dve.tensor_scalar(am2[:, 3, :], am2[:, 3, :], 1e-5, 1.0 / 127.0, ALU.max, ALU.mult)
                dve.drain()
                dve.reciprocal(am2[:, 4, :], am2[:, 3, :])
                dve.drain()
                dve.tensor_tensor(am2[:, 5, :], am2[:, 4, :], am2[:, 2, :], ALU.mult)
                dve.tensor_scalar(am2[:, 6, :], am2[:, 3, :], s2[:, 0:1], None, ALU.mult)
                dve.drain()
                with dve.Fori(0, HALF) as i:
                    for j in range(2):
                        t = bass.ds(i * 2 + j, 1)
                        dve.wait_ge(s["turned2"], i * 2 + 1)
                        quantize(dve, q[:, j:j + 1, :], g[:, t, :], t_f[:, j:j + 1, :], am2[:, 5, t]).then_inc(s["q2"], 1)
                    for j in range(2):
                        t = bass.ds(i * 2 + j, 1)
                        dve.wait_ge(s["mult2"], i * 2 + (j + 2))
                        dve.scalar_tensor_tensor(out=h[:, j:j + 1, 0:D], in0=ps[:, j, 0:1, 0:D], scalar=am2[:, 6, t],
                                                 in1=c.x[:, t, :], op0=ALU.mult, op1=ALU.add).then_inc(s["added"], 1)
                        dve.drain()
                        dve.tensor_tensor(c.x[:, t, :], h[:, j:j + 1, 0:D], b2_sb[:].rearrange("p (a d) -> p a d", a=1), ALU.add)

            @block.tensor
            def _(pe):
                for q_s, t_s, qT_s, m_s, h_s, nk, wide in ((s["q"], s["turned"], s["qT"], s["mult"], s["h"], KC, True),
                                                           (s["q2"], s["turned2"], s["qT2"], s["mult2"], s["added"], FC, False)):
                    with pe.Fori(0, HALF) as i:
                        for j in range(2):
                            pe.wait_ge(q_s, i * 2 + (j + 1))
                            pe.wait_ge(qT_s, i * 2 + 1)
                            for k in range(nk):
                                last = pe.transpose(tp[:, j, k * P:(k + 1) * P], q[:, j, k * P:(k + 1) * P], idb[:])
                            last.then_inc(t_s, 1)
                        for j in range(2):
                            pe.wait_ge(qT_s, i * 2 + (j + 2))
                            pe.wait_ge(h_s, i * 2 + 1)
                            for n in range(F // 512 if wide else 1):
                                for k in range(nk):
                                    rhs = w1q[:, k, n * 512:(n + 1) * 512] if wide else w2q[:, k, :]
                                    last = pe.matmul(ps[:, j, n, 0:512 if wide else D], qT[:, j, k * P:(k + 1) * P], rhs,
                                                     start=(k == 0), stop=(k == nk - 1))
                            last.then_inc(m_s, 1)

            @block.scalar
            def _(act):
                with act.Fori(0, HALF) as i:
                    for j in range(2):
                        act.wait_ge(s["turned"], i * 2 + (j + 2))
                        act.wait_ge(s["mult"], i * 2 + 1)
                        act.activation(qT[:, j, 0:D], tp[:, j, 0:D], ACT.Copy).then_inc(s["qT"], 1)
                    for j in range(2):
                        act.wait_ge(s["h"], i * 2 + (j + 2))
                        g_t = g[:, bass.ds(i * 2 + j, 1), :]
                        act.activation(g_t, h[:, j:j + 1, :], ACT.Gelu)
                        act.drain()
                        act.activation(sq[:].rearrange("p (a n) -> p a n", a=1), g_t, ACT.Square,
                                       accum_out=am2[:, 7, bass.ds(i * 2 + j, 1)]).then_inc(s["gelu"], 1)
                        act.drain()
                act.wait_ge(s["var"], 1)
                act.activation(am2[:, 1, :], am2[:, 1, :], ACT.Sqrt).then_inc(s["sd"], 1)
                with act.Fori(0, HALF) as i:
                    for j in range(2):
                        act.wait_ge(s["turned2"], i * 2 + (j + 2))
                        act.wait_ge(s["mult2"], i * 2 + 1)
                        act.activation(qT[:, j, :], tp[:, j, :], ACT.Copy).then_inc(s["qT2"], 1)


def per_head_T(c, name, qT, kT, gT, wq, wk, scale):
    nc = c.nc
    with Stage(nc, name) as st:
        w = st.sb("w", [P, 2, KC, P])
        ps = st.ps("ps", [P, 2, 4, 512])
        w_in, mult_q, mult_k, out_q, out_k = (st.sem(n) for n in ("w_in", "mult_q", "mult_k", "out_q", "out_k"))
        units = [(k, n) for k in range(KC) for n in range(N // 512)]
        with nc.Block() as block:
            @block.sync
            def _(sp):
                load_weights(sp, [(w[:, i], v.rearrange("k p m -> p k m")) for i, v in enumerate((wq, wk))], w_in)
                sp.wait_ge(w_in, 32)

            @block.tensor
            def _(pe):
                pe.wait_ge(w_in, 32)
                for u, (k, n) in enumerate(units):
                    for i, (t, mult, out) in enumerate(((qT, mult_q, out_q), (kT, mult_k, out_k))):
                        if u >= 4:
                            pe.wait_ge(out, u - 3)
                        pe.matmul(ps[:, i, u % 4, :], w[:, i, k, :], t[:, k, n * 512:(n + 1) * 512],
                                  start=True, stop=True).then_inc(mult, 1)

            @block.scalar
            def _(act):
                for u, (k, n) in enumerate(units):
                    act.wait_ge(mult_q, u + 1)
                    act.activation(qT[:, k, n * 512:(n + 1) * 512], ps[:, 0, u % 4, :], ACT.Copy).then_inc(out_q, 1)

            @block.vector
            def _(dve):
                for u, (k, n) in enumerate(units):
                    cols = slice(n * 512, (n + 1) * 512)
                    dve.wait_ge(mult_k, u + 1)
                    dve.scalar_tensor_tensor(out=kT[:, k, cols], in0=ps[:, 1, u % 4, :], scalar=scale, in1=gT[:, k, cols],
                                             op0=ALU.mult, op1=ALU.mult).then_inc(out_k, 1)


def recurrence(c, name, qT, kT, vT, decay_logits, spread, gather):
    nc = c.nc
    with Stage(nc, name) as st:
        dl = st.sb("dl", [P, KC])
        sg = st.sb("sg", [P, 2, DH, P])
        kv = st.sb("kv", [P, 2, S])
        M = st.sb("M", [P, 2, S])
        qM = st.sb("qM", [P, 2, S])
        qb = st.sb("qb", [P, KC, S])
        vb = st.ps("vb", [P, 2, 2, 512])
        y = st.ps("y", [P, KC, 2, 512])
        names = ("w_in", "decay", "spread", "kv", "M", "q", "qM", "gathered", "y_out")
        s = {n: st.sem(n, primed=n in ("kv", "y_out", "qM", "gathered",)) for n in names}
        U = KC * DH
        with nc.Block() as block:
            @block.sync
            def _(sp):
                load_weights(sp, [(dl[:], decay_logits), (sg[:, 0], spread), (sg[:, 1], gather)], s["w_in"])
                sp.wait_ge(s["w_in"], 48)

            @block.tensor
            def _(pe):
                pe.wait_ge(s["w_in"], 48)
                with pe.Fori(0, B) as bi:
                    def copies(u):
                        k, d = u // DH, u % DH
                        pe.wait_ge(s["kv"], bi * U + u if u >= 2 else bi * U + 1)
                        for h in range(2):
                            last = pe.matmul(vb[:, u % 2, h, :], sg[:, 0, d, :], vT[:, k, bass.ds(bi * S + h * 512, 512)],
                                             start=True, stop=True)
                        last.then_inc(s["spread"], 1)

                    def sums(u):
                        k, d = u // DH, u % DH
                        if d == 0:
                            pe.wait_ge(s["y_out"], bi * KC + 1)
                        pe.wait_ge(s["qM"], bi * U + (u + 2))
                        for h in range(2):
                            last = pe.matmul(y[:, k, h, :], sg[:, 1, d, :], qM[:, u % 2, h * 512:(h + 1) * 512],
                                             start=(d == 0), stop=(d == DH - 1))
                        last.then_inc(s["gathered"], 1)

                    for u in range(U + 2):
                        if u < U:
                            copies(u)
                        if u >= 2:
                            sums(u - 2)

            @block.vector
            def _(dve):
                dve.wait_ge(s["decay"], 1)
                with dve.Fori(0, B) as bi:
                    for u in range(U):
                        k, d = u // DH, u % DH
                        dve.wait_ge(s["spread"], bi * U + (u + 1))
                        dve.tensor_tensor(kv[:, u % 2, :].rearrange("p (h n) -> p h n", h=2),
                                          kT[:, k, bass.ds(bi * S, S)].rearrange("p (h n) -> p h n", h=2), vb[:, u % 2], ALU.mult).then_inc(s["kv"], 1)
                        dve.drain()
                        dve.wait_ge(s["qM"], bi * U + u if u >= 2 else bi * U + 1)
                        dve.tensor_tensor_scan(M[:, u % 2, :], dl[:, k:k + 1].broadcast_to([P, S]), kv[:, u % 2, :], 0.0,
                                               ALU.mult, ALU.add).then_inc(s["M"], 1)

            @block.gpsimd
            def _(pool):
                with pool.Fori(0, B) as bi:
                    for u in range(U):
                        k = u // DH
                        pool.wait_ge(s["q"], bi + 1)
                        pool.wait_ge(s["M"], bi * U + (u + 1))
                        pool.wait_ge(s["gathered"], bi * U + u if u >= 2 else bi * U + 1)
                        pool.tensor_tensor(qM[:, u % 2, :], M[:, u % 2, :], qb[:, k, :], ALU.mult).then_inc(s["qM"], 1)

            @block.scalar
            def _(act):
                act.wait_ge(s["w_in"], 48)
                act.activation(dl[:], dl[:], ACT.Sigmoid).then_inc(s["decay"], 1)
                with act.Fori(0, B) as bi:
                    act.activation(qb[:], qT[:, :, bass.ds(bi * S, S)], ACT.Copy).then_inc(s["q"], 1)
                    for k in range(KC):
                        act.wait_ge(s["gathered"], bi * U + ((k + 1) * DH + 1))
                        act.activation(vT[:, k, bass.ds(bi * S, S)].rearrange("p (h n) -> p h n", h=2), y[:, k], ACT.Copy).then_inc(s["y_out"], 1)


def cross_heads(c, name, qT, kT, v, out, clip=None):
    nc = c.nc
    HK = P // DH
    W = HK * S2
    HW = W // 2
    with Stage(nc, name) as st:
        hm = st.sb("hm", [P, HK])
        kb = st.sb("kb", [P, KC, B, HK, S2])
        sc = st.sb("sc", [P, 2, HK, S2])
        ex = st.sb("ex", [P, 2, HK, S2])
        mx = st.sb("mx", [P, 2, HK])
        sm = st.sb("sm", [P, 2, HK])
        eT = st.sb("eT", [S2, 2, HK, P])
        ps = st.ps("ps", [P, 2, 2, 512])
        tp = st.ps("tp", [P, 2, 512])
        po = st.ps("po", [P, 2, 512])
        names = ("w_in", "kb", "score", "read", "shift", "exp", "turned", "copied", "pv", "out")
        s = {n: st.sem(n) for n in names}
        units = [(t, k) for t in range(NT) for k in range(KC)]
        with nc.Block() as block:
            @block.sync
            def _(sp):
                sp.dma_start(hm[:], c.dram["head_mask"]).then_inc(s["w_in"], 16)
                sp.wait_ge(s["w_in"], 16)

            @block.tensor
            def _(pe):
                pe.wait_ge(s["kb"], 1)

                def scores(u):
                    t, k = units[u]
                    if u >= 2:
                        pe.wait_ge(s["read"], u - 1)
                    rhs = kb[:, k, t // ST].rearrange("p h n -> p (h n)")
                    for a in range(2):
                        last = pe.matmul(ps[:, u % 2, a, 0:HW], qT[:, k, t * P:(t + 1) * P], rhs[:, a * HW:(a + 1) * HW],
                                         start=True, stop=True)
                    last.then_inc(s["score"], 1)

                def weigh(u):
                    t, k = units[u]
                    pe.wait_ge(s["exp"], u + 1)
                    if u >= 1:
                        pe.wait_ge(s["copied"], u)
                    for h in range(HK):
                        last = pe.transpose(tp[0:S2, h // 4, (h % 4) * P:(h % 4 + 1) * P], ex[:, u % 2, h, :], c.ident[:])
                    last.then_inc(s["turned"], 1)
                    pe.wait_ge(s["copied"], u + 1)
                    if u >= 2:
                        pe.wait_ge(s["out"], u - 1)
                    for h in range(HK):
                        col = k * P + h * DH
                        last = pe.matmul(po[:, u % 2, h * DH:(h + 1) * DH], eT[:, u % 2, h, :], v[0:S2, t // ST, col:col + DH],
                                         start=True, stop=True)
                    last.then_inc(s["pv"], 1)

                for u in range(len(units) + 1):
                    if u < len(units):
                        scores(u)
                    if u >= 1:
                        weigh(u - 1)

            @block.scalar
            def _(act):
                for u in range(len(units)):
                    act.wait_ge(s["shift"], u + 1)
                    if u >= 2:
                        act.wait_ge(s["turned"], u - 1)
                    act.activation(ex[:, u % 2], sc[:, u % 2], ACT.Exp, scale=DH ** -0.5).then_inc(s["exp"], 1)
                    act.wait_ge(s["turned"], u + 1)
                    if u >= 2:
                        act.wait_ge(s["pv"], u - 1)
                    act.activation(eT[:, u % 2].rearrange("p (a h) n -> p a (h n)", a=2), tp[0:S2, :, :], ACT.Copy).then_inc(s["copied"], 1)

            @block.vector
            def _(dve):
                dve.wait_ge(s["w_in"], 16)
                shape = [P, HK, S2]
                for k in range(KC):
                    for b in range(B):
                        keys = kT[:, k:k + 1, b * S2:(b + 1) * S2].broadcast_to(shape)
                        mask = hm[:].rearrange("p (h a) -> p h a", a=1).broadcast_to(shape)
                        dve.tensor_tensor(kb[:, k, b], keys, mask, ALU.mult)
                dve.drain()
                dve.sem_inc(s["kb"], 1)

                def top(u):
                    dve.wait_ge(s["score"], u + 1)
                    if u >= 2:
                        dve.wait_ge(s["exp"], u - 1)
                    o, src = sc[:, u % 2].rearrange("p (a h) n -> p a (h n)", a=2), ps[:, u % 2, :, 0:HW]
                    if clip is None:
                        dve.tensor_copy(o, src).then_inc(s["read"], 1)
                    else:
                        dve.tensor_scalar(o, src, clip, -clip, ALU.min, ALU.max).then_inc(s["read"], 1)
                    dve.drain()
                    dve.tensor_reduce(mx[:, u % 2, :], sc[:, u % 2], AX.X, ALU.max)
                    dve.drain()
                    m = mx[:, u % 2, :].rearrange("p (h a) -> p h a", a=1).broadcast_to(shape)
                    dve.tensor_tensor(sc[:, u % 2], sc[:, u % 2], m, ALU.subtract).then_inc(s["shift"], 1)

                def finish(u):
                    t, k = units[u]
                    dve.wait_ge(s["exp"], u + 1)
                    dve.tensor_reduce(sm[:, u % 2, :], ex[:, u % 2], AX.X, ALU.add)
                    dve.drain()
                    dve.reciprocal(sm[:, u % 2, :], sm[:, u % 2, :])
                    dve.drain()
                    dve.wait_ge(s["pv"], u + 1)
                    r = sm[:, u % 2, :].rearrange("p (h a) -> p h a", a=1).broadcast_to([P, HK, DH])
                    dve.tensor_tensor(out[:, t, k * P:(k + 1) * P].rearrange("p (h d) -> p h d", h=HK),
                                      po[:, u % 2, 0:P].rearrange("p (h d) -> p h d", h=HK), r, ALU.mult).then_inc(s["out"], 1)

                for u in range(len(units) + 1):
                    if u < len(units):
                        top(u)
                    if u >= 1:
                        finish(u - 1)


def tree_ffn(c, name, srcT, w_in_T, b_in, w_out_T):
    nc = c.nc
    DEPTH, PAR = 7, 8
    NODES = 2 ** (DEPTH + 1) - 1
    W = PAR * NODES
    Q = W // 4
    WC = w_out_T.shape[0] // P
    with Stage(nc, name) as st:
        wi = st.sb("wi", [P, KC, W])
        bi_sb = st.sb("bi", [P, W])
        wo = st.sb("wo", [P, WC, D])
        l = st.sb("l", [P, 2, W])
        go = st.sb("go", [P, 2, W])
        on = st.sb("on", [P, 2, W])
        act_ = st.sb("act", [P, 2, WC * P])
        aT = st.sb("aT", [P, 2, 4, P])
        xt = st.sb("xt", [P, 2, KC, P])
        ps = st.ps("ps", [P, 4, 512])
        tp = st.ps("tp", [P, 2, 512])
        po = st.ps("po", [P, 2, 512])
        names = ("w_in", "x", "init", "logit", "l", "silu", "path", "masked", "turned", "aT", "out", "added")
        s = {n: st.sem(n, primed=n in ("l", "aT", "added", "logit", "turned", "out", "silu", "masked",)) for n in names}
        GT = WC // 4
        with nc.Block() as block:
            @block.sync
            def _(sp):
                load_weights(sp, [(wi[:], w_in_T.rearrange("(k p) m -> p k m", p=P)), (bi_sb[:], row_bcast(b_in, W)),
                                  (wo[:], w_out_T.rearrange("(k p) m -> p k m", p=P))], s["w_in"])
                sp.wait_ge(s["w_in"], 48)

            @block.tensor
            def _(pe):
                pe.wait_ge(s["w_in"], 48)
                with pe.Fori(0, NT // 2) as i:
                    def logits(j):
                        pe.wait_ge(s["x"], i * 2 + (j + 1))
                        pe.wait_ge(s["l"], i * 2 + (j + 1))
                        for g in range(4):
                            for k in range(KC):
                                last = pe.matmul(ps[:, g, 0:Q], xt[:, j, k, :], wi[:, k, g * Q:(g + 1) * Q],
                                                 start=(k == 0), stop=(k == KC - 1))
                        last.then_inc(s["logit"], 1)

                    def turn(j, g):
                        q = j * GT + g
                        if g == 0:
                            pe.wait_ge(s["masked"], i * 2 + (j + 2))
                        pe.wait_ge(s["aT"], i * (2 * GT) + q if q >= 2 else i * (2 * GT) + 1)
                        for m in range(4):
                            last = pe.transpose(tp[:, q % 2, m * P:(m + 1) * P], act_[:, j, (4 * g + m) * P:(4 * g + m + 1) * P], c.ident[:])
                        last.then_inc(s["turned"], 1)

                    def project(j, g):
                        q = j * GT + g
                        if g == 0:
                            pe.wait_ge(s["added"], i * 2 + 1)
                        pe.wait_ge(s["aT"], i * (2 * GT) + (q + 2))
                        for m in range(4):
                            last = pe.matmul(po[:, j, 0:D], aT[:, q % 2, m, :], wo[:, 4 * g + m, :],
                                             start=(g == 0 and m == 0), stop=(g == GT - 1 and m == 3))
                        last.then_inc(s["out"], 1)

                    logits(0)
                    logits(1)
                    for q in range(2 * GT + 1):
                        if q < 2 * GT:
                            turn(q // GT, q % GT)
                        if q >= 1:
                            project((q - 1) // GT, (q - 1) % GT)

            @block.gpsimd
            def _(pool):
                pool.memset(act_[:, :, W:WC * P], 0.0)
                on4 = on[:].rearrange("p r (a n) -> p r a n", a=PAR)
                pool.memset(on4[:, :, :, 0:1], 1.0)
                pool.drain()
                pool.sem_inc(s["init"], 1)
                with pool.Fori(0, NT // 2) as i:
                    for j in range(2):
                        pool.wait_ge(s["logit"], i * 2 + 1)
                        pool.tensor_copy(xt[:, j], srcT[:, :, bass.ds((i * 2 + j) * P, P)]).then_inc(s["x"], 1)
                    for j in range(2):
                        pool.wait_ge(s["silu"], i * 2 + (j + 2))
                        pool.wait_ge(s["path"], i * 2 + (j + 1))
                        pool.tensor_tensor(act_[:, j, 0:W], act_[:, j, 0:W], on[:, j, :], ALU.mult).then_inc(s["masked"], 1)

            @block.scalar
            def _(act):
                with act.Fori(0, NT // 2) as i:
                    for j in range(2):
                        act.wait_ge(s["l"], i * 2 + (j + 2))
                        act.wait_ge(s["turned"], i * (2 * GT) + 1)
                        act.activation(act_[:, j, 0:W], l[:, j, :], ACT.Silu).then_inc(s["silu"], 1)
                    for q in range(2 * GT):
                        act.wait_ge(s["turned"], i * (2 * GT) + (q + 2))
                        act.wait_ge(s["out"], i * (2 * GT) + q if q >= 2 else i * (2 * GT) + 1)
                        act.activation(aT[:, q % 2].rearrange("p m n -> p (m n)"), tp[:, q % 2, :], ACT.Copy).then_inc(s["aT"], 1)

            @block.vector
            def _(dve):
                dve.wait_ge(s["w_in"], 48)
                dve.wait_ge(s["init"], 1)
                with dve.Fori(0, NT // 2) as i:
                    for j in range(2):
                        dve.wait_ge(s["logit"], i * 2 + (j + 2))
                        dve.wait_ge(s["silu"], i * 2 + 1)
                        dve.tensor_tensor(l[:, j, :].rearrange("p (g n) -> p g n", g=4), ps[:, :, 0:Q],
                                          bi_sb[:].rearrange("p (g n) -> p g n", g=4), ALU.add).then_inc(s["l"], 1)
                        dve.drain()
                        dve.tensor_scalar(go[:, j, :], l[:, j, :], 0.0, None, ALU.is_gt)
                        dve.drain()
                        dve.wait_ge(s["masked"], i * 2 + 1)
                        on3 = on[:, j, :].rearrange("p (a n) -> p a n", a=PAR)
                        go3 = go[:, j, :].rearrange("p (a n) -> p a n", a=PAR)
                        for lev in range(DEPTH):
                            here, n = 2 ** lev - 1, 2 ** lev
                            below = 2 * here + 1
                            right = on3[:, :, below + 1:below + 2 * n:2]
                            dve.tensor_tensor(right, on3[:, :, here:here + n], go3[:, :, here:here + n], ALU.mult)
                            dve.drain()
                            last = dve.tensor_tensor(on3[:, :, below:below + 2 * n:2], on3[:, :, here:here + n], right, ALU.subtract)
                            if lev < DEPTH - 1:
                                dve.drain()
                        last.then_inc(s["path"], 1)
                    for j in range(2):
                        x_t = c.x[:, bass.ds(i * 2 + j, 1), :]
                        dve.wait_ge(s["out"], i * (2 * GT) + ((j + 1) * GT + 1))
                        dve.tensor_tensor(x_t, x_t, po[:, j:j + 1, 0:D], ALU.add).then_inc(s["added"], 1)


H3 = 8
DK = 128
M_INCL, M_STRICT, M_BLOCK, M_J16, M_J32, M_J64 = range(6)


def delta_gates(c, name, ba, dt_bias, a_log, coef):
    nc = c.nc
    with Stage(nc, name) as st:
        rows = st.sb("rows", [P, 2, H3])
        masks = st.sb("masks", [P, P])
        z = st.sb("z", [P, H3, NT])
        l = st.sb("l", [P, H3, NT])
        ps = st.ps("ps", [P, 4, 512])
        s = {n: st.sem(n) for n in ("in", "z", "log", "g", "sum")}
        with nc.Block() as block:
            @block.sync
            def _(sp):
                load_weights(sp, [(rows[:, 0], row_bcast(dt_bias, H3)), (rows[:, 1], row_bcast(a_log, H3)),
                                  (masks[:], c.dram["masks"][:, M_STRICT, :])], s["in"])
                sp.wait_ge(s["in"], 48)

            @block.vector
            def _(dve):
                dve.wait_ge(s["in"], 48)
                dt = rows[:, 0].rearrange("p (h a) -> p h a", a=1).broadcast_to([P, H3, NT])
                dve.tensor_tensor(z[:], ba[:, :, H3:2 * H3].rearrange("p t h -> p h t"), dt, ALU.add)
                dve.tensor_copy(coef[:, 0], ba[:, :, 0:H3].rearrange("p t h -> p h t"))
                dve.drain()
                dve.sem_inc(s["z"], 1)
                dve.wait_ge(s["log"], 1)
                dve.scalar_tensor_tensor(out=z[:], in0=z[:], scalar=0.0, in1=l[:], op0=ALU.max, op1=ALU.add)
                dve.drain()
                ea = rows[:, 1].rearrange("p (h a) -> p h a", a=1).broadcast_to([P, H3, NT])
                dve.scalar_tensor_tensor(out=coef[:, 1], in0=z[:], scalar=-1.0, in1=ea, op0=ALU.mult, op1=ALU.mult).then_inc(s["g"], 1)

            @block.tensor
            def _(pe):
                pe.wait_ge(s["in"], 48)
                pe.wait_ge(s["g"], 1)
                g = coef[:, 1].rearrange("p h t -> p (h t)")
                for i, m in enumerate((c.lower, masks, c.ones)):
                    last = pe.matmul(ps[:, i, 0:H3 * NT], m[:], g, start=True, stop=True)
                last.then_inc(s["sum"], 1)

            @block.scalar
            def _(act):
                act.wait_ge(s["z"], 1)
                act.activation(coef[:, 0], coef[:, 0], ACT.Sigmoid)
                act.activation(l[:], z[:], ACT.Abs)
                act.drain()
                act.activation(l[:], l[:], ACT.Exp, scale=-1.0)
                act.activation(rows[:, 1], rows[:, 1], ACT.Exp)
                act.drain()
                act.activation(l[:], l[:], ACT.Ln, bias=1.0).then_inc(s["log"], 1)
                act.wait_ge(s["sum"], 1)
                for i in range(3):
                    act.activation(coef[:, 2 + i].rearrange("p h t -> p (h t)"), ps[:, i, 0:H3 * NT], ACT.Exp)


def delta_project(c, name, head, w, coef, hc, qkvg, bgk, kT, qT, qgT):
    nc = c.nc
    with Stage(nc, name) as st:
        w_sb = st.sb("w", [P, KC, 4 * DK])
        sq = st.sb("sq", [P, 2, 4, 2 * DK])
        ss = st.sb("ss", [P, NT, 2])
        bg = st.sb("bg", [P, NT])
        ps = st.ps("ps", [P, 4, 512])
        tp = st.ps("tp", [P, 4, 512])
        s = {n: st.sem(n) for n in ("w_in", "proj", "silu", "ss", "sd", "k", "q", "hc", "turned", "copied", "qg")}
        with nc.Block() as block:
            @block.sync
            def _(sp):
                sp.dma_start(w_sb[:], w[bass.ds(head, 1)].rearrange("a (k p) m -> p (a k) m", p=P)).then_inc(s["w_in"], 16)
                sp.wait_ge(s["w_in"], 16)

            @block.gpsimd
            def _(pool):
                pool.wait_ge(s["silu"], NT)
                pool.wait_ge(s["hc"], 1)
                v = qkvg[:, :, 2 * DK:3 * DK]
                pool.tensor_tensor(v, v, hc[:, 0, :].rearrange("p (t a) -> p t a", a=1).broadcast_to([P, NT, DK]), ALU.mult)

            @block.tensor
            def _(pe):
                pe.wait_ge(s["w_in"], 16)
                for t in range(NT):
                    if t >= 4:
                        pe.wait_ge(s["silu"], t - 3)
                    for k in range(KC):
                        last = pe.matmul(ps[:, t % 4, :], c.xT[:, k, t * P:(t + 1) * P], w_sb[:, k, :], start=(k == 0), stop=(k == KC - 1))
                    last.then_inc(s["proj"], 1)
                for g in range(12):
                    kind = g // 4
                    if g % 4 == 0:
                        pe.wait_ge((s["k"], s["q"], s["qg"])[kind], 1)
                    if g >= 4:
                        pe.wait_ge(s["copied"], g - 3)
                    a = (DK, 0, 0)[kind]
                    for m in range(4):
                        last = pe.transpose(tp[:, g % 4, m * P:(m + 1) * P], qkvg[:, 4 * (g % 4) + m, a:a + DK], c.ident[:])
                    last.then_inc(s["turned"], 1)

            @block.scalar
            def _(act):
                for t in range(NT):
                    act.wait_ge(s["proj"], t + 1)
                    act.activation(qkvg[:, t, :], ps[:, t % 4, :], ACT.Silu).then_inc(s["silu"], 1)
                act.wait_ge(s["ss"], 1)
                act.activation(ss[:], ss[:], ACT.Sqrt).then_inc(s["sd"], 1)
                for g in range(12):
                    act.wait_ge(s["turned"], g + 1)
                    dst = (kT, qT, qgT)[g // 4]
                    act.activation(dst[:, 4 * (g % 4):4 * (g % 4) + 4, :].rearrange("p t d -> p (t d)"), tp[:, g % 4, :],
                                   ACT.Copy).then_inc(s["copied"], 1)

            @block.vector
            def _(dve):
                dve.tensor_copy(hc[:], coef[:, :, bass.ds(head, 1), :].rearrange("p c a t -> p c (a t)"))
                dve.drain()
                dve.sem_inc(s["hc"], 1)
                dve.tensor_tensor(bg[:], hc[:, 0, :], hc[:, 2, :], ALU.mult)
                for g in range(4):
                    dve.wait_ge(s["silu"], 4 * (g + 1))
                    qk = qkvg[:, 4 * g:4 * g + 4, 0:2 * DK]
                    dve.tensor_tensor(sq[:, g % 2], qk, qk, ALU.mult)
                    dve.drain()
                    dve.tensor_reduce(ss[:, 4 * g:4 * g + 4, :], sq[:, g % 2].rearrange("p t (w d) -> p t w d", w=2), AX.X, ALU.add)
                dve.drain()
                dve.tensor_scalar(ss[:], ss[:], 1e-6, None, ALU.add).then_inc(s["ss"], 1)
                dve.wait_ge(s["sd"], 1)
                dve.reciprocal(ss[:], ss[:])
                dve.drain()
                dve.tensor_scalar(ss[:, :, 0:1], ss[:, :, 0:1], DK ** -0.5, None, ALU.mult)
                q, k = qkvg[:, :, 0:DK], qkvg[:, :, DK:2 * DK]
                full = [P, NT, DK]

                def col(v):
                    return v.rearrange("p (t a) -> p t a", a=1).broadcast_to(full)
                dve.tensor_tensor(k, k, ss[:, :, 1:2].broadcast_to(full), ALU.mult).then_inc(s["k"], 1)
                dve.drain()
                dve.tensor_tensor(q, q, ss[:, :, 0:1].broadcast_to(full), ALU.mult).then_inc(s["q"], 1)
                dve.tensor_tensor(bgk[:], k, col(bg[:]), ALU.mult)
                dve.drain()
                dve.wait_ge(s["turned"], 4)
                dve.tensor_tensor(k, k, col(hc[:, 3, :]), ALU.mult)
                dve.wait_ge(s["turned"], 8)
                dve.tensor_tensor(q, q, col(hc[:, 2, :]), ALU.mult).then_inc(s["qg"], 1)


def delta_invert(c, name, masks, hc, qkvg, bgk, kT, qT, U, WT, PT):
    nc = c.nc
    STEPS = 13
    with Stage(nc, name) as st:
        def four(n):
            return st.sb(n, [P, 2, 4, P])
        gs, bs, Dm, DT, L, LT, n1, n1T, n2, n2T, T, TT, X, Lm = (four(n) for n in (
            "gs", "bs", "D", "DT", "L", "LT", "n1", "n1T", "n2", "n2T", "T", "TT", "X", "Lm"))
        ps = st.ps("ps", [P, 2, 3, 512])
        s = {n: st.sem(n) for n in ("gs", "mm", "act", "dve", "lm")}

        def wide(m, g):
            return m[:, g].rearrange("p t d -> p (t d)")

        def mask(m):
            return masks[:, m:m + 1, :].broadcast_to([P, 4, P])

        A = [1, 2, 1, 1, 1, 0, 1, 0, 0, 0, 0, 0, 1]

        def done(r, n, g, per=None):
            if per is None:
                return 2 * STEPS * r + 2 * n + g + 1
            return 2 * sum(per) * r + 2 * sum(per[:n]) + per[n] * (g + 1)

        with nc.Block() as block:
            @block.tensor
            def _(pe):
                for r in range(2):
                    for n in range(STEPS):
                        for g in range(2):
                            t0 = (2 * r + g) * 4
                            if n == 0:
                                pe.wait_ge(s["gs"], 2 * r + g + 1)
                                if r == 1:
                                    pe.wait_ge(s["dve"], done(0, STEPS - 1, g))
                                    pe.wait_ge(s["act"], done(0, STEPS - 1, g, A))
                            else:
                                pe.wait_ge(s["dve"], done(r, n - 1, g))
                                pe.wait_ge(s["act"], done(r, n - 1, g, A))

                            def mm(bank, lhs, rhs):
                                for m in range(4):
                                    q = pe.matmul(ps[:, g, bank, m * P:(m + 1) * P], lhs(m), rhs(m), start=True, stop=True)
                                return q

                            def turn(bank, src):
                                for m in range(4):
                                    q = pe.transpose(ps[:, g, bank, m * P:(m + 1) * P], src[:, g, m, :], c.ident[:])
                                return q

                            def of(b):
                                return lambda m: b[:, g, m, :]

                            def tok(b):
                                return lambda m: b[:, t0 + m, :]
                            if n == 0:
                                pe.matmul(ps[:, g, 0, :], c.lower[:], wide(gs, g), start=True, stop=True)
                                last = mm(1, tok(kT), tok(kT))
                            elif n == 1:
                                turn(0, L)
                                last = turn(1, Dm)
                            elif n == 2:
                                mm(0, of(n1T), of(n1))
                                mm(1, of(n1), of(n1T))
                                last = mm(2, tok(kT), tok(qT))
                            elif n == 3:
                                mm(0, of(n2T), of(n2))
                                mm(1, of(n2), of(n2T))
                                last = mm(2, of(n2T), of(T))
                            elif n == 4:
                                mm(0, of(n1), of(n1T))
                                last = mm(2, of(n1T), of(T))
                            elif n == 5:
                                last = mm(2, of(n2T), of(T))
                            elif n in (6, 8, 10):
                                if n == 6:
                                    turn(0, T)
                                pe.wait_ge(s["lm"], 6 * r + (n - 6) + g + 1)
                                last = mm(1, of(Lm), of(T))
                            elif n in (7, 9):
                                mm(0, of(TT), of(X))
                                last = mm(1, of(X), of(TT))
                            elif n == 11:
                                last = mm(1, of(X), of(TT))
                            else:
                                mm(0, of(TT), lambda m: qkvg[:, t0 + m, 2 * DK:3 * DK])
                                last = mm(1, tok(bgk), of(TT))
                            last.then_inc(s["mm"], 1)

            @block.scalar
            def _(act):
                for r in range(2):
                    for n in range(STEPS):
                        for g in range(2):
                            t0 = (2 * r + g) * 4
                            copies = {1: [(LT, 0), (DT, 1)], 2: [(n2, 0)], 3: [(n1, 0)], 4: [(n2T, 0)], 6: [(TT, 0)]}
                            if not A[n]:
                                continue
                            act.wait_ge(s["mm"], done(r, n, g))
                            if n == 0:
                                act.activation(wide(Dm, g), ps[:, g, 0, :], ACT.Exp).then_inc(s["act"], 1)
                            elif n == STEPS - 1:
                                act.activation(U[:, t0:t0 + 4, :].rearrange("p t d -> p (t d)"), ps[:, g, 0, :],
                                               ACT.Copy).then_inc(s["act"], 1)
                            else:
                                for dst, bank in copies[n]:
                                    act.activation(wide(dst, g), ps[:, g, bank, :], ACT.Copy).then_inc(s["act"], 1)

            @block.gpsimd
            def _(pool):
                for r in range(2):
                    for n in (6, 8, 10):
                        for g in range(2):
                            if n == 6:
                                pool.wait_ge(s["act"], done(r, 1, g, A))
                                if r == 1:
                                    pool.wait_ge(s["mm"], done(0, 10, g))
                            else:
                                pool.wait_ge(s["mm"], done(r, n - 2, g))
                            pool.tensor_tensor(Lm[:, g], LT[:, g], mask((M_J16, M_J32, M_J64)[(n - 6) // 2]), ALU.mult).then_inc(s["lm"], 1)

            @block.vector
            def _(dve):
                def col(v):
                    return v.rearrange("p (t a) -> p t a", a=1).broadcast_to([P, 4, P])

                for r in range(2):
                    for g in range(2):
                        t0 = (2 * r + g) * 4
                        dve.tensor_tensor(gs[:, g], mask(M_STRICT), col(hc[:, 1, t0:t0 + 4]), ALU.mult).then_inc(s["gs"], 1)
                        dve.tensor_tensor(bs[:, g], mask(M_STRICT), col(hc[:, 0, t0:t0 + 4]), ALU.mult)
                    dve.drain()
                    for n in range(STEPS):
                        for g in range(2):
                            t0 = (2 * r + g) * 4

                            def bank(i):
                                return ps[:, g, i, :].rearrange("p (t d) -> p t d", t=4)
                            dve.wait_ge(s["mm"], done(r, n, g))
                            if n == 0:
                                dve.wait_ge(s["act"], done(r, 0, g, A))
                                dve.tensor_tensor(Dm[:, g], Dm[:, g], mask(M_INCL), ALU.mult)
                                dve.tensor_tensor(L[:, g], bank(1), bs[:, g], ALU.mult)
                                dve.drain()
                                last = dve.tensor_tensor(L[:, g], L[:, g], Dm[:, g], ALU.mult)
                            elif n == 1:
                                dve.wait_ge(s["act"], done(r, 1, g, A))
                                dve.scalar_tensor_tensor(out=n1[:, g], in0=L[:, g], scalar=-1.0, in1=mask(M_BLOCK), op0=ALU.mult, op1=ALU.mult)
                                dve.scalar_tensor_tensor(out=n1T[:, g], in0=LT[:, g], scalar=-1.0, in1=mask(M_BLOCK), op0=ALU.mult, op1=ALU.mult)
                                dve.drain()
                                idb = c.ident[:].rearrange("p (a n) -> p a n", a=1).broadcast_to([P, 4, P])
                                last = dve.tensor_tensor(T[:, g], n1[:, g], idb, ALU.add)
                            elif n == 2:
                                dve.tensor_tensor(PT[:, t0:t0 + 4, :], bank(2), DT[:, g], ALU.mult)
                                last = dve.tensor_copy(n2T[:, g], bank(1))
                            elif n == 3:
                                dve.tensor_copy(n1T[:, g], bank(1))
                                last = dve.tensor_tensor(T[:, g], T[:, g], bank(2), ALU.add)
                            elif n in (4, 5):
                                last = dve.tensor_tensor(T[:, g], T[:, g], bank(2), ALU.add)
                            elif n in (6, 8, 10):
                                last = dve.tensor_copy(X[:, g], bank(1))
                            elif n in (7, 9):
                                dve.tensor_tensor(T[:, g], T[:, g], bank(0), ALU.subtract)
                                last = dve.tensor_tensor(TT[:, g], TT[:, g], bank(1), ALU.subtract)
                            elif n == 11:
                                last = dve.tensor_tensor(TT[:, g], TT[:, g], bank(1), ALU.subtract)
                            else:
                                last = dve.tensor_copy(WT[:, t0:t0 + 4, :], bank(1))
                            dve.drain()
                            dve.sem_inc(s["dve"], 1)


def delta_scan(c, name, hc, qkvg, qgT, U, WT, PT, o):
    nc = c.nc
    with Stage(nc, name) as st:
        Sst = st.sb("S", [P, B, DK])
        dl = st.sb("dl", [P, 2, B, DK])
        ws = st.ps("ws", [P, 512])
        op = st.ps("op", [P, 2, 512])
        sp_ = st.ps("sp", [P, 512])
        s = {n: st.sem(n) for n in ("S", "ws", "dl", "o", "o_out")}
        U4, o4 = (m[:].rearrange("p (b t) d -> p b t d", b=B) for m in (U, o))
        with nc.Block() as block:
            @block.tensor
            def _(pe):
                for n in range(ST):
                    pe.wait_ge(s["S"], n + 1)
                    for b in range(B):
                        last = pe.matmul(ws[:, b * DK:(b + 1) * DK], WT[:, b * ST + n, :], Sst[:, b, :], start=True, stop=True)
                    last.then_inc(s["ws"], 1)
                    pe.wait_ge(s["dl"], n + 1)
                    if n >= 2:
                        pe.wait_ge(s["o_out"], n - 1)
                    for b in range(B):
                        t = b * ST + n
                        dst = op[:, n % 2, b * DK:(b + 1) * DK]
                        pe.matmul(dst, qgT[:, t, :], Sst[:, b, :], start=True, stop=False)
                        pe.matmul(dst, PT[:, t, :], dl[:, n % 2, b, :], start=False, stop=True)
                        last = pe.matmul(sp_[:, b * DK:(b + 1) * DK], qkvg[:, t, DK:2 * DK], dl[:, n % 2, b, :], start=True, stop=True)
                    last.then_inc(s["o"], 1)

            @block.scalar
            def _(act):
                for n in range(ST):
                    act.wait_ge(s["o"], n + 1)
                    act.activation(o4[:, :, n, :], op[:, n % 2, 0:B * DK].rearrange("p (b d) -> p b d", b=B), ACT.Copy).then_inc(s["o_out"], 1)

            @block.vector
            def _(dve):
                dve.memset(Sst[:], 0.0).then_inc(s["S"], 1)
                for n in range(ST):
                    dve.wait_ge(s["ws"], n + 1)
                    dve.tensor_tensor(dl[:, n % 2], U4[:, :, n, :], ws[:, 0:B * DK].rearrange("p (b d) -> p b d", b=B), ALU.subtract).then_inc(s["dl"], 1)
                    dve.wait_ge(s["o"], n + 1)
                    for b in range(B):
                        t = b * ST + n
                        dve.scalar_tensor_tensor(out=Sst[:, b, :], in0=Sst[:, b, :], scalar=hc[:, 4, t:t + 1], in1=sp_[:, b * DK:(b + 1) * DK],
                                                 op0=ALU.mult, op1=ALU.add)
                    dve.drain()
                    dve.sem_inc(s["S"], 1)


def delta_output(c, name, head, w_o, norm_w, qkvg, o, xi):
    nc = c.nc
    with Stage(nc, name) as st:
        w_sb = st.sb("w", [P, D])
        nw = st.sb("nw", [P, DK])
        sq = st.sb("sq", [P, NT, DK])
        ss = st.sb("ss", [P, NT])
        tp = st.ps("tp", [P, 4, 512])
        ps = st.ps("ps", [P, 4, 512])
        s = {n: st.sem(n) for n in ("w_in", "ss", "sd", "gate", "o", "turned", "oT", "mult", "added")}
        full = [P, NT, DK]
        with nc.Block() as block:
            @block.sync
            def _(sp):
                sp.dma_start(w_sb[:], w_o[bass.ds(head, 1)].rearrange("a p m -> p (a m)")).then_inc(s["w_in"], 16)
                sp.dma_start(nw[:], row_bcast(norm_w, DK)).then_inc(s["w_in"], 16)
                sp.wait_ge(s["w_in"], 32)

            @block.gpsimd
            def _(pool):
                pool.wait_ge(s["w_in"], 32)
                gate = qkvg[:, :, 3 * DK:4 * DK]
                pool.tensor_tensor(gate, gate, nw[:].rearrange("p (a d) -> p a d", a=1).broadcast_to(full), ALU.mult).then_inc(s["gate"], 1)

            @block.vector
            def _(dve):
                dve.tensor_tensor(sq[:], o[:], o[:], ALU.mult)
                dve.drain()
                dve.tensor_reduce(ss[:], sq[:], AX.X, ALU.add)
                dve.drain()
                dve.tensor_scalar(ss[:], ss[:], 1.0 / DK, 1e-6, ALU.mult, ALU.add).then_inc(s["ss"], 1)
                dve.wait_ge(s["sd"], 1)
                dve.reciprocal(ss[:], ss[:])
                dve.drain()
                dve.tensor_tensor(o[:], o[:], ss[:].rearrange("p (t a) -> p t a", a=1).broadcast_to(full), ALU.mult)
                dve.drain()
                dve.wait_ge(s["gate"], 1)
                dve.tensor_tensor(o[:], o[:], qkvg[:, :, 3 * DK:4 * DK], ALU.mult).then_inc(s["o"], 1)
                for g in range(NT // 2):
                    dve.wait_ge(s["mult"], g + 1)
                    x2 = xi[:, 2 * g:2 * g + 2, :]
                    dve.tensor_tensor(x2, x2, ps[:, g % 4, :].rearrange("p (t d) -> p t d", t=2), ALU.add).then_inc(s["added"], 1)

            @block.scalar
            def _(act):
                act.wait_ge(s["ss"], 1)
                act.activation(ss[:], ss[:], ACT.Sqrt).then_inc(s["sd"], 1)
                for g in range(4):
                    act.wait_ge(s["turned"], g + 1)
                    act.activation(sq[:, 4 * g:4 * g + 4, :].rearrange("p t d -> p (t d)"), tp[:, g, :], ACT.Copy).then_inc(s["oT"], 1)

            @block.tensor
            def _(pe):
                pe.wait_ge(s["o"], 1)
                for g in range(4):
                    for m in range(4):
                        last = pe.transpose(tp[:, g, m * P:(m + 1) * P], o[:, 4 * g + m, :], c.ident[:])
                    last.then_inc(s["turned"], 1)
                pe.wait_ge(s["w_in"], 32)
                for g in range(NT // 2):
                    pe.wait_ge(s["oT"], g // 2 + 1)
                    if g >= 4:
                        pe.wait_ge(s["added"], g - 3)
                    for m in range(2):
                        last = pe.matmul(ps[:, g % 4, m * D:(m + 1) * D], sq[:, 2 * g + m, :], w_sb[:], start=True, stop=True)
                    last.then_inc(s["mult"], 1)


def mix_heads(c, name, main, aux, gate_row):
    nc = c.nc
    with Stage(nc, name) as st:
        g = st.sb("g", [P, 2, D])
        g_in, g_ready = st.sem("g_in"), st.sem("g_ready")
        with nc.Block() as block:
            @block.sync
            def _(sp):
                sp.dma_start(g[:, 0], row_bcast(gate_row, D)).then_inc(g_in, 16)
                sp.wait_ge(g_in, 16)

            @block.scalar
            def _(act):
                act.wait_ge(g_in, 16)
                act.activation(g[:, 0], g[:, 0], ACT.Sigmoid).then_inc(g_ready, 1)

            @block.vector
            def _(dve):
                dve.wait_ge(g_ready, 1)
                dve.tensor_scalar(g[:, 1], g[:, 0], -1.0, 1.0, ALU.mult, ALU.add)
                dve.drain()
                dve.tensor_tensor(aux[:], aux[:], g[:, 0:1].broadcast_to([P, NT, D]), ALU.mult)
                dve.tensor_tensor(main[:], main[:], g[:, 1:2].broadcast_to([P, NT, D]), ALU.mult)
                dve.drain()
                dve.tensor_tensor(main[:], main[:], aux[:], ALU.add)


def fill(c, name, dst, value):
    with Stage(c.nc, name) as st:
        with c.nc.Block() as block:
            @block.vector
            def _(dve):
                dve.memset(dst, value)


def rope_table(lanes):
    inv = (np.float32(10000.0) ** (-(np.arange(DH // 2, dtype=np.float32) * np.float32(2.0) / np.float32(DH)))).astype(np.float32)
    ang = np.arange(S, dtype=np.float32)[:, None] * inv[None, :]
    co, si = np.cos(ang), np.sin(ang)
    out = np.zeros((2, P, S), np.float32)
    out[0] = 1.0
    for p, j in enumerate(lanes):
        if j >= 0:
            out[0, p] = co[:, j // 2]
            out[1, p] = si[:, j // 2] * (1.0 if j % 2 else -1.0)
    return out


def part_place():
    m = np.zeros((SLOT, 2, 3, SR), np.float32)
    for j, parts in enumerate(PART_PRODUCTS):
        for which in range(2):
            for f in range(DH):
                m[f, which, parts[which], j * DH + f] = 1
    m[DH, 1, 0, SR - 3:] = 1
    return np.tile(m, (HC, 1, 1, 1))


def head_blocks(w):
    out = np.zeros((KC, P, P), np.float32)
    n = P // DH
    for h in range(H):
        a = (h % n) * DH
        out[h // n, a:a + DH, a:a + DH] = w[h].T
    return out


def spread_gather():
    spread = np.zeros((DH, P, P), np.float32)
    for d in range(DH):
        for m in range(P):
            spread[d, m // DH * DH + d, m] = 1.0
    return spread.transpose(1, 0, 2), spread.transpose(2, 0, 1)


def chunk_masks():
    i, j = np.arange(P)[:, None], np.arange(P)[None, :]
    m = [j <= i, j < i, i // 16 == j // 16]
    for w in (16, 32, 64):
        m.append((i // w % 2 == 0) & (j // w == i // w + 1))
    return np.stack(m, 1).astype(np.float32)


def rotation_table():
    ang = np.outer(np.arange(S, dtype=np.float32), np.arange(D // 2, dtype=np.float32))[::-1]
    co, si = np.repeat(np.cos(ang), 2, 1).T, np.repeat(np.sin(ang), 2, 1).T.copy()
    si[1::2] *= -1.0
    return np.stack([co, si]).reshape(2, KC, P, S).astype(np.float32)


SLOT_LANES = [p % SLOT if p % SLOT < DH else -1 for p in range(P)]


def slotted(w):
    out = np.zeros((NC4, P, KC, P), np.float32)
    a = np.asarray(w).reshape(KC, P, NC4, HC, DH).transpose(2, 1, 0, 3, 4)
    out.reshape(NC4, P, KC, HC, SLOT)[..., 0:DH] = a
    return out


def slotted_bias(b, extra):
    out = np.zeros((NC4, HC, SLOT), np.float32)
    if b is not None:
        out[:, :, 0:DH] = np.asarray(b).reshape(NC4, HC, DH)
    out[:, :, DH] = extra
    return out.reshape(NC4, P)


def chunked_v(w):
    return np.ascontiguousarray(np.asarray(w).reshape(KC, P, NC4, HC * DH).transpose(2, 1, 0, 3))


def swap_pairs(w):
    w = np.asarray(w)
    return w.reshape(*w.shape[:-1], -1, 2)[..., ::-1].reshape(w.shape)


def as_cols(b):
    return np.asarray(b).reshape(-1, P).T


def lay_out(i):
    a = {"x": i["x"], "ctxT": i["ctx_1024"].reshape(B * S2, D).T, "mask2T": i["mask_BxS2_ik0"].T}
    qT, kT = i["L0_attn_w_q"].T, i["L0_attn_w_k"].T
    a["l0a_wqk"] = np.stack([slotted(qT), slotted(kT), slotted(swap_pairs(qT)), slotted(swap_pairs(kT))], 2)
    a["l0a_b"] = np.stack([slotted_bias(None, 0.0), slotted_bias(None, 1.0)], 2)
    a["l0a_wv"] = chunked_v(i["L0_attn_w_v"].T)
    a["l0a_wo"] = i["L0_attn_w_o"].T
    a["part_place"] = part_place()
    a["rope_slots"] = rope_table(SLOT_LANES)
    for n in ("Ws", "W", "bcw", "bcb"):
        a["l0x_" + n] = i["L0_xattn_" + n]
    a["l0x_w"] = as_cols(i["L0_xattn_w"])
    a["l0x_b"] = as_cols(i["L0_xattn_b"])
    a["l0x_wcw"] = np.broadcast_to(i["L0_xattn_Wcw"].T, (D, P))
    a["l0x_wcb"] = np.broadcast_to(i["L0_xattn_Wcb"].T, (D, P))
    for n in ("Wr", "W1", "W2", "b2"):
        a["l0f_" + n] = i["L0_ffn_" + n]
    a["l0f_br"] = i["L0_ffn_br"].reshape(E, 1)
    a["l0f_b1"] = i["L0_ffn_b1"].reshape(E, -1, P).transpose(0, 2, 1)
    for n in "kqvp":
        a["l1a_W" + n] = i["L1_attn_W" + n]
    for n in "kq":
        a["l1a_W" + n + "s"] = swap_pairs(i["L1_attn_W" + n])
        a["l1a_b" + n] = as_cols(i["L1_attn_b" + n])
        a["l1a_b" + n + "s"] = as_cols(swap_pairs(i["L1_attn_b" + n]))
    a["l1a_bv"], a["l1a_bp"] = i["L1_attn_bv"], i["L1_attn_bp"]
    a["l1a_cs"] = rotation_table()
    for n in ("Wq", "Wk", "Wv", "Wcq", "Wck", "Wcv", "gamma", "beta", "W1", "b1"):
        a["l1x_" + n] = i["L1_xattn_" + n]
    a["l1f_w1"], a["l1f_w2"] = i["L1_ffn_w1"].T, i["L1_ffn_w2"].T
    a["l1f_b1"], a["l1f_b2"] = i["L1_ffn_b1"], i["L1_ffn_b2"]
    for n in "qkvg":
        a["l2a_w" + n] = i["L2_attn_" + n + "_w"].T
    a["l2a_wqs"], a["l2a_wks"] = swap_pairs(a["l2a_wq"]), swap_pairs(a["l2a_wk"])
    a["l2a_bg"] = as_cols(i["L2_attn_g_b"])
    a["rope_heads"] = rope_table([p % DH for p in range(P)])
    a["l2a_Wq"], a["l2a_Wk"] = head_blocks(i["L2_attn_Wq"]), head_blocks(i["L2_attn_Wk"])
    a["l2a_decay"] = as_cols(i["L2_attn_base_decay_logits"])
    a["spread"], a["gather"] = spread_gather()
    a["l2a_wo"] = i["L2_attn_out_w"].T
    for n in ("out_b", "ln_g", "ln_b"):
        a["l2a_" + n] = i["L2_attn_" + n]
    a["head_mask"] = (np.arange(P)[:, None] // DH == np.arange(P // DH)[None, :]).astype(np.float32)
    a["l2x_wq"], a["l2x_bq"], a["l2x_wo"], a["l2x_bo"] = i["L2_xattn_Wq"], as_cols(i["L2_xattn_bq"]), i["L2_xattn_Wo"], i["L2_xattn_bo"]
    a["l2x_wk"], a["l2x_bk"] = np.tile(i["L2_xattn_Wk"], (1, H)), as_cols(np.tile(i["L2_xattn_bk"], H))
    a["l2x_wv"], a["l2x_bv"] = np.tile(i["L2_xattn_Wv"], (1, H)), np.tile(i["L2_xattn_bv"], H)
    a["l2f_wi"], a["l2f_bi"] = i["L2_ffn_W_in"].T, i["L2_ffn_b_in"]
    width = i["L2_ffn_W_out"].shape[1]
    a["l2f_wo"] = np.pad(i["L2_ffn_W_out"].T, ((0, -width % P), (0, 0)))
    per_head = [i["L3_attn_W" + n].reshape(D, H3, DK) for n in "qkvg"]
    a["l3a_w"] = np.concatenate(per_head, 2).transpose(1, 0, 2)
    a["l3a_wba"] = np.concatenate([i["L3_attn_Wb"], i["L3_attn_Wa"]], 1)
    a["l3a_alog"], a["l3a_dt"] = i["L3_attn_A_log"], i["L3_attn_dt_bias"]
    a["l3a_nw"] = i["L3_attn_o_norm_w"]
    a["l3a_wo"] = i["L3_attn_Wo"].reshape(H3, DK, D)
    a["l3a_fc"] = i["L3_attn_W_fc"].reshape(D, 2, -1).transpose(1, 0, 2)
    a["l3a_pr"] = i["L3_attn_W_proj"].reshape(2, -1, D)
    a["masks"] = chunk_masks()
    wq, wk, wv = np.split(i["L3_xattn_Wqkv"], 3, 1)
    bq, bk, bv = np.split(i["L3_xattn_bqkv"], 3)
    a["l3x_wqk"] = np.stack([slotted(wq), slotted(wk)], 2)
    a["l3x_b"] = np.stack([slotted_bias(bq, 0.0), slotted_bias(bk, 1.0)], 2)
    a["l3x_wv"] = chunked_v(wv)
    a["l3x_bv"] = np.broadcast_to(bv.reshape(NC4, 1, HC * DH), (NC4, P, HC * DH))
    a["l3x_q"], a["l3x_bq"] = wq, as_cols(bq)
    _, a["l3x_ka"], a["l3x_va"] = np.split(i["L3_xattn_Wqkv_aux"], 3, 1)
    _, bka, a["l3x_bva"] = np.split(i["L3_xattn_bqkv_aux"], 3)
    a["l3x_bka"] = as_cols(bka)
    a["l3x_g"] = np.repeat(i["L3_xattn_g"], DH)
    a["l3x_wo"], a["l3x_bo"] = i["L3_xattn_Wo"], i["L3_xattn_bo"]
    a["l3f_r"] = i["L3_ffn_router_w"].T
    a["l3f_g"], a["l3f_u"], a["l3f_d"] = i["L3_ffn_rg"], i["L3_ffn_ru"], i["L3_ffn_rd"]
    a["l3f_sg"], a["l3f_su"] = (i[f"L3_ffn_s{m}"].reshape(D, 2, -1).transpose(1, 0, 2) for m in "gu")
    a["l3f_sd"] = i["L3_ffn_sd"].reshape(2, -1, D)
    a["l3f_rows"] = np.arange(CAPACITY, dtype=np.float32)
    chunks = -(-CAPACITY // P)
    a["l3f_cols"] = np.arange(chunks * P, dtype=np.float32).reshape(chunks, P).T
    a["l3f_heads"] = np.repeat(np.eye(E, dtype=np.float32), P, axis=1).reshape(E, E, P)
    return a


def l0_attn(c):
    nc, d = c.nc, c.dram
    norm_transpose(c, "l0a_ln", c.x, dst_T=c.xT)
    with nc.sbuf_tensor("l0a_ao", [P, NT, D], F32) as ao:
        self_attention(c, "l0a", d["l0a_wqk"], d["l0a_wv"], ao, True, d["rope_slots"], d["l0a_b"])
        project_add(c, "l0a_o", ao, d["l0a_wo"])


def l0_xattn(c):
    nc, d = c.nc, c.dram
    with nc.sbuf_tensor("l0x_feat", [P, NT, D], F32) as feat, nc.sbuf_tensor("l0x_feT", [P, KC, N], F32) as feT, \
            nc.sbuf_tensor("l0x_txb", [P, KC, B * S2], F32) as txb, nc.sbuf_tensor("l0x_sw", [P, B, S2], F32) as sw, \
            nc.sbuf_tensor("l0x_sb", [P, B, S2], F32) as sbr:
        norm_transpose(c, "l0x_ln", c.x, dst_tok=feat, dst_T=c.xT)
        linear_T(c, "l0x_f", c.xT, [(d["l0x_W"], feT, None, None)])
        linear_T(c, "l0x_t", c.ctxT, [(d["l0x_Ws"], txb, d["l0x_b"], None)], width=B * S2)
        ctx_rows(c, "l0x_s", [d["l0x_wcw"], d["l0x_wcb"]], [sw, sbr])
        additive_attention(c, "l0x", feat, feT, txb, sw, sbr)


def l0_ffn(c):
    nc, d = c.nc, c.dram
    norm_transpose(c, "l0f_ln", c.x, dst_T=c.xT)
    with nc.sbuf_tensor("l0f_wgt", [P, NT, E], F32) as wgt:
        route(c, "l0f_r", c.xT, d["l0f_Wr"], wgt, bias=d["l0f_br"])
        experts(c, "l0f_e", c.xT, wgt, E, 512, d["l0f_W1"], d["l0f_W2"], b1=d["l0f_b1"])
        add_expert_bias(c, "l0f_b", wgt, d["l0f_b2"])


def tile_ctx(c, names):
    ctx = ExitStack()
    return ctx, [ctx.enter_context(c.nc.sbuf_tensor(n, shape, dt)) for n, shape, dt in names]


def l1_attn(c):
    d = c.dram
    norm_transpose(c, "l1a_ln", c.x, dst_T=c.xT)
    ctx, (qT, kT, v) = tile_ctx(c, [("l1a_qT", [P, KC, N], F32), ("l1a_kT", [P, KC, N], F32), ("l1a_v", [P, NT, D], F32)])
    with ctx:
        rope_T(c, "l1a_qk", c.xT, [(d["l1a_Wq"], d["l1a_Wqs"], qT, d["l1a_bq"], d["l1a_bqs"]),
                                   (d["l1a_Wk"], d["l1a_Wks"], kT, d["l1a_bk"], d["l1a_bks"])], d["l1a_cs"], True)
        linear_tok(c, "l1a_vp", c.xT, d["l1a_Wv"], v, bias=d["l1a_bv"])
        with c.nc.sbuf_tensor("l1a_ao", [P, NT, D], F32) as ao:
            softplus_attention(c, "l1a", qT, kT, v, ao)
            project_add(c, "l1a_o", ao, d["l1a_Wp"], bias=d["l1a_bp"])


def l1_xattn(c):
    d = c.dram
    big = [P, NT, D]
    ctx, (hn, qT, kT, v, a) = tile_ctx(c, [("l1x_hn", big, F32), ("l1x_qT", [P, KC, N], F32), ("l1x_kT", [P, KC, N], F32),
                                           ("l1x_v", big, F32), ("l1x_a", big, F32)])
    gb = dict(eps=1e-3, gamma=d["l1x_gamma"], beta=d["l1x_beta"])
    with ctx:
        norm_transpose(c, "l1x_ln", c.x, dst_tok=hn, dst_T=c.xT)
        linear_T(c, "l1x_qk", c.xT, [(d["l1x_Wq"], qT, None, None), (d["l1x_Wk"], kT, None, None)])
        linear_tok(c, "l1x_vp", c.xT, d["l1x_Wv"], v)
        softmax_attention(c, "l1x_self", qT, kT, v, a, hn, True)
        norm_transpose(c, "l1x_ln1", a, dst_tok=hn, dst_T=c.xT, **gb)
        linear_T(c, "l1x_cq", c.xT, [(d["l1x_Wcq"], qT, None, None)])
        linear_T(c, "l1x_ck", c.ctxT, [(d["l1x_Wck"], kT, None, None)], width=B * S2)
        linear_tok(c, "l1x_cv", c.ctxT, d["l1x_Wcv"], v, tiles=B, rows=S2)
        softmax_attention(c, "l1x_cross", qT, kT, v, a, hn, False)
        norm_transpose(c, "l1x_ln2", a, dst_tok=hn, dst_T=c.xT, **gb)
        linear_tok(c, "l1x_f", c.xT, d["l1x_W1"], a, bias=d["l1x_b1"], resid=hn, relu=True)
        norm_transpose(c, "l1x_ln3", a, dst_tok=hn, **gb)
        add_to_x(c, "l1x_add", hn, relu=True)


def l1_ffn(c):
    d = c.dram
    F = d["l1f_b1"].shape[0]
    ctx, (r, w1q, w2q, s1, s2) = tile_ctx(c, [("l1f_r", [P, NT, D], F32), ("l1f_w1q", [P, KC, F], BF16),
                                              ("l1f_w2q", [P, F // P, D], BF16), ("l1f_s1", [P, 1], F32), ("l1f_s2", [P, 1], F32)])
    with ctx:
        norm_transpose(c, "l1f_ln", c.x, dst_tok=r)
        norm_transpose(c, "l1f_rms", r, dst_tok=r, rms=True)
        quantize_weights(c, "l1f_q1", d["l1f_w1"], w1q, s1)
        quantize_weights(c, "l1f_q2", d["l1f_w2"], w2q, s2)
        quantized_ffn(c, "l1f", r, w1q, s1, w2q, s2, d["l1f_b1"], d["l1f_b2"])


def l2_attn(c):
    d = c.dram
    big = [P, NT, D]
    bigT = [P, KC, N]
    ctx, (xn, qT, kT, vT, gT) = tile_ctx(c, [("l2a_xn", big, F32), ("l2a_qT", bigT, F32), ("l2a_kT", bigT, F32),
                                             ("l2a_vT", bigT, F32), ("l2a_gT", bigT, F32)])
    with ctx:
        norm_transpose(c, "l2a_ln", c.x, dst_tok=xn, dst_T=c.xT)
        rope_T(c, "l2a_qk", c.xT, [(d["l2a_wq"], d["l2a_wqs"], qT, None, None), (d["l2a_wk"], d["l2a_wks"], kT, None, None)],
               d["rope_heads"], False)
        linear_T(c, "l2a_vg", c.xT, [(d["l2a_wv"], vT, None, None), (d["l2a_wg"], gT, d["l2a_bg"], ACT.Sigmoid)])
        per_head_T(c, "l2a_h", qT, kT, gT, d["l2a_Wq"], d["l2a_Wk"], DH ** -0.5)
        recurrence(c, "l2a_r", qT, kT, vT, d["l2a_decay"], d["spread"], d["gather"])
        with c.nc.sbuf_tensor("l2a_a", big, F32) as a:
            linear_tok(c, "l2a_o", vT, d["l2a_wo"], a, bias=d["l2a_out_b"], resid=xn)
            norm_transpose(c, "l2a_ln1", a, dst_tok=xn, gamma=d["l2a_ln_g"], beta=d["l2a_ln_b"])
        add_to_x(c, "l2a_add", xn)


def l2_xattn(c):
    d = c.dram
    ctx, (qT, kT, v, ao) = tile_ctx(c, [("l2x_qT", [P, KC, N], F32), ("l2x_kT", [P, KC, B * S2], F32),
                                        ("l2x_v", [P, B, D], F32), ("l2x_ao", [P, NT, D], F32)])
    with ctx:
        norm_transpose(c, "l2x_ln", c.x, dst_T=c.xT)
        linear_T(c, "l2x_q", c.xT, [(d["l2x_wq"], qT, d["l2x_bq"], None)])
        linear_T(c, "l2x_k", c.ctxT, [(d["l2x_wk"], kT, d["l2x_bk"], None)], width=B * S2)
        linear_tok(c, "l2x_vp", c.ctxT, d["l2x_wv"], v, bias=d["l2x_bv"], tiles=B, rows=S2)
        cross_heads(c, "l2x", qT, kT, v, ao, clip=1e6 * DH ** 0.5)
        project_add(c, "l2x_o", ao, d["l2x_wo"], bias=d["l2x_bo"])


def l2_ffn(c):
    d = c.dram
    norm_transpose(c, "l2f_ln", c.x, dst_T=c.xT)
    tree_ffn(c, "l2f", c.xT, d["l2f_wi"], d["l2f_bi"], d["l2f_wo"])


def l3_attn(c):
    nc, d = c.nc, c.dram
    with nc.sbuf_tensor("l3a_xi", [P, NT, D], F32) as xi:
        norm_transpose(c, "l3a_ln", c.x, dst_tok=xi)
        norm_transpose(c, "l3a_rms", xi, dst_T=c.xT, eps=1e-6, rms=True)
        tiles = [P, NT, DK]
        ctx, (masks, coef, hc, qkvg, bgk, kT, qT, qgT, U, WT, PT) = tile_ctx(c, [
            ("l3a_masks", [P, 6, P], F32), ("l3a_coef", [P, 5, H3, NT], F32), ("l3a_hc", [P, 5, NT], F32),
            ("l3a_qkvg", [P, NT, 4 * DK], F32)] + [("l3a_" + n, tiles, F32) for n in ("bgk", "kT", "qT", "qgT", "U", "WT", "PT")])
        with ctx:
            with nc.sbuf_tensor("l3a_ba", [P, NT, 2 * H3], F32) as ba:
                linear_tok(c, "l3a_bap", c.xT, d["l3a_wba"], ba)
                delta_gates(c, "l3a_g", ba, d["l3a_dt"], d["l3a_alog"], coef)
            load(c, "l3a_m", masks, d["masks"])
            with nc.Fori(0, H3) as head:
                delta_project(c, "l3a_p", head, d["l3a_w"], coef, hc, qkvg, bgk, kT, qT, qgT)
                delta_invert(c, "l3a_i", masks, hc, qkvg, bgk, kT, qT, U, WT, PT)
                delta_scan(c, "l3a_s", hc, qkvg, qgT, U, WT, PT, qT)
                delta_output(c, "l3a_o", head, d["l3a_wo"], d["l3a_nw"], qkvg, qT, xi)
        norm_transpose(c, "l3a_ln2", xi, dst_T=c.xT, eps=1e-6, rms=True)
        add_to_x(c, "l3a_add", xi)
    with nc.sbuf_tensor("l3a_one", [P, NT, 2], F32) as one:
        fill(c, "l3a_f1", one[:], 1.0)
        experts(c, "l3a_mlp", c.xT, one, 2, d["l3a_fc"].shape[2], d["l3a_fc"], d["l3a_pr"], square=True)


def l3_xattn(c):
    nc, d = c.nc, c.dram
    norm_transpose(c, "l3x_ln", c.x, dst_T=c.xT)
    with nc.sbuf_tensor("l3x_ao", [P, NT, D], F32) as ao:
        self_attention(c, "l3x_s", d["l3x_wqk"], d["l3x_wv"], ao, False, None, d["l3x_b"], d["l3x_bv"])
        ctx, (qT, kT, v, aux) = tile_ctx(c, [("l3x_qT", [P, KC, N], F32), ("l3x_kT", [P, KC, B * S2], F32),
                                             ("l3x_v", [P, B, D], F32), ("l3x_aux", [P, NT, D], F32)])
        with ctx:
            linear_T(c, "l3x_qp", c.xT, [(d["l3x_q"], qT, d["l3x_bq"], None)])
            linear_T(c, "l3x_kp", c.ctxT, [(d["l3x_ka"], kT, d["l3x_bka"], None)], width=B * S2)
            linear_tok(c, "l3x_vp", c.ctxT, d["l3x_va"], v, bias=d["l3x_bva"], tiles=B, rows=S2)
            cross_heads(c, "l3x_c", qT, kT, v, aux)
            mix_heads(c, "l3x_m", ao, aux, d["l3x_g"])
        project_add(c, "l3x_o", ao, d["l3x_wo"], bias=d["l3x_bo"])


def l3_ffn(c):
    nc, d = c.nc, c.dram
    ctx, (wgt, slot, one, feat) = tile_ctx(c, [("l3f_wgt", [P, NT, E], F32), ("l3f_slot", [P, NT, E + 2], F32),
                                               ("l3f_one", [P, NT, 2], F32), ("l3f_feat", [P, NT, D], F32)])
    with ctx:
        fill(c, "l3f_ones", one[:], 1.0)
        norm_transpose(c, "l3f_ln", c.x, dst_tok=feat, dst_T=c.xT)
        experts(c, "l3f_s", c.xT, one, 2, d["l3f_sg"].shape[2], d["l3f_su"], d["l3f_sd"], gate=d["l3f_sg"])
        with nc.sbuf_tensor("l3f_rT", [P, KC, N], F32) as rT:
            norm_transpose(c, "l3f_rms", feat, dst_T=rT, eps=float(np.finfo(np.float32).eps), rms=True)
            route(c, "l3f_route", rT, d["l3f_r"], wgt, top=2, slot=slot)
        routed_experts(c, "l3f_e", feat, wgt, slot, d["l3f_g"].shape[2], d["l3f_g"], d["l3f_u"], d["l3f_d"],
                       d["l3f_rows"], d["l3f_cols"], d["l3f_heads"])


SUBLAYERS = [l0_attn, l0_xattn, l0_ffn, l1_attn, l1_xattn, l1_ffn, l2_attn, l2_xattn, l2_ffn, l3_attn, l3_xattn, l3_ffn]


def store(c, out):
    with Stage(c.nc, "store") as st:
        stored = st.sem("stored")
        with c.nc.Block() as block:
            @block.sync
            def _(sp):
                sp.dma_start(out.rearrange("b (t p) d -> p (b t) d", p=P), c.x[:]).then_inc(stored, 16)
                sp.wait_ge(stored, 16)


def decoder_kernel(nc, dram, out, sublayers):
    with ExitStack() as ctx:
        c = Core(nc, ctx, dram)
        setup(c)
        for f in sublayers:
            f(c)
        store(c, out)


def build(nc, inputs, sublayers):
    arrays, dram = {}, {}
    for name, a in lay_out({k: np.asarray(v) for k, v in inputs.items()}).items():
        a = np.ascontiguousarray(a)
        arrays[f"in_{name}"] = a
        dram[name] = nc.dram_tensor(f"in_{name}", a.shape, mybir.dt.from_np(a.dtype), kind="ExternalInput").ap()
    out = nc.dram_tensor("out_x", (B, S, D), F32, kind="ExternalOutput").ap()
    decoder_kernel(nc, dram, out, sublayers)
    return arrays


def kernel(**inputs):
    import concourse.bacc as bacc
    from concourse.bass_utils import run_bass_kernel_spmd
    nc = bacc.Bacc("TRN2", target_bir_lowering=False, num_devices=1)
    arrays = build(nc, inputs, SUBLAYERS)
    r = run_bass_kernel_spmd(nc, [arrays], core_ids=[0])
    return r.results[0]["out_x"]
```

```python
from contextlib import ExitStack

import numpy as np
import concourse.bass as bass
from concourse import mybir

P = 128
B = 2
S = 1024
N = B * S
NT = N // P
ST = S // P
D = 256
KC = D // P
S2 = 77
H = 16
DH = D // H

F32 = mybir.dt.float32
BF16 = mybir.dt.bfloat16
I32 = mybir.dt.int32
ALU = mybir.AluOpType
ACT = mybir.ActivationFunctionType
AX = mybir.AxisListType


class Stage(ExitStack):

    def __init__(self, nc, name):
        super().__init__()
        self.nc, self.name, self.sems = nc, name, []

    def sb(self, name, shape, dt=F32):
        return self.enter_context(self.nc.sbuf_tensor(f"{self.name}_{name}", shape, dt))

    def ps(self, name, shape, dt=F32):
        return self.enter_context(self.nc.psum_tensor(f"{self.name}_{name}", shape, dt))

    def sem(self, name, primed=False):
        s = self.enter_context(self.nc.semaphore(f"{self.name}_{name}"))
        self.sems.append(s)
        if primed:
            self.nc.gpsimd.sem_inc(s, 1)
        return s

    def __exit__(self, *exc):
        if exc[0] is None:
            for s in self.sems:
                self.nc.gpsimd.sem_clear(s)
            self.nc.all_engine_barrier()
        return super().__exit__(*exc)


class Core:

    def __init__(self, nc, ctx, dram):
        def sb(name, shape, dt=F32):
            return ctx.enter_context(nc.sbuf_tensor(name, shape, dt))

        self.nc, self.dram = nc, dram
        self.x = sb("x_res", [P, NT, D])
        self.xT = sb("xT", [P, KC, N])
        self.ident = sb("ident", [P, P])
        self.lower = sb("lower", [P, P])
        self.ones = sb("ones", [P, P])
        self.ctxT = sb("ctxT", [P, KC, B * S2])


def setup(c):
    nc = c.nc
    with Stage(nc, "setup") as st:
        x_in, zeroed, done = st.sem("x_in"), st.sem("zeroed"), st.sem("done")
        with nc.Block() as block:
            @block.sync
            def _(sp):
                sp.dma_start(c.x[:], c.dram["x"].rearrange("b (t p) d -> p (b t) d", p=P)).then_inc(x_in, 16)
                sp.dma_start(c.ctxT[:], c.dram["ctxT"].rearrange("(k p) n -> p k n", p=P)).then_inc(x_in, 16)
                sp.wait_ge(x_in, 32)

            @block.gpsimd
            def _(pool):
                pool.memset(c.ident[:], 0.0).then_inc(zeroed, 1)
                pool.memset(c.ones[:], 1.0).then_inc(zeroed, 1)
                pool.wait_ge(zeroed, 2)
                pool.affine_select(out=c.ident[:], in_=c.ident[:], compare_op=ALU.not_equal, fill=1.0,
                                   base=0, pattern=[[-1, P]], channel_multiplier=1).then_inc(done, 1)
                pool.affine_select(out=c.lower[:], in_=c.ones[:], compare_op=ALU.is_ge, fill=0.0,
                                   base=0, pattern=[[1, P]], channel_multiplier=-1).then_inc(done, 1)
                pool.wait_ge(done, 2)


def norm_transpose(c, name, src, dst_tok=None, dst_T=None, eps=1e-5, gamma=None, beta=None, rms=False, ahead=()):
    nc = c.nc
    PAIRS = NT // 2
    with Stage(nc, name) as st:
        stats = st.sb("stats", [P, NT, 6])
        mv = st.sb("mv", [P, NT, 2])
        std = st.sb("std", [P, NT])
        rstd = st.sb("rstd", [P, NT])
        shift = st.sb("shift", [P, NT])
        rows = dst_tok if dst_tok is not None else st.sb("rows", [P, NT, D])
        gb = st.sb("gb", [P, 2, 1, D])
        tp = st.ps("tp", [P, 4, 512])
        s = {n: st.sem(n) for n in ("ahead_in", "affine_in", "var", "std", "shaped", "scaled", "ready", "turned", "copied")}
        affine = gamma is not None
        with nc.Block() as block:
            @block.sync
            def _(sp):
                if affine:
                    load_weights(sp, [(gb[:, i, 0, :], row_bcast(v, D)) for i, v in enumerate((gamma, beta))], s["affine_in"])
                    sp.wait_ge(s["affine_in"], 32)
                if ahead:
                    sp.wait_ge(s["ahead_in"], load_weights(sp, ahead, s["ahead_in"]))

            @block.vector
            def _(dve):
                for t in range(NT):
                    dve.bn_stats(stats[:, t, :], src[:, t, :])
                dve.drain()
                for t in range(NT):
                    dve.bn_aggr(mv[:, t, :], stats[:, t, :])
                dve.drain()
                if rms:
                    dve.tensor_tensor(shift[:], mv[:, :, 0], mv[:, :, 0], ALU.mult)
                    dve.drain()
                    dve.tensor_tensor(mv[:, :, 1], mv[:, :, 1], shift[:], ALU.add)
                    dve.drain()
                dve.tensor_scalar(std[:], mv[:, :, 1], eps, None, ALU.add).then_inc(s["var"], 1)
                dve.wait_ge(s["std"], 1)
                dve.reciprocal(rstd[:], std[:])
                dve.drain()
                dve.scalar_tensor_tensor(out=shift[:], in0=mv[:, :, 0], scalar=0.0 if rms else -1.0, in1=rstd[:],
                                         op0=ALU.mult, op1=ALU.mult)
                dve.drain()
                if affine:
                    dve.wait_ge(s["affine_in"], 32)
                for pr in range(PAIRS + 2):
                    if pr < PAIRS:
                        for t in (2 * pr, 2 * pr + 1):
                            last = dve.tensor_scalar(rows[:, t, :], src[:, t, :], rstd[:, t:t + 1], shift[:, t:t + 1], ALU.mult, ALU.add)
                        last.then_inc(s["shaped"] if affine else s["ready"], 1)
                    if affine and pr >= 2:
                        dve.wait_ge(s["scaled"], pr - 1)
                        two = rows[:, 2 * pr - 4:2 * pr - 2, :]
                        dve.tensor_tensor(two, two, gb[:, 1].broadcast_to([P, 2, D]), ALU.add).then_inc(s["ready"], 1)

            @block.gpsimd
            def _(pool):
                if affine:
                    pool.wait_ge(s["affine_in"], 32)
                    for pr in range(PAIRS):
                        pool.wait_ge(s["shaped"], pr + 1)
                        two = rows[:, 2 * pr:2 * pr + 2, :]
                        pool.tensor_tensor(two, two, gb[:, 0].broadcast_to([P, 2, D]), ALU.mult).then_inc(s["scaled"], 1)

            if dst_T is not None:
                @block.tensor
                def _(pe):
                    for pr in range(PAIRS):
                        pe.wait_ge(s["ready"], pr + 1)
                        if pr >= 4:
                            pe.wait_ge(s["copied"], pr - 3)
                        for k in range(KC):
                            for j in range(2):
                                last = pe.transpose(tp[:, pr % 4, (2 * k + j) * P:(2 * k + j + 1) * P],
                                                    rows[:, 2 * pr + j, k * P:(k + 1) * P], c.ident[:])
                        last.then_inc(s["turned"], 1)

            @block.scalar
            def _(act):
                act.wait_ge(s["var"], 1)
                act.activation(std[:], std[:], ACT.Sqrt).then_inc(s["std"], 1)
                if dst_T is not None:
                    for pr in range(PAIRS):
                        act.wait_ge(s["turned"], pr + 1)
                        act.activation(dst_T[:, :, 2 * pr * P:2 * (pr + 1) * P], tp[:, pr % 4, :].rearrange("p (k n) -> p k n", k=KC),
                                       ACT.Copy).then_inc(s["copied"], 1)


def project_add(c, name, src, w, bias=None):
    nc = c.nc
    PAIRS = NT // 2
    with Stage(nc, name) as st:
        rowT = st.sb("rowT", [P, 2, KC, 2, P])
        w_sb = st.sb("w", [P, KC, D])
        b_sb = st.sb("b", [P, 1, D])
        tp = st.ps("tp", [P, 2, 512])
        out = st.ps("out", [P, 4, 512])
        s = {n: st.sem(n) for n in ("w_in", "turned", "rowT", "mult", "added")}
        loads = [(w_sb[:], w.rearrange("(k p) n -> p k n", p=P))]
        if bias is not None:
            loads.append((b_sb[:, 0, :], row_bcast(bias, D)))
        with nc.Block() as block:
            @block.sync
            def _(sp):
                load_weights(sp, loads, s["w_in"])
                sp.wait_ge(s["w_in"], 16 * len(loads))

            @block.tensor
            def _(pe):
                for pr in range(PAIRS + 1):
                    if pr < PAIRS:
                        if pr >= 2:
                            pe.wait_ge(s["rowT"], pr - 1)
                        for k in range(KC):
                            for j in range(2):
                                last = pe.transpose(tp[:, pr % 2, (2 * k + j) * P:(2 * k + j + 1) * P],
                                                    src[:, 2 * pr + j, k * P:(k + 1) * P], c.ident[:])
                        last.then_inc(s["turned"], 1)
                    if pr == 0:
                        pe.wait_ge(s["w_in"], 16 * len(loads))
                        continue
                    q = pr - 1
                    pe.wait_ge(s["rowT"], q + 1)
                    if q >= 4:
                        pe.wait_ge(s["added"], q - 3)
                    for j in range(2):
                        for k in range(KC):
                            last = pe.matmul(out[:, q % 4, j * D:(j + 1) * D], rowT[:, q % 2, k, j, :], w_sb[:, k, :],
                                             start=(k == 0), stop=(k == KC - 1))
                    last.then_inc(s["mult"], 1)

            @block.scalar
            def _(act):
                for pr in range(PAIRS):
                    act.wait_ge(s["turned"], pr + 1)
                    if pr >= 2:
                        act.wait_ge(s["mult"], pr - 1)
                    act.activation(rowT[:, pr % 2].rearrange("p k j n -> p (k j n)"), tp[:, pr % 2, :], ACT.Copy).then_inc(s["rowT"], 1)

            if bias is not None:
                @block.gpsimd
                def _(pool):
                    pool.wait_ge(s["w_in"], 16 * len(loads))
                    for pr in range(PAIRS):
                        pool.wait_ge(s["added"], pr + 1)
                        two = c.x[:, 2 * pr:2 * pr + 2, :]
                        pool.tensor_tensor(two, two, b_sb[:].broadcast_to([P, 2, D]), ALU.add)

            @block.vector
            def _(dve):
                for pr in range(PAIRS):
                    dve.wait_ge(s["mult"], pr + 1)
                    two = c.x[:, 2 * pr:2 * pr + 2, :]
                    dve.tensor_tensor(two, two, out[:, pr % 4, :].rearrange("p (t d) -> p t d", t=2), ALU.add).then_inc(s["added"], 1)


PART_PRODUCTS = ((0, 0), (1, 0), (2, 0), (0, 1), (1, 1), (0, 2), (1, 2))
SR = len(PART_PRODUCTS) * DH + 3
HC = 4
SLOT = 32
NC4 = H // HC


def self_attention(c, name, wqk, wv, ao, causal_after, rope, bias, bv=None):
    nc = c.nc
    kinds = wqk.shape[2]
    LH = S // 512
    nU = 2 * LH
    ROW = DH
    CD = HC * DH
    with Stage(nc, name) as st:
        xb = st.sb("xb", [P, KC, S])
        w = st.sb("w", [P, kinds, KC, P])
        w_v = st.sb("w_v", [P, KC, CD])
        b = st.sb("b", [P, 2])
        bv_sb = st.sb("bv", [P, CD])
        cs = st.sb("cs", [P, 2, S]) if rope is not None else None
        t1 = st.sb("t1", [P, 2, 512])
        t2 = st.sb("t2", [P, 2, 512])
        qk = st.sb("qk", [P, 2, S])
        part = st.sb("part", [P, 3, 2, S], BF16)
        stacked = st.sb("stacked", [P, 2, HC, S], BF16)
        place16 = st.sb("place16", [P, HC * 2 * 3, SR], BF16)
        qm = st.sb("qm", [P, HC, S], BF16)
        ident16 = st.sb("ident16", [P, P], BF16)
        v = st.sb("v", [P, ST, HC, SLOT])
        ones_v = st.sb("ones_v", [P, SLOT])
        upper = st.sb("upper", [P, P])
        negmax = st.sb("negmax", [P, ST, HC, 1])
        nm_row = st.sb("nm_row", [P, ST, HC, SR], BF16)
        pt = st.sb("pt", [P, 4, 2, 512])
        diag = st.sb("diag", [P, 4, 2, 2, P])
        oT = st.sb("oT", [P, 512])
        recip = st.sb("recip", [P, 4, HC])
        later = st.sb("later", [P, 4, HC])
        ps = st.ps("ps", [P, 8, 512])
        names = ("w_in", "c_in", "x_ready", "init", "proj", "rot", "sum", "v_mm", "v_ready",
                 "mx_mm", "mx_done", "nm", "p1", "rest", "p2", "p3", "qm", "stack", "stacked", "sc", "ex", "dg", "pv", "oT_ready", "o_T", "o_done", "pv_used")
        s = {n: st.sem(n, primed=n in ("v_mm", "o_done",)) for n in names}
        C_IN = 32 if rope is not None else 16
        WI = 64 if bv is not None else 48
        NU2 = ST * 2 * LH
        MH = HC * ST // 2
        LATE = 3
        NR = 4 * HC

        def sums_alone(n):
            return causal_after and n < NU2 // LH and n // 2 % ST >= ST // 2

        place = pt[:].rearrange("p a b n -> p (a b n)")[:, 0:HC * 2 * 3 * SR]

        def slot(hd):
            return slice(SLOT * hd, SLOT * hd + SLOT)

        def kind_half(u):
            return 1 - u // LH, u % LH

        def unit(a, u):
            which, h = kind_half(u)
            return a[:, which, h * 512:(h + 1) * 512]

        with nc.Block() as block:
            @block.sync
            def _(sp):
                sp.dma_start(place, c.dram["part_place"]).then_inc(s["c_in"], 16)
                if rope is not None:
                    sp.dma_start(cs[:], rope.rearrange("a p n -> p a n")).then_inc(s["c_in"], 16)
                for it in range(B * NC4):
                    ci = it % NC4
                    sp.wait_ge(s["v_mm"], it + 1)
                    sp.wait_ge(s["v_ready"], it)
                    sp.dma_start(w[:], wqk[ci]).then_inc(s["w_in"], 16)
                    sp.dma_start(w_v[:], wv[ci]).then_inc(s["w_in"], 16)
                    sp.dma_start(b[:], bias[ci]).then_inc(s["w_in"], 16)
                    if bv is not None:
                        sp.dma_start(bv_sb[:], bv[ci]).then_inc(s["w_in"], 16)
                sp.wait_ge(s["c_in"], C_IN)
                sp.wait_ge(s["w_in"], B * NC4 * WI)

            @block.gpsimd
            def _(pool):
                pool.memset(v[:], 0.0)
                pool.memset(ones_v[:], 0.0)
                pool.memset(nm_row[:], 0.0)
                pool.memset(qm[:], 0.0)
                pool.tensor_copy(ident16[:], c.ident[:])
                pool.memset(upper[:], 1.0)
                pool.drain()
                pool.memset(v[:, :, :, ROW:ROW + 1], 1.0)
                pool.memset(ones_v[:, ROW:ROW + 1], 1.0)
                pool.tensor_tensor(upper[:], upper[:], c.lower[:], ALU.subtract)
                pool.drain()
                pool.wait_ge(s["c_in"], C_IN)
                pool.tensor_copy(place16[:].rearrange("p a r -> p (a r)"), place)
                pool.drain()
                pool.sem_inc(s["init"], 1)
                with pool.Fori(0, B) as bi:
                    pool.wait_ge(s["v_mm"], bi * NC4 + 1)
                    pool.tensor_copy(xb[:], c.xT[:, :, bass.ds(bi * S, S)]).then_inc(s["x_ready"], 1)
                    with pool.Fori(0, NC4) as ci:
                        it = bi * NC4 + ci
                        for u in range(nU + 2):
                            if rope is not None and u < nU:
                                pool.wait_ge(s["rot"], it * nU + (u + 1))
                                pool.tensor_tensor(unit(qk[:], u), t1[:, u % 2, :], t2[:, u % 2, :], ALU.add).then_inc(s["sum"], 1)
                            if 1 <= u <= nU:
                                pool.wait_ge(s["p1"], it * nU + u)
                                pool.tensor_tensor(unit(qk[:], u - 1), unit(qk[:], u - 1), unit(part[:, 0], u - 1),
                                                   ALU.subtract).then_inc(s["rest"], 1)
                            if u >= 2:
                                pool.wait_ge(s["p2"], it * nU + (u - 1))
                                pool.tensor_tensor(unit(part[:, 2], u - 2), unit(qk[:], u - 2), unit(part[:, 1], u - 2),
                                                   ALU.subtract).then_inc(s["p3"], 1)

            @block.tensor
            def _(pe):
                pe.wait_ge(s["init"], 1)
                with pe.Fori(0, B) as bi:
                    with pe.Fori(0, NC4) as ci:
                        it = bi * NC4 + ci
                        pe.wait_ge(s["x_ready"], bi + 1)
                        pe.wait_ge(s["w_in"], it * WI + WI)
                        for u in range(nU):
                            which, h = kind_half(u)
                            if u >= 2:
                                pe.wait_ge(s["rot"], it * nU + (u - 1))
                            for g in range(kinds // 2):
                                for k in range(KC):
                                    last = pe.matmul(ps[:, 2 * (u % 2) + g, :], w[:, which + 2 * g, k, :],
                                                     xb[:, k, h * 512:(h + 1) * 512], start=(k == 0), stop=(k == KC - 1))
                            last.then_inc(s["proj"], 1)

                        def value(t):
                            for k in range(KC):
                                last = pe.matmul(ps[:, 4, t * CD:(t + 1) * CD], xb[:, k, t * P:(t + 1) * P],
                                                 w_v[:, k, :], start=(k == 0), stop=(k == KC - 1))
                            if t == ST - 1:
                                last.then_inc(s["v_mm"], 1)

                        def maxima(m, bank):
                            hd, t = m % HC, m // HC
                            for h in range(LH):
                                last = pe.matmul(ps[:, bank + h, :], qm[:, hd, t * P:(t + 1) * P], part[:, 0, 1, h * 512:(h + 1) * 512],
                                                 start=True, stop=True)
                            last.then_inc(s["mx_mm"], 1)

                        def stack(r):
                            which = 1 if r < 2 * HC else 0
                            hd, h = (r // 2, r % 2) if which else (r % HC, (r - 2 * HC) // HC)
                            if r >= 2:
                                pe.wait_ge(s["stacked"], it * NR + (r - 1))
                            out = ps[0:SR, 6 + r % 2, :]
                            for a in range(3):
                                last = pe.matmul(out, place16[:, (hd * 2 + which) * 3 + a, :], part[:, a, which, h * 512:(h + 1) * 512],
                                                 start=(a == 0), stop=(a == 2), skip_group_check=True)
                            if which == 0:
                                for t in range(4):
                                    last = pe.matmul(out[:, t * P:(t + 1) * P], nm_row[:, 4 * h + t, hd, :], ident16[:],
                                                     start=False, stop=True, skip_group_check=True)
                            last.then_inc(s["stack"], 1)

                        pe.wait_ge(s["p1"], it * nU + (nU - 1))
                        pe.wait_ge(s["qm"], it * LH + 1)
                        for m in range(MH):
                            if m >= 2:
                                pe.wait_ge(s["mx_done"], it * (2 * MH) + (m - 1))
                            if m == 1:
                                pe.wait_ge(s["rot"], it * nU + nU)
                            maxima(m, 2 * (m % 2))
                            if m == 0:
                                pe.wait_ge(s["o_done"], it * LH + 1)
                            if m < ST:
                                value(m)
                            elif m < MH - LATE:
                                if m == ST:
                                    pe.wait_ge(s["p3"], it * nU + 2)
                                stack(m - ST)
                        for r in range(2 * HC - LATE, 2 * HC):
                            stack(r)
                        pe.wait_ge(s["p3"], it * nU + 3)
                        pe.wait_ge(s["nm"], it * 2 + 1)
                        for q in range(HC):
                            stack(2 * HC + q)
                        pe.wait_ge(s["v_ready"], it + 1)

                        def scores(n):
                            qh, kt, pr = n // (2 * ST), (n // 2) % ST, n % 2
                            if n >= 2:
                                pe.wait_ge(s["ex"], it * NU2 + (n - 1))
                            if kt == 0:
                                pe.wait_ge(s["stacked"], it * NR + ((2 + qh) * HC + 2 * pr + 2))
                            if sums_alone(n):
                                t = kt - ST // 2
                                for e in range(2):
                                    last = pe.matmul(ps[:, 2 * pr + e, :], stacked[0:SR, 0, 2 * pr + e, t * P:(t + 1) * P],
                                                     stacked[0:SR, 1, 2 * pr + e, S // 2:S], start=True, stop=True)
                                last.then_inc(s["sc"], 1)
                                return
                            for e in range(2):
                                last = pe.matmul(ps[:, 2 * pr + e, :], stacked[0:SR, 1, 2 * pr + e, kt * P:(kt + 1) * P],
                                                 stacked[0:SR, 0, 2 * pr + e, qh * 512:(qh + 1) * 512], start=True, stop=True)
                            last.then_inc(s["sc"], 1)

                        def weigh(n):
                            qh, kt = n // (2 * ST), n // 2 % ST
                            pe.wait_ge(s["ex"], it * NU2 + (n + 2))
                            if sums_alone(n):
                                pe.sem_inc(s["pv"], 2)
                                return
                            j = kt - 4 * qh
                            last_kt = 3 if causal_after and qh == 0 else ST - 1
                            if causal_after and 0 <= j < 4:
                                pe.wait_ge(s["dg"], it * 2 * ST + (2 * kt + 2))
                            parts = []
                            for hd in range(HC):
                                u, e = n + hd // 2, hd % 2
                                src, vv = pt[:, u % 4, e, :], v[:, kt, hd, :]
                                if not causal_after or j < 0:
                                    own = [(vv, src, 0, 512)]
                                else:
                                    own = [(vv, diag[:, u % 4, 0, e, :], j * P, (j + 1) * P),
                                           (ones_v[:], diag[:, u % 4, 1, e, :], j * P, (j + 1) * P)]
                                    if j > 0:
                                        own.append((ones_v[:], src[:, 0:j * P], 0, j * P))
                                    if j < 3:
                                        own.append((vv, src[:, (j + 1) * P:512], (j + 1) * P, 512))
                                parts.append(own)
                            for q, four in enumerate(zip(*parts)):
                                for hd, (lhs, rhs, a, z) in enumerate(four):
                                    last = pe.matmul(ps[SLOT * hd:SLOT * hd + SLOT, 4 + qh, a:z], lhs, rhs, start=(kt == 0 and q == 0),
                                                     stop=(kt == last_kt), skip_group_check=True)
                            last.then_inc(s["pv"], 2)

                        def turn(qh):
                            pe.wait_ge(s["oT_ready"], it * LH + (qh + 1))
                            for t in range(4):
                                last = pe.transpose(ps[:, 6, t * P:(t + 1) * P], oT[:, t * P:(t + 1) * P], c.ident[:])
                            last.then_inc(s["o_T"], 1)

                        def second_maxima(n):
                            pe.wait_ge(s["mx_done"], it * (2 * MH) + (MH + n))
                            maxima(MH + n, 6)

                        for n in range(0, NU2 + 2, 2):
                            if n == 0:
                                pe.wait_ge(s["qm"], it * LH + 2)
                                pe.wait_ge(s["stacked"], it * NR + 3 * HC)
                            if n < MH:
                                second_maxima(n)
                            if n < NU2:
                                scores(n)
                                scores(n + 1)
                            if n < MH:
                                second_maxima(n + 1)
                            if n >= 2 and n != MH:
                                weigh(n - 2)
                            if n == MH - 2:
                                weigh(n)
                                pe.wait_ge(s["p3"], it * nU + nU)
                                pe.wait_ge(s["nm"], it * 2 + 2)
                                for q in range(HC):
                                    stack(3 * HC + q)
                            if n == MH + 4:
                                turn(0)
                        turn(1)

            @block.scalar
            def _(act):
                with act.Fori(0, B * NC4) as it:
                    for u in range(nU + 1):
                        if u < nU:
                            act.wait_ge(s["sum"] if rope is not None else s["rot"], it * nU + (u + 1))
                            act.activation(unit(part[:, 0], u), unit(qk[:], u), ACT.Copy).then_inc(s["p1"], 1)
                        if u >= 1:
                            act.wait_ge(s["rest"], it * nU + u)
                            act.activation(unit(part[:, 1], u - 1), unit(qk[:], u - 1), ACT.Copy).then_inc(s["p2"], 1)

                    def take(r):
                        which = 1 if r < 2 * HC else 0
                        hd, h = (r // 2, r % 2) if which else (r % HC, (r - 2 * HC) // HC)
                        act.wait_ge(s["stack"], it * NR + (r + 1))
                        act.activation(stacked[0:SR, which, hd, h * 512:(h + 1) * 512], ps[0:SR, 6 + r % 2, :],
                                       ACT.Copy).then_inc(s["stacked"], 1)

                    for q in range(3 * HC):
                        take(q)
                    for n in range(NU2):
                        if n == MH:
                            for q in range(HC):
                                take(3 * HC + q)
                        act.wait_ge(s["sc"], it * NU2 + (n + 1))
                        if n >= 4:
                            act.wait_ge(s["pv"], it * NU2 + (n - 3))
                        if sums_alone(n):
                            kt, pr = n // 2 % ST, n % 2
                            for e in range(2):
                                last = act.activation(pt[:, n % 4, e, :], ps[:, 2 * pr + e, :], ACT.Exp, scale=DH ** -0.5,
                                                      accum_out=later[:, kt - ST // 2, 2 * pr + e:2 * pr + e + 1])
                            last.then_inc(s["ex"], 1)
                            continue
                        act.activation(pt[:, n % 4, :, :], ps[:, 2 * (n % 2):2 * (n % 2) + 2, :], ACT.Exp,
                                       scale=DH ** -0.5).then_inc(s["ex"], 1)

            @block.vector
            def _(dve):
                dve.wait_ge(s["init"], 1)
                if rope is not None:
                    dve.wait_ge(s["c_in"], C_IN)
                with dve.Fori(0, B) as bi:
                    with dve.Fori(0, NC4) as ci:
                        it = bi * NC4 + ci
                        dve.wait_ge(s["w_in"], it * WI + WI)
                        for u in range(nU):
                            which, h = kind_half(u)
                            dve.wait_ge(s["proj"], it * nU + (u + 1))
                            src0, src1 = ps[:, 2 * (u % 2), :], ps[:, 2 * (u % 2) + 1, :]
                            if rope is not None:
                                if u >= 2:
                                    dve.wait_ge(s["sum"], it * nU + (u - 1))
                                if which == 1:
                                    dve.scalar_tensor_tensor(out=t1[:, u % 2, :], in0=src0, scalar=b[:, 1:2],
                                                             in1=cs[:, 0, h * 512:(h + 1) * 512], op0=ALU.add, op1=ALU.mult)
                                else:
                                    dve.tensor_tensor(t1[:, u % 2, :], src0, cs[:, 0, h * 512:(h + 1) * 512], ALU.mult)
                                dve.tensor_tensor(t2[:, u % 2, :], src1, cs[:, 1, h * 512:(h + 1) * 512], ALU.mult).then_inc(s["rot"], 1)
                            else:
                                dve.tensor_scalar(qk[:, which, h * 512:(h + 1) * 512], src0, b[:, which:which + 1], None,
                                                  ALU.add).then_inc(s["rot"], 1)
                        def maximum(m, bank):
                            dve.wait_ge(s["mx_mm"], it * (2 * MH) + (m + 1))
                            dve.tensor_reduce(negmax[:, m // HC, m % HC, :], ps[:, bank:bank + 2, :],
                                              AX.XY, ALU.max, negate=True).then_inc(s["mx_done"], 1)

                        def place_maxima(h):
                            nm, row = negmax[:, 4 * h:4 * h + 4], nm_row[:, 4 * h:4 * h + 4]
                            dve.drain()
                            for a in range(3):
                                last = dve.tensor_copy(row[:, :, :, SR - 3 + a:SR - 2 + a], nm)
                                if a < 2:
                                    dve.drain()
                                    dve.tensor_tensor(nm, nm, row[:, :, :, SR - 3 + a:SR - 2 + a], ALU.subtract)
                                    dve.drain()
                            last.then_inc(s["nm"], 1)

                        def single_out(h):
                            dve.wait_ge(s["p1"], it * nU + (nU - 1 + h))
                            for hd in range(HC):
                                last = dve.tensor_copy(qm[slot(hd), hd, h * 512:(h + 1) * 512], part[slot(hd), 0, 0, h * 512:(h + 1) * 512])
                            last.then_inc(s["qm"], 1)

                        single_out(0)
                        for m in range(MH):
                            maximum(m, 2 * (m % 2))
                        place_maxima(0)
                        single_out(1)
                        dve.wait_ge(s["v_mm"], it + 2)
                        vsrc = ps[:, 4, :].rearrange("p (t h d) -> p t h d", t=ST, h=HC)
                        if bv is not None:
                            vb = bv_sb[:].rearrange("p (a h d) -> p a h d", a=1, h=HC).broadcast_to([P, ST, HC, DH])
                            dve.tensor_tensor(v[:, :, :, 0:DH], vsrc, vb, ALU.add).then_inc(s["v_ready"], 1)
                        else:
                            dve.tensor_copy(v[:, :, :, 0:DH], vsrc).then_inc(s["v_ready"], 1)

                        def finish(qh):
                            dve.wait_ge(s["pv"], it * NU2 + NU2 // LH * (qh + 1))
                            dve.tensor_copy(oT[:], ps[:, 4 + qh, :]).then_inc(s["oT_ready"], 1)
                            dve.wait_ge(s["o_T"], it * LH + (qh + 1))
                            o = ps[:, 6, :].rearrange("p (t h s) -> p t h s", t=4, h=HC)
                            if causal_after and qh == 0:
                                dve.tensor_tensor(recip[:], o[:, :, :, ROW], later[:], ALU.add)
                                dve.drain()
                                dve.reciprocal(recip[:], recip[:])
                            else:
                                dve.reciprocal(recip[:], o[:, :, :, ROW])
                            dve.drain()
                            r4 = recip[:].rearrange("p t (h a) -> p t h a", a=1).broadcast_to([P, 4, HC, DH])
                            dst = ao[:, bass.ds(bi * ST + 4 * qh, 4), bass.ds(ci * CD, CD)].rearrange("p t (h d) -> p t h d", h=HC)
                            dve.tensor_tensor(dst, o[:, :, :, 0:DH], r4, ALU.mult).then_inc(s["o_done"], 1)

                        for n in range(NU2):
                            qh, kt, pr = n // (2 * ST), (n // 2) % ST, n % 2
                            j = kt - 4 * qh
                            if n < MH:
                                maximum(MH + n, 6)
                            if n == MH - 1:
                                place_maxima(1)
                            if causal_after and 0 <= j < 4:
                                dve.wait_ge(s["ex"], it * NU2 + (n + 1))
                                if n >= 4:
                                    dve.wait_ge(s["pv"], it * NU2 + (n - 3))
                                for z, mask in enumerate((c.lower, upper)):
                                    mk = mask[:].rearrange("p (a n) -> p a n", a=1).broadcast_to([P, 2, P])
                                    last = dve.tensor_tensor(diag[:, n % 4, z, :, :], pt[:, n % 4, :, j * P:(j + 1) * P],
                                                             mk, ALU.mult)
                                last.then_inc(s["dg"], 1)
                            if n == NU2 // LH + 1:
                                finish(0)
                        finish(1)



def load_weights(sp, pairs, sem):
    for dst, src in pairs:
        sp.dma_start(dst, src).then_inc(sem, 16)
    return 16 * len(pairs)


def row_bcast(v, n, parts=P):
    return v.rearrange("(a n) -> a n", a=1).broadcast_to([parts, n])


def linear_T(c, name, srcT, jobs, width=N):
    nc = c.nc
    step = min(512, width)
    nb = width // step
    with Stage(nc, name) as st:
        ps = st.ps("ps", [P, 8, 512])
        w_in, proj_a, proj_v, free_a, free_v = (st.sem(n) for n in ("w_in", "proj_a", "proj_v", "free_a", "free_v"))
        loads, chunks = [], []
        for q, (w, dst, bias, func) in enumerate(jobs):
            M = w.shape[1]
            w_sb = st.sb(f"w{q}", [P, KC, M])
            loads.append((w_sb[:], w.rearrange("(k p) m -> p k m", p=P)))
            b_sb = None
            if bias is not None:
                b_sb = st.sb(f"b{q}", [P, M // P])
                loads.append((b_sb[:], bias))
            for m in range(M // P):
                lane = "a" if func is not None or len(chunks) % 2 == 0 else "v"
                at = sum(x[0] == lane for x in chunks)
                chunks.append((lane, at, w_sb, b_sb, dst, m, func))
        per = {lane: sum(x[0] == lane for x in chunks) for lane in "av"}
        assert all(n <= 4 or n % 4 == 0 for n in per.values())
        total = 16 * len(loads)
        proj, free = {"a": proj_a, "v": proj_v}, {"a": free_a, "v": free_v}
        bank = {"a": 0, "v": 4}
        with nc.Block() as block:
            @block.sync
            def _(sp):
                load_weights(sp, loads, w_in)
                sp.wait_ge(w_in, total)

            @block.tensor
            def _(pe):
                pe.wait_ge(w_in, total)
                with pe.Fori(0, nb) as n:
                    for lane, at, w_sb, b_sb, dst, m, func in chunks:
                        pe.wait_ge(free[lane], n * per[lane] + (at + 1))
                        for k in range(KC):
                            last = pe.matmul(ps[:, bank[lane] + at % 4, 0:step], w_sb[:, k, m * P:(m + 1) * P],
                                             srcT[:, k, bass.ts(n, step)], start=(k == 0), stop=(k == KC - 1))
                        last.then_inc(proj[lane], 1)

            @block.scalar
            def _(act):
                act.sem_inc(free_a, min(4, per["a"]))
                act.wait_ge(w_in, total)
                with act.Fori(0, nb) as n:
                    for lane, at, w_sb, b_sb, dst, m, func in chunks:
                        if lane == "a":
                            act.wait_ge(proj_a, n * per["a"] + (at + 1))
                            act.activation(dst[:, m, bass.ts(n, step)], ps[:, at % 4, 0:step], func or ACT.Identity,
                                           bias=0.0 if b_sb is None else b_sb[:, m:m + 1]).then_inc(free_a, 1)

            @block.vector
            def _(dve):
                if per["v"]:
                    dve.sem_inc(free_v, min(4, per["v"]))
                    dve.wait_ge(w_in, total)
                    with dve.Fori(0, nb) as n:
                        for lane, at, w_sb, b_sb, dst, m, func in chunks:
                            if lane == "v":
                                dve.wait_ge(proj_v, n * per["v"] + (at + 1))
                                dve.tensor_scalar(dst[:, m, bass.ts(n, step)], ps[:, 4 + at % 4, 0:step],
                                                  0.0 if b_sb is None else b_sb[:, m:m + 1], None, ALU.add).then_inc(free_v, 1)


def rope_weights(c, ctx, name, jobs, table, per_chunk):
    def sb(n, shape):
        return ctx.enter_context(c.nc.sbuf_tensor(f"{name}_{n}", shape, F32))

    tk = KC if per_chunk else 1
    cs = sb("cs", [P, 2, tk, S])
    loads, sbs = [], []
    for q, (w, ws, dst, b, bs) in enumerate(jobs):
        w_sb, b_sb = sb(f"w{q}", [P, 2, KC, D]), None
        loads += [(w_sb[:, 0], w.rearrange("(k p) m -> p k m", p=P)), (w_sb[:, 1], ws.rearrange("(k p) m -> p k m", p=P))]
        if b is not None:
            b_sb = sb(f"b{q}", [P, 2, KC])
            loads += [(b_sb[:, 0], b), (b_sb[:, 1], bs)]
        sbs.append((w_sb, b_sb, dst))
    loads += [(cs[:, i, :, :], table[i].rearrange("k p s -> p k s") if per_chunk else table[i].rearrange("p (a s) -> p a s", a=1))
              for i in range(2)]
    return cs, sbs, loads


def rope_T(c, name, srcT, weights, per_chunk):
    nc = c.nc
    with Stage(nc, name) as st:
        ps = st.ps("ps", [P, 8, 512])
        t12 = st.sb("t12", [P, 4, 2, 512])
        cs, sbs = weights[:2]
        proj, rot, summed = (st.sem(n, primed=n != "proj") for n in ("proj", "rot", "summed"))
        units = [(h, q, m) for h in range(S // 512) for q in range(len(sbs)) for m in range(KC)]
        U = len(units)
        assert U % 4 == 0
        with nc.Block() as block:
            @block.tensor
            def _(pe):
                with pe.Fori(0, B) as bi:
                    for i, (h, q, m) in enumerate(units):
                        pe.wait_ge(rot, bi * U + (i - 2) if i >= 4 else bi * U + 1)
                        for g in range(2):
                            for k in range(KC):
                                last = pe.matmul(ps[:, 2 * (i % 4) + g, :], sbs[q][0][:, g, k, m * P:(m + 1) * P],
                                                 srcT[:, k, bass.ds(bi * S + h * 512, 512)], start=(k == 0), stop=(k == KC - 1))
                        last.then_inc(proj, 1)

            @block.vector
            def _(dve):
                with dve.Fori(0, B) as bi:
                    for i, (h, q, m) in enumerate(units):
                        dve.wait_ge(proj, bi * U + (i + 1))
                        dve.wait_ge(summed, bi * U + (i - 2) if i >= 4 else bi * U + 1)
                        for g in range(2):
                            out, src = t12[:, i % 4, g, :], ps[:, 2 * (i % 4) + g, :]
                            tab = cs[:, g, m if per_chunk else 0, h * 512:(h + 1) * 512]
                            if sbs[q][1] is None:
                                last = dve.tensor_tensor(out, src, tab, ALU.mult)
                            else:
                                last = dve.scalar_tensor_tensor(out=out, in0=src, scalar=sbs[q][1][:, g, m:m + 1], in1=tab,
                                                                op0=ALU.add, op1=ALU.mult)
                        last.then_inc(rot, 1)

            @block.gpsimd
            def _(pool):
                with pool.Fori(0, B) as bi:
                    for i, (h, q, m) in enumerate(units):
                        pool.wait_ge(rot, bi * U + (i + 2))
                        pool.tensor_tensor(sbs[q][2][:, m, bass.ds(bi * S + h * 512, 512)], t12[:, i % 4, 0, :],
                                           t12[:, i % 4, 1, :], ALU.add).then_inc(summed, 1)


def linear_tok(c, name, srcT, w, dst=None, bias=None, resid=None, relu=False, tiles=NT, rows=P):
    nc = c.nc
    M = w.shape[1]
    with Stage(nc, name) as st:
        ps = st.ps("ps", [P, 4, 512])
        w_sb = st.sb("w", [P, KC, M])
        b_sb = st.sb("b", [P, M])
        w_in, mult, out = st.sem("w_in"), st.sem("mult"), st.sem("out")
        loads = [(w_sb[:], w.rearrange("(k p) m -> p k m", p=P))]
        if bias is not None:
            loads.append((b_sb[:], row_bcast(bias, M)))
        total = 16 * len(loads)
        with nc.Block() as block:
            @block.sync
            def _(sp):
                load_weights(sp, loads, w_in)
                sp.wait_ge(w_in, total)

            @block.tensor
            def _(pe):
                pe.wait_ge(w_in, total)
                for t in range(tiles):
                    if t >= 4:
                        pe.wait_ge(out, t - 3)
                    for k in range(KC):
                        last = pe.matmul(ps[0:rows, t % 4, 0:M], srcT[:, k, t * rows:(t + 1) * rows], w_sb[:, k, :],
                                         start=(k == 0), stop=(k == KC - 1))
                    last.then_inc(mult, 1)

            @block.vector
            def _(dve):
                dve.wait_ge(w_in, total)
                for t in range(tiles):
                    dve.wait_ge(mult, t + 1)
                    d, p_ = dst[0:rows, t, :], ps[0:rows, t % 4, 0:M]
                    if bias is None and not relu and resid is None:
                        dve.tensor_copy(d, p_).then_inc(out, 1)
                        continue
                    if bias is not None:
                        last = dve.tensor_tensor(d, p_, b_sb[0:rows, :], ALU.add)
                        src = d
                    else:
                        src = p_
                    if relu:
                        if bias is not None:
                            dve.drain()
                        last = dve.scalar_tensor_tensor(out=d, in0=src, scalar=0.0, in1=resid[0:rows, t, :],
                                                        op0=ALU.max, op1=ALU.add)
                    elif resid is not None:
                        if bias is not None:
                            dve.drain()
                        last = dve.tensor_tensor(d, src, resid[0:rows, t, :], ALU.add)
                    last.then_inc(out, 1)


def additive_attention(c, name, feat, feT, txb, sw, sb_rows):
    nc, d = c.nc, c.dram
    HALVES = S // 512
    G = ST // 2
    with Stage(nc, name) as st:
        h = st.sb("h", [P, 2, KC, S])
        z0 = st.sb("z0", [P, 2, S])
        z = st.sb("z", [P, 2, S])
        w_col = st.sb("w_col", [P, KC])
        sel = st.sb("sel", [P, 2 * S2 - 1])
        m_i = st.sb("m_i", [S2, B], I32)
        m_f = st.sb("m_f", [S2, B])
        bc = st.sb("bc", [P, 2])
        rT = st.sb("rT", [S2, S])
        nmax = st.sb("nmax", [P, ST])
        e = st.sb("e", [P, ST, S2])
        es = st.sb("es", [P, 2, ST, S2])
        sums = st.sb("sums", [P, 3, ST])
        gate = st.sb("gate", [P, 2, ST])
        tmp = st.sb("tmp", [P, 2, D])
        rho = st.ps("rho", [P, 2, 512])
        rT_ps = st.ps("rT_ps", [P, 2, 512])
        names = ("w_in", "init", "tanh", "z", "row", "rho_read", "turned", "nmax", "exp", "sums", "gate", "added")
        s = {n: st.sem(n, primed=n in ("z", "row", "rho_read", "exp",)) for n in names}
        loads = [(w_col[:], d["l0x_w"]), (m_i[:], d["mask2T"]),
                 (bc[:, 0:1], row_bcast(d["l0x_bcw"], 1)), (bc[:, 1:2], row_bcast(d["l0x_bcb"], 1))]
        total = 16 * len(loads)
        with nc.Block() as block:
            @block.sync
            def _(sp):
                load_weights(sp, loads, s["w_in"])
                sp.wait_ge(s["w_in"], total)

            @block.gpsimd
            def _(pool):
                pool.memset(sel[:], 0.0)
                pool.drain()
                pool.memset(sel[:, S2 - 1:S2], 1.0)
                pool.drain()
                pool.sem_inc(s["init"], 1)

            @block.scalar
            def _(act):
                act.wait_ge(s["w_in"], total)
                with act.Fori(0, B) as bi:
                    for t in range(S2):
                        if t >= 2:
                            act.wait_ge(s["z"], bi * S2 + t)
                        else:
                            act.wait_ge(s["z"], bi * S2 + 1)
                        for k in range(KC):
                            last = act.activation(h[:, t % 2, k, :], feT[:, k, bass.ds(bi * S, S)], ACT.Tanh,
                                                  bias=txb[:, k, bass.ds(bi * S2 + t, 1)])
                        last.then_inc(s["tanh"], 1)
                    act.wait_ge(s["nmax"], bi + 1)
                    for t in range(ST):
                        last = act.activation(e[:, t, :], rT_ps[:, t // G, (t % G) * S2:(t % G + 1) * S2], ACT.Exp,
                                              bias=nmax[:, t:t + 1])
                    last.then_inc(s["exp"], 1)
                    act.wait_ge(s["sums"], bi + 1)
                    for g in range(2):
                        last = act.activation(gate[:, g, :], gate[:, g, :], ACT.Tanh, bias=bc[:, g:g + 1])
                    last.then_inc(s["gate"], 1)

            @block.vector
            def _(dve):
                dve.wait_ge(s["w_in"], total)
                dve.tensor_copy(m_f[:], m_i[:])
                dve.drain()
                dve.tensor_scalar(m_f[:], m_f[:], -1.0, 1.0, ALU.mult, ALU.add)
                dve.drain()
                dve.tensor_scalar(m_f[:], m_f[:], -1e30, None, ALU.mult)
                with dve.Fori(0, B) as bi:
                    for t in range(S2):
                        dve.wait_ge(s["tanh"], bi * S2 + (t + 1))
                        dve.wait_ge(s["row"], bi * S2 + t if t >= 2 else bi * S2 + 1)
                        dve.tensor_scalar(z0[:, t % 2, :], h[:, t % 2, 1, :], w_col[:, 1:2], None, ALU.mult)
                        dve.drain()
                        dve.scalar_tensor_tensor(out=z[:, t % 2, :], in0=h[:, t % 2, 0, :], scalar=w_col[:, 0:1],
                                                 in1=z0[:, t % 2, :], op0=ALU.mult, op1=ALU.add).then_inc(s["z"], 1)
                    dve.wait_ge(s["row"], bi * S2 + (S2 + 1))
                    dve.tensor_scalar(rT[:].rearrange("p (a n) -> p a n", a=HALVES), rho[0:S2, :, :],
                                      m_f[:, bass.ds(bi, 1)], None, ALU.add).then_inc(s["rho_read"], 1)
                    dve.wait_ge(s["turned"], bi + 1)
                    for q in range(2):
                        last = dve.tensor_reduce(nmax[:, q * G:(q + 1) * G], rT_ps[:, q, 0:G * S2].rearrange("p (t n) -> p t n", t=G),
                                                 AX.X, ALU.max, negate=True)
                    last.then_inc(s["nmax"], 1)
                    dve.wait_ge(s["exp"], bi + 2)
                    dve.tensor_reduce(sums[:, 0, :], e[:], AX.X, ALU.add)
                    for g, rowv in enumerate((sw, sb_rows)):
                        r = rowv[:, bass.ds(bi, 1), :].broadcast_to([P, ST, S2])
                        dve.tensor_tensor(es[:, g], e[:], r, ALU.mult)
                    dve.drain()
                    dve.tensor_reduce(sums[:, 1:3, :], es[:], AX.X, ALU.add)
                    dve.reciprocal(sums[:, 0, :], sums[:, 0, :])
                    dve.drain()
                    dve.tensor_tensor(gate[:], sums[:, 1:3, :], sums[:, 0:1, :].broadcast_to([P, 2, ST]), ALU.mult).then_inc(s["sums"], 1)
                    dve.wait_ge(s["gate"], bi + 1)
                    for t in range(ST):
                        dve.tensor_scalar(tmp[:, t % 2:t % 2 + 1, :], feat[:, bass.ds(bi * ST + t, 1), :], gate[:, 0, t:t + 1],
                                          gate[:, 1, t:t + 1], ALU.mult, ALU.add)
                        dve.drain()
                        x_t = c.x[:, bass.ds(bi * ST + t, 1), :]
                        dve.tensor_tensor(x_t, x_t, tmp[:, t % 2:t % 2 + 1, :], ALU.add)

            @block.tensor
            def _(pe):
                pe.wait_ge(s["init"], 1)
                with pe.Fori(0, B) as bi:
                    pe.wait_ge(s["rho_read"], bi + 1)
                    for t in range(S2):
                        pe.wait_ge(s["z"], bi * S2 + (t + 2))
                        for hf in range(HALVES):
                            last = pe.matmul(rho[0:S2, hf, :], sel[:, S2 - 1 - t:2 * S2 - 1 - t], z[:, t % 2, hf * 512:(hf + 1) * 512],
                                             start=(t == 0), stop=(t == S2 - 1))
                        last.then_inc(s["row"], 1)
                    pe.wait_ge(s["rho_read"], bi + 2)
                    pe.wait_ge(s["exp"], bi + 1)
                    for t in range(ST):
                        last = pe.transpose(rT_ps[:, t // G, (t % G) * S2:(t % G + 1) * S2], rT[:, t * P:(t + 1) * P],
                                            c.ident[0:S2, 0:S2])
                    last.then_inc(s["turned"], 1)


def ctx_rows(c, name, cols, dst):
    nc = c.nc
    with Stage(nc, name) as st:
        w = st.sb("w", [P, len(cols), KC, P])
        ps = st.ps("ps", [P, 2, 512])
        w_in, mult, out = st.sem("w_in"), st.sem("mult"), st.sem("out")
        with nc.Block() as block:
            @block.sync
            def _(sp):
                load_weights(sp, [(w[:, i], v.rearrange("(k p) m -> p k m", p=P)) for i, v in enumerate(cols)], w_in)
                sp.wait_ge(w_in, 16 * len(cols))

            @block.tensor
            def _(pe):
                pe.wait_ge(w_in, 16 * len(cols))
                for i in range(len(cols)):
                    for k in range(KC):
                        last = pe.matmul(ps[:, i, 0:B * S2], w[:, i, k, :], c.ctxT[:, k, :], start=(k == 0), stop=(k == KC - 1))
                last.then_inc(mult, 1)

            @block.vector
            def _(dve):
                dve.wait_ge(mult, 1)
                for i in range(len(cols)):
                    dve.tensor_copy(dst[i][:].rearrange("p b t -> p (b t)"), ps[:, i, 0:B * S2])


E = 8
CAPACITY = N * 5 // 4 // E
NO_SLOT = 1024.0


def route(c, name, srcT, w, wgt, bias=None, top=1, slot=None):
    nc = c.nc
    with Stage(nc, name) as st:
        w_sb = st.sb("w", [P, KC, E])
        b_sb = st.sb("b", [E, 1])
        lT = st.sb("lT", [E, N])
        L = st.sb("L", [P, NT, E])
        rank = st.sb("rank", [P, E])
        m = st.sb("m", [P, 2, NT, 1])
        p_ = st.sb("p", [P, NT, E])
        rk = st.sb("rk", [P, NT, 1])
        sel = st.sb("sel", [P, 2, NT, E])
        tmp = st.sb("tmp", [P, NT, E])
        tot = st.sb("tot", [P, 2, NT, 1])
        strict = st.sb("strict", [P, P])
        cum = st.sb("cum", [P, NT, E])
        before = st.sb("before", [P, NT, E])
        lps = st.ps("lps", [P, 4, 512])
        tps = st.ps("tps", [P, 512])
        cps = st.ps("cps", [P, 2, 512])
        names = ("w_in", "mult", "lT_ready", "turned", "shifted", "exp", "chosen", "counted", "rank_ready")
        s = {n: st.sem(n) for n in names}
        loads = [(w_sb[:], w.rearrange("(k p) e -> p k e", p=P))]
        if bias is not None:
            loads.append((b_sb[:], bias))
        total = 16 * len(loads)
        flat = [P, NT, E]
        with nc.Block() as block:
            @block.sync
            def _(sp):
                load_weights(sp, loads, s["w_in"])
                sp.wait_ge(s["w_in"], total)

            @block.gpsimd
            def _(pool):
                for e in range(E):
                    last = pool.memset(rank[:, e:e + 1], float(E - e))
                pool.tensor_tensor(strict[:], c.lower[:], c.ident[:], ALU.subtract)
                pool.drain()
                pool.sem_inc(s["rank_ready"], 1)

            @block.tensor
            def _(pe):
                pe.wait_ge(s["w_in"], total)
                for n in range(4):
                    for k in range(KC):
                        last = pe.matmul(lps[0:E, n, :], w_sb[:, k, :], srcT[:, k, n * 512:(n + 1) * 512],
                                         start=(k == 0), stop=(k == KC - 1))
                last.then_inc(s["mult"], 1)
                pe.wait_ge(s["lT_ready"], 1)
                for t in range(NT):
                    last = pe.transpose(tps[:, t * E:(t + 1) * E], lT[:, t * P:(t + 1) * P], c.ident[0:E, 0:E])
                last.then_inc(s["turned"], 1)
                if top == 2:
                    pe.wait_ge(s["chosen"], 1)
                    pe.wait_ge(s["rank_ready"], 1)
                    mask = cum[:].rearrange("p t e -> p (t e)")
                    pe.matmul(cps[:, 0, 0:NT * E], strict[:], mask, start=True, stop=True)
                    pe.matmul(cps[:, 1, 0:NT * E], c.ones[:], mask, start=True, stop=True).then_inc(s["counted"], 1)

            @block.scalar
            def _(act):
                act.wait_ge(s["shifted"], 1)
                act.activation(p_[:], p_[:], ACT.Exp).then_inc(s["exp"], 1)

            @block.vector
            def _(dve):
                dve.wait_ge(s["w_in"], total)
                dve.wait_ge(s["mult"], 1)
                lv = lT[:].rearrange("e (n q) -> e n q", n=4)
                if bias is not None:
                    dve.tensor_scalar(lv, lps[0:E, :, :], b_sb[:, 0:1], None, ALU.add).then_inc(s["lT_ready"], 1)
                else:
                    dve.tensor_copy(lv, lps[0:E, :, :]).then_inc(s["lT_ready"], 1)
                dve.wait_ge(s["turned"], 1)
                dve.tensor_copy(L[:].rearrange("p t e -> p (t e)"), tps[:, 0:NT * E])
                dve.drain()
                dve.wait_ge(s["rank_ready"], 1)
                rb = rank[:].rearrange("p (a e) -> p a e", a=1).broadcast_to(flat)

                def choose(i):
                    dve.tensor_reduce(m[:, i, :, 0], L[:], AX.X, ALU.max)
                    dve.drain()
                    if i == 0:
                        dve.tensor_tensor(p_[:], L[:], m[:, 0].broadcast_to(flat), ALU.subtract)
                        dve.drain()
                        dve.sem_inc(s["shifted"], 1)
                    dve.tensor_tensor(sel[:, i], L[:], m[:, i].broadcast_to(flat), ALU.is_equal)
                    dve.drain()
                    dve.tensor_tensor(sel[:, i], sel[:, i], rb, ALU.mult)
                    dve.drain()
                    dve.tensor_reduce(rk[:, :, 0], sel[:, i], AX.X, ALU.max)
                    dve.drain()
                    dve.tensor_tensor(sel[:, i], sel[:, i], rk[:].broadcast_to(flat), ALU.is_equal)
                    dve.drain()

                choose(0)
                if top == 1:
                    dve.wait_ge(s["exp"], 1)
                    dve.tensor_reduce(tot[:, 0, :, 0], p_[:], AX.X, ALU.add)
                    dve.drain()
                    dve.reciprocal(tot[:, 0], tot[:, 0])
                    dve.drain()
                    dve.tensor_tensor(wgt[:, :, 0:E], sel[:, 0], tot[:, 0].broadcast_to(flat), ALU.mult)
                    return
                dve.scalar_tensor_tensor(out=L[:], in0=sel[:, 0], scalar=-3e38, in1=L[:], op0=ALU.mult, op1=ALU.add)
                dve.drain()
                choose(1)
                dve.wait_ge(s["exp"], 1)
                dve.tensor_tensor(cum[:], sel[:, 0], sel[:, 1], ALU.add)
                dve.drain()
                dve.sem_inc(s["chosen"], 1)
                dve.tensor_tensor(tmp[:], p_[:], cum[:], ALU.mult)
                dve.drain()
                dve.tensor_reduce(tot[:, 0, :, 0], tmp[:], AX.X, ALU.add)
                dve.drain()
                dve.reciprocal(tot[:, 0], tot[:, 0])
                dve.drain()
                dve.tensor_tensor(tmp[:], tmp[:], tot[:, 0].broadcast_to(flat), ALU.mult)
                dve.wait_ge(s["counted"], 1)
                dve.memset(before[:, 0, :], 0.0)
                dve.drain()
                for t in range(1, NT):
                    dve.tensor_tensor(before[:, t, :], before[:, t - 1, :], cps[:, 1, (t - 1) * E:t * E], ALU.add)
                    dve.drain()
                dve.tensor_tensor(before[:].rearrange("p t e -> p (t e)"), before[:].rearrange("p t e -> p (t e)"),
                                  cps[:, 0, 0:NT * E], ALU.add)
                dve.drain()
                dve.tensor_scalar(slot[:, :, 0:E], before[:], -NO_SLOT, None, ALU.add)
                dve.tensor_scalar(before[:], before[:], float(CAPACITY), None, ALU.is_lt)
                dve.memset(slot[:, :, E:E + 2], NO_SLOT)
                dve.drain()
                dve.tensor_tensor(wgt[:, :, 0:E], tmp[:], before[:], ALU.mult)
                dve.tensor_tensor(before[:], before[:], cum[:], ALU.mult)
                dve.drain()
                dve.tensor_tensor(slot[:, :, 0:E], slot[:, :, 0:E], before[:], ALU.mult)
                dve.drain()
                dve.tensor_scalar(slot[:, :, 0:E], slot[:, :, 0:E], NO_SLOT, None, ALU.add)


def experts(c, name, srcT, wgt, n_experts, inner, w1, w2, gate=None, b1=None, square=False):
    nc = c.nc
    MI = inner // P
    NB = N // 512
    G = 1 if gate is None else 2
    with Stage(nc, name) as st:
        w1_sb = st.sb("w1", [P, 2, G, KC, inner])
        w2_sb = st.sb("w2", [P, 2, MI, D])
        b_sb = st.sb("b", [P, 2, MI])
        hT = st.sb("hT", [P, 2, MI, 512])
        gated = st.sb("gated", [P, 2, 512])
        ps = st.ps("ps", [P, 8, 512])
        names = ("w_in0", "w_in1", "w_free0", "w_free1", "up", "sil", "h", "down", "added")
        s = {n: st.sem(n, primed=n in ("h", "added", "down",)) for n in names}
        UI = 2 * NB
        loads = G + 1 + (b1 is not None)
        with nc.Block() as block:
            @block.sync
            def _(sp):
                for e in range(n_experts):
                    j = e % 2
                    sp.wait_ge(s[f"w_free{j}"], e // 2)
                    for g, ww in enumerate([w1] if gate is None else [gate, w1]):
                        sp.dma_start(w1_sb[:, j, g], ww[e].rearrange("(k p) m -> p k m", p=P)).then_inc(s[f"w_in{j}"], 16)
                    sp.dma_start(w2_sb[:, j], w2[e].rearrange("(k p) m -> p k m", p=P)).then_inc(s[f"w_in{j}"], 16)
                    if b1 is not None:
                        sp.dma_start(b_sb[:, j], b1[e]).then_inc(s[f"w_in{j}"], 16)
                for j in range(2):
                    sp.wait_ge(s[f"w_in{j}"], n_experts // 2 * 16 * loads)

            @block.tensor
            def _(pe):
                with pe.Fori(0, n_experts // 2) as i:
                    def up(u):
                        j, n = u // NB, u % NB
                        if n == 0:
                            pe.wait_ge(s[f"w_in{j}"], (i + 1) * (16 * loads))
                        for m in range(MI):
                            q = u * MI + m
                            pe.wait_ge(s["h"], i * (UI * MI) + q if q >= 2 else i * (UI * MI) + 1)
                            for g in range(G):
                                for k in range(KC):
                                    last = pe.matmul(ps[:, 2 * (m % 2) + g, :], w1_sb[:, j, g, k, m * P:(m + 1) * P],
                                                     srcT[:, k, n * 512:(n + 1) * 512], start=(k == 0), stop=(k == KC - 1))
                            last.then_inc(s["up"], 1)

                    def down(u):
                        j = u // NB
                        pe.wait_ge(s["h"], i * (UI * MI) + ((u + 1) * MI + 1))
                        for t in range(4):
                            q = u * 4 + t
                            pe.wait_ge(s["added"], i * (UI * 4) + (q - 2) if q >= 4 else i * (UI * 4) + 1)
                            for m in range(MI):
                                last = pe.matmul(ps[:, 4 + t, 0:D], hT[:, u % 2, m, t * P:(t + 1) * P], w2_sb[:, j, m, :],
                                                 start=(m == 0), stop=(m == MI - 1))
                            last.then_inc(s["down"], 1)

                    for u in range(UI + 1):
                        if u < UI:
                            up(u)
                        if u >= 1:
                            down(u - 1)

            @block.scalar
            def _(act):
                with act.Fori(0, n_experts // 2) as i:
                    for u in range(UI):
                        j = u // NB
                        for m in range(MI):
                            q = u * MI + m
                            act.wait_ge(s["up"], i * (UI * MI) + (q + 1))
                            if m == 0:
                                act.wait_ge(s["down"], i * (UI * 4) + ((u - 1) * 4 + 1) if u >= 2 else i * (UI * 4) + 1)
                            if square:
                                act.wait_ge(s["h"], i * (UI * MI) + q if q >= 2 else i * (UI * MI) + 1)
                                act.activation(gated[:, m % 2, :], ps[:, 2 * (m % 2), :], ACT.Relu).then_inc(s["sil"], 1)
                            elif gate is None:
                                act.activation(hT[:, u % 2, m, :], ps[:, 2 * (m % 2), :], ACT.Relu,
                                               bias=b_sb[:, j, m:m + 1]).then_inc(s["h"], 1)
                            else:
                                act.wait_ge(s["h"], i * (UI * MI) + q if q >= 2 else i * (UI * MI) + 1)
                                act.activation(gated[:, m % 2, :], ps[:, 2 * (m % 2), :], ACT.Silu).then_inc(s["sil"], 1)

            @block.vector
            def _(dve):
                with dve.Fori(0, n_experts // 2) as i:
                    def add_out(u):
                        j, n = u // NB, u % NB
                        if n == 0:
                            dve.drain()
                        for t in range(4):
                            dve.wait_ge(s["down"], i * (UI * 4) + (u * 4 + t + 2))
                            x_t = c.x[:, 4 * n + t, :]
                            dve.scalar_tensor_tensor(out=x_t, in0=ps[:, 4 + t, 0:D], scalar=wgt[:, 4 * n + t, bass.ds(i * 2 + j, 1)],
                                                     in1=x_t, op0=ALU.mult, op1=ALU.add).then_inc(s["added"], 1)
                        if n == NB - 1:
                            dve.sem_inc(s[f"w_free{j}"], 1)

                    for u in range(UI + 1):
                        if u < UI and (gate is not None or square):
                            for m in range(MI):
                                q = u * MI + m
                                dve.wait_ge(s["sil"], i * (UI * MI) + (q + 1))
                                if m == 0:
                                    dve.wait_ge(s["down"], i * (UI * 4) + ((u - 1) * 4 + 1) if u >= 2 else i * (UI * 4) + 1)
                                other = gated[:, m % 2, :] if square else ps[:, 2 * (m % 2) + 1, :]
                                dve.tensor_tensor(hT[:, u % 2, m, :], gated[:, m % 2, :], other, ALU.mult).then_inc(s["h"], 1)
                        if u >= 1:
                            add_out(u - 1)


def routed_experts(c, name, feat, wgt, slot, inner, w_gate, w_up, w_down, row_slots, part_slots, head_rows):
    nc = c.nc
    C = CAPACITY
    MI = inner // P
    SC = -(-C // P)
    CW = [min(P, C - P * k) for k in range(SC)]
    BT = 512 // P
    NB = NT // BT
    PAIRS = NT // 2
    with Stage(nc, name) as st:
        parts = st.sb("parts", [P, 3, NT, D], BF16)
        sel = st.sb("sel", [P, 2, NT, C], BF16)
        xg = st.sb("xg", [P, KC, C])
        hT = st.sb("hT", [P, MI, C])
        gated = st.sb("gated", [P, 2, C])
        w1 = st.sb("w1", [P, 2, 2, KC, inner])
        w2 = st.sb("w2", [P, 2, MI, D])
        ep = st.sb("ep", [P, 3, SC, D], BF16)
        er = st.sb("er", [P, SC, D])
        selT = st.sb("selT", [P, 2, SC, 512], BF16)
        slotT = st.sb("slotT", [E, N])
        rsel = st.sb("rsel", [E, 1, P])
        heads = st.sb("heads", [E, E, P])
        row = st.sb("row", [P, C])
        col = st.sb("col", [P, SC])
        ps = st.ps("ps", [P, 8, 512])
        names = ("w_in0", "w_in1", "c_in", "parts0", "parts1", "slots", "slotT", "sel", "gath", "xg", "rsel", "up", "sil", "h",
                 "down", "bc", "selT", "ep", "sc", "added")
        s = {n: st.sem(n, primed=n in ("h", "added")) for n in names}
        with nc.Block() as block:
            @block.sync
            def _(sp):
                load_weights(sp, [(row[:], row_bcast(row_slots, C)), (col[:], part_slots), (heads[:], head_rows)], s["c_in"])
                for e in range(E):
                    j = e % 2
                    if e >= 2:
                        sp.wait_ge(s["down"], e - 1)
                    load_weights(sp, [(w1[:, j, 0], w_gate[e].rearrange("(k p) m -> p k m", p=P)),
                                      (w1[:, j, 1], w_up[e].rearrange("(k p) m -> p k m", p=P)),
                                      (w2[:, j], w_down[e].rearrange("(k p) m -> p k m", p=P))], s[f"w_in{j}"])
                sp.wait_ge(s["c_in"], 48)
                for j in range(2):
                    sp.wait_ge(s[f"w_in{j}"], E // 2 * 48)

            @block.gpsimd
            def _(pool):
                f = feat[:, NT // 2:NT, :]
                pool.tensor_copy(parts[:, 0, NT // 2:NT, :], f)
                pool.drain()
                pool.tensor_tensor(f, f, parts[:, 0, NT // 2:NT, :], ALU.subtract)
                pool.drain()
                pool.tensor_copy(parts[:, 1, NT // 2:NT, :], f)
                pool.drain()
                pool.tensor_tensor(parts[:, 2, NT // 2:NT, :], f, parts[:, 1, NT // 2:NT, :], ALU.subtract).then_inc(s["parts1"], 1)

            @block.tensor
            def _(pe):
                for t in range(NT):
                    last = pe.transpose(ps[0:E, 2 + t // BT, (t % BT) * P:(t % BT + 1) * P], slot[:, t, 0:E], c.ident[:])
                last.then_inc(s["slots"], 1)
                pe.wait_ge(s["c_in"], 48)
                pe.wait_ge(s["slotT"], 1)
                pe.wait_ge(s["parts0"], 1)
                with pe.Fori(0, E // 2) as i:
                    def gather(j):
                        for t in range(NT):
                            if j == 0 and t == NT // 2:
                                pe.wait_ge(s["parts1"], 1)
                            pe.wait_ge(s["sel"], i * (2 * NT) + (j * NT + t + 1))
                            for k in range(KC):
                                for a in range(3):
                                    last = pe.matmul(ps[:, k, 0:C], parts[:, a, t, k * P:(k + 1) * P], sel[:, j, t, :],
                                                     start=(t == 0 and a == 0), stop=(t == NT - 1 and a == 2))
                        last.then_inc(s["gath"], 1)

                    def spread(n):
                        pe.matmul(ps[:, 2 + n % 2, :], rsel[:, 0, :], slotT[:, n * 512:(n + 1) * 512],
                                  start=True, stop=True).then_inc(s["bc"], 1)

                    def feed_forward(j):
                        pe.wait_ge(s[f"w_in{j}"], (i + 1) * 48)
                        pe.wait_ge(s["xg"], i * 2 + (j + 1))
                        for m in range(MI):
                            pe.wait_ge(s["h"], i * (2 * MI) + max(j * MI + m, 1))
                            if m == 1:
                                pe.wait_ge(s["added"], i * (2 * PAIRS) + (j * PAIRS + 1))
                            for g in range(2):
                                for k in range(KC):
                                    last = pe.matmul(ps[:, 2 + 2 * (m % 2) + g, 0:C], w1[:, j, g, k, m * P:(m + 1) * P], xg[:, k, :],
                                                     start=(k == 0), stop=(k == KC - 1))
                            last.then_inc(s["up"], 1)
                        pe.wait_ge(s["rsel"], i * 2 + (j + 1))
                        pe.wait_ge(s["h"], i * (2 * MI) + (j * MI + MI))
                        spread(0)
                        spread(1)
                        pe.wait_ge(s["h"], i * (2 * MI) + (j * MI + MI + 1))
                        for k in range(SC):
                            for m in range(MI):
                                last = pe.matmul(ps[0:CW[k], 6 + k // 2, (k % 2) * D:(k % 2 + 1) * D], hT[:, m, k * P:k * P + CW[k]],
                                                 w2[:, j, m, :], start=(m == 0), stop=(m == MI - 1))
                        last.then_inc(s["down"], 1)

                    def scatter(j):
                        pe.wait_ge(s["ep"], i * 2 + (j + 1))
                        for pr in range(PAIRS):
                            n = pr // 2
                            if pr % 2 == 0:
                                pe.wait_ge(s["selT"], i * (2 * NB) + (j * NB + n + 1))
                            if pr >= 2:
                                pe.wait_ge(s["added"], i * (2 * PAIRS) + (j * PAIRS + pr))
                            for q in range(2):
                                t = 2 * (pr % 2) + q
                                for k in range(SC):
                                    for a in range(3):
                                        last = pe.matmul(ps[:, 4 + pr % 2, q * D:(q + 1) * D], selT[0:CW[k], n % 2, k, t * P:(t + 1) * P],
                                                         ep[0:CW[k], a, k, :], start=(k == 0 and a == 0), stop=(k == SC - 1 and a == 2))
                            last.then_inc(s["sc"], 1)
                            if pr % 2 == 1 and n + 2 < NB:
                                spread(n + 2)

                    gather(0)
                    feed_forward(0)
                    gather(1)
                    scatter(0)
                    feed_forward(1)
                    scatter(1)

            @block.scalar
            def _(act):
                with act.Fori(0, E // 2) as i:
                    for j in range(2):
                        act.wait_ge(s["gath"], i * 2 + (j + 1))
                        act.activation(xg[:], ps[:, 0:KC, 0:C], ACT.Copy).then_inc(s["xg"], 1)
                        for m in range(MI):
                            act.wait_ge(s["up"], i * (2 * MI) + (j * MI + m + 1))
                            act.wait_ge(s["h"], i * (2 * MI) + max(j * MI + m, 1))
                            act.activation(gated[:, m % 2, :], ps[:, 2 + 2 * (m % 2), 0:C], ACT.Silu).then_inc(s["sil"], 1)

            @block.vector
            def _(dve):
                f = feat[:, 0:NT // 2, :]
                dve.tensor_copy(parts[:, 0, 0:NT // 2, :], f)
                dve.drain()
                dve.tensor_tensor(f, f, parts[:, 0, 0:NT // 2, :], ALU.subtract)
                dve.wait_ge(s["slots"], 1)
                dve.tensor_copy(slotT[:].rearrange("e (n q) -> e n q", n=NB), ps[0:E, 2:2 + NB, :]).then_inc(s["slotT"], 1)
                dve.drain()
                dve.tensor_copy(parts[:, 1, 0:NT // 2, :], f)
                dve.drain()
                dve.tensor_tensor(parts[:, 2, 0:NT // 2, :], f, parts[:, 1, 0:NT // 2, :], ALU.subtract).then_inc(s["parts0"], 1)
                dve.wait_ge(s["c_in"], 48)

                def choose(t, j, e):
                    dve.tensor_scalar(sel[:, j, t, :], row[:], slot[:, t, e], None, ALU.is_equal).then_inc(s["sel"], 1)

                for t in range(NT):
                    choose(t, 0, slice(0, 1))
                with dve.Fori(0, E // 2) as i:
                    for j in range(2):
                        dve.tensor_copy(rsel[:], heads[:, bass.ds(i * 2 + j, 1), :]).then_inc(s["rsel"], 1)
                        dve.wait_ge(s["gath"], i * 2 + (j + 1))
                        for m in range(MI):
                            for t in range(m * NT // MI, (m + 1) * NT // MI):
                                choose(t, 1 - j, bass.ds(i * 2 + (j + 1), 1))
                            dve.wait_ge(s["sil"], i * (2 * MI) + (j * MI + m + 1))
                            dve.tensor_tensor(hT[:, m, :], gated[:, m % 2, :], ps[:, 3 + 2 * (m % 2), 0:C], ALU.mult).then_inc(s["h"], 1)

                        def compare(n):
                            dve.wait_ge(s["bc"], i * (2 * NB) + (j * NB + n + 1))
                            if n >= 2:
                                dve.wait_ge(s["sc"], i * (2 * PAIRS) + (j * PAIRS + 2 * (n - 1)))
                            for k in range(SC):
                                last = dve.tensor_scalar(selT[:, n % 2, k, :], ps[:, 2 + n % 2, :], col[:, k:k + 1], None, ALU.is_equal)
                            last.then_inc(s["selT"], 1)

                        compare(0)
                        compare(1)
                        dve.wait_ge(s["down"], i * 2 + (j + 1))
                        full, rest = SC // 2 * 2, SC % 2
                        out = [(er[:, 0:full, :], [ep[:, a, 0:full, :] for a in range(3)],
                                ps[:, 6, :].rearrange("p (k d) -> p k d", d=D))]
                        if rest:
                            out.append((er[0:CW[-1], full:SC, :], [ep[0:CW[-1], a, full:SC, :] for a in range(3)],
                                        ps[0:CW[-1], 7:8, 0:D]))
                        for r_, e_, o_ in out:
                            dve.tensor_copy(e_[0], o_)
                        dve.drain()
                        for r_, e_, o_ in out:
                            dve.tensor_tensor(r_, o_, e_[0], ALU.subtract)
                        dve.drain()
                        for r_, e_, o_ in out:
                            dve.tensor_copy(e_[1], r_)
                        dve.drain()
                        for r_, e_, o_ in out:
                            last = dve.tensor_tensor(e_[2], r_, e_[1], ALU.subtract)
                        last.then_inc(s["ep"], 1)
                        for pr in range(PAIRS):
                            dve.wait_ge(s["sc"], i * (2 * PAIRS) + (j * PAIRS + pr + 1))
                            for q in range(2):
                                x_t = c.x[:, 2 * pr + q, :]
                                last = dve.scalar_tensor_tensor(out=x_t, in0=ps[:, 4 + pr % 2, q * D:(q + 1) * D],
                                                                scalar=wgt[:, 2 * pr + q, bass.ds(i * 2 + j, 1)], in1=x_t,
                                                                op0=ALU.mult, op1=ALU.add)
                            last.then_inc(s["added"], 1)
                            if pr % 2 == 1 and pr // 2 + 2 < NB:
                                compare(pr // 2 + 2)


def add_expert_bias(c, name, wgt, b2):
    nc = c.nc
    with Stage(nc, name) as st:
        wT = st.sb("wT", [E, N])
        b_sb = st.sb("b", [E, D])
        tps = st.ps("tps", [P, 4, 512])
        ps = st.ps("ps", [P, 4, 512])
        w_in, turned, copied, mult, added = (st.sem(n) for n in ("w_in", "turned", "copied", "mult", "added"))
        with nc.Block() as block:
            @block.sync
            def _(sp):
                sp.dma_start(b_sb[:], b2).then_inc(w_in, 16)
                sp.wait_ge(w_in, 16)

            @block.tensor
            def _(pe):
                for t in range(NT):
                    last = pe.transpose(tps[0:E, t // 4, (t % 4) * P:(t % 4 + 1) * P], wgt[:, t, 0:E], c.ident[:])
                last.then_inc(turned, 1)
                pe.wait_ge(w_in, 16)
                pe.wait_ge(copied, 1)
                for t in range(NT):
                    if t >= 4:
                        pe.wait_ge(added, t - 3)
                    pe.matmul(ps[:, t % 4, 0:D], wT[:, t * P:(t + 1) * P], b_sb[:], start=True, stop=True).then_inc(mult, 1)

            @block.scalar
            def _(act):
                act.wait_ge(turned, 1)
                act.activation(wT[:].rearrange("e (n q) -> e n q", n=4), tps[0:E, :, :], ACT.Copy).then_inc(copied, 1)

            @block.vector
            def _(dve):
                for t in range(NT):
                    dve.wait_ge(mult, t + 1)
                    dve.tensor_tensor(c.x[:, t, :], c.x[:, t, :], ps[:, t % 4, 0:D], ALU.add).then_inc(added, 1)


def softplus_attention(c, name, qT, kT, v, out):
    nc = c.nc
    units = [(b, qb, j) for b in range(B) for qb in range(S // 512) for j in range(4 * (qb + 1))]
    R = 3
    with Stage(nc, name) as st:
        la = st.sb("la", [P, R, 512])
        wt = st.sb("wt", [P, R, 512])
        ps = st.ps("ps", [P, R, 512])
        po = st.ps("po", [P, 2, 2, 512])
        s = {n: st.sem(n) for n in ("score", "abs", "log", "w", "pv", "read")}
        blocks = {}
        for u, (b, qb, j) in enumerate(units):
            blocks.setdefault((b, qb), []).append(u)
        order = list(blocks)
        with nc.Block() as block:
            @block.tensor
            def _(pe):
                def scores(u):
                    b, qb, j = units[u]
                    if u >= R:
                        pe.wait_ge(s["w"], u - R + 1)
                    for k in range(KC):
                        last = pe.matmul(ps[:, u % R, :], qT[:, k, b * S + j * P:b * S + (j + 1) * P],
                                         kT[:, k, b * S + qb * 512:b * S + (qb + 1) * 512], start=(k == 0), stop=(k == KC - 1))
                    last.then_inc(s["score"], 1)

                def weigh(u):
                    b, qb, j = units[u]
                    o = order.index((b, qb))
                    if j == 0 and o >= 2:
                        pe.wait_ge(s["read"], o - 1)
                    pe.wait_ge(s["w"], u + 1)
                    for t in range(max(0, j - 4 * qb), 4):
                        last = pe.matmul(po[:, o % 2, t // 2, (t % 2) * D:(t % 2 + 1) * D], wt[:, u % R, t * P:(t + 1) * P],
                                         v[:, b * ST + j, :], start=(j == 0 and t % 2 == 0), stop=(j == 4 * qb + t),
                                         skip_group_check=True)
                    last.then_inc(s["pv"], 1)

                for u in range(len(units) + 2):
                    if u < len(units):
                        scores(u)
                    if u >= 2:
                        weigh(u - 2)

            @block.scalar
            def _(act):
                for u in range(len(units)):
                    act.wait_ge(s["score"], u + 1)
                    if u >= R:
                        act.wait_ge(s["w"], u - R + 1)
                    a = la[:, u % R, :]
                    act.activation(a, ps[:, u % R, :], ACT.Abs, scale=D ** -0.5).then_inc(s["abs"], 1)
                    act.drain()
                    act.activation(a, a, ACT.Exp, scale=-1.0)
                    act.drain()
                    act.activation(a, a, ACT.Ln, bias=1.0).then_inc(s["log"], 1)

            @block.vector
            def _(dve):
                def copy_out(o):
                    b, qb = order[o]
                    dve.wait_ge(s["pv"], blocks[(b, qb)][-1] + 1)
                    dve.tensor_copy(out[:, b * ST + 4 * qb:b * ST + 4 * qb + 4, :].rearrange("p (g t) d -> p g (t d)", g=2),
                                    po[:, o % 2, :, :]).then_inc(s["read"], 1)

                for u, (b, qb, j) in enumerate(units):
                    dve.wait_ge(s["abs"], u + 1)
                    if u >= R:
                        dve.wait_ge(s["pv"], u - R + 1)
                    wu = wt[:, u % R, :]
                    dve.tensor_scalar(wu, ps[:, u % R, :], D ** -0.5, 0.0, ALU.mult, ALU.max)
                    dve.drain()
                    dve.wait_ge(s["log"], u + 1)
                    last = dve.tensor_tensor(wu, wu, la[:, u % R, :], ALU.add)
                    jj = j - 4 * qb
                    if jj >= 0:
                        dve.drain()
                        dg = wt[:, u % R, jj * P:(jj + 1) * P]
                        last = dve.tensor_tensor(dg, dg, c.lower[:], ALU.mult)
                    last.then_inc(s["w"], 1)
                    o = order.index((b, qb))
                    if j == 1 and o >= 1:
                        copy_out(o - 1)
                copy_out(len(order) - 1)


def softmax_attention(c, name, qT, kT, v, out, resid, causal):
    nc = c.nc
    with Stage(nc, name) as st:
        upper = st.sb("upper", [P, P])
        nm = st.sb("nm", [P, 2, 2])
        total = st.sb("total", [P, 3, 2])
        p_ = st.sb("p", [P, 2, S])
        pT = st.sb("pT", [P, 2, S])
        ps = st.ps("ps", [P, 2, 2, 512])
        pTp = st.ps("pTp", [P, 2, 512])
        po = st.ps("po", [P, 2, 512])
        s = {n: st.sem(n) for n in ("mask", "score", "nmax", "exp", "turned", "copied", "pv", "out")}

        def keys(t):
            b, q = t // ST, t % ST
            return (b * S, (q + 1) * P) if causal else (b * S2, S2)

        with nc.Block() as block:
            @block.gpsimd
            def _(pool):
                pool.memset(upper[:], 0.0)
                pool.drain()
                pool.affine_select(out=upper[:], in_=upper[:], compare_op=ALU.is_ge, fill=-1e30, base=0,
                                   pattern=[[-1, P]], channel_multiplier=1).then_inc(s["mask"], 1)

            @block.tensor
            def _(pe):
                def scores(t):
                    k0, nk = keys(t)
                    if t >= 2:
                        pe.wait_ge(s["exp"], t - 1)
                    for a in range(0, nk, 512):
                        w = min(512, nk - a)
                        for k in range(KC):
                            last = pe.matmul(ps[:, t % 2, a // 512, 0:w], qT[:, k, t * P:(t + 1) * P],
                                             kT[:, k, k0 + a:k0 + a + w], start=(k == 0), stop=(k == KC - 1))
                    last.then_inc(s["score"], 1)

                def turn(t):
                    k0, nk = keys(t)
                    pe.wait_ge(s["exp"], t + 1)
                    if t >= 1:
                        pe.wait_ge(s["copied"], t)
                    nj = (nk + P - 1) // P
                    for j in range(nj):
                        w = min(P, nk - j * P)
                        last = pe.transpose(pTp[0:w, j // 4, (j % 4) * P:(j % 4 + 1) * P], p_[:, t % 2, j * P:j * P + w], c.ident[:])
                    last.then_inc(s["turned"], 1)

                def weigh(t):
                    k0, nk = keys(t)
                    nj = (nk + P - 1) // P
                    pe.wait_ge(s["copied"], t + 1)
                    if t >= 2:
                        pe.wait_ge(s["out"], t - 1)
                    for j in range(nj):
                        w = min(P, nk - j * P)
                        vt = v[0:w, t // ST * ST + j, :] if causal else v[0:w, t // ST, :]
                        last = pe.matmul(po[:, t % 2, 0:D], pT[0:w, t % 2, j * P:(j + 1) * P], vt, start=(j == 0), stop=(j == nj - 1))
                    last.then_inc(s["pv"], 1)

                for t in range(NT + 2):
                    if t < NT:
                        scores(t)
                    if 1 <= t <= NT:
                        turn(t - 1)
                    if t >= 2:
                        weigh(t - 2)

            @block.scalar
            def _(act):
                def exponent(t):
                    k0, nk = keys(t)
                    act.wait_ge(s["nmax"], t + 1)
                    if t >= 2:
                        act.wait_ge(s["turned"], t - 1)
                    act.activation(p_[:, t % 2, 0:nk], ps[:, t % 2].rearrange("p g n -> p (g n)")[:, 0:nk], ACT.Exp, scale=D ** -0.5,
                                   bias=nm[:, t % 2, 1:2], accum_out=total[:, t % 3, 0:1]).then_inc(s["exp"], 1)

                def copy(t):
                    k0, nk = keys(t)
                    act.wait_ge(s["turned"], t + 1)
                    if t >= 2:
                        act.wait_ge(s["pv"], t - 1)
                    rows = min(nk, P)
                    cols = (nk + P - 1) // P * P
                    act.activation(pT[0:rows, t % 2, 0:cols], pTp[:].rearrange("p g n -> p (g n)")[0:rows, 0:cols],
                                   ACT.Copy).then_inc(s["copied"], 1)

                for t in range(NT + 1):
                    if t < NT:
                        exponent(t)
                    if t >= 1:
                        copy(t - 1)

            @block.vector
            def _(dve):
                dve.wait_ge(s["mask"], 1)

                def top(t):
                    k0, nk = keys(t)
                    dve.wait_ge(s["score"], t + 1)
                    flat = ps[:, t % 2].rearrange("p g n -> p (g n)")
                    if causal:
                        dg = flat[:, nk - P:nk]
                        dve.tensor_tensor(dg, dg, upper[:], ALU.add)
                        dve.drain()
                    dve.tensor_reduce(nm[:, t % 2, 0:1], flat[:, 0:nk], AX.X, ALU.max, negate=True)
                    dve.drain()
                    dve.tensor_scalar(nm[:, t % 2, 1:2], nm[:, t % 2, 0:1], D ** -0.5, None, ALU.mult).then_inc(s["nmax"], 1)

                def finish(t):
                    dve.wait_ge(s["exp"], t + 1)
                    dve.reciprocal(total[:, t % 3, 1:2], total[:, t % 3, 0:1])
                    dve.drain()
                    dve.wait_ge(s["pv"], t + 1)
                    dve.scalar_tensor_tensor(out=out[:, t, :], in0=po[:, t % 2, 0:D], scalar=total[:, t % 3, 1:2],
                                             in1=resid[:, t, :], op0=ALU.mult, op1=ALU.add).then_inc(s["out"], 1)

                for t in range(NT + 2):
                    if t < NT:
                        top(t)
                    if t >= 2:
                        finish(t - 2)


def load(c, name, pairs):
    with Stage(c.nc, name) as st:
        came = st.sem("in")
        with c.nc.Block() as block:
            @block.sync
            def _(sp):
                sp.wait_ge(came, load_weights(sp, pairs, came))


def add_to_x(c, name, src, relu=False):
    with Stage(c.nc, name) as st:
        with c.nc.Block() as block:
            @block.vector
            def _(dve):
                if relu:
                    dve.scalar_tensor_tensor(out=c.x[:], in0=src[:], scalar=0.0, in1=c.x[:], op0=ALU.max, op1=ALU.add)
                else:
                    dve.tensor_tensor(c.x[:], src[:], c.x[:], ALU.add)


MAGIC = 12582912.0


def quantize_weights(c, name, w, dst, size):
    nc = c.nc
    K, M = w.shape
    k_ = K // P
    with Stage(nc, name) as st:
        w_sb = st.sb("w", [P, k_, M])
        part = st.sb("part", [P, 2])
        ps = st.ps("ps", [P, 8])
        w_in, summed, total = st.sem("w_in"), st.sem("summed"), st.sem("total")
        with nc.Block() as block:
            @block.sync
            def _(sp):
                sp.dma_start(w_sb[:], w.rearrange("(k p) m -> p k m", p=P)).then_inc(w_in, 16)
                sp.wait_ge(w_in, 16)

            @block.tensor
            def _(pe):
                pe.wait_ge(summed, 1)
                pe.matmul(ps[:, 0:1], c.ones[:], part[:, 0:1], start=True, stop=True).then_inc(total, 1)

            @block.vector
            def _(dve):
                dve.wait_ge(w_in, 16)
                dve.tensor_reduce(part[:, 0:1], w_sb[:], AX.XY, ALU.add, apply_absolute_value=True).then_inc(summed, 1)
                dve.wait_ge(total, 1)
                dve.tensor_scalar(size[:], ps[:, 0:1], 1.0 / (K * M), 1e-5, ALU.mult, ALU.max)
                dve.drain()
                dve.reciprocal(part[:, 1:2], size[:])
                dve.drain()
                dve.tensor_scalar(w_sb[:], w_sb[:], part[:, 1:2], -1.0, ALU.mult, ALU.max)
                dve.drain()
                dve.tensor_scalar(w_sb[:], w_sb[:], 1.0, MAGIC, ALU.min, ALU.add)
                dve.drain()
                dve.tensor_scalar(dst[:], w_sb[:], MAGIC, None, ALU.subtract)


def quantized_ffn(c, name, r, w1q, s1, w2q, s2, b1, b2):
    nc = c.nc
    F = w1q.shape[2]
    FC = F // P
    with Stage(nc, name) as st:
        b1_sb = st.sb("b1", [P, F])
        b2_sb = st.sb("b2", [P, D])
        idb = st.sb("idb", [P, P], BF16)
        am = st.sb("am", [P, 6, NT])
        am2 = st.sb("am2", [P, 8, NT])
        t_f = st.sb("t_f", [P, 2, F])
        q = st.sb("q", [P, 2, F], BF16)
        qT = st.sb("qT", [P, 2, F], BF16)
        g = st.sb("g", [P, NT, F])
        h = st.sb("h", [P, 2, F])
        sq = st.sb("sq", [P, F])
        tp = st.ps("tp", [P, 2, 1024], BF16)
        ps = st.ps("ps", [P, 2, 2, 512])
        names = ("w_in", "q", "turned", "qT", "mult", "h", "gelu", "var", "sd", "q2", "turned2", "qT2", "mult2", "added")
        s = {n: st.sem(n) for n in names}

        def quantize(dve, dst, src, tmp, scale):
            dve.tensor_scalar(tmp, src, scale, -128.0, ALU.mult, ALU.max)
            dve.drain()
            dve.tensor_scalar(tmp, tmp, 127.0, MAGIC, ALU.min, ALU.add)
            dve.drain()
            return dve.tensor_scalar(dst, tmp, MAGIC, None, ALU.subtract)

        with nc.Block() as block:
            @block.sync
            def _(sp):
                load_weights(sp, [(b1_sb[:], row_bcast(b1, F)), (b2_sb[:], row_bcast(b2, D))], s["w_in"])
                sp.wait_ge(s["w_in"], 32)

            @block.vector
            def _(dve):
                dve.tensor_copy(idb[:], c.ident[:])
                dve.tensor_reduce(am[:, 0, :], r[:], AX.X, ALU.max, apply_absolute_value=True)
                dve.drain()
                dve.tensor_scalar(am[:, 0, :], am[:, 0, :], 1e-5, 1.0 / 127.0, ALU.max, ALU.mult)
                dve.drain()
                dve.reciprocal(am[:, 1, :], am[:, 0, :])
                dve.tensor_scalar(am[:, 2, :], am[:, 0, :], s1[:, 0:1], None, ALU.mult)
                dve.drain()
                dve.wait_ge(s["w_in"], 32)
                for t in range(NT + 2):
                    if t < NT:
                        if t >= 2:
                            dve.wait_ge(s["turned"], t - 1)
                        quantize(dve, q[:, t % 2, 0:D], r[:, t, :], t_f[:, t % 2, 0:D], am[:, 1, t:t + 1]).then_inc(s["q"], 1)
                    if t >= 2:
                        u = t - 2
                        dve.wait_ge(s["mult"], u + 1)
                        if u >= 2:
                            dve.wait_ge(s["gelu"], u - 1)
                        dve.scalar_tensor_tensor(out=h[:, u % 2, :].rearrange("p (a n) -> p a n", a=2), in0=ps[:, u % 2],
                                                 scalar=am[:, 2, u:u + 1], in1=b1_sb[:].rearrange("p (a n) -> p a n", a=2),
                                                 op0=ALU.mult, op1=ALU.add).then_inc(s["h"], 1)
                dve.wait_ge(s["gelu"], NT)
                dve.tensor_reduce(am2[:, 0, :], g[:], AX.X, ALU.max, apply_absolute_value=True)
                dve.tensor_scalar(am2[:, 1, :], am2[:, 7, :], 1.0 / F, 1e-5, ALU.mult, ALU.add).then_inc(s["var"], 1)
                dve.drain()
                dve.wait_ge(s["sd"], 1)
                dve.reciprocal(am2[:, 2, :], am2[:, 1, :])
                dve.drain()
                dve.tensor_tensor(am2[:, 3, :], am2[:, 0, :], am2[:, 2, :], ALU.mult)
                dve.drain()
                dve.tensor_scalar(am2[:, 3, :], am2[:, 3, :], 1e-5, 1.0 / 127.0, ALU.max, ALU.mult)
                dve.drain()
                dve.reciprocal(am2[:, 4, :], am2[:, 3, :])
                dve.drain()
                dve.tensor_tensor(am2[:, 5, :], am2[:, 4, :], am2[:, 2, :], ALU.mult)
                dve.tensor_scalar(am2[:, 6, :], am2[:, 3, :], s2[:, 0:1], None, ALU.mult)
                dve.drain()
                for t in range(NT + 2):
                    if t < NT:
                        if t >= 2:
                            dve.wait_ge(s["turned2"], t - 1)
                        quantize(dve, q[:, t % 2, :], g[:, t, :], t_f[:, t % 2, :], am2[:, 5, t:t + 1]).then_inc(s["q2"], 1)
                    if t >= 2:
                        u = t - 2
                        dve.wait_ge(s["mult2"], u + 1)
                        dve.scalar_tensor_tensor(out=c.x[:, u, :], in0=ps[:, u % 2, 0, 0:D], scalar=am2[:, 6, u:u + 1],
                                                 in1=c.x[:, u, :], op0=ALU.mult, op1=ALU.add).then_inc(s["added"], 1)

            @block.gpsimd
            def _(pool):
                pool.wait_ge(s["w_in"], 32)
                for t in range(NT):
                    pool.wait_ge(s["added"], t + 1)
                    pool.tensor_tensor(c.x[:, t, :], c.x[:, t, :], b2_sb[:], ALU.add)

            @block.tensor
            def _(pe):
                for q_s, t_s, qT_s, m_s, h_s, nk, wide in ((s["q"], s["turned"], s["qT"], s["mult"], s["h"], KC, True),
                                                           (s["q2"], s["turned2"], s["qT2"], s["mult2"], s["added"], FC, False)):
                    for t in range(NT + 1):
                        if t < NT:
                            pe.wait_ge(q_s, t + 1)
                            if t >= 2:
                                pe.wait_ge(qT_s, t - 1)
                            for k in range(nk):
                                last = pe.transpose(tp[:, t % 2, k * P:(k + 1) * P], q[:, t % 2, k * P:(k + 1) * P], idb[:])
                            last.then_inc(t_s, 1)
                        if t >= 1:
                            u = t - 1
                            pe.wait_ge(qT_s, u + 1)
                            if u >= 2:
                                pe.wait_ge(h_s, u - 1)
                            for n in range(F // 512 if wide else 1):
                                for k in range(nk):
                                    rhs = w1q[:, k, n * 512:(n + 1) * 512] if wide else w2q[:, k, :]
                                    last = pe.matmul(ps[:, u % 2, n, 0:512 if wide else D], qT[:, u % 2, k * P:(k + 1) * P], rhs,
                                                     start=(k == 0), stop=(k == nk - 1))
                            last.then_inc(m_s, 1)

            @block.scalar
            def _(act):
                def copy(t, turned, mult, qT_s, width):
                    act.wait_ge(turned, t + 1)
                    if t >= 2:
                        act.wait_ge(mult, t - 1)
                    act.activation(qT[:, t % 2, 0:width], tp[:, t % 2, 0:width], ACT.Copy).then_inc(qT_s, 1)

                for t in range(NT + 2):
                    if t < NT:
                        copy(t, s["turned"], s["mult"], s["qT"], D)
                    if t >= 2:
                        u = t - 2
                        act.wait_ge(s["h"], u + 1)
                        act.activation(g[:, u, :], h[:, u % 2, :], ACT.Gelu)
                        act.drain()
                        act.activation(sq[:], g[:, u, :], ACT.Square, accum_out=am2[:, 7, u:u + 1]).then_inc(s["gelu"], 1)
                        act.drain()
                act.wait_ge(s["var"], 1)
                act.activation(am2[:, 1, :], am2[:, 1, :], ACT.Sqrt).then_inc(s["sd"], 1)
                for t in range(NT):
                    copy(t, s["turned2"], s["mult2"], s["qT2"], F)


def per_head_T(c, name, qT, kT, gT, wq, wk, scale):
    nc = c.nc
    with Stage(nc, name) as st:
        w = st.sb("w", [P, 2, KC, P])
        ps = st.ps("ps", [P, 2, 4, 512])
        w_in, mult_q, mult_k, out_q, out_k = (st.sem(n) for n in ("w_in", "mult_q", "mult_k", "out_q", "out_k"))
        units = [(k, n) for k in range(KC) for n in range(N // 512)]
        with nc.Block() as block:
            @block.sync
            def _(sp):
                load_weights(sp, [(w[:, i], v.rearrange("k p m -> p k m")) for i, v in enumerate((wq, wk))], w_in)
                sp.wait_ge(w_in, 32)

            @block.tensor
            def _(pe):
                pe.wait_ge(w_in, 32)
                for u, (k, n) in enumerate(units):
                    for i, (t, mult, out) in enumerate(((qT, mult_q, out_q), (kT, mult_k, out_k))):
                        if u >= 4:
                            pe.wait_ge(out, u - 3)
                        pe.matmul(ps[:, i, u % 4, :], w[:, i, k, :], t[:, k, n * 512:(n + 1) * 512],
                                  start=True, stop=True).then_inc(mult, 1)

            @block.scalar
            def _(act):
                for u, (k, n) in enumerate(units):
                    act.wait_ge(mult_q, u + 1)
                    act.activation(qT[:, k, n * 512:(n + 1) * 512], ps[:, 0, u % 4, :], ACT.Copy).then_inc(out_q, 1)

            @block.vector
            def _(dve):
                for u, (k, n) in enumerate(units):
                    cols = slice(n * 512, (n + 1) * 512)
                    dve.wait_ge(mult_k, u + 1)
                    dve.scalar_tensor_tensor(out=kT[:, k, cols], in0=ps[:, 1, u % 4, :], scalar=scale, in1=gT[:, k, cols],
                                             op0=ALU.mult, op1=ALU.mult).then_inc(out_k, 1)


def recurrence(c, name, qT, kT, vT, decay_logits, spread, gather):
    nc = c.nc
    with Stage(nc, name) as st:
        dl = st.sb("dl", [P, KC])
        sg = st.sb("sg", [P, 2, DH, P])
        kv = st.sb("kv", [P, 2, S])
        M = st.sb("M", [P, 2, S])
        qM = st.sb("qM", [P, 2, S])
        qb = st.sb("qb", [P, KC, S])
        vb = st.ps("vb", [P, 2, 2, 512])
        y = st.ps("y", [P, KC, 2, 512])
        names = ("w_in", "decay", "spread", "kv", "M", "q", "qM", "gathered", "y_out")
        s = {n: st.sem(n, primed=n in ("kv", "y_out", "qM", "gathered",)) for n in names}
        U = KC * DH
        with nc.Block() as block:
            @block.sync
            def _(sp):
                load_weights(sp, [(dl[:], decay_logits), (sg[:, 0], spread), (sg[:, 1], gather)], s["w_in"])
                sp.wait_ge(s["w_in"], 48)

            @block.tensor
            def _(pe):
                pe.wait_ge(s["w_in"], 48)
                with pe.Fori(0, B) as bi:
                    def copies(u):
                        k, d = u // DH, u % DH
                        pe.wait_ge(s["kv"], bi * U + u if u >= 2 else bi * U + 1)
                        for h in range(2):
                            last = pe.matmul(vb[:, u % 2, h, :], sg[:, 0, d, :], vT[:, k, bass.ds(bi * S + h * 512, 512)],
                                             start=True, stop=True)
                        last.then_inc(s["spread"], 1)

                    def sums(u):
                        k, d = u // DH, u % DH
                        if d == 0:
                            pe.wait_ge(s["y_out"], bi * KC + 1)
                        pe.wait_ge(s["qM"], bi * U + (u + 2))
                        for h in range(2):
                            last = pe.matmul(y[:, k, h, :], sg[:, 1, d, :], qM[:, u % 2, h * 512:(h + 1) * 512],
                                             start=(d == 0), stop=(d == DH - 1))
                        last.then_inc(s["gathered"], 1)

                    for u in range(U + 2):
                        if u < U:
                            copies(u)
                        if u >= 2:
                            sums(u - 2)

            @block.vector
            def _(dve):
                dve.wait_ge(s["decay"], 1)
                with dve.Fori(0, B) as bi:
                    for u in range(U):
                        k, d = u // DH, u % DH
                        dve.wait_ge(s["spread"], bi * U + (u + 1))
                        dve.tensor_tensor(kv[:, u % 2, :].rearrange("p (h n) -> p h n", h=2),
                                          kT[:, k, bass.ds(bi * S, S)].rearrange("p (h n) -> p h n", h=2), vb[:, u % 2], ALU.mult).then_inc(s["kv"], 1)
                        dve.drain()
                        dve.wait_ge(s["qM"], bi * U + u if u >= 2 else bi * U + 1)
                        dve.tensor_tensor_scan(M[:, u % 2, :], dl[:, k:k + 1].broadcast_to([P, S]), kv[:, u % 2, :], 0.0,
                                               ALU.mult, ALU.add).then_inc(s["M"], 1)

            @block.gpsimd
            def _(pool):
                with pool.Fori(0, B) as bi:
                    for u in range(U):
                        k = u // DH
                        pool.wait_ge(s["q"], bi + 1)
                        pool.wait_ge(s["M"], bi * U + (u + 1))
                        pool.wait_ge(s["gathered"], bi * U + u if u >= 2 else bi * U + 1)
                        pool.tensor_tensor(qM[:, u % 2, :], M[:, u % 2, :], qb[:, k, :], ALU.mult).then_inc(s["qM"], 1)

            @block.scalar
            def _(act):
                act.wait_ge(s["w_in"], 48)
                act.activation(dl[:], dl[:], ACT.Sigmoid).then_inc(s["decay"], 1)
                with act.Fori(0, B) as bi:
                    act.activation(qb[:], qT[:, :, bass.ds(bi * S, S)], ACT.Copy).then_inc(s["q"], 1)
                    for k in range(KC):
                        act.wait_ge(s["gathered"], bi * U + ((k + 1) * DH + 1))
                        act.activation(vT[:, k, bass.ds(bi * S, S)].rearrange("p (h n) -> p h n", h=2), y[:, k], ACT.Copy).then_inc(s["y_out"], 1)


def cross_heads(c, name, qT, kT, v, out, clip=None):
    nc = c.nc
    HK = P // DH
    W = HK * S2
    HW = W // 2
    with Stage(nc, name) as st:
        hm = st.sb("hm", [P, HK])
        kb = st.sb("kb", [P, KC, B, HK, S2])
        sc = st.sb("sc", [P, 2, HK, S2])
        ex = st.sb("ex", [P, 2, HK, S2])
        mx = st.sb("mx", [P, 2, HK])
        sm = st.sb("sm", [P, 3, HK])
        eT = st.sb("eT", [S2, 2, HK, P])
        ps = st.ps("ps", [P, 2, 2, 512])
        tp = st.ps("tp", [P, 2, 512])
        po = st.ps("po", [P, 2, 512])
        names = ("w_in", "kb", "score", "read", "shift", "exp", "summed", "turned", "copied", "pv", "out")
        s = {n: st.sem(n) for n in names}
        units = [(t, k) for t in range(NT) for k in range(KC)]
        with nc.Block() as block:
            @block.sync
            def _(sp):
                sp.dma_start(hm[:], c.dram["head_mask"]).then_inc(s["w_in"], 16)
                sp.wait_ge(s["w_in"], 16)

            @block.tensor
            def _(pe):
                pe.wait_ge(s["kb"], 1)

                def scores(u):
                    t, k = units[u]
                    if u >= 2:
                        pe.wait_ge(s["read"], u - 1)
                    rhs = kb[:, k, t // ST].rearrange("p h n -> p (h n)")
                    for a in range(2):
                        last = pe.matmul(ps[:, u % 2, a, 0:HW], qT[:, k, t * P:(t + 1) * P], rhs[:, a * HW:(a + 1) * HW],
                                         start=True, stop=True)
                    last.then_inc(s["score"], 1)

                def turn(u):
                    pe.wait_ge(s["exp"], u + 1)
                    if u >= 1:
                        pe.wait_ge(s["copied"], u)
                    for h in range(HK):
                        last = pe.transpose(tp[0:S2, h // 4, (h % 4) * P:(h % 4 + 1) * P], ex[:, u % 2, h, :], c.ident[:])
                    last.then_inc(s["turned"], 1)

                def weigh(u):
                    t, k = units[u]
                    pe.wait_ge(s["copied"], u + 1)
                    if u >= 2:
                        pe.wait_ge(s["out"], u - 1)
                    for h in range(HK):
                        col = k * P + h * DH
                        last = pe.matmul(po[:, u % 2, h * DH:(h + 1) * DH], eT[:, u % 2, h, :], v[0:S2, t // ST, col:col + DH],
                                         start=True, stop=True)
                    last.then_inc(s["pv"], 1)

                for u in range(len(units) + 2):
                    if u < len(units):
                        scores(u)
                    if 1 <= u <= len(units):
                        turn(u - 1)
                    if u >= 2:
                        weigh(u - 2)

            @block.scalar
            def _(act):
                def copy(u):
                    act.wait_ge(s["turned"], u + 1)
                    if u >= 2:
                        act.wait_ge(s["pv"], u - 1)
                    act.activation(eT[:, u % 2].rearrange("p (a h) n -> p a (h n)", a=2), tp[0:S2, :, :], ACT.Copy).then_inc(s["copied"], 1)

                for u in range(len(units) + 1):
                    if u < len(units):
                        act.wait_ge(s["shift"], u + 1)
                        if u >= 2:
                            act.wait_ge(s["turned"], u - 1)
                            act.wait_ge(s["summed"], u - 1)
                        act.activation(ex[:, u % 2], sc[:, u % 2], ACT.Exp, scale=DH ** -0.5).then_inc(s["exp"], 1)
                    if u >= 1:
                        copy(u - 1)

            @block.vector
            def _(dve):
                dve.wait_ge(s["w_in"], 16)
                shape = [P, HK, S2]
                for k in range(KC):
                    for b in range(B):
                        keys = kT[:, k:k + 1, b * S2:(b + 1) * S2].broadcast_to(shape)
                        mask = hm[:].rearrange("p (h a) -> p h a", a=1).broadcast_to(shape)
                        dve.tensor_tensor(kb[:, k, b], keys, mask, ALU.mult)
                dve.drain()
                dve.sem_inc(s["kb"], 1)

                def top(u):
                    dve.wait_ge(s["score"], u + 1)
                    if u >= 2:
                        dve.wait_ge(s["exp"], u - 1)
                    o, src = sc[:, u % 2].rearrange("p (a h) n -> p a (h n)", a=2), ps[:, u % 2, :, 0:HW]
                    if clip is None:
                        dve.tensor_copy(o, src).then_inc(s["read"], 1)
                    else:
                        dve.tensor_scalar(o, src, clip, -clip, ALU.min, ALU.max).then_inc(s["read"], 1)
                    dve.drain()
                    dve.tensor_reduce(mx[:, u % 2, :], sc[:, u % 2], AX.X, ALU.max)
                    dve.drain()
                    m = mx[:, u % 2, :].rearrange("p (h a) -> p h a", a=1).broadcast_to(shape)
                    dve.tensor_tensor(sc[:, u % 2], sc[:, u % 2], m, ALU.subtract).then_inc(s["shift"], 1)

                def total(u):
                    dve.wait_ge(s["exp"], u + 1)
                    dve.tensor_reduce(sm[:, u % 3, :], ex[:, u % 2], AX.X, ALU.add).then_inc(s["summed"], 1)
                    dve.drain()
                    dve.reciprocal(sm[:, u % 3, :], sm[:, u % 3, :])

                def finish(u):
                    t, k = units[u]
                    dve.wait_ge(s["pv"], u + 1)
                    r = sm[:, u % 3, :].rearrange("p (h a) -> p h a", a=1).broadcast_to([P, HK, DH])
                    dve.tensor_tensor(out[:, t, k * P:(k + 1) * P].rearrange("p (h d) -> p h d", h=HK),
                                      po[:, u % 2, 0:P].rearrange("p (h d) -> p h d", h=HK), r, ALU.mult).then_inc(s["out"], 1)

                for u in range(len(units) + 2):
                    if u < len(units):
                        top(u)
                    if 1 <= u <= len(units):
                        total(u - 1)
                    if u > len(units):
                        dve.drain()
                    if u >= 2:
                        finish(u - 2)


TREE_DEPTH, TREES = 7, 8


def tree_ffn(c, name, srcT, wi, bi_sb, wo):
    nc = c.nc
    DEPTH, PAR = TREE_DEPTH, TREES
    W, WC = bi_sb.shape[1], wo.shape[1]
    Q = W // 4
    with Stage(nc, name) as st:
        l = st.sb("l", [P, 2, W])
        go = st.sb("go", [P, 2, W])
        on = st.sb("on", [P, 2, W])
        act_ = st.sb("act", [P, 2, WC * P])
        aT = st.sb("aT", [P, 2, 4, P])
        xt = st.sb("xt", [P, 2, KC, P])
        ps = st.ps("ps", [P, 4, 512])
        tp = st.ps("tp", [P, 2, 512])
        po = st.ps("po", [P, 2, 512])
        names = ("x", "init", "logit", "l", "silu", "path", "masked", "turned", "aT", "out", "added")
        s = {n: st.sem(n, primed=n in ("l", "aT", "added", "logit", "turned", "out", "silu", "masked",)) for n in names}
        GT = WC // 4
        with nc.Block() as block:
            LAST = NT // 2 - 1

            def n(i, k, q):
                return i * (2 * k) + q

            @block.tensor
            def _(pe):
                def logits(i, j):
                    pe.wait_ge(s["x"], n(i, 1, j + 1))
                    pe.wait_ge(s["l"], n(i, 1, j + 1))
                    for g in range(4):
                        for k in range(KC):
                            last = pe.matmul(ps[:, g, 0:Q], xt[:, j % 2, k, :], wi[:, k, g * Q:(g + 1) * Q],
                                             start=(k == 0), stop=(k == KC - 1))
                    last.then_inc(s["logit"], 1)

                def turn(i, j, g):
                    q = j * GT + g
                    if g == 0:
                        pe.wait_ge(s["masked"], n(i, 1, j + 2))
                    pe.wait_ge(s["aT"], n(i, GT, max(q, 1)))
                    for m in range(4):
                        last = pe.transpose(tp[:, q % 2, m * P:(m + 1) * P], act_[:, j, (4 * g + m) * P:(4 * g + m + 1) * P], c.ident[:])
                    last.then_inc(s["turned"], 1)

                def project(i, j, g):
                    q = j * GT + g
                    if g == 0:
                        pe.wait_ge(s["added"], n(i, 1, max(j, 1)))
                    pe.wait_ge(s["aT"], n(i, GT, q + 2))
                    for m in range(4):
                        last = pe.matmul(po[:, j, 0:D], aT[:, q % 2, m, :], wo[:, 4 * g + m, :],
                                         start=(g == 0 and m == 0), stop=(g == GT - 1 and m == 3))
                    last.then_inc(s["out"], 1)

                def body(i, more):
                    for j in range(2):
                        if j == 0 or more:
                            logits(i, j + 1)
                        for g in range(GT + 1):
                            if g < GT:
                                turn(i, j, g)
                            if g >= 1:
                                project(i, j, g - 1)

                logits(0, 0)
                with pe.Fori(0, LAST) as i:
                    body(i, True)
                body(LAST, False)

            @block.gpsimd
            def _(pool):
                def fetch(i, j):
                    pool.wait_ge(s["logit"], n(i, 1, max(j, 1)))
                    pool.tensor_copy(xt[:, j % 2], srcT[:, :, bass.ds((i * 2 + j) * P, P)]).then_inc(s["x"], 1)

                def mask(i, j):
                    pool.wait_ge(s["silu"], n(i, 1, j + 2))
                    pool.wait_ge(s["path"], n(i, 1, j + 1))
                    pool.tensor_tensor(act_[:, j, 0:W], act_[:, j, 0:W], on[:, j, :], ALU.mult).then_inc(s["masked"], 1)

                def body(i, more):
                    for j in range(2):
                        mask(i, j)
                        if more:
                            fetch(i, j + 2)

                pool.memset(act_[:, :, W:WC * P], 0.0)
                on4 = on[:].rearrange("p r (a n) -> p r a n", a=PAR)
                pool.memset(on4[:, :, :, 0:1], 1.0)
                pool.drain()
                pool.sem_inc(s["init"], 1)
                fetch(0, 0)
                fetch(0, 1)
                with pool.Fori(0, LAST) as i:
                    body(i, True)
                body(LAST, False)

            @block.scalar
            def _(act):
                def silu(i, j):
                    act.wait_ge(s["l"], n(i, 1, j + 2))
                    act.wait_ge(s["turned"], n(i, GT, max((j - 1) * GT, 0) + 1))
                    act.activation(act_[:, j % 2, 0:W], l[:, j % 2, :], ACT.Silu).then_inc(s["silu"], 1)

                def copies(i, j, groups):
                    for q in range(j * GT + groups[0], j * GT + groups[1]):
                        act.wait_ge(s["turned"], n(i, GT, q + 2))
                        act.wait_ge(s["out"], n(i, GT, max(q, 1)))
                        act.activation(aT[:, q % 2].rearrange("p m n -> p (m n)"), tp[:, q % 2, :], ACT.Copy).then_inc(s["aT"], 1)

                def body(i, more):
                    for j in range(2):
                        copies(i, j, (0, 2))
                        if j == 0 or more:
                            silu(i, j + 1)
                        copies(i, j, (2, GT))

                silu(0, 0)
                with act.Fori(0, LAST) as i:
                    body(i, True)
                body(LAST, False)

            @block.vector
            def _(dve):
                def path(i, j):
                    r = j % 2
                    dve.wait_ge(s["logit"], n(i, 1, j + 2))
                    dve.wait_ge(s["silu"], n(i, 1, max(j, 1)))
                    dve.tensor_tensor(l[:, r, :].rearrange("p (g n) -> p g n", g=4), ps[:, :, 0:Q],
                                      bi_sb[:].rearrange("p (g n) -> p g n", g=4), ALU.add).then_inc(s["l"], 1)
                    dve.drain()
                    dve.tensor_scalar(go[:, r, :], l[:, r, :], 0.0, None, ALU.is_gt)
                    dve.drain()
                    dve.wait_ge(s["masked"], n(i, 1, max(j, 1)))
                    on3 = on[:, r, :].rearrange("p (a n) -> p a n", a=PAR)
                    go3 = go[:, r, :].rearrange("p (a n) -> p a n", a=PAR)
                    for lev in range(DEPTH):
                        here, nodes = 2 ** lev - 1, 2 ** lev
                        below = 2 * here + 1
                        right = on3[:, :, below + 1:below + 2 * nodes:2]
                        dve.tensor_tensor(right, on3[:, :, here:here + nodes], go3[:, :, here:here + nodes], ALU.mult)
                        dve.drain()
                        last = dve.tensor_tensor(on3[:, :, below:below + 2 * nodes:2], on3[:, :, here:here + nodes], right, ALU.subtract)
                        if lev < DEPTH - 1:
                            dve.drain()
                    last.then_inc(s["path"], 1)

                def add(i, j):
                    x_t = c.x[:, bass.ds(i * 2 + j, 1), :]
                    dve.wait_ge(s["out"], n(i, GT, (j + 1) * GT + 1))
                    dve.tensor_tensor(x_t, x_t, po[:, j:j + 1, 0:D], ALU.add).then_inc(s["added"], 1)

                def body(i, more):
                    for j in range(2):
                        if j == 0 or more:
                            path(i, j + 1)
                        add(i, j)

                dve.wait_ge(s["init"], 1)
                path(0, 0)
                with dve.Fori(0, LAST) as i:
                    body(i, True)
                body(LAST, False)


H3 = 8
DK = 128
M_INCL, M_STRICT, M_BLOCK, M_J16, M_J32, M_J64 = range(6)


def delta_gates(c, name, ba, dt_bias, a_log, coef):
    nc = c.nc
    with Stage(nc, name) as st:
        rows = st.sb("rows", [P, 2, H3])
        masks = st.sb("masks", [P, P])
        z = st.sb("z", [P, H3, NT])
        l = st.sb("l", [P, H3, NT])
        ps = st.ps("ps", [P, 4, 512])
        s = {n: st.sem(n) for n in ("in", "z", "log", "g", "sum")}
        with nc.Block() as block:
            @block.sync
            def _(sp):
                load_weights(sp, [(rows[:, 0], row_bcast(dt_bias, H3)), (rows[:, 1], row_bcast(a_log, H3)),
                                  (masks[:], c.dram["masks"][:, M_STRICT, :])], s["in"])
                sp.wait_ge(s["in"], 48)

            @block.vector
            def _(dve):
                dve.wait_ge(s["in"], 48)
                dt = rows[:, 0].rearrange("p (h a) -> p h a", a=1).broadcast_to([P, H3, NT])
                dve.tensor_tensor(z[:], ba[:, :, H3:2 * H3].rearrange("p t h -> p h t"), dt, ALU.add)
                dve.tensor_copy(coef[:, 0], ba[:, :, 0:H3].rearrange("p t h -> p h t"))
                dve.drain()
                dve.sem_inc(s["z"], 1)
                dve.wait_ge(s["log"], 1)
                dve.scalar_tensor_tensor(out=z[:], in0=z[:], scalar=0.0, in1=l[:], op0=ALU.max, op1=ALU.add)
                dve.drain()
                ea = rows[:, 1].rearrange("p (h a) -> p h a", a=1).broadcast_to([P, H3, NT])
                dve.scalar_tensor_tensor(out=coef[:, 1], in0=z[:], scalar=-1.0, in1=ea, op0=ALU.mult, op1=ALU.mult).then_inc(s["g"], 1)

            @block.tensor
            def _(pe):
                pe.wait_ge(s["in"], 48)
                pe.wait_ge(s["g"], 1)
                g = coef[:, 1].rearrange("p h t -> p (h t)")
                for i, m in enumerate((c.lower, masks, c.ones)):
                    last = pe.matmul(ps[:, i, 0:H3 * NT], m[:], g, start=True, stop=True)
                last.then_inc(s["sum"], 1)

            @block.scalar
            def _(act):
                act.wait_ge(s["z"], 1)
                act.activation(coef[:, 0], coef[:, 0], ACT.Sigmoid)
                act.activation(l[:], z[:], ACT.Abs)
                act.drain()
                act.activation(l[:], l[:], ACT.Exp, scale=-1.0)
                act.activation(rows[:, 1], rows[:, 1], ACT.Exp)
                act.drain()
                act.activation(l[:], l[:], ACT.Ln, bias=1.0).then_inc(s["log"], 1)
                act.wait_ge(s["sum"], 1)
                for i in range(3):
                    act.activation(coef[:, 2 + i].rearrange("p h t -> p (h t)"), ps[:, i, 0:H3 * NT], ACT.Exp)


def delta_project(c, name, head, w_sb, coef, hc, qkvg, bgk, kT, qT, qgT):
    nc = c.nc
    with Stage(nc, name) as st:
        NH = NT // 2
        turns = [("k", 0), ("k", 1), ("q", 0), ("q", 1), ("k", 2), ("k", 3), ("q", 2), ("q", 3)] + [("qg", g) for g in range(4)]
        sq = st.sb("sq", [P, 2, 4, 2 * DK])
        ss = st.sb("ss", [P, NT, 2])
        bg = st.sb("bg", [P, NT])
        ps = st.ps("ps", [P, 4, 512])
        tp = st.ps("tp", [P, 4, 512])
        s = {n: st.sem(n) for n in ("proj", "silu", "ss", "sd", "k", "q", "hc", "turned", "copied", "qg")}
        with nc.Block() as block:
            @block.gpsimd
            def _(pool):
                pool.wait_ge(s["silu"], NT)
                pool.wait_ge(s["hc"], 1)
                v = qkvg[:, :, 2 * DK:3 * DK]
                pool.tensor_tensor(v, v, hc[:, 0, :].rearrange("p (t a) -> p t a", a=1).broadcast_to([P, NT, DK]), ALU.mult)

            @block.tensor
            def _(pe):
                for t in range(NT):
                    if t >= 4:
                        pe.wait_ge(s["silu"], t - 3)
                    for k in range(KC):
                        last = pe.matmul(ps[:, t % 4, :], c.xT[:, k, t * P:(t + 1) * P], w_sb[:, k, :], start=(k == 0), stop=(k == KC - 1))
                    last.then_inc(s["proj"], 1)
                for i, (kind, g) in enumerate(turns):
                    if g % 2 == 0:
                        pe.wait_ge(s[kind], g // 2 + 1)
                    if i >= 4:
                        pe.wait_ge(s["copied"], i - 3)
                    a = DK if kind == "k" else 0
                    for m in range(4):
                        last = pe.transpose(tp[:, i % 4, m * P:(m + 1) * P], qkvg[:, 4 * g + m, a:a + DK], c.ident[:])
                    last.then_inc(s["turned"], 1)

            @block.scalar
            def _(act):
                def root(h):
                    act.wait_ge(s["ss"], h + 1)
                    act.activation(ss[:, h * NH:(h + 1) * NH, :], ss[:, h * NH:(h + 1) * NH, :], ACT.Sqrt).then_inc(s["sd"], 1)

                for t in range(NT):
                    act.wait_ge(s["proj"], t + 1)
                    act.activation(qkvg[:, t, :], ps[:, t % 4, :], ACT.Silu).then_inc(s["silu"], 1)
                    if t == NH + 3:
                        root(0)
                root(1)
                for i, (kind, g) in enumerate(turns):
                    act.wait_ge(s["turned"], i + 1)
                    dst = {"k": kT, "q": qT, "qg": qgT}[kind]
                    act.activation(dst[:, 4 * g:4 * g + 4, :].rearrange("p t d -> p (t d)"), tp[:, i % 4, :],
                                   ACT.Copy).then_inc(s["copied"], 1)

            @block.vector
            def _(dve):
                dve.tensor_copy(hc[:], coef[:, :, bass.ds(head, 1), :].rearrange("p c a t -> p c (a t)"))
                dve.drain()
                dve.sem_inc(s["hc"], 1)
                dve.tensor_tensor(bg[:], hc[:, 0, :], hc[:, 2, :], ALU.mult)

                def norms(h):
                    ts = slice(h * NH, (h + 1) * NH)
                    for g in (2 * h, 2 * h + 1):
                        dve.wait_ge(s["silu"], 4 * (g + 1))
                        qk = qkvg[:, 4 * g:4 * g + 4, 0:2 * DK]
                        dve.tensor_tensor(sq[:, g % 2], qk, qk, ALU.mult)
                        dve.drain()
                        dve.tensor_reduce(ss[:, 4 * g:4 * g + 4, :], sq[:, g % 2].rearrange("p t (w d) -> p t w d", w=2), AX.X, ALU.add)
                    dve.drain()
                    dve.tensor_scalar(ss[:, ts, :], ss[:, ts, :], 1e-6, None, ALU.add).then_inc(s["ss"], 1)
                    dve.wait_ge(s["sd"], h + 1)
                    dve.reciprocal(ss[:, ts, :], ss[:, ts, :])
                    dve.drain()
                    dve.tensor_scalar(ss[:, ts, 0:1], ss[:, ts, 0:1], DK ** -0.5, None, ALU.mult)
                    q, k = qkvg[:, ts, 0:DK], qkvg[:, ts, DK:2 * DK]
                    dve.tensor_tensor(k, k, ss[:, ts, 1:2].broadcast_to(half), ALU.mult).then_inc(s["k"], 1)
                    dve.drain()
                    dve.tensor_tensor(q, q, ss[:, ts, 0:1].broadcast_to(half), ALU.mult).then_inc(s["q"], 1)
                    dve.tensor_tensor(bgk[:, ts, :], k, col(bg[:, ts]), ALU.mult)

                def decays(h):
                    ts = slice(h * NH, (h + 1) * NH)
                    q, k = qkvg[:, ts, 0:DK], qkvg[:, ts, DK:2 * DK]
                    dve.wait_ge(s["turned"], 4 * h + 4)
                    dve.tensor_tensor(q, q, col(hc[:, 2, ts]), ALU.mult).then_inc(s["qg"], 1)
                    dve.tensor_tensor(k, k, col(hc[:, 3, ts]), ALU.mult)

                half = [P, NH, DK]

                def col(v):
                    return v.rearrange("p (t a) -> p t a", a=1).broadcast_to(half)

                norms(0)
                norms(1)
                dve.drain()
                decays(0)
                decays(1)


def delta_invert(c, name, head, w, w_o, w_sb, wo_sb, masks, hc, qkvg, bgk, kT, qT, U, WT, PT):
    nc = c.nc
    STEPS = 13
    with Stage(nc, name) as st:
        def four(n):
            return st.sb(n, [P, 2, 4, P])
        gs, bs, Dm, DT, L, LT, n1, n1T, n2, n2T, T, TT, X, Lm = (four(n) for n in (
            "gs", "bs", "D", "DT", "L", "LT", "n1", "n1T", "n2", "n2T", "T", "TT", "X", "Lm"))
        ps = st.ps("ps", [P, 2, 3, 512])
        s = {n: st.sem(n) for n in ("w_in", "gs", "mm", "act", "dve", "lm")}

        def wide(m, g):
            return m[:, g].rearrange("p t d -> p (t d)")

        def mask(m):
            return masks[:, m:m + 1, :].broadcast_to([P, 4, P])

        A = [1, 2, 1, 1, 1, 0, 1, 0, 0, 0, 0, 0, 1]

        def done(r, n, g, per=None):
            if per is None:
                return 2 * STEPS * r + 2 * n + g + 1
            return 2 * sum(per) * r + 2 * sum(per[:n]) + per[n] * (g + 1)

        with nc.Block() as block:
            @block.sync
            def _(sp):
                load_weights(sp, [(w_sb[:], w[bass.ds(head + 1, 1)].rearrange("a (k p) m -> p (a k) m", p=P)),
                                  (wo_sb[:], w_o[bass.ds(head, 1)].rearrange("a p m -> p (a m)"))], s["w_in"])
                sp.wait_ge(s["w_in"], 32)

            @block.tensor
            def _(pe):
                for r in range(2):
                    for n in range(STEPS):
                        for g in range(2):
                            t0 = (2 * r + g) * 4
                            if n == 0:
                                pe.wait_ge(s["gs"], 2 * r + g + 1)
                                if r == 1:
                                    pe.wait_ge(s["dve"], done(0, STEPS - 1, g))
                                    pe.wait_ge(s["act"], done(0, STEPS - 1, g, A))
                            else:
                                pe.wait_ge(s["dve"], done(r, n - 1, g))
                                pe.wait_ge(s["act"], done(r, n - 1, g, A))

                            def mm(bank, lhs, rhs):
                                for m in range(4):
                                    q = pe.matmul(ps[:, g, bank, m * P:(m + 1) * P], lhs(m), rhs(m), start=True, stop=True)
                                return q

                            def turn(bank, src):
                                for m in range(4):
                                    q = pe.transpose(ps[:, g, bank, m * P:(m + 1) * P], src[:, g, m, :], c.ident[:])
                                return q

                            def of(b):
                                return lambda m: b[:, g, m, :]

                            def tok(b):
                                return lambda m: b[:, t0 + m, :]
                            if n == 0:
                                pe.matmul(ps[:, g, 0, :], c.lower[:], wide(gs, g), start=True, stop=True)
                                last = mm(1, tok(kT), tok(kT))
                            elif n == 1:
                                turn(0, L)
                                last = turn(1, Dm)
                            elif n == 2:
                                mm(0, of(n1T), of(n1))
                                mm(1, of(n1), of(n1T))
                                last = mm(2, tok(kT), tok(qT))
                            elif n == 3:
                                mm(0, of(n2T), of(n2))
                                mm(1, of(n2), of(n2T))
                                last = mm(2, of(n2T), of(T))
                            elif n == 4:
                                mm(0, of(n1), of(n1T))
                                last = mm(2, of(n1T), of(T))
                            elif n == 5:
                                last = mm(2, of(n2T), of(T))
                            elif n in (6, 8, 10):
                                if n == 6:
                                    turn(0, T)
                                pe.wait_ge(s["lm"], 6 * r + (n - 6) + g + 1)
                                last = mm(1, of(Lm), of(T))
                            elif n in (7, 9):
                                mm(0, of(TT), of(X))
                                last = mm(1, of(X), of(TT))
                            elif n == 11:
                                last = mm(1, of(X), of(TT))
                            else:
                                mm(0, of(TT), lambda m: qkvg[:, t0 + m, 2 * DK:3 * DK])
                                last = mm(1, tok(bgk), of(TT))
                            last.then_inc(s["mm"], 1)

            @block.scalar
            def _(act):
                for r in range(2):
                    for n in range(STEPS):
                        for g in range(2):
                            t0 = (2 * r + g) * 4
                            copies = {1: [(LT, 0), (DT, 1)], 2: [(n2, 0)], 3: [(n1, 0)], 4: [(n2T, 0)], 6: [(TT, 0)]}
                            if not A[n]:
                                continue
                            act.wait_ge(s["mm"], done(r, n, g))
                            if n == 0:
                                act.activation(wide(Dm, g), ps[:, g, 0, :], ACT.Exp).then_inc(s["act"], 1)
                            elif n == STEPS - 1:
                                act.activation(U[:, t0:t0 + 4, :].rearrange("p t d -> p (t d)"), ps[:, g, 0, :],
                                               ACT.Copy).then_inc(s["act"], 1)
                            else:
                                for dst, bank in copies[n]:
                                    act.activation(wide(dst, g), ps[:, g, bank, :], ACT.Copy).then_inc(s["act"], 1)

            @block.gpsimd
            def _(pool):
                for r in range(2):
                    for n in (6, 8, 10):
                        for g in range(2):
                            if n == 6:
                                pool.wait_ge(s["act"], done(r, 1, g, A))
                                if r == 1:
                                    pool.wait_ge(s["mm"], done(0, 10, g))
                            else:
                                pool.wait_ge(s["mm"], done(r, n - 2, g))
                            pool.tensor_tensor(Lm[:, g], LT[:, g], mask((M_J16, M_J32, M_J64)[(n - 6) // 2]), ALU.mult).then_inc(s["lm"], 1)

            @block.vector
            def _(dve):
                def col(v):
                    return v.rearrange("p (t a) -> p t a", a=1).broadcast_to([P, 4, P])

                for r in range(2):
                    for g in range(2):
                        t0 = (2 * r + g) * 4
                        dve.tensor_tensor(gs[:, g], mask(M_STRICT), col(hc[:, 1, t0:t0 + 4]), ALU.mult).then_inc(s["gs"], 1)
                        dve.tensor_tensor(bs[:, g], mask(M_STRICT), col(hc[:, 0, t0:t0 + 4]), ALU.mult)
                    dve.drain()
                    for n in range(STEPS):
                        for g in range(2):
                            t0 = (2 * r + g) * 4

                            def bank(i):
                                return ps[:, g, i, :].rearrange("p (t d) -> p t d", t=4)
                            dve.wait_ge(s["mm"], done(r, n, g))
                            if n == 0:
                                dve.wait_ge(s["act"], done(r, 0, g, A))
                                dve.tensor_tensor(Dm[:, g], Dm[:, g], mask(M_INCL), ALU.mult)
                                dve.tensor_tensor(L[:, g], bank(1), bs[:, g], ALU.mult)
                                dve.drain()
                                last = dve.tensor_tensor(L[:, g], L[:, g], Dm[:, g], ALU.mult)
                            elif n == 1:
                                dve.wait_ge(s["act"], done(r, 1, g, A))
                                dve.scalar_tensor_tensor(out=n1[:, g], in0=L[:, g], scalar=-1.0, in1=mask(M_BLOCK), op0=ALU.mult, op1=ALU.mult)
                                dve.scalar_tensor_tensor(out=n1T[:, g], in0=LT[:, g], scalar=-1.0, in1=mask(M_BLOCK), op0=ALU.mult, op1=ALU.mult)
                                dve.drain()
                                idb = c.ident[:].rearrange("p (a n) -> p a n", a=1).broadcast_to([P, 4, P])
                                last = dve.tensor_tensor(T[:, g], n1[:, g], idb, ALU.add)
                            elif n == 2:
                                dve.tensor_tensor(PT[:, t0:t0 + 4, :], bank(2), DT[:, g], ALU.mult)
                                last = dve.tensor_copy(n2T[:, g], bank(1))
                            elif n == 3:
                                dve.tensor_copy(n1T[:, g], bank(1))
                                last = dve.tensor_tensor(T[:, g], T[:, g], bank(2), ALU.add)
                            elif n in (4, 5):
                                last = dve.tensor_tensor(T[:, g], T[:, g], bank(2), ALU.add)
                            elif n in (6, 8, 10):
                                last = dve.tensor_copy(X[:, g], bank(1))
                            elif n in (7, 9):
                                dve.tensor_tensor(T[:, g], T[:, g], bank(0), ALU.subtract)
                                last = dve.tensor_tensor(TT[:, g], TT[:, g], bank(1), ALU.subtract)
                            elif n == 11:
                                last = dve.tensor_tensor(TT[:, g], TT[:, g], bank(1), ALU.subtract)
                            else:
                                last = dve.tensor_copy(WT[:, t0:t0 + 4, :], bank(1))
                            dve.drain()
                            dve.sem_inc(s["dve"], 1)


def delta_scan(c, name, hc, qkvg, nw, qgT, U, WT, PT, o):
    nc = c.nc
    with Stage(nc, name) as st:
        Sst = st.sb("S", [P, 2, B, DK])
        dl = st.sb("dl", [P, 2, B, DK])
        ws = st.ps("ws", [P, B, 512])
        sp_ = st.ps("sp", [P, B, 512])
        op = st.ps("op", [P, 2, 512])
        s = {n: st.sem(n) for n in ("S", "ws", "dl", "kd", "o", "o_out")}
        o4 = o[:].rearrange("p (b t) d -> p b t d", b=B)
        with nc.Block() as block:
            @block.gpsimd
            def _(pool):
                gate = qkvg[:, :, 3 * DK:4 * DK]
                pool.tensor_tensor(gate, gate, nw[:].rearrange("p (a d) -> p a d", a=1).broadcast_to([P, NT, DK]), ALU.mult)

            @block.tensor
            def _(pe):
                for n in range(ST):
                    for b in range(B):
                        pe.wait_ge(s["S"], n * B + b + 1)
                        pe.matmul(ws[:, b, 0:DK], WT[:, b * ST + n, :], Sst[:, n % 2, b, :], start=True, stop=True).then_inc(s["ws"], 1)
                    for b in range(B):
                        t = b * ST + n
                        pe.wait_ge(s["dl"], n * B + b + 1)
                        pe.matmul(sp_[:, b, 0:DK], qkvg[:, t, DK:2 * DK], dl[:, n % 2, b, :], start=True, stop=True).then_inc(s["kd"], 1)
                    if n >= 2:
                        pe.wait_ge(s["o_out"], n - 1)
                    for b in range(B):
                        t = b * ST + n
                        dst = op[:, n % 2, b * DK:(b + 1) * DK]
                        pe.matmul(dst, qgT[:, t, :], Sst[:, n % 2, b, :], start=True, stop=False)
                        last = pe.matmul(dst, PT[:, t, :], dl[:, n % 2, b, :], start=False, stop=True)
                    last.then_inc(s["o"], 1)

            @block.scalar
            def _(act):
                for n in range(ST):
                    act.wait_ge(s["o"], n + 1)
                    act.activation(o4[:, :, n, :], op[:, n % 2, 0:B * DK].rearrange("p (b d) -> p b d", b=B), ACT.Copy).then_inc(s["o_out"], 1)

            @block.vector
            def _(dve):
                dve.memset(Sst[:, 0], 0.0).then_inc(s["S"], B)
                for n in range(ST):
                    for b in range(B):
                        t = b * ST + n
                        dve.wait_ge(s["ws"], n * B + b + 1)
                        if n >= 2:
                            dve.wait_ge(s["o"], n - 1)
                        dve.tensor_tensor(dl[:, n % 2, b, :], U[:, t, :], ws[:, b, 0:DK], ALU.subtract).then_inc(s["dl"], 1)
                    for b in range(B) if n < ST - 1 else ():
                        t = b * ST + n
                        dve.wait_ge(s["kd"], n * B + b + 1)
                        if n >= 1:
                            dve.wait_ge(s["o"], n)
                        dve.scalar_tensor_tensor(out=Sst[:, (n + 1) % 2, b, :], in0=Sst[:, n % 2, b, :], scalar=hc[:, 4, t:t + 1],
                                                 in1=sp_[:, b, 0:DK], op0=ALU.mult, op1=ALU.add).then_inc(s["S"], 1)
                    dve.drain()


def delta_output(c, name, w_sb, qkvg, o, og, oT, xi):
    nc = c.nc
    GN = NT // 4
    with Stage(nc, name) as st:
        sq = st.sb("sq", [P, NT, DK])
        ss = st.sb("ss", [P, NT])
        tp = st.ps("tp", [P, 4, 512])
        ps = st.ps("ps", [P, 4, 512])
        s = {n: st.sem(n) for n in ("ss", "sd", "o", "turned", "oT", "mult", "added")}
        with nc.Block() as block:
            @block.vector
            def _(dve):
                for g in range(GN):
                    ts = slice(4 * g, 4 * g + 4)
                    dve.tensor_tensor(og[:, ts, :], o[:, ts, :], qkvg[:, ts, 3 * DK:4 * DK], ALU.mult).then_inc(s["o"], 1)
                dve.tensor_tensor(sq[:], o[:], o[:], ALU.mult)
                dve.drain()
                dve.tensor_reduce(ss[:], sq[:], AX.X, ALU.add)
                dve.drain()
                dve.tensor_scalar(ss[:], ss[:], 1.0 / DK, 1e-6, ALU.mult, ALU.add).then_inc(s["ss"], 1)
                dve.wait_ge(s["sd"], 1)
                dve.reciprocal(ss[:], ss[:])
                dve.drain()
                for t in range(NT):
                    dve.wait_ge(s["mult"], t // 2 + 1)
                    last = dve.scalar_tensor_tensor(out=xi[:, t, :], in0=ps[:, t // 2 % 4, t % 2 * D:(t % 2 + 1) * D],
                                                    scalar=ss[:, t:t + 1], in1=xi[:, t, :], op0=ALU.mult, op1=ALU.add)
                    if t % 2:
                        last.then_inc(s["added"], 1)

            @block.scalar
            def _(act):
                def copy(g):
                    act.wait_ge(s["turned"], g + 1)
                    act.activation(oT[:, 4 * g:4 * g + 4, :].rearrange("p t d -> p (t d)"), tp[:, g, :], ACT.Copy).then_inc(s["oT"], 1)

                for g in range(GN):
                    copy(g)
                act.wait_ge(s["ss"], 1)
                act.activation(ss[:], ss[:], ACT.Sqrt).then_inc(s["sd"], 1)

            @block.tensor
            def _(pe):
                for g in range(GN + 1):
                    if g < GN:
                        pe.wait_ge(s["o"], g + 1)
                        for m in range(4):
                            last = pe.transpose(tp[:, g, m * P:(m + 1) * P], og[:, 4 * g + m, :], c.ident[:])
                        last.then_inc(s["turned"], 1)
                    if g >= 1:
                        pe.wait_ge(s["oT"], g)
                        for pr in (2 * g - 2, 2 * g - 1):
                            if pr >= 4:
                                pe.wait_ge(s["added"], pr - 3)
                            for m in range(2):
                                last = pe.matmul(ps[:, pr % 4, m * D:(m + 1) * D], oT[:, 2 * pr + m, :], w_sb[:], start=True, stop=True)
                            last.then_inc(s["mult"], 1)


def mix_heads(c, name, main, aux, gate_row):
    nc = c.nc
    with Stage(nc, name) as st:
        g = st.sb("g", [P, 2, D])
        g_in, g_ready = st.sem("g_in"), st.sem("g_ready")
        with nc.Block() as block:
            @block.sync
            def _(sp):
                sp.dma_start(g[:, 0], row_bcast(gate_row, D)).then_inc(g_in, 16)
                sp.wait_ge(g_in, 16)

            @block.scalar
            def _(act):
                act.wait_ge(g_in, 16)
                act.activation(g[:, 0], g[:, 0], ACT.Sigmoid).then_inc(g_ready, 1)

            @block.vector
            def _(dve):
                dve.wait_ge(g_ready, 1)
                dve.tensor_scalar(g[:, 1], g[:, 0], -1.0, 1.0, ALU.mult, ALU.add)
                dve.drain()
                dve.tensor_tensor(aux[:], aux[:], g[:, 0:1].broadcast_to([P, NT, D]), ALU.mult)
                dve.tensor_tensor(main[:], main[:], g[:, 1:2].broadcast_to([P, NT, D]), ALU.mult)
                dve.drain()
                dve.tensor_tensor(main[:], main[:], aux[:], ALU.add)


def fill(c, name, dst, value):
    with Stage(c.nc, name) as st:
        with c.nc.Block() as block:
            @block.vector
            def _(dve):
                dve.memset(dst, value)


def rope_table(lanes):
    inv = (np.float32(10000.0) ** (-(np.arange(DH // 2, dtype=np.float32) * np.float32(2.0) / np.float32(DH)))).astype(np.float32)
    ang = np.arange(S, dtype=np.float32)[:, None] * inv[None, :]
    co, si = np.cos(ang), np.sin(ang)
    out = np.zeros((2, P, S), np.float32)
    out[0] = 1.0
    for p, j in enumerate(lanes):
        if j >= 0:
            out[0, p] = co[:, j // 2]
            out[1, p] = si[:, j // 2] * (1.0 if j % 2 else -1.0)
    return out


def part_place():
    m = np.zeros((SLOT, 2, 3, SR), np.float32)
    for j, parts in enumerate(PART_PRODUCTS):
        for which in range(2):
            for f in range(DH):
                m[f, which, parts[which], j * DH + f] = 1
    m[DH, 1, 0, SR - 3:] = 1
    heads = np.zeros((P, HC, 2, 3, SR), np.float32)
    for hd in range(HC):
        heads[SLOT * hd:SLOT * (hd + 1), hd] = m
    return heads.reshape(P, -1)


def head_blocks(w):
    out = np.zeros((KC, P, P), np.float32)
    n = P // DH
    for h in range(H):
        a = (h % n) * DH
        out[h // n, a:a + DH, a:a + DH] = w[h].T
    return out


def spread_gather():
    spread = np.zeros((DH, P, P), np.float32)
    for d in range(DH):
        for m in range(P):
            spread[d, m // DH * DH + d, m] = 1.0
    return spread.transpose(1, 0, 2), spread.transpose(2, 0, 1)


def chunk_masks():
    i, j = np.arange(P)[:, None], np.arange(P)[None, :]
    m = [j <= i, j < i, i // 16 == j // 16]
    for w in (16, 32, 64):
        m.append((i // w % 2 == 0) & (j // w == i // w + 1))
    return np.stack(m, 1).astype(np.float32)


def rotation_table():
    ang = np.outer(np.arange(S, dtype=np.float32), np.arange(D // 2, dtype=np.float32))[::-1]
    co, si = np.repeat(np.cos(ang), 2, 1).T, np.repeat(np.sin(ang), 2, 1).T.copy()
    si[1::2] *= -1.0
    return np.stack([co, si]).reshape(2, KC, P, S).astype(np.float32)


SLOT_LANES = [p % SLOT if p % SLOT < DH else -1 for p in range(P)]


def slotted(w):
    out = np.zeros((NC4, P, KC, P), np.float32)
    a = np.asarray(w).reshape(KC, P, NC4, HC, DH).transpose(2, 1, 0, 3, 4)
    out.reshape(NC4, P, KC, HC, SLOT)[..., 0:DH] = a
    return out


def slotted_bias(b, extra):
    out = np.zeros((NC4, HC, SLOT), np.float32)
    if b is not None:
        out[:, :, 0:DH] = np.asarray(b).reshape(NC4, HC, DH)
    out[:, :, DH] = extra
    return out.reshape(NC4, P)


def chunked_v(w):
    return np.ascontiguousarray(np.asarray(w).reshape(KC, P, NC4, HC * DH).transpose(2, 1, 0, 3))


def swap_pairs(w):
    w = np.asarray(w)
    return w.reshape(*w.shape[:-1], -1, 2)[..., ::-1].reshape(w.shape)


def as_cols(b):
    return np.asarray(b).reshape(-1, P).T


def lay_out(i):
    a = {"x": i["x"], "ctxT": i["ctx_1024"].reshape(B * S2, D).T, "mask2T": i["mask_BxS2_ik0"].T}
    qT, kT = i["L0_attn_w_q"].T, i["L0_attn_w_k"].T
    a["l0a_wqk"] = np.stack([slotted(qT), slotted(kT), slotted(swap_pairs(qT)), slotted(swap_pairs(kT))], 2)
    a["l0a_b"] = np.stack([slotted_bias(None, 0.0), slotted_bias(None, 1.0)], 2)
    a["l0a_wv"] = chunked_v(i["L0_attn_w_v"].T)
    a["l0a_wo"] = i["L0_attn_w_o"].T
    a["part_place"] = part_place()
    a["rope_slots"] = rope_table(SLOT_LANES)
    for n in ("Ws", "W", "bcw", "bcb"):
        a["l0x_" + n] = i["L0_xattn_" + n]
    a["l0x_w"] = as_cols(i["L0_xattn_w"])
    a["l0x_b"] = as_cols(i["L0_xattn_b"])
    a["l0x_wcw"] = np.broadcast_to(i["L0_xattn_Wcw"].T, (D, P))
    a["l0x_wcb"] = np.broadcast_to(i["L0_xattn_Wcb"].T, (D, P))
    for n in ("Wr", "W1", "W2", "b2"):
        a["l0f_" + n] = i["L0_ffn_" + n]
    a["l0f_br"] = i["L0_ffn_br"].reshape(E, 1)
    a["l0f_b1"] = i["L0_ffn_b1"].reshape(E, -1, P).transpose(0, 2, 1)
    for n in "kqvp":
        a["l1a_W" + n] = i["L1_attn_W" + n]
    for n in "kq":
        a["l1a_W" + n + "s"] = swap_pairs(i["L1_attn_W" + n])
        a["l1a_b" + n] = as_cols(i["L1_attn_b" + n])
        a["l1a_b" + n + "s"] = as_cols(swap_pairs(i["L1_attn_b" + n]))
    a["l1a_bv"], a["l1a_bp"] = i["L1_attn_bv"], i["L1_attn_bp"]
    a["l1a_cs"] = rotation_table()
    for n in ("Wq", "Wk", "Wv", "Wcq", "Wck", "Wcv", "gamma", "beta", "W1", "b1"):
        a["l1x_" + n] = i["L1_xattn_" + n]
    a["l1f_w1"], a["l1f_w2"] = i["L1_ffn_w1"].T, i["L1_ffn_w2"].T
    a["l1f_b1"], a["l1f_b2"] = i["L1_ffn_b1"], i["L1_ffn_b2"]
    for n in "qkvg":
        a["l2a_w" + n] = i["L2_attn_" + n + "_w"].T
    a["l2a_wqs"], a["l2a_wks"] = swap_pairs(a["l2a_wq"]), swap_pairs(a["l2a_wk"])
    a["l2a_bg"] = as_cols(i["L2_attn_g_b"])
    a["rope_heads"] = rope_table([p % DH for p in range(P)])
    a["l2a_Wq"], a["l2a_Wk"] = head_blocks(i["L2_attn_Wq"]), head_blocks(i["L2_attn_Wk"])
    a["l2a_decay"] = as_cols(i["L2_attn_base_decay_logits"])
    a["spread"], a["gather"] = spread_gather()
    a["l2a_wo"] = i["L2_attn_out_w"].T
    for n in ("out_b", "ln_g", "ln_b"):
        a["l2a_" + n] = i["L2_attn_" + n]
    a["head_mask"] = (np.arange(P)[:, None] // DH == np.arange(P // DH)[None, :]).astype(np.float32)
    a["l2x_wq"], a["l2x_bq"], a["l2x_wo"], a["l2x_bo"] = i["L2_xattn_Wq"], as_cols(i["L2_xattn_bq"]), i["L2_xattn_Wo"], i["L2_xattn_bo"]
    a["l2x_wk"], a["l2x_bk"] = np.tile(i["L2_xattn_Wk"], (1, H)), as_cols(np.tile(i["L2_xattn_bk"], H))
    a["l2x_wv"], a["l2x_bv"] = np.tile(i["L2_xattn_Wv"], (1, H)), np.tile(i["L2_xattn_bv"], H)
    a["l2f_wi"], a["l2f_bi"] = i["L2_ffn_W_in"].T, i["L2_ffn_b_in"]
    width = i["L2_ffn_W_out"].shape[1]
    a["l2f_wo"] = np.pad(i["L2_ffn_W_out"].T, ((0, -width % P), (0, 0)))
    per_head = [i["L3_attn_W" + n].reshape(D, H3, DK) for n in "qkvg"]
    heads = np.concatenate(per_head, 2).transpose(1, 0, 2)
    a["l3a_w"] = np.concatenate([heads, heads[:1]])
    a["l3a_wba"] = np.concatenate([i["L3_attn_Wb"], i["L3_attn_Wa"]], 1)
    a["l3a_alog"], a["l3a_dt"] = i["L3_attn_A_log"], i["L3_attn_dt_bias"]
    a["l3a_nw"] = i["L3_attn_o_norm_w"]
    a["l3a_wo"] = i["L3_attn_Wo"].reshape(H3, DK, D)
    a["l3a_fc"] = i["L3_attn_W_fc"].reshape(D, 2, -1).transpose(1, 0, 2)
    a["l3a_pr"] = i["L3_attn_W_proj"].reshape(2, -1, D)
    a["masks"] = chunk_masks()
    wq, wk, wv = np.split(i["L3_xattn_Wqkv"], 3, 1)
    bq, bk, bv = np.split(i["L3_xattn_bqkv"], 3)
    a["l3x_wqk"] = np.stack([slotted(wq), slotted(wk)], 2)
    a["l3x_b"] = np.stack([slotted_bias(bq, 0.0), slotted_bias(bk, 1.0)], 2)
    a["l3x_wv"] = chunked_v(wv)
    a["l3x_bv"] = np.broadcast_to(bv.reshape(NC4, 1, HC * DH), (NC4, P, HC * DH))
    a["l3x_q"], a["l3x_bq"] = wq, as_cols(bq)
    _, a["l3x_ka"], a["l3x_va"] = np.split(i["L3_xattn_Wqkv_aux"], 3, 1)
    _, bka, a["l3x_bva"] = np.split(i["L3_xattn_bqkv_aux"], 3)
    a["l3x_bka"] = as_cols(bka)
    a["l3x_g"] = np.repeat(i["L3_xattn_g"], DH)
    a["l3x_wo"], a["l3x_bo"] = i["L3_xattn_Wo"], i["L3_xattn_bo"]
    a["l3f_r"] = i["L3_ffn_router_w"].T
    a["l3f_g"], a["l3f_u"], a["l3f_d"] = i["L3_ffn_rg"], i["L3_ffn_ru"], i["L3_ffn_rd"]
    a["l3f_sg"], a["l3f_su"] = (i[f"L3_ffn_s{m}"].reshape(D, 2, -1).transpose(1, 0, 2) for m in "gu")
    a["l3f_sd"] = i["L3_ffn_sd"].reshape(2, -1, D)
    a["l3f_rows"] = np.arange(CAPACITY, dtype=np.float32)
    chunks = -(-CAPACITY // P)
    a["l3f_cols"] = np.arange(chunks * P, dtype=np.float32).reshape(chunks, P).T
    a["l3f_heads"] = np.repeat(np.eye(E, dtype=np.float32), P, axis=1).reshape(E, E, P)
    return a


def l0_attn(c):
    nc, d = c.nc, c.dram
    norm_transpose(c, "l0a_ln", c.x, dst_T=c.xT)
    with nc.sbuf_tensor("l0a_ao", [P, NT, D], F32) as ao:
        self_attention(c, "l0a", d["l0a_wqk"], d["l0a_wv"], ao, True, d["rope_slots"], d["l0a_b"])
        project_add(c, "l0a_o", ao, d["l0a_wo"])


def l0_xattn(c):
    nc, d = c.nc, c.dram
    with nc.sbuf_tensor("l0x_feat", [P, NT, D], F32) as feat, nc.sbuf_tensor("l0x_feT", [P, KC, N], F32) as feT, \
            nc.sbuf_tensor("l0x_txb", [P, KC, B * S2], F32) as txb, nc.sbuf_tensor("l0x_sw", [P, B, S2], F32) as sw, \
            nc.sbuf_tensor("l0x_sb", [P, B, S2], F32) as sbr:
        norm_transpose(c, "l0x_ln", c.x, dst_tok=feat, dst_T=c.xT)
        linear_T(c, "l0x_f", c.xT, [(d["l0x_W"], feT, None, None)])
        linear_T(c, "l0x_t", c.ctxT, [(d["l0x_Ws"], txb, d["l0x_b"], None)], width=B * S2)
        ctx_rows(c, "l0x_s", [d["l0x_wcw"], d["l0x_wcb"]], [sw, sbr])
        additive_attention(c, "l0x", feat, feT, txb, sw, sbr)


def l0_ffn(c):
    nc, d = c.nc, c.dram
    norm_transpose(c, "l0f_ln", c.x, dst_T=c.xT)
    with nc.sbuf_tensor("l0f_wgt", [P, NT, E], F32) as wgt:
        route(c, "l0f_r", c.xT, d["l0f_Wr"], wgt, bias=d["l0f_br"])
        experts(c, "l0f_e", c.xT, wgt, E, 512, d["l0f_W1"], d["l0f_W2"], b1=d["l0f_b1"])
        add_expert_bias(c, "l0f_b", wgt, d["l0f_b2"])


def tile_ctx(c, names):
    ctx = ExitStack()
    return ctx, [ctx.enter_context(c.nc.sbuf_tensor(n, shape, dt)) for n, shape, dt in names]


def l1_attn(c):
    d = c.dram
    ctx, (qT, kT, v) = tile_ctx(c, [("l1a_qT", [P, KC, N], F32), ("l1a_kT", [P, KC, N], F32), ("l1a_v", [P, NT, D], F32)])
    with ctx:
        with ExitStack() as early:
            weights = rope_weights(c, early, "l1a_qkw", [(d["l1a_Wq"], d["l1a_Wqs"], qT, d["l1a_bq"], d["l1a_bqs"]),
                                                         (d["l1a_Wk"], d["l1a_Wks"], kT, d["l1a_bk"], d["l1a_bks"])], d["l1a_cs"], True)
            norm_transpose(c, "l1a_ln", c.x, dst_T=c.xT, ahead=weights[2])
            rope_T(c, "l1a_qk", c.xT, weights, True)
        linear_tok(c, "l1a_vp", c.xT, d["l1a_Wv"], v, bias=d["l1a_bv"])
        with c.nc.sbuf_tensor("l1a_ao", [P, NT, D], F32) as ao:
            softplus_attention(c, "l1a", qT, kT, v, ao)
            project_add(c, "l1a_o", ao, d["l1a_Wp"], bias=d["l1a_bp"])


def l1_xattn(c):
    d = c.dram
    big = [P, NT, D]
    ctx, (hn, qT, kT, v, a) = tile_ctx(c, [("l1x_hn", big, F32), ("l1x_qT", [P, KC, N], F32), ("l1x_kT", [P, KC, N], F32),
                                           ("l1x_v", big, F32), ("l1x_a", big, F32)])
    gb = dict(eps=1e-3, gamma=d["l1x_gamma"], beta=d["l1x_beta"])
    with ctx:
        norm_transpose(c, "l1x_ln", c.x, dst_tok=hn, dst_T=c.xT)
        linear_T(c, "l1x_qk", c.xT, [(d["l1x_Wq"], qT, None, None), (d["l1x_Wk"], kT, None, None)])
        linear_tok(c, "l1x_vp", c.xT, d["l1x_Wv"], v)
        softmax_attention(c, "l1x_self", qT, kT, v, a, hn, True)
        norm_transpose(c, "l1x_ln1", a, dst_tok=hn, dst_T=c.xT, **gb)
        linear_T(c, "l1x_cq", c.xT, [(d["l1x_Wcq"], qT, None, None)])
        linear_T(c, "l1x_ck", c.ctxT, [(d["l1x_Wck"], kT, None, None)], width=B * S2)
        linear_tok(c, "l1x_cv", c.ctxT, d["l1x_Wcv"], v, tiles=B, rows=S2)
        softmax_attention(c, "l1x_cross", qT, kT, v, a, hn, False)
        norm_transpose(c, "l1x_ln2", a, dst_tok=hn, dst_T=c.xT, **gb)
        linear_tok(c, "l1x_f", c.xT, d["l1x_W1"], a, bias=d["l1x_b1"], resid=hn, relu=True)
        norm_transpose(c, "l1x_ln3", a, dst_tok=hn, **gb)
        add_to_x(c, "l1x_add", hn, relu=True)


def l1_ffn(c):
    d = c.dram
    F = d["l1f_b1"].shape[0]
    ctx, (r, w1q, w2q, s1, s2) = tile_ctx(c, [("l1f_r", [P, NT, D], F32), ("l1f_w1q", [P, KC, F], BF16),
                                              ("l1f_w2q", [P, F // P, D], BF16), ("l1f_s1", [P, 1], F32), ("l1f_s2", [P, 1], F32)])
    with ctx:
        norm_transpose(c, "l1f_ln", c.x, dst_tok=r)
        norm_transpose(c, "l1f_rms", r, dst_tok=r, rms=True)
        quantize_weights(c, "l1f_q1", d["l1f_w1"], w1q, s1)
        quantize_weights(c, "l1f_q2", d["l1f_w2"], w2q, s2)
        quantized_ffn(c, "l1f", r, w1q, s1, w2q, s2, d["l1f_b1"], d["l1f_b2"])


def l2_attn(c):
    d = c.dram
    big = [P, NT, D]
    bigT = [P, KC, N]
    ctx, (xn, qT, kT, vT, gT) = tile_ctx(c, [("l2a_xn", big, F32), ("l2a_qT", bigT, F32), ("l2a_kT", bigT, F32),
                                             ("l2a_vT", bigT, F32), ("l2a_gT", bigT, F32)])
    with ctx:
        with ExitStack() as early:
            weights = rope_weights(c, early, "l2a_qkw", [(d["l2a_wq"], d["l2a_wqs"], qT, None, None),
                                                         (d["l2a_wk"], d["l2a_wks"], kT, None, None)], d["rope_heads"], False)
            norm_transpose(c, "l2a_ln", c.x, dst_tok=xn, dst_T=c.xT, ahead=weights[2])
            rope_T(c, "l2a_qk", c.xT, weights, False)
        linear_T(c, "l2a_vg", c.xT, [(d["l2a_wv"], vT, None, None), (d["l2a_wg"], gT, d["l2a_bg"], ACT.Sigmoid)])
        per_head_T(c, "l2a_h", qT, kT, gT, d["l2a_Wq"], d["l2a_Wk"], DH ** -0.5)
        recurrence(c, "l2a_r", qT, kT, vT, d["l2a_decay"], d["spread"], d["gather"])
        with c.nc.sbuf_tensor("l2a_a", big, F32) as a:
            linear_tok(c, "l2a_o", vT, d["l2a_wo"], a, bias=d["l2a_out_b"], resid=xn)
            norm_transpose(c, "l2a_ln1", a, dst_tok=xn, gamma=d["l2a_ln_g"], beta=d["l2a_ln_b"])
        add_to_x(c, "l2a_add", xn)


def l2_xattn(c):
    d = c.dram
    ctx, (qT, kT, v, ao) = tile_ctx(c, [("l2x_qT", [P, KC, N], F32), ("l2x_kT", [P, KC, B * S2], F32),
                                        ("l2x_v", [P, B, D], F32), ("l2x_ao", [P, NT, D], F32)])
    with ctx:
        norm_transpose(c, "l2x_ln", c.x, dst_T=c.xT)
        linear_T(c, "l2x_q", c.xT, [(d["l2x_wq"], qT, d["l2x_bq"], None)])
        linear_T(c, "l2x_k", c.ctxT, [(d["l2x_wk"], kT, d["l2x_bk"], None)], width=B * S2)
        linear_tok(c, "l2x_vp", c.ctxT, d["l2x_wv"], v, bias=d["l2x_bv"], tiles=B, rows=S2)
        cross_heads(c, "l2x", qT, kT, v, ao, clip=1e6 * DH ** 0.5)
        project_add(c, "l2x_o", ao, d["l2x_wo"], bias=d["l2x_bo"])


def l2_ffn(c):
    d = c.dram
    W = TREES * (2 ** (TREE_DEPTH + 1) - 1)
    ctx, (wi, bi, wo) = tile_ctx(c, [("l2f_wisb", [P, KC, W], F32), ("l2f_bisb", [P, W], F32),
                                     ("l2f_wosb", [P, d["l2f_wo"].shape[0] // P, D], F32)])
    with ctx:
        norm_transpose(c, "l2f_ln", c.x, dst_T=c.xT, ahead=[
            (wi[:], d["l2f_wi"].rearrange("(k p) m -> p k m", p=P)), (bi[:], row_bcast(d["l2f_bi"], W)),
            (wo[:], d["l2f_wo"].rearrange("(k p) m -> p k m", p=P))])
        tree_ffn(c, "l2f", c.xT, wi, bi, wo)


def l3_attn(c):
    nc, d = c.nc, c.dram
    with nc.sbuf_tensor("l3a_xi", [P, NT, D], F32) as xi:
        norm_transpose(c, "l3a_ln", c.x, dst_tok=xi)
        norm_transpose(c, "l3a_rms", xi, dst_T=c.xT, eps=1e-6, rms=True)
        tiles = [P, NT, DK]
        ctx, (masks, w_sb, wo_sb, nw, coef, hc, qkvg, bgk, kT, qT, qgT, U, WT, PT) = tile_ctx(c, [
            ("l3a_masks", [P, 6, P], F32), ("l3a_wsb", [P, KC, 4 * DK], F32), ("l3a_wosb", [P, D], F32), ("l3a_nwsb", [P, DK], F32), ("l3a_coef", [P, 5, H3, NT], F32), ("l3a_hc", [P, 5, NT], F32),
            ("l3a_qkvg", [P, NT, 4 * DK], F32)] + [("l3a_" + n, tiles, F32) for n in ("bgk", "kT", "qT", "qgT", "U", "WT", "PT")])
        with ctx:
            with nc.sbuf_tensor("l3a_ba", [P, NT, 2 * H3], F32) as ba:
                linear_tok(c, "l3a_bap", c.xT, d["l3a_wba"], ba)
                delta_gates(c, "l3a_g", ba, d["l3a_dt"], d["l3a_alog"], coef)
            load(c, "l3a_m", [(masks[:], d["masks"]), (nw[:], row_bcast(d["l3a_nw"], DK)),
                              (w_sb[:], d["l3a_w"][0].rearrange("(k p) m -> p k m", p=P))])
            with nc.Fori(0, H3) as head:
                delta_project(c, "l3a_p", head, w_sb, coef, hc, qkvg, bgk, kT, qT, qgT)
                delta_invert(c, "l3a_i", head, d["l3a_w"], d["l3a_wo"], w_sb, wo_sb, masks, hc, qkvg, bgk, kT, qT, U, WT, PT)
                delta_scan(c, "l3a_s", hc, qkvg, nw, qgT, U, WT, PT, qT)
                delta_output(c, "l3a_o", wo_sb, qkvg, qT, U, WT, xi)
        norm_transpose(c, "l3a_ln2", xi, dst_T=c.xT, eps=1e-6, rms=True)
        add_to_x(c, "l3a_add", xi)
    with nc.sbuf_tensor("l3a_one", [P, NT, 2], F32) as one:
        fill(c, "l3a_f1", one[:], 1.0)
        experts(c, "l3a_mlp", c.xT, one, 2, d["l3a_fc"].shape[2], d["l3a_fc"], d["l3a_pr"], square=True)


def l3_xattn(c):
    nc, d = c.nc, c.dram
    norm_transpose(c, "l3x_ln", c.x, dst_T=c.xT)
    with nc.sbuf_tensor("l3x_ao", [P, NT, D], F32) as ao:
        self_attention(c, "l3x_s", d["l3x_wqk"], d["l3x_wv"], ao, False, None, d["l3x_b"], d["l3x_bv"])
        ctx, (qT, kT, v, aux) = tile_ctx(c, [("l3x_qT", [P, KC, N], F32), ("l3x_kT", [P, KC, B * S2], F32),
                                             ("l3x_v", [P, B, D], F32), ("l3x_aux", [P, NT, D], F32)])
        with ctx:
            linear_T(c, "l3x_qp", c.xT, [(d["l3x_q"], qT, d["l3x_bq"], None)])
            linear_T(c, "l3x_kp", c.ctxT, [(d["l3x_ka"], kT, d["l3x_bka"], None)], width=B * S2)
            linear_tok(c, "l3x_vp", c.ctxT, d["l3x_va"], v, bias=d["l3x_bva"], tiles=B, rows=S2)
            cross_heads(c, "l3x_c", qT, kT, v, aux)
            mix_heads(c, "l3x_m", ao, aux, d["l3x_g"])
        project_add(c, "l3x_o", ao, d["l3x_wo"], bias=d["l3x_bo"])


def l3_ffn(c):
    nc, d = c.nc, c.dram
    ctx, (wgt, slot, one, feat) = tile_ctx(c, [("l3f_wgt", [P, NT, E], F32), ("l3f_slot", [P, NT, E + 2], F32),
                                               ("l3f_one", [P, NT, 2], F32), ("l3f_feat", [P, NT, D], F32)])
    with ctx:
        fill(c, "l3f_ones", one[:], 1.0)
        norm_transpose(c, "l3f_ln", c.x, dst_tok=feat, dst_T=c.xT)
        experts(c, "l3f_s", c.xT, one, 2, d["l3f_sg"].shape[2], d["l3f_su"], d["l3f_sd"], gate=d["l3f_sg"])
        with nc.sbuf_tensor("l3f_rT", [P, KC, N], F32) as rT:
            norm_transpose(c, "l3f_rms", feat, dst_T=rT, eps=float(np.finfo(np.float32).eps), rms=True)
            route(c, "l3f_route", rT, d["l3f_r"], wgt, top=2, slot=slot)
        routed_experts(c, "l3f_e", feat, wgt, slot, d["l3f_g"].shape[2], d["l3f_g"], d["l3f_u"], d["l3f_d"],
                       d["l3f_rows"], d["l3f_cols"], d["l3f_heads"])


SUBLAYERS = [l0_attn, l0_xattn, l0_ffn, l1_attn, l1_xattn, l1_ffn, l2_attn, l2_xattn, l2_ffn, l3_attn, l3_xattn, l3_ffn]


def store(c, out):
    with Stage(c.nc, "store") as st:
        stored = st.sem("stored")
        with c.nc.Block() as block:
            @block.sync
            def _(sp):
                sp.dma_start(out.rearrange("b (t p) d -> p (b t) d", p=P), c.x[:]).then_inc(stored, 16)
                sp.wait_ge(stored, 16)


def decoder_kernel(nc, dram, out, sublayers):
    with ExitStack() as ctx:
        c = Core(nc, ctx, dram)
        setup(c)
        for f in sublayers:
            f(c)
        store(c, out)


def build(nc, inputs, sublayers):
    arrays, dram = {}, {}
    for name, a in lay_out({k: np.asarray(v) for k, v in inputs.items()}).items():
        a = np.ascontiguousarray(a)
        arrays[f"in_{name}"] = a
        dram[name] = nc.dram_tensor(f"in_{name}", a.shape, mybir.dt.from_np(a.dtype), kind="ExternalInput").ap()
    out = nc.dram_tensor("out_x", (B, S, D), F32, kind="ExternalOutput").ap()
    decoder_kernel(nc, dram, out, sublayers)
    return arrays


def kernel(**inputs):
    import concourse.bacc as bacc
    from concourse.bass_utils import run_bass_kernel_spmd
    nc = bacc.Bacc("TRN2", target_bir_lowering=False, num_devices=1)
    arrays = build(nc, inputs, SUBLAYERS)
    r = run_bass_kernel_spmd(nc, [arrays], core_ids=[0])
    return r.results[0]["out_x"]
```
